# Optimizing a Trainium2 kernel written in Bass

```python
import numpy as np
import jax
import jax.numpy as jnp

def _softmax(x, axis=-1):
    return jax.nn.softmax(x, axis=axis)

def _gelu(x):
    return jax.nn.gelu(x, approximate=True)

def _silu(x):
    return jax.nn.silu(x)

def _sigmoid(x):
    return jax.nn.sigmoid(x)

def _layernorm(x, axis=-1, eps=1e-05):
    m = jnp.mean(x, axis=axis, keepdims=True)
    v = jnp.var(x, axis=axis, keepdims=True)
    return (x - m) / jnp.sqrt(v + eps)

def _scatter_add(tgt, idx, src, axis=0):
    return tgt.at[idx].add(src)

def _segment_sum(src, seg, n):
    return jax.ops.segment_sum(src, seg, n)
kernel_name = 'mk_perceiver_d2_seqx_r4_5500a8'

def setup_inputs(seed: int=0):
    np.random.seed(seed)
    _w = jnp.asarray

    def _rec_inputs():
        import jax
        import jax.numpy as jnp
        _rk = jax.random.key(seed)
        x = -0.0002928 + 1 * jax.random.normal(jax.random.fold_in(_rk, 1), (8, 64, 256), jnp.float32)
        _lenS = 64 - jax.random.randint(jax.random.fold_in(_rk, 7), (8,), 0, max(1, 64 // 4) + 1, jnp.int32)
        _lenS2 = 1601 - jax.random.randint(jax.random.fold_in(_rk, 8), (8,), 0, max(1, 1601 // 4) + 1, jnp.int32)
        _ctx_768P = jax.random.normal(jax.random.fold_in(_rk, 11), (8, 16, 192), jnp.float32)
        _ctx_768c = jax.random.dirichlet(jax.random.fold_in(_rk, 511), 0.3 * jnp.ones((16,), jnp.float32), (8, 1601))
        _ctx_768t = jnp.einsum('bsk,bkd->bsd', _ctx_768c, _ctx_768P)
        _ctx_768t = _ctx_768t * jax.lax.rsqrt(jnp.mean(jnp.square(_ctx_768t)) + 1e-12) * 0.953939
        ctx_768 = 2.09791e-05 + 1.00001 * (_ctx_768t + 0.3 * jax.random.normal(jax.random.fold_in(_rk, 611), (8, 1601, 192), jnp.float32))
        return (x, ctx_768)
    x, ctx_768 = _rec_inputs()

    def _L0_xattn_setup():
        import jax, jax.numpy as jnp
        import numpy as np
        QUERY_DIM, KV_DIM, EMBED_DIM, NUM_HEADS = (256, 192, 256, 16)
        HEAD_DIM = EMBED_DIM // NUM_HEADS
        SCALE = HEAD_DIM ** (-0.5)
        LN_EPS = 1e-05

        def _l2norm(x, eps=1e-12):
            n = jnp.sqrt(jnp.sum(x * x, axis=-1, keepdims=True))
            return x / jnp.maximum(n, eps)
        key = jax.random.key(seed)
        ks = jax.random.split(key, 12)
        B, Nq, Nk = (2, 512, 512)
        s = lambda d: 1.0 / np.sqrt(d)
        return {'query': jax.random.normal(ks[0], (B, Nq, QUERY_DIM), jnp.float32), 'key': jax.random.normal(ks[1], (B, Nk, KV_DIM), jnp.float32), 'value': jax.random.normal(ks[2], (B, Nk, KV_DIM), jnp.float32), 'Wq': jax.random.normal(ks[3], (QUERY_DIM, EMBED_DIM), jnp.float32) * s(QUERY_DIM), 'bq': jnp.zeros((EMBED_DIM,), jnp.float32), 'Wk': jax.random.normal(ks[4], (KV_DIM, EMBED_DIM), jnp.float32) * s(KV_DIM), 'bk': jnp.zeros((EMBED_DIM,), jnp.float32), 'Wv': jax.random.normal(ks[5], (KV_DIM, EMBED_DIM), jnp.float32) * s(KV_DIM), 'bv': jnp.zeros((EMBED_DIM,), jnp.float32), 'Wo': jax.random.normal(ks[6], (EMBED_DIM, EMBED_DIM), jnp.float32) * s(EMBED_DIM), 'bo': jnp.zeros((EMBED_DIM,), jnp.float32), 'ln_gamma': jnp.ones((EMBED_DIM,), jnp.float32), 'ln_beta': jnp.zeros((EMBED_DIM,), jnp.float32)}
    _L0_xattn_all = _L0_xattn_setup()
    _L0_xattn_in = {k: v for k, v in _L0_xattn_all.items() if k in ('Wq', 'bq', 'Wk', 'bk', 'Wv', 'bv', 'Wo', 'bo', 'ln_gamma', 'ln_beta')}
    del _L0_xattn_all

    def _L0_attn_setup():
        import math
        import jax, jax.numpy as jnp
        import numpy as np
        HEADS = 16
        DIM_HEAD = 64
        NUM_NULL_KV = 2
        ATTN_SCALE = 8.0
        LN_EPS = 1e-05

        def _alibi_slopes(heads):
            start = 2.0 ** (-2.0 ** (-(math.log2(heads) - 3.0)))
            return np.array([start * start ** i for i in range(heads)], dtype=np.float32)

        def _l2norm(t):
            return t / jnp.maximum(jnp.linalg.norm(t, axis=-1, keepdims=True), 1e-12)
        key = jax.random.key(seed)
        ks = jax.random.split(key, 5)
        b, n, dim = (4, 512, 256)
        return {'x': jax.random.normal(ks[0], (b, n, dim), dtype=jnp.float32), 'gamma': jnp.ones((dim,), dtype=jnp.float32), 'w_q': jax.random.normal(ks[1], (dim, HEADS * DIM_HEAD), dtype=jnp.float32) * 0.02, 'w_kv': jax.random.normal(ks[2], (dim, 2 * HEADS * DIM_HEAD), dtype=jnp.float32) * 0.02, 'null_kv': jax.random.normal(ks[3], (HEADS, 2 * NUM_NULL_KV, DIM_HEAD), dtype=jnp.float32), 'q_scale': jnp.ones((DIM_HEAD,), dtype=jnp.float32), 'k_scale': jnp.ones((DIM_HEAD,), dtype=jnp.float32), 'w_out': jax.random.normal(ks[4], (HEADS * DIM_HEAD, dim), dtype=jnp.float32) * 0.02}
    _L0_attn_all = _L0_attn_setup()
    _L0_attn_in = {k: v for k, v in _L0_attn_all.items() if k in ('gamma', 'w_q', 'w_kv', 'null_kv', 'q_scale', 'k_scale', 'w_out')}
    del _L0_attn_all

    def _L0_ffn_setup():
        import jax, jax.numpy as jnp
        import numpy as np
        H = 256
        I = 512
        E = 8
        B, S = (2, 1024)
        EPS = 1e-05
        INIT = 0.02

        def _layernorm(x, w, b):
            mu = jnp.mean(x, axis=-1, keepdims=True)
            var = jnp.mean(jnp.square(x - mu), axis=-1, keepdims=True)
            return (x - mu) * jax.lax.rsqrt(var + EPS) * w + b
        key = jax.random.key(seed)
        ks = jax.random.split(key, 9)
        return {'hidden_states': jax.random.normal(ks[0], (B, S, H), jnp.float32), 'ln_w': jnp.ones((H,), jnp.float32), 'ln_b': jnp.zeros((H,), jnp.float32), 'router_w': jax.random.normal(ks[1], (H, E), jnp.float32) * INIT, 'gate_w': jax.random.normal(ks[2], (E, H, I), jnp.float32) * INIT, 'up_w': jax.random.normal(ks[3], (E, H, I), jnp.float32) * INIT, 'down_w': jax.random.normal(ks[4], (E, I, H), jnp.float32) * INIT, 'sh_gate': jax.random.normal(ks[5], (H, I), jnp.float32) * INIT, 'sh_up': jax.random.normal(ks[6], (H, I), jnp.float32) * INIT, 'sh_down': jax.random.normal(ks[7], (I, H), jnp.float32) * INIT}
    _L0_ffn_all = _L0_ffn_setup()
    _L0_ffn_in = {k: v for k, v in _L0_ffn_all.items() if k in ('ln_w', 'ln_b', 'router_w', 'gate_w', 'up_w', 'down_w', 'sh_gate', 'sh_up', 'sh_down')}
    del _L0_ffn_all

    def _L1_xattn_setup():
        import jax, jax.numpy as jnp
        import numpy as np
        DIM = 256
        CTX_DIM = 192
        H = 16
        DH = 64
        INNER = H * DH
        EPS = 1e-05

        def layer_norm(x, gamma, beta):
            mu = jnp.mean(x, axis=-1, keepdims=True)
            var = jnp.mean(jnp.square(x - mu), axis=-1, keepdims=True)
            return (x - mu) * jax.lax.rsqrt(var + EPS) * gamma + beta
        key = jax.random.key(seed)
        ks = jax.random.split(key, 8)
        B, N, M = (4, 512, 512)
        x = jax.random.normal(ks[0], (B, N, DIM), dtype=jnp.float32)
        context = jax.random.normal(ks[1], (B, M, CTX_DIM), dtype=jnp.float32)
        g_x = jnp.ones((DIM,), jnp.float32)
        b_x = jnp.zeros((DIM,), jnp.float32)
        g_c = jnp.ones((CTX_DIM,), jnp.float32)
        b_c = jnp.zeros((CTX_DIM,), jnp.float32)
        Wq = jax.random.normal(ks[2], (DIM, INNER), dtype=jnp.float32) / np.sqrt(DIM)
        Wk = jax.random.normal(ks[3], (CTX_DIM, INNER), dtype=jnp.float32) / np.sqrt(CTX_DIM)
        Wv = jax.random.normal(ks[4], (CTX_DIM, INNER), dtype=jnp.float32) / np.sqrt(CTX_DIM)
        Wo = jax.random.normal(ks[5], (INNER, DIM), dtype=jnp.float32) / np.sqrt(INNER)
        return {'x': x, 'context': context, 'g_x': g_x, 'b_x': b_x, 'g_c': g_c, 'b_c': b_c, 'Wq': Wq, 'Wk': Wk, 'Wv': Wv, 'Wo': Wo}
    _L1_xattn_all = _L1_xattn_setup()
    _L1_xattn_in = {k: v for k, v in _L1_xattn_all.items() if k in ('g_x', 'b_x', 'g_c', 'b_c', 'Wq', 'Wk', 'Wv', 'Wo')}
    del _L1_xattn_all

    def _L1_attn_setup():
        import jax, jax.numpy as jnp
        import numpy as np
        B, N, DIM = (4, 256, 256)
        H, DH = (16, 64)
        NUM_MEM = 4
        TOPK = 64
        QK_SCALE = 10.0

        def l2norm(t, eps=1e-12):
            return t / jnp.clip(jnp.linalg.norm(t, axis=-1, keepdims=True), eps)
        key = jax.random.key(seed)
        ks = jax.random.split(key, 12)
        s = 0.02
        inp = {'x': jax.random.normal(ks[0], (B, N, DIM), dtype=jnp.float32), 'Wq': jax.random.normal(ks[1], (DIM, H * DH), dtype=jnp.float32) * s, 'Wk': jax.random.normal(ks[2], (DIM, H * DH), dtype=jnp.float32) * s, 'Wv': jax.random.normal(ks[3], (DIM, H * DH), dtype=jnp.float32) * s, 'W_pre_th': jax.random.normal(ks[4], (H, H), dtype=jnp.float32) * (1.0 / H) ** 0.5, 'W_post_th': jax.random.normal(ks[5], (H, H), dtype=jnp.float32) * (1.0 / H) ** 0.5, 'mem_k': jax.random.normal(ks[6], (H, NUM_MEM, DH), dtype=jnp.float32), 'mem_v': jax.random.normal(ks[7], (H, NUM_MEM, DH), dtype=jnp.float32), 'head_scale_params': jnp.ones((1, H, 1, 1), dtype=jnp.float32), 'Wg': jax.random.normal(ks[8], (DIM, H * DH), dtype=jnp.float32) * s, 'bg': jnp.ones((H * DH,), dtype=jnp.float32), 'Wo': jax.random.normal(ks[9], (H * DH, DIM), dtype=jnp.float32) * s}
        return inp
    _L1_attn_all = _L1_attn_setup()
    _L1_attn_in = {k: v for k, v in _L1_attn_all.items() if k in ('Wq', 'Wk', 'Wv', 'W_pre_th', 'W_post_th', 'mem_k', 'mem_v', 'head_scale_params', 'Wg', 'bg', 'Wo')}
    del _L1_attn_all

    def _L1_ffn_setup():
        import jax, jax.numpy as jnp
        import numpy as np
        D_MODEL = 256
        NUM_EXPERTS = 8
        TOP_K = 2
        key = jax.random.key(seed)
        k_x, k_g, k_w1, k_w2 = jax.random.split(key, 4)
        B, S, D, E = (4, 512, D_MODEL, NUM_EXPERTS)
        s_in = 1.0 / np.sqrt(D)
        s_hid = 1.0 / np.sqrt(4 * D)
        return {'x': jax.random.normal(k_x, (B, S, D), dtype=jnp.float32), 'gate_w': jax.random.uniform(k_g, (E, D), jnp.float32, -s_in, s_in), 'w1': jax.random.uniform(k_w1, (E, 4 * D, D), jnp.float32, -s_in, s_in), 'w2': jax.random.uniform(k_w2, (E, D, 4 * D), jnp.float32, -s_hid, s_hid)}
    _L1_ffn_all = _L1_ffn_setup()
    _L1_ffn_in = {k: v for k, v in _L1_ffn_all.items() if k in ('gate_w', 'w1', 'w2')}
    del _L1_ffn_all
    return {'x': x, 'ctx_768': ctx_768, 'L0_xattn_Wq': _L0_xattn_in['Wq'], 'L0_xattn_bq': _L0_xattn_in['bq'], 'L0_xattn_Wk': _L0_xattn_in['Wk'], 'L0_xattn_bk': _L0_xattn_in['bk'], 'L0_xattn_Wv': _L0_xattn_in['Wv'], 'L0_xattn_bv': _L0_xattn_in['bv'], 'L0_xattn_Wo': _L0_xattn_in['Wo'], 'L0_xattn_bo': _L0_xattn_in['bo'], 'L0_xattn_ln_gamma': _L0_xattn_in['ln_gamma'], 'L0_xattn_ln_beta': _L0_xattn_in['ln_beta'], 'L0_attn_gamma': _L0_attn_in['gamma'], 'L0_attn_w_q': _L0_attn_in['w_q'], 'L0_attn_w_kv': _L0_attn_in['w_kv'], 'L0_attn_null_kv': _L0_attn_in['null_kv'], 'L0_attn_q_scale': _L0_attn_in['q_scale'], 'L0_attn_k_scale': _L0_attn_in['k_scale'], 'L0_attn_w_out': _L0_attn_in['w_out'], 'L0_ffn_ln_w': _L0_ffn_in['ln_w'], 'L0_ffn_ln_b': _L0_ffn_in['ln_b'], 'L0_ffn_router_w': _L0_ffn_in['router_w'], 'L0_ffn_gate_w': _L0_ffn_in['gate_w'], 'L0_ffn_up_w': _L0_ffn_in['up_w'], 'L0_ffn_down_w': _L0_ffn_in['down_w'], 'L0_ffn_sh_gate': _L0_ffn_in['sh_gate'], 'L0_ffn_sh_up': _L0_ffn_in['sh_up'], 'L0_ffn_sh_down': _L0_ffn_in['sh_down'], 'L1_xattn_g_x': _L1_xattn_in['g_x'], 'L1_xattn_b_x': _L1_xattn_in['b_x'], 'L1_xattn_g_c': _L1_xattn_in['g_c'], 'L1_xattn_b_c': _L1_xattn_in['b_c'], 'L1_xattn_Wq': _L1_xattn_in['Wq'], 'L1_xattn_Wk': _L1_xattn_in['Wk'], 'L1_xattn_Wv': _L1_xattn_in['Wv'], 'L1_xattn_Wo': _L1_xattn_in['Wo'], 'L1_attn_Wq': _L1_attn_in['Wq'], 'L1_attn_Wk': _L1_attn_in['Wk'], 'L1_attn_Wv': _L1_attn_in['Wv'], 'L1_attn_W_pre_th': _L1_attn_in['W_pre_th'], 'L1_attn_W_post_th': _L1_attn_in['W_post_th'], 'L1_attn_mem_k': _L1_attn_in['mem_k'], 'L1_attn_mem_v': _L1_attn_in['mem_v'], 'L1_attn_head_scale_params': _L1_attn_in['head_scale_params'], 'L1_attn_Wg': _L1_attn_in['Wg'], 'L1_attn_bg': _L1_attn_in['bg'], 'L1_attn_Wo': _L1_attn_in['Wo'], 'L1_ffn_gate_w': _L1_ffn_in['gate_w'], 'L1_ffn_w1': _L1_ffn_in['w1'], 'L1_ffn_w2': _L1_ffn_in['w2']}

def reference(x, ctx_768, L0_xattn_Wq, L0_xattn_bq, L0_xattn_Wk, L0_xattn_bk, L0_xattn_Wv, L0_xattn_bv, L0_xattn_Wo, L0_xattn_bo, L0_xattn_ln_gamma, L0_xattn_ln_beta, L0_attn_gamma, L0_attn_w_q, L0_attn_w_kv, L0_attn_null_kv, L0_attn_q_scale, L0_attn_k_scale, L0_attn_w_out, L0_ffn_ln_w, L0_ffn_ln_b, L0_ffn_router_w, L0_ffn_gate_w, L0_ffn_up_w, L0_ffn_down_w, L0_ffn_sh_gate, L0_ffn_sh_up, L0_ffn_sh_down, L1_xattn_g_x, L1_xattn_b_x, L1_xattn_g_c, L1_xattn_b_c, L1_xattn_Wq, L1_xattn_Wk, L1_xattn_Wv, L1_xattn_Wo, L1_attn_Wq, L1_attn_Wk, L1_attn_Wv, L1_attn_W_pre_th, L1_attn_W_post_th, L1_attn_mem_k, L1_attn_mem_v, L1_attn_head_scale_params, L1_attn_Wg, L1_attn_bg, L1_attn_Wo, L1_ffn_gate_w, L1_ffn_w1, L1_ffn_w2):
    import jax
    import jax.numpy as jnp

    def _L0_xattn_ref(query, key, value, Wq, bq, Wk, bk, Wv, bv, Wo, bo, ln_gamma, ln_beta):
        import jax, jax.numpy as jnp
        import numpy as np
        QUERY_DIM, KV_DIM, EMBED_DIM, NUM_HEADS = (256, 192, 256, 16)
        HEAD_DIM = EMBED_DIM // NUM_HEADS
        SCALE = HEAD_DIM ** (-0.5)
        LN_EPS = 1e-05

        def _l2norm(x, eps=1e-12):
            n = jnp.sqrt(jnp.sum(x * x, axis=-1, keepdims=True))
            return x / jnp.maximum(n, eps)
        B, Nq, _ = query.shape
        Nk = key.shape[1]
        Qp = query @ Wq + bq
        K = _l2norm(key @ Wk + bk)
        V = value @ Wv + bv
        Q = _l2norm(Qp)
        Q = Q.reshape(B, Nq, NUM_HEADS, HEAD_DIM).transpose(0, 2, 1, 3)
        K = K.reshape(B, Nk, NUM_HEADS, HEAD_DIM).transpose(0, 2, 1, 3)
        V = V.reshape(B, Nk, NUM_HEADS, HEAD_DIM).transpose(0, 2, 1, 3)
        scores = jnp.einsum('bhqd,bhkd->bhqk', Q, K) * SCALE
        attn = jax.nn.softmax(scores, axis=-1)
        out = jnp.einsum('bhqk,bhkd->bhqd', attn, V)
        out = out.transpose(0, 2, 1, 3).reshape(B, Nq, EMBED_DIM)
        out = out @ Wo + bo
        x = out + Qp
        mu = jnp.mean(x, axis=-1, keepdims=True)
        var = jnp.mean((x - mu) ** 2, axis=-1, keepdims=True)
        return (x - mu) / jnp.sqrt(var + LN_EPS) * ln_gamma + ln_beta

    def _L0_attn_ref(x, gamma, w_q, w_kv, null_kv, q_scale, k_scale, w_out):
        import math
        import jax, jax.numpy as jnp
        import numpy as np
        HEADS = 16
        DIM_HEAD = 64
        NUM_NULL_KV = 2
        ATTN_SCALE = 8.0
        LN_EPS = 1e-05

        def _alibi_slopes(heads):
            start = 2.0 ** (-2.0 ** (-(math.log2(heads) - 3.0)))
            return np.array([start * start ** i for i in range(heads)], dtype=np.float32)

        def _l2norm(t):
            return t / jnp.maximum(jnp.linalg.norm(t, axis=-1, keepdims=True), 1e-12)
        b, n, dim = x.shape
        mu = jnp.mean(x, axis=-1, keepdims=True)
        var = jnp.mean(jnp.square(x - mu), axis=-1, keepdims=True)
        xn = (x - mu) * jax.lax.rsqrt(var + LN_EPS) * gamma
        q = (xn @ w_q).reshape(b, n, HEADS, DIM_HEAD).transpose(0, 2, 1, 3)
        kv = xn @ w_kv
        k, v = jnp.split(kv, 2, axis=-1)
        k = k.reshape(b, n, HEADS, DIM_HEAD).transpose(0, 2, 1, 3)
        v = v.reshape(b, n, HEADS, DIM_HEAD).transpose(0, 2, 1, 3)
        nkv = null_kv.reshape(HEADS, NUM_NULL_KV, 2, DIM_HEAD)
        nk = jnp.broadcast_to(nkv[:, :, 0][None], (b, HEADS, NUM_NULL_KV, DIM_HEAD))
        nv = jnp.broadcast_to(nkv[:, :, 1][None], (b, HEADS, NUM_NULL_KV, DIM_HEAD))
        k = jnp.concatenate([nk, k], axis=2)
        v = jnp.concatenate([nv, v], axis=2)
        q = _l2norm(q) * q_scale
        k = _l2norm(k) * k_scale
        sim = jnp.einsum('bhid,bhjd->bhij', q, k) * ATTN_SCALE
        j = n + NUM_NULL_KV
        rows = jnp.arange(n)
        cols = jnp.arange(j)
        dist = -jnp.abs(cols[None, :] - (rows[:, None] + NUM_NULL_KV)).astype(sim.dtype)
        slopes = jnp.asarray(_alibi_slopes(HEADS))
        sim = sim + dist[None, None] * slopes[None, :, None, None]
        causal_mask = cols[None, :] > rows[:, None] + NUM_NULL_KV
        neg = -jnp.finfo(sim.dtype).max
        sim = jnp.where(causal_mask[None, None], neg, sim)
        attn = jax.nn.softmax(sim, axis=-1)
        out = jnp.einsum('bhij,bhjd->bhid', attn, v)
        out = out.transpose(0, 2, 1, 3).reshape(b, n, HEADS * DIM_HEAD)
        return out @ w_out

    def _L0_ffn_ref(hidden_states, ln_w, ln_b, router_w, gate_w, up_w, down_w, sh_gate, sh_up, sh_down):
        import jax, jax.numpy as jnp
        import numpy as np
        H = 256
        I = 512
        E = 8
        B, S = (2, 1024)
        EPS = 1e-05
        INIT = 0.02

        def _layernorm(x, w, b):
            mu = jnp.mean(x, axis=-1, keepdims=True)
            var = jnp.mean(jnp.square(x - mu), axis=-1, keepdims=True)
            return (x - mu) * jax.lax.rsqrt(var + EPS) * w + b
        b, s, h = hidden_states.shape
        normed = _layernorm(hidden_states, ln_w, ln_b)
        xf = normed.reshape(-1, h)
        logits = xf @ router_w
        top_idx = jnp.argmax(logits, axis=-1)
        top_score = jax.nn.sigmoid(jnp.max(logits, axis=-1))

        def body(acc, ew):
            g, u, d, e = ew
            w = jnp.where(top_idx == e, top_score, 0.0)[:, None]
            xe = xf * w
            hmid = jax.nn.silu(xe @ g) * (xe @ u)
            return (acc + hmid @ d, None)
        routed, _ = jax.lax.scan(body, jnp.zeros_like(xf), (gate_w, up_w, down_w, jnp.arange(E)))
        shared = jax.nn.silu(xf @ sh_gate) * (xf @ sh_up) @ sh_down
        moe_out = (routed + shared).reshape(b, s, h)
        return hidden_states + moe_out

    def _L1_xattn_ref(x, context, g_x, b_x, g_c, b_c, Wq, Wk, Wv, Wo):
        import jax, jax.numpy as jnp
        import numpy as np
        DIM = 256
        CTX_DIM = 192
        H = 16
        DH = 64
        INNER = H * DH
        EPS = 1e-05

        def layer_norm(x, gamma, beta):
            mu = jnp.mean(x, axis=-1, keepdims=True)
            var = jnp.mean(jnp.square(x - mu), axis=-1, keepdims=True)
            return (x - mu) * jax.lax.rsqrt(var + EPS) * gamma + beta
        B, N, _ = x.shape
        M = context.shape[1]
        xn = layer_norm(x, g_x, b_x)
        cn = layer_norm(context, g_c, b_c)
        q = (xn @ Wq).reshape(B, N, H, DH).transpose(0, 2, 1, 3)
        k = (cn @ Wk).reshape(B, M, H, DH).transpose(0, 2, 1, 3)
        v = (cn @ Wv).reshape(B, M, H, DH).transpose(0, 2, 1, 3)
        scale = jnp.float32(1.0 / np.sqrt(DH))
        sim = jnp.einsum('bhid,bhjd->bhij', q, k) * scale
        attn = jax.nn.softmax(sim, axis=-1)
        out = jnp.einsum('bhij,bhjd->bhid', attn, v)
        out = out.transpose(0, 2, 1, 3).reshape(B, N, INNER)
        return out @ Wo

    def _L1_attn_ref(x, Wq, Wk, Wv, W_pre_th, W_post_th, mem_k, mem_v, head_scale_params, Wg, bg, Wo):
        import jax, jax.numpy as jnp
        import numpy as np
        B, N, DIM = (4, 256, 256)
        H, DH = (16, 64)
        NUM_MEM = 4
        TOPK = 64
        QK_SCALE = 10.0

        def l2norm(t, eps=1e-12):
            return t / jnp.clip(jnp.linalg.norm(t, axis=-1, keepdims=True), eps)
        b, n, _ = x.shape
        q = (x @ Wq).reshape(b, n, H, DH).transpose(0, 2, 1, 3)
        k = (x @ Wk).reshape(b, n, H, DH).transpose(0, 2, 1, 3)
        v = (x @ Wv).reshape(b, n, H, DH).transpose(0, 2, 1, 3)
        mk = jnp.broadcast_to(mem_k[None], (b, H, NUM_MEM, DH))
        mv = jnp.broadcast_to(mem_v[None], (b, H, NUM_MEM, DH))
        k = jnp.concatenate([mk, k], axis=2)
        v = jnp.concatenate([mv, v], axis=2)
        q = l2norm(q)
        k = l2norm(k)
        dots = jnp.einsum('bhid,bhjd->bhij', q, k) * QK_SCALE
        dots = jnp.einsum('hg,bgij->bhij', W_pre_th, dots)
        mask_value = -jnp.finfo(dots.dtype).max
        j = n + NUM_MEM
        col_pos = jnp.arange(j) - NUM_MEM
        causal = jnp.arange(n)[:, None] < col_pos[None, :]
        dots = jnp.where(causal[None, None], mask_value, dots)
        top = jax.lax.top_k(dots, TOPK)[0]
        vk = top[..., -1:]
        dots = jnp.where(dots < vk, mask_value, dots)
        attn = jax.nn.softmax(dots, axis=-1)
        attn = jnp.einsum('hg,bgij->bhij', W_post_th, attn)
        out = jnp.einsum('bhij,bhjd->bhid', attn, v)
        out = out * head_scale_params
        out = out.transpose(0, 2, 1, 3).reshape(b, n, H * DH)
        gates = x @ Wg + bg
        out = out * jax.nn.sigmoid(gates)
        return out @ Wo

    def _L1_ffn_ref(x, gate_w, w1, w2):
        import jax, jax.numpy as jnp
        import numpy as np
        D_MODEL = 256
        NUM_EXPERTS = 8
        TOP_K = 2
        gate_logits = jnp.einsum('bsd,ed->bse', x, gate_w)
        top_v, top_i = jax.lax.top_k(gate_logits, TOP_K)
        gates = jax.nn.softmax(top_v, axis=-1)
        combine = jnp.sum(jax.nn.one_hot(top_i, NUM_EXPERTS, dtype=x.dtype) * gates[..., None], axis=-2)
        out = jnp.zeros_like(x)
        for e in range(NUM_EXPERTS):
            h = jax.nn.relu(jnp.einsum('bsd,fd->bsf', x, w1[e]))
            y = jnp.einsum('bsf,df->bsd', h, w2[e])
            out = out + combine[..., e, None] * y
        return out
    x = x + _L0_xattn_ref(_layernorm(x, axis=-1), ctx_768, ctx_768, L0_xattn_Wq, L0_xattn_bq, L0_xattn_Wk, L0_xattn_bk, L0_xattn_Wv, L0_xattn_bv, L0_xattn_Wo, L0_xattn_bo, L0_xattn_ln_gamma, L0_xattn_ln_beta)
    x = x + _L0_attn_ref(_layernorm(x, axis=-1), L0_attn_gamma, L0_attn_w_q, L0_attn_w_kv, L0_attn_null_kv, L0_attn_q_scale, L0_attn_k_scale, L0_attn_w_out)
    x = x + _L0_ffn_ref(_layernorm(x, axis=-1), L0_ffn_ln_w, L0_ffn_ln_b, L0_ffn_router_w, L0_ffn_gate_w, L0_ffn_up_w, L0_ffn_down_w, L0_ffn_sh_gate, L0_ffn_sh_up, L0_ffn_sh_down)
    x = x + _L1_xattn_ref(_layernorm(x, axis=-1), ctx_768, L1_xattn_g_x, L1_xattn_b_x, L1_xattn_g_c, L1_xattn_b_c, L1_xattn_Wq, L1_xattn_Wk, L1_xattn_Wv, L1_xattn_Wo)
    x = x + _L1_attn_ref(_layernorm(x, axis=-1), L1_attn_Wq, L1_attn_Wk, L1_attn_Wv, L1_attn_W_pre_th, L1_attn_W_post_th, L1_attn_mem_k, L1_attn_mem_v, L1_attn_head_scale_params, L1_attn_Wg, L1_attn_bg, L1_attn_Wo)
    x = x + _L1_ffn_ref(_layernorm(x, axis=-1), L1_ffn_gate_w, L1_ffn_w1, L1_ffn_w2)
    return x

_drawn_inputs = setup_inputs


def setup_inputs(seed=0):
    import zlib

    import numpy as np

    out = dict(_drawn_inputs(seed))
    spreads = {'L0_xattn_bq': (0.0, 0.1),
     'L0_xattn_bk': (0.0, 2.0),
     'L0_xattn_bv': (0.0, 0.1),
     'L0_xattn_bo': (0.0, 0.1),
     'L0_xattn_ln_gamma': (1.0, 0.2),
     'L0_xattn_ln_beta': (0.0, 0.1),
     'L0_attn_gamma': (1.0, 0.6),
     'L0_attn_q_scale': (1.0, 0.6),
     'L0_attn_k_scale': (1.0, 0.6),
     'L0_ffn_ln_w': (1.0, 0.6),
     'L0_ffn_ln_b': (0.0, 0.8),
     'L1_xattn_g_x': (1.0, 0.6),
     'L1_xattn_b_x': (0.0, 2.0),
     'L1_xattn_g_c': (1.0, 0.6),
     'L1_xattn_b_c': (0.0, 0.8),
     'L1_attn_head_scale_params': (1.0, 0.6),
     'L1_attn_bg': (1.0, 0.6)}
    factors = {'L0_xattn_Wk': 64.0,
     'L0_ffn_router_w': 8.0,
     'L0_ffn_gate_w': 8.0,
     'L0_ffn_up_w': 8.0,
     'L0_ffn_down_w': 8.0,
     'L0_ffn_sh_gate': 4.726,
     'L0_ffn_sh_up': 4.837,
     'L0_ffn_sh_down': 4.949,
     'L1_attn_Wg': 64.0,
     'L1_xattn_Wq': 7.83,
     'L1_xattn_Wk': 7.965,
     'L1_xattn_Wv': 3.914,
     'L1_xattn_Wo': 3.907,
     'L1_attn_Wq': 8.0,
     'L1_attn_Wk': 8.0,
     'L1_attn_Wv': 8.0,
     'L1_attn_W_pre_th': 8.0,
     'L1_attn_W_post_th': 8.0,
     'L1_attn_mem_k': 8.0,
     'L1_attn_mem_v': 8.0,
     'L1_attn_Wo': 8.0,
     'L1_ffn_gate_w': 8.0,
     'L1_ffn_w1': 8.0,
     'L1_ffn_w2': 8.0}
    for name, (base, spread) in spreads.items():
        noise = np.random.default_rng([zlib.crc32(name.encode()), seed]).standard_normal(out[name].shape)
        drawn = base * np.exp(spread * noise) if base else spread * noise
        out[name] = jnp.asarray(drawn.astype(out[name].dtype))
    for name, factor in factors.items():
        out[name] = (out[name] * factor).astype(out[name].dtype)
    return out
```

```python
from contextlib import ExitStack

import concourse.bass as bass
from concourse import mybir

F32 = mybir.dt.float32
F16 = mybir.dt.float16
U32 = mybir.dt.uint32
ALU = mybir.AluOpType
ACT = mybir.ActivationFunctionType
AX = mybir.AxisListType

P = 128
B, N, D = 8, 64, 256
TOK = B * N
TT = TOK // P
DC = D // P
M, CD = 1601, 192
KT = -(-M // P)
MP = KT * P
TAIL = M - (KT - 1) * P
CB = CD - P
H = 16
E = 8
EPS = 1e-5
BIG = 1e30


class Steps:

    def __init__(self, sem, names):
        self.sem, self.names, self.said = sem, names.split(), 0

    def done(self, name):
        assert self.names[self.said % len(self.names)] == name, (name, self.names[self.said % len(self.names)])
        self.said += 1
        return self.sem

    def at(self, name, turn=0):
        return turn * len(self.names) + self.names.index(name) + 1


def wait_apart(eng, sem, value, spare):
    eng.wait_ge(sem, value)
    eng.sem_inc(spare, 1)


def norm_steps(tag):
    return f"{tag}_stats {tag}_aggr {tag}"


def layer_norm(dve, steps, roots, tag, dst, src, work):
    stats, aggr, rstd = work
    for t in range(TT):
        ins = dve.bn_stats(stats[:, t, :], src[:, t, :])
    ins.then_inc(steps.done(f"{tag}_stats"), 1)
    dve.wait_ge(steps.sem, steps.at(f"{tag}_stats"))
    for t in range(TT):
        ins = dve.bn_aggr(aggr[:, t, :], stats[:, t, :])
    ins.then_inc(steps.done(f"{tag}_aggr"), 1)
    dve.wait_ge(roots.sem, roots.at(tag))
    for t in range(TT):
        ins = dve.tensor_scalar(dst[:, t, :], src[:, t, :], aggr[:, t, 0:1], rstd[:, t:t + 1],
                                ALU.subtract, ALU.mult)
    ins.then_inc(steps.done(tag), 1)
    dve.wait_ge(steps.sem, steps.at(tag))


def layer_norm_root(pool, steps, roots, tag, work, minus_half):
    stats, aggr, rstd = work
    pool.wait_ge(steps.sem, steps.at(f"{tag}_aggr"))
    pool.tensor_scalar(rstd[:, :], aggr[:, :, 1], EPS, None, ALU.add).then_inc(roots.done(f"{tag}_var"), 1)
    pool.wait_ge(roots.sem, roots.at(f"{tag}_var"))
    pool.tensor_tensor(rstd[:, :], rstd[:, :], minus_half, ALU.pow).then_inc(roots.done(tag), 1)


class Core:

    def __init__(self, nc, ctx, dram):
        self.nc, self.dram = nc, dram
        sb = lambda name, shape, dt=F32: ctx.enter_context(nc.sbuf_tensor(name, shape, dt))
        self.sems = []
        self.spare = nc.alloc_semaphore(name="spare")
        self.x = sb("x", [P, TT, D])
        self.y = sb("y", [P, TT, D])
        self.yT = sb("yT", [P, DC, TOK])
        self.ident = sb("ident", [P, P])
        self.ident16 = sb("ident16", [P, P], F16)
        self.ones = sb("ones", [P, P])
        self.minus_half = sb("minus_half", [P, 64])
        self.norm_work = (sb("ln_stats", [P, TT, 6]), sb("ln_aggr", [P, TT, 2]), sb("ln_rstd", [P, TT]))


    def sem(self, name):
        self.sems.append(self.nc.alloc_semaphore(name=name))
        return self.sems[-1]

    def clear_sems(self):
        self.nc.clear_and_free_semaphores(self.sems)
        self.nc.all_engine_barrier()
        self.sems = []


def stage_load(core):
    nc, d = core.nc, core.dram
    loaded, made = core.sem("load_loaded"), core.sem("load_made")
    with nc.Block() as block:
        @block.sync
        def _(sp):
            sp.dma_start(core.x[:, :, :], d["x"].rearrange("(a b) n d -> (b n) a d", b=2)).then_inc(loaded, 16)
            sp.dma_start(core.ident[:, :], d["c_ident"]).then_inc(loaded, 16)
            sp.wait_ge(loaded, 32)

        @block.vector
        def _(dve):
            dve.memset(core.ones[:, :], 1.0)
            dve.memset(core.minus_half[:, :], -0.5)
            dve.wait_ge(loaded, 32)
            dve.tensor_copy(core.ident16[:, :], core.ident[:, :]).then_inc(made, 1)


def stage_store(core):
    nc, d = core.nc, core.dram
    stored = core.sem("stored")
    with nc.Block() as block:
        @block.sync
        def _(sp):
            sp.dma_start(d["out"].rearrange("(a b) n d -> (b n) a d", b=2), core.x[:, :, :]).then_inc(stored, 16)
            sp.wait_ge(stored, 16)


def stage_norm(core, tag, inner=None):
    nc, d = core.nc, core.dram
    gamma, beta, keep = inner or (None, None, False)
    with ExitStack() as ctx:
        sb = lambda name, shape, dt=F32: ctx.enter_context(nc.sbuf_tensor(f"{tag}_{name}", shape, dt))
        g = sb("gamma", [P, D])
        b = sb("beta", [P, D])
        psT = ctx.enter_context(nc.psum_tensor(f"{tag}_psT", [P, DC, TOK], F32))
        loaded = core.sem(f"{tag}_loaded")
        n_loads = sum(v is not None for v in (gamma, beta))
        names = norm_steps("outer")
        if inner:
            names += " " + ("kept " if keep else "") + norm_steps("inner") + " gamma" + (" beta" if beta else "")
        vec = Steps(core.sem(f"{tag}_vector"), names)
        pe_s = Steps(core.sem(f"{tag}_tensor"), "transposed0 transposed1")
        roots = Steps(core.sem(f"{tag}_roots"), "outer_var outer" + (" inner_var inner" if inner else ""))
        last = vec.names[-1]
        done = core.sem(f"{tag}_evacuated")
        with nc.Block() as block:
            @block.sync
            def _(sp):
                if gamma:
                    sp.dma_start(g[:, :], d[gamma].partition_broadcast(P)).then_inc(loaded, 16)
                if beta:
                    sp.dma_start(b[:, :], d[beta].partition_broadcast(P)).then_inc(loaded, 16)

            @block.gpsimd
            def _(pool):
                for which in roots.names[1::2]:
                    layer_norm_root(pool, vec, roots, which, core.norm_work, core.minus_half[:, 0:TT])

            @block.vector
            def _(dve):
                layer_norm(dve, vec, roots, "outer", core.y, core.x, core.norm_work)
                if inner:
                    if keep:
                        dve.tensor_tensor(core.x[:, :, :], core.x[:, :, :], core.y[:, :, :], ALU.add)\
                           .then_inc(vec.done("kept"), 1)
                        dve.wait_ge(vec.sem, vec.at("kept"))
                    layer_norm(dve, vec, roots, "inner", core.y, core.y, core.norm_work)
                    dve.wait_ge(loaded, 16 * n_loads)
                    dve.tensor_tensor(core.y[:, :, :], core.y[:, :, :],
                                      g[:, None, :].to_broadcast([P, TT, D]), ALU.mult).then_inc(vec.done("gamma"), 1)
                    if beta:
                        dve.wait_ge(vec.sem, vec.at("gamma"))
                        dve.tensor_tensor(core.y[:, :, :], core.y[:, :, :],
                                          b[:, None, :].to_broadcast([P, TT, D]), ALU.add).then_inc(vec.done("beta"), 1)
                dve.wait_ge(pe_s.sem, pe_s.at("transposed0"))
                dve.tensor_copy(core.yT[:, 0, :], psT[:, 0, :]).then_inc(done, 1)

            @block.scalar
            def _(act):
                act.wait_ge(pe_s.sem, pe_s.at("transposed1"))
                act.activation(core.yT[:, 1, :], psT[:, 1, :], ACT.Copy).then_inc(done, 1)

            @block.tensor
            def _(pe):
                pe.wait_ge(vec.sem, vec.at(last))
                for c in range(DC):
                    for t in range(TT):
                        ins = pe.transpose(psT[:, c, t * P:(t + 1) * P], core.y[:, t, c * P:(c + 1) * P],
                                           core.ident[:, :])
                    ins.then_inc(pe_s.done(f"transposed{c}"), 1)


def stage_l0_cross(core):
    nc, d = core.nc, core.dram
    HD = D // H
    HC = H // DC
    PR = H // 2
    VW = 4 * HD + 1
    UNITS = DC * KT
    LATE = 4
    with ExitStack() as ctx:
        sb = lambda name, shape, dt=F32: ctx.enter_context(nc.sbuf_tensor(f"l0x_{name}", shape, dt))
        pb = lambda name, shape, dt=F32: ctx.enter_context(nc.psum_tensor(f"l0x_{name}", shape, dt))
        sem = lambda name: core.sem(f"l0x_{name}")

        wq, wo = sb("wq", [P, DC, D]), sb("wo", [P, 2, D])
        wA, wB = sb("wA", [P, 2 * D]), sb("wB", [P, 2 * D])
        bias = sb("bias", [97, 2 * D])
        rows = sb("rows", [1, 2, D])
        wAh, wAl, wBh = sb("wAh", [P, 2 * D], F16), sb("wAl", [P, 2 * D], F16), sb("wBh", [P, 2 * D], F16)
        biash = sb("biash", [97, 2 * D], F16)
        w5 = sb("w5", [P, 2 * D], F16)
        gam, bet = sb("gam", [P, D]), sb("bet", [P, D])
        headmask = sb("headmask", [P, HC])
        headmask16 = sb("headmask16", [P, HC], F16)
        qp = sb("qp", [P, TT, D])
        sq = sb("sq", [P, TT, D])
        qn = sb("qn", [P, TT, D])
        qss = sb("qss", [P, TT])
        qT = sb("qT", [P, DC, TOK])
        qTh, qTl = sb("qTh", [P, DC, TOK], F16), sb("qTl", [P, DC, TOK], F16)
        qbh, qbl = sb("qbh", [P, DC, B, HC, N], F16), sb("qbl", [P, DC, B, HC, N], F16)
        cA, cB = sb("cA", [P, MP]), sb("cB", [P, MP])
        cAh, cAl, cS = sb("cAh", [P, MP], F16), sb("cAl", [P, MP], F16), sb("cS", [P, MP], F16)
        c5, cBh, cBm = sb("c5", [P, MP], F16), sb("cBh", [P, P], F16), sb("cBm", [P, P], F16)
        half = sb("half", [P, 3])
        kh, kl = sb("kh", [P, 2, D], F16), sb("kl", [P, 2, D], F16)
        ksq = sb("ksq", [P, 2, D])
        kss, rn = sb("kss", [P, 2]), sb("rn", [P, 2])
        v = sb("v", [P, 2, PR, VW], F16)
        e32 = sb("e32", [P, 2, DC, 512])
        eh, el = sb("eh", [P, 2, DC, 512], F16), sb("el", [P, 2, DC, 512], F16)
        o = sb("o", [P, B, PR, VW])
        rd = sb("rd", [P, B, PR])
        att = sb("att", [P, B, PR, HD])
        attT = sb("attT", [P, 2, TOK])

        loaded, consts, ctx_hi = sem("loaded"), sem("consts"), sem("ctx_hi")
        ctx_loaded, ctx_split = sem("ctx_loaded"), sem("ctx_split")

        vec = Steps(sem("setup_vector"), "w_hi w_lo bias_hi w5 mask squares sums guarded qn qT_hi qT_lo queries")
        roots = Steps(sem("setup_roots"), "rnorm")
        pe_s = Steps(sem("setup_tensor"), "qp qT")
        act_s = Steps(sem("setup_scalar"), "qp qT")
        N_LOADS = 16 * (3 + 8 + 4 + 2 * PR)
        with ExitStack() as pctx, nc.Block() as block:
            psQ = pctx.enter_context(nc.psum_tensor("l0x_psQ", [P, TT, D], F32))
            psT = pctx.enter_context(nc.psum_tensor("l0x_psT", [P, DC, TOK], F32))

            @block.sync
            def _(sp):
                sp.dma_start(wq[:, :, :], d["L0_xattn_Wq"].rearrange("(c p) n -> p c n", p=P)).then_inc(loaded, 16)
                sp.dma_start(rows[0:1, 0, :], d["L0_xattn_bq"].partition_broadcast(1)).then_inc(loaded, 16)
                sp.dma_start(rows[0:1, 1, :], d["L0_xattn_bo"].partition_broadcast(1)).then_inc(loaded, 16)
                for j, (w, b) in enumerate((("L0_xattn_Wk", "L0_xattn_bk"), ("L0_xattn_Wv", "L0_xattn_bv"))):
                    cols = slice(j * D, (j + 1) * D)
                    sp.dma_start(wA[:, cols], d[w][0:P, :]).then_inc(loaded, 16)
                    sp.dma_start(wB[0:CB, cols], d[w][P:CD, :]).then_inc(loaded, 16)
                    sp.dma_start(wB[CB:P, cols], d[w][P:CD, :]).then_inc(loaded, 16)
                    sp.dma_start(bias[64:97, cols], d[b].partition_broadcast(33)).then_inc(loaded, 16)
                sp.dma_start(gam[:, :], d["L0_xattn_ln_gamma"].partition_broadcast(P)).then_inc(loaded, 16)
                sp.dma_start(bet[:, :], d["L0_xattn_ln_beta"].partition_broadcast(P)).then_inc(loaded, 16)
                sp.dma_start(headmask[:, :], d["c_headmask"]).then_inc(loaded, 16)
                sp.dma_start(half[:, :], d["c_half"]).then_inc(loaded, 16)
                for pr in range(PR):
                    for hh in range(2):
                        r = (2 * pr + hh) * HD
                        sp.dma_start(wo[pr * HD:(pr + 1) * HD, hh, :], d["L0_xattn_Wo"][r:r + HD, :]).then_inc(loaded, 16)

            @block.gpsimd
            def _(pool):
                pool.wait_ge(vec.sem, vec.at("guarded"))
                pool.tensor_tensor(qss[:, :], qss[:, :], core.minus_half[:, 0:TT], ALU.pow).then_inc(roots.done("rnorm"), 1)

            @block.tensor
            def _(pe):
                pe.wait_ge(loaded, N_LOADS)
                for t in range(TT):
                    for c in range(DC):
                        pe.matmul(psQ[:, t, :], core.yT[:, c, t * P:(t + 1) * P], wq[:, c, :], start=(c == 0), stop=False)
                    ins = pe.matmul(psQ[:, t, :], core.ones[0:1, :], rows[0:1, 0, :], start=False, stop=True)
                ins.then_inc(pe_s.done("qp"), 1)
                pe.wait_ge(vec.sem, vec.at("qn"))
                for c in range(DC):
                    for t in range(TT):
                        ins = pe.transpose(psT[:, c, t * P:(t + 1) * P], qn[:, t, c * P:(c + 1) * P], core.ident[:, :])
                ins.then_inc(pe_s.done("qT"), 1)

            @block.scalar
            def _(act):
                act.wait_ge(pe_s.sem, pe_s.at("qp"))
                act.activation(qp[:, :, :], psQ[:, :, :], ACT.Copy).then_inc(act_s.done("qp"), 1)
                act.wait_ge(pe_s.sem, pe_s.at("qT"))
                act.activation(qT[:, :, :], psT[:, :, :], ACT.Copy).then_inc(act_s.done("qT"), 1)

            @block.vector
            def _(dve):
                dve.memset(w5[CB:P, :], 0.0).then_inc(consts, 1)
                for s in range(2):
                    dve.memset(v[:, s, :, VW - 1:VW], 1.0)
                dve.wait_ge(loaded, N_LOADS)
                dve.tensor_copy(wAh[:, :], wA[:, :])
                dve.tensor_copy(wBh[:, :], wB[:, :])
                dve.tensor_copy(biash[64:97, :], bias[64:97, :]).then_inc(vec.done("w_hi"), 1)
                dve.wait_ge(vec.sem, vec.at("w_hi"))
                dve.tensor_tensor(wAl[:, :], wA[:, :], wAh[:, :], ALU.subtract).then_inc(vec.done("w_lo"), 1)
                dve.wait_ge(consts, 1)
                dve.tensor_copy(w5[64:65, :], biash[64:65, :]).then_inc(vec.done("bias_hi"), 1)
                dve.tensor_tensor(w5[0:CB, :], wB[0:CB, :], wBh[0:CB, :], ALU.subtract)
                dve.tensor_tensor(w5[96:97, :], bias[96:97, :], biash[96:97, :], ALU.subtract).then_inc(vec.done("w5"), 1)
                dve.tensor_copy(headmask16[:, :], headmask[:, :]).then_inc(vec.done("mask"), 1)
                dve.wait_ge(act_s.sem, act_s.at("qp"))
                dve.tensor_tensor(sq[:, :, :], qp[:, :, :], qp[:, :, :], ALU.mult).then_inc(vec.done("squares"), 1)
                dve.wait_ge(vec.sem, vec.at("squares"))
                dve.tensor_reduce(qss[:, :], sq[:, :, :], AX.X, ALU.add).then_inc(vec.done("sums"), 1)
                dve.wait_ge(vec.sem, vec.at("sums"))
                dve.tensor_scalar(qss[:, :], qss[:, :], 1e-24, None, ALU.max).then_inc(vec.done("guarded"), 1)
                dve.wait_ge(roots.sem, roots.at("rnorm"))
                for t in range(TT):
                    ins = dve.tensor_scalar(qn[:, t, :], qp[:, t, :], qss[:, t:t + 1], float(HD) ** -0.5, ALU.mult, ALU.mult)
                ins.then_inc(vec.done("qn"), 1)
                dve.wait_ge(act_s.sem, act_s.at("qT"))
                dve.tensor_copy(qTh[:, :, :], qT[:, :, :]).then_inc(vec.done("qT_hi"), 1)
                dve.wait_ge(vec.sem, vec.at("qT_hi"))
                dve.tensor_tensor(qTl[:, :, :], qT[:, :, :], qTh[:, :, :], ALU.subtract).then_inc(vec.done("qT_lo"), 1)
                dve.wait_ge(vec.sem, vec.at("qT_lo"))
                for q, blocks in ((qTh, qbh), (qTl, qbl)):
                    for c in range(DC):
                        for b in range(B):
                            ins = dve.tensor_tensor(
                                blocks[:, c, b, :, :], q[:, c, None, b * N:(b + 1) * N].to_broadcast([P, HC, N]),
                                headmask16[:, :, None].to_broadcast([P, HC, N]), ALU.mult)
                ins.then_inc(vec.done("queries"), 1)

        projected, squares = sem("projected"), sem("squares")
        k_hi, k_lo, v_hi, v_lo = sem("k_hi"), sem("k_lo"), sem("v_hi"), sem("v_lo")
        norms, key_sums, rnorms = sem("norms"), sem("key_sums"), sem("rnorms")
        scored, exped, e_hi, e_split = sem("scored"), sem("exped"), sem("e_hi"), sem("e_split")
        weighted, out_taken = sem("weighted"), sem("out_taken")
        START = 1
        with ExitStack() as pctx, nc.Block() as block:
            psP = pctx.enter_context(nc.psum_tensor("l0x_psP", [P, 2, 2 * D], F32))
            psS = pctx.enter_context(nc.psum_tensor("l0x_psS", [P, 3, 512], F32))
            psO = pctx.enter_context(nc.psum_tensor("l0x_psO", [P, 2, 512], F32))
            psN = pctx.enter_context(nc.psum_tensor("l0x_psN", [P, 512], F32))

            @block.sync
            def _(sp):
                def load(src):
                    sp.dma_start(cA[:, :], src[0:P, :]).then_inc(ctx_loaded, 16)
                    sp.dma_start(cB[0:CB, :], src[P:CD, :]).then_inc(ctx_loaded, 16)
                    sp.dma_start(cB[CB:P, :], src[P:CD, :]).then_inc(ctx_loaded, 16)

                load(d["c_ctxT"][0, :, :])
                with sp.Fori(0, B) as b:
                    sp.wait_ge(ctx_split, KT * b + KT)
                    load(d["c_ctxT"][bass.ds(b + 1, 1), :, :].rearrange("a k m -> (a k) m"))

            @block.gpsimd
            def _(pool):
                def split(n, turn):
                    cols = slice(n * P, (n + 1) * P)
                    if not isinstance(turn, int):
                        wait_apart(pool, ctx_split, turn * KT + n, core.spare)
                    elif n:
                        pool.wait_ge(ctx_split, n)
                    pool.tensor_copy(cAh[:, cols], cA[:, cols])
                    pool.tensor_scalar(c5[:, cols], cB[:, cols], half[:, 0:1], half[:, 1:2], ALU.mult, ALU.add)
                    pool.tensor_copy(cBh[:, :], cB[:, cols]).then_inc(ctx_hi, 1)
                    wait_apart(pool, ctx_hi, 2 * (turn * KT + n) + 1, core.spare)
                    pool.tensor_scalar(cBm[:, :], cBh[:, :], half[:, 2:3], None, ALU.mult).then_inc(ctx_hi, 1)
                    pool.tensor_tensor(cAl[:, cols], cA[:, cols], cAh[:, cols], ALU.subtract)
                    pool.wait_ge(ctx_hi, 2 * (turn * KT + n) + 2)
                    pool.tensor_tensor(cS[:, cols], cB[:, cols], cBm[:, :], ALU.add)\
                        .then_inc(ctx_split, 1)

                pool.wait_ge(ctx_loaded, 48)
                for n in range(KT):
                    split(n, 0)
                with pool.Fori(0, B) as b:
                    for n in range(KT):
                        pool.wait_ge(key_sums, START + b * KT + n + 1)
                        pool.wait_ge(exped, START + b * UNITS + DC * max(n - 1, 0))
                        pool.tensor_tensor(rn[:, n % 2:n % 2 + 1], kss[:, n % 2:n % 2 + 1],
                                           core.minus_half[:, 0:1], ALU.pow)\
                            .then_inc(rnorms, 1)
                        if n == LATE:
                            pool.wait_ge(ctx_loaded, 48 * b + 96)
                        if n >= LATE:
                            turns = KT - LATE
                            for m in range((n - LATE) * KT // turns, (n - LATE + 1) * KT // turns):
                                pool.wait_ge(projected, b * KT + m + 1)
                                split(m, b + 1)

            @block.tensor
            def _(pe):
                def project(n):
                    keys, out = slice(n * P, (n + 1) * P), psP[:, n % 2, :]
                    passes = ((wAh, cAh), (wAh, cAl), (wAl, cAh), (wBh, cS), (w5, c5))
                    for c in range(DC):
                        for i, (w, x) in enumerate(passes):
                            pe.matmul(out[:, c * P:(c + 1) * P], w[:, c * P:(c + 1) * P], x[:, keys],
                                      start=(i == 0), stop=(i == 4))
                    for i, (w, x) in enumerate(passes):
                        ins = pe.matmul(out[:, D:2 * D], x[:, keys], w[:, D:2 * D], start=(i == 0), stop=(i == 4))
                    ins.then_inc(projected, 1)

                def key_norms(n, b):
                    pe.wait_ge(squares, b * KT + n + 1)
                    pe.wait_ge(key_sums, START + b * KT + n)
                    for c in range(DC):
                        ins = pe.matmul(psN[:, n:n + 1], ksq[:, n % 2, c * P:(c + 1) * P], core.ones[:, 0:1],
                                        start=(c == 0), stop=(c == 1))
                    ins.then_inc(norms, 1)

                def score(n, b):
                    pe.wait_ge(k_lo, b * KT + n + 1)
                    for c in range(DC):
                        u = DC * n + c
                        pe.wait_ge(exped, START + b * UNITS + max(u - 2, 0))
                        cols = slice(c * P, (c + 1) * P)
                        for i, (k, q) in enumerate(((kh, qbh), (kl, qbh), (kh, qbl))):
                            ins = pe.matmul(psS[:, u % 3, :], k[:, n % 2, cols],
                                            q[:, c, bass.ds(b, 1), :, :].rearrange("p a h q -> p (a h q)"),
                                            start=(i == 0), stop=(i == 2))
                        ins.then_inc(scored, 1)

                def weigh(n, b):
                    rows = P if n < KT - 1 else TAIL
                    pe.wait_ge(v_lo, START + b * KT + n + 1)
                    pe.wait_ge(e_split, START + b * UNITS + DC * n + DC)
                    if n == 0:
                        pe.wait_ge(out_taken, START + b)
                    for pr in range(PR):
                        c, col = pr // (PR // 2), (pr % (PR // 2)) * P
                        out = psO[:, c, (pr % (PR // 2)) * VW:(pr % (PR // 2) + 1) * VW]
                        pe.matmul(out, eh[0:rows, n % 2, c, col:col + P], v[0:rows, n % 2, pr, :],
                                  start=(n == 0 and pr % (PR // 2) == 0), stop=False, skip_group_check=True)
                        ins = pe.matmul(out[:, 2 * HD:VW], el[0:rows, n % 2, c, col:col + P],
                                        v[0:rows, n % 2, pr, 2 * HD:VW], start=False, stop=(n == KT - 1),
                                        skip_group_check=True)
                    ins.then_inc(weighted, 1)

                pe.wait_ge(ctx_split, 1)
                project(0)
                with pe.Fori(0, B) as b:
                    for n in range(KT):
                        if n + 1 < KT:
                            pe.wait_ge(ctx_split, b * KT + n + 2)
                            pe.wait_ge(v_lo, START + b * KT + n)
                            project(n + 1)
                        key_norms(n, b)
                        score(n, b)
                        if n >= 1:
                            weigh(n - 1, b)
                    pe.wait_ge(ctx_split, b * KT + KT + 1)
                    pe.wait_ge(v_lo, START + b * KT + KT)
                    project(0)
                    weigh(KT - 1, b)

            @block.scalar
            def _(act):
                def take(n, b):
                    act.wait_ge(projected, b * KT + n + 1)
                    act.wait_ge(norms, START + b * KT + max(n - 1, 0))
                    act.activation(ksq[:, n % 2, :], psP[:, n % 2, 0:D], ACT.Square).then_inc(squares, 1)
                    act.wait_ge(scored, START + b * UNITS + DC * max(n - 1, 0))
                    act.activation(kh[:, n % 2, :], psP[:, n % 2, 0:D], ACT.Copy).then_inc(k_hi, 1)
                    act.wait_ge(weighted, START + b * KT + max(n - 1, 0))
                    act.activation(v[:, n % 2, :, 2 * HD:4 * HD],
                                   psP[:, n % 2, D:2 * D].rearrange("p (a k) -> p a k", k=2 * HD),
                                   ACT.Copy).then_inc(v_hi, 1)

                with act.Fori(0, B) as b:
                    take(0, b)
                    for n in range(KT):
                        if n + 1 < KT:
                            take(n + 1, b)
                        act.wait_ge(rnorms, START + b * KT + n + 1)
                        for c in range(DC):
                            u = DC * n + c
                            act.wait_ge(scored, START + b * UNITS + u + 1)
                            act.wait_ge(e_split, START + b * UNITS + max(u - 3, 0))
                            act.activation(e32[:, n % 2, c, :], psS[:, u % 3, :], ACT.Exp,
                                           scale=rn[:, n % 2:n % 2 + 1]).then_inc(exped, 1)

            @block.vector
            def _(dve):
                def take(n, b):
                    dve.wait_ge(v_hi, b * KT + n + 1)
                    dve.wait_ge(scored, START + b * UNITS + DC * max(n - 1, 0))
                    dve.tensor_tensor(kl[:, n % 2, :], psP[:, n % 2, 0:D], kh[:, n % 2, :], ALU.subtract).then_inc(k_lo, 1)
                    dve.tensor_tensor(v[:, n % 2, :, 0:2 * HD],
                                      psP[:, n % 2, D:2 * D].rearrange("p (a k) -> p a k", k=2 * HD),
                                      v[:, n % 2, :, 2 * HD:4 * HD], ALU.subtract).then_inc(v_lo, 1)

                for sem_ in (norms, scored, weighted, exped, e_split, v_lo, key_sums, out_taken, rnorms):
                    dve.sem_inc(sem_, START)
                with dve.Fori(0, B) as b:
                    take(0, b)
                    for n in range(KT):
                        if n + 1 < KT:
                            take(n + 1, b)
                        dve.wait_ge(norms, START + b * KT + n + 1)
                        dve.wait_ge(rnorms, START + b * KT + max(n - 1, 0))
                        dve.tensor_scalar(kss[:, n % 2:n % 2 + 1], psN[:, n:n + 1], 1e-24, None, ALU.max)\
                            .then_inc(key_sums, 1)
                        for c in range(DC):
                            u = DC * n + c
                            dve.wait_ge(exped, START + b * UNITS + u + 1)
                            dve.wait_ge(weighted, START + b * KT + max(n - 1, 0))
                            dve.tensor_copy(eh[:, n % 2, c, :], e32[:, n % 2, c, :]).then_inc(e_hi, 1)
                            dve.wait_ge(e_hi, b * UNITS + u + 1)
                            dve.tensor_tensor(el[:, n % 2, c, :], e32[:, n % 2, c, :], eh[:, n % 2, c, :],
                                              ALU.subtract).then_inc(e_split, 1)
                    dve.wait_ge(weighted, START + b * KT + KT)
                    dve.tensor_copy(o[:, bass.ds(b, 1), :, :].rearrange("p a (c r) w -> p (a c) (r w)", c=2),
                                    psO[:, :, 0:PR // 2 * VW]).then_inc(out_taken, 1)

        vec = Steps(sem("out_vector"), "rden sums att x " + norm_steps("ln") + " gamma beta residual")
        pe_s = Steps(sem("out_tensor"), "attT out")
        roots = Steps(sem("out_roots"), "ln_var ln")
        evac = sem("attT_taken")
        with ExitStack() as pctx, nc.Block() as block:
            psT = pctx.enter_context(nc.psum_tensor("l0x_psA", [P, B, P], F32))
            psX = pctx.enter_context(nc.psum_tensor("l0x_psX", [P, TT, D], F32))

            @block.gpsimd
            def _(pool):
                layer_norm_root(pool, vec, roots, "ln", core.norm_work, core.minus_half[:, 0:TT])

            @block.vector
            def _(dve):
                dve.reciprocal(rd[:, :, :], o[:, :, :, VW - 1]).then_inc(vec.done("rden"), 1)
                for hh in range(2):
                    rows, k = slice(hh * N, (hh + 1) * N), hh * HD
                    ins = dve.tensor_tensor(att[rows, :, :, :], o[rows, :, :, k:k + HD],
                                            o[rows, :, :, 2 * HD + k:2 * HD + k + HD], ALU.add)
                ins.then_inc(vec.done("sums"), 1)
                dve.wait_ge(vec.sem, vec.at("sums"))
                dve.tensor_tensor(att[:, :, :, :], att[:, :, :, :], rd[:, :, :, None].to_broadcast([P, B, PR, HD]),
                                  ALU.mult).then_inc(vec.done("att"), 1)
                dve.wait_ge(pe_s.sem, pe_s.at("out"))
                dve.tensor_tensor(qn[:, :, :], psX[:, :, :], qp[:, :, :], ALU.add).then_inc(vec.done("x"), 1)
                dve.wait_ge(vec.sem, vec.at("x"))
                layer_norm(dve, vec, roots, "ln", qn, qn, core.norm_work)
                dve.tensor_tensor(qn[:, :, :], qn[:, :, :], gam[:, None, :].to_broadcast([P, TT, D]), ALU.mult)\
                    .then_inc(vec.done("gamma"), 1)
                dve.wait_ge(vec.sem, vec.at("gamma"))
                dve.tensor_tensor(qn[:, :, :], qn[:, :, :], bet[:, None, :].to_broadcast([P, TT, D]), ALU.add)\
                    .then_inc(vec.done("beta"), 1)
                dve.wait_ge(vec.sem, vec.at("beta"))
                dve.tensor_tensor(core.x[:, :, :], core.x[:, :, :], qn[:, :, :], ALU.add).then_inc(vec.done("residual"), 1)

            @block.tensor
            def _(pe):
                pe.wait_ge(vec.sem, vec.at("att"))
                for b in range(B):
                    ins = pe.transpose(psT[:, b, :], att[:, b, :, :].rearrange("p a k -> p (a k)"), core.ident[:, :])
                ins.then_inc(pe_s.done("attT"), 1)
                pe.wait_ge(evac, 1)
                for t in range(TT):
                    for hh in range(2):
                        pe.matmul(psX[:, t, :], attT[:, hh, t * P:(t + 1) * P], wo[:, hh, :], start=(hh == 0), stop=False)
                    ins = pe.matmul(psX[:, t, :], core.ones[0:1, :], rows[0:1, 1, :], start=False, stop=True)
                ins.then_inc(pe_s.done("out"), 1)

            @block.scalar
            def _(act):
                act.wait_ge(pe_s.sem, pe_s.at("attT"))
                act.activation(attT[:, :, :].rearrange("p h (b q) -> p b h q", b=B),
                               psT[:, :, :].rearrange("p b (h q) -> p b h q", h=2), ACT.Copy).then_inc(evac, 1)


def stage_l0_self(core):
    nc, d = core.nc, core.dram
    DH = 64
    NN = 2
    J = NN + N
    PR = H // 2
    W = H * DH
    halves = [slice(0, N), slice(N, P)]
    place = lambda h: h % 2 * PR + h // 2
    with ExitStack() as ctx:
        sb = lambda name, shape, dt=F32: ctx.enter_context(nc.sbuf_tensor(f"l0a_{name}", shape, dt))
        pb = lambda name, shape: ctx.enter_context(nc.psum_tensor(f"l0a_{name}", shape, F32))
        sem = lambda name: core.sem(f"l0a_{name}")
        w = sb("w", [P, DC, 3 * W])
        wo = sb("wo", [P, PR, D])
        scale = sb("scale", [P, 2, DH])
        bias = sb("bias", [P, H, J])
        nk, nks = sb("nk", [2 * H, DH]), sb("nks", [2 * H, DH])
        nss = sb("nss", [2 * H, 1])
        nkb = sb("nkb", [2 * H, H, DH])
        blockmask = sb("blockmask", [2 * H, H])
        nkT = sb("nkT", [P, PR, 4])
        nv = sb("nv", [2 * H, W])
        yt = sb("yt", [P, DC, P])
        qk = sb("qk", [P, 2, H, DH])
        sq = sb("sq", [P, 2, H, DH])
        ss = sb("ss", [P, 2, H])
        v = sb("v", [P, W])
        qkT = sb("qkT", [P, 2, PR, P])
        s, e = sb("s", [P, H, J]), sb("e", [P, H, J])
        en = sb("en", [P, H * NN])
        top, den = sb("top", [P, H]), sb("den", [P, H])
        eT, nT = sb("eT", [P, H, N]), sb("nT", [2 * H, P])
        o, oT = sb("o", [P, H, DH]), sb("oT", [P, PR, P])
        psA, psB = pb("psA", [P, 4, 512]), pb("psB", [P, 4, 512])
        psA_heads = psA[:, :, :].rearrange("p a (b q) -> p (a b) q", q=P)
        psB_heads = psB[:, :, :].rearrange("p a (b q) -> p (a b) q", q=P)

        loaded = sem("loaded")
        setup = Steps(sem("setup"), "squares sums guarded scaled scaled2 blocks nkT")
        setup_root = sem("setup_root")
        setup_T = sem("setup_T")
        vec = Steps(sem("vector"), "yt v squares sums guarded normed scaled biased top shifted den rden eT o x")
        act_s = Steps(sem("scalar"), "qk qkT exp nT oT")
        pe_s = Steps(sem("tensor"), "qkv qkT scores eT out oT proj")
        roots = Steps(sem("roots"), "norms")
        N_LOADS = 16 * 9

        with nc.Block() as block:
            @block.sync
            def _(sp):
                sp.dma_start(w[:, :, 0:W], d["L0_attn_w_q"].rearrange("(c p) n -> p c n", p=P)).then_inc(loaded, 16)
                sp.dma_start(w[:, :, W:3 * W], d["L0_attn_w_kv"].rearrange("(c p) n -> p c n", p=P)).then_inc(loaded, 16)
                sp.dma_start(wo[:, :, :], d["L0_attn_w_out"].rearrange("(c p) n -> p c n", p=P)).then_inc(loaded, 16)
                sp.dma_start(scale[:, 0, :], d["L0_attn_q_scale"].partition_broadcast(P)).then_inc(loaded, 16)
                sp.dma_start(scale[:, 1, :], d["L0_attn_k_scale"].partition_broadcast(P)).then_inc(loaded, 16)
                sp.dma_start(bias[:, :, :], d["c_alibi"]).then_inc(loaded, 16)
                sp.dma_start(nk[:, :], d["c_null_k"]).then_inc(loaded, 16)
                sp.dma_start(nv[:, :], d["c_null_v"]).then_inc(loaded, 16)
                sp.dma_start(blockmask[:, :], d["c_blockmask"]).then_inc(loaded, 16)

            @block.gpsimd
            def _(pool):
                pool.wait_ge(setup.sem, setup.at("guarded"))
                pool.tensor_tensor(nss[:, :], nss[:, :], core.minus_half[0:2 * H, 0:1], ALU.pow).then_inc(setup_root, 1)
                with pool.Fori(0, TT) as i:
                    pool.wait_ge(vec.sem, vec.at("guarded", i))
                    pool.tensor_tensor(ss[:, :, :], ss[:, :, :],
                                       core.minus_half[:, 0:2 * H].rearrange("p (a h) -> p a h", a=2), ALU.pow)\
                        .then_inc(roots.done("norms"), 1)

            @block.tensor
            def _(pe):
                pe.wait_ge(setup.sem, setup.at("blocks"))
                for pr in range(PR):
                    ins = pe.transpose(psA[:, 0, pr * 32:(pr + 1) * 32],
                                       nkb[:, 2 * pr:2 * pr + 2, :].rearrange("k a d -> k (a d)"),
                                       core.ident[0:2 * H, 0:2 * H])
                ins.then_inc(setup_T, 1)
                pe.wait_ge(setup.sem, setup.at("nkT"))
                with pe.Fori(0, TT) as i:
                    pe.wait_ge(vec.sem, vec.at("yt", i))
                    for part in range(6):
                        ps = (psA[:, part, :] if part < 4 else psB[:, part - 4, :])
                        for c in range(DC):
                            ins = pe.matmul(ps, yt[:, c, :], w[:, c, part * 512:(part + 1) * 512],
                                            start=(c == 0), stop=(c == 1))
                    ins.then_inc(pe_s.done("qkv"), 1)
                    pe.wait_ge(vec.sem, vec.at("scaled", i))
                    for a in range(2):
                        for pr in range(PR):
                            ins = pe.transpose(psA_heads[:, a * PR + pr, :],
                                               qk[:, a, 2 * pr:2 * pr + 2, :].rearrange("p h k -> p (h k)"),
                                               core.ident[:, :])
                    ins.then_inc(pe_s.done("qkT"), 1)
                    wait_apart(pe, act_s.sem, act_s.at("qkT", i), core.spare)
                    for pr in range(PR):
                        for odd, r in enumerate(halves):
                            for half in halves:
                                pe.matmul(psB_heads[half, odd * PR + pr, 0:N], qkT[r, 0, pr, half], qkT[r, 1, pr, half],
                                          start=True, stop=True)
                    for pr in range(PR):
                        ins = pe.matmul(psA[:, 0, pr * 2 * NN:(pr + 1) * 2 * NN], qkT[:, 0, pr, :], nkT[:, pr, :],
                                        start=True, stop=True)
                    ins.then_inc(pe_s.done("scores"), 1)
                    wait_apart(pe, act_s.sem, act_s.at("exp", i), core.spare)
                    for h in range(H):
                        for half in halves:
                            pe.matmul(psA[half, h // 8, (h % 8) * N:(h % 8 + 1) * N], e[half, h, NN:J],
                                      core.ident[half, half], start=True, stop=True)
                    ins = pe.matmul(psA[0:2 * H, 2, 0:P], en[:, :], core.ident[:, :], start=True, stop=True)
                    ins.then_inc(pe_s.done("eT"), 1)
                    pe.wait_ge(vec.sem, vec.at("eT", i))
                    pe.wait_ge(act_s.sem, act_s.at("nT", i))
                    for bank in range(2):
                        pe.matmul(psB[:, bank, :], nT[:, :], nv[:, bank * 512:(bank + 1) * 512], start=True, stop=False,
                                  skip_group_check=True)
                        for h in range(8 * bank, 8 * bank + 8):
                            for half in halves:
                                ins = pe.matmul(psB[half, bank, (h % 8) * DH:(h % 8 + 1) * DH], eT[half, place(h), :],
                                                v[half, h * DH:(h + 1) * DH], start=False, stop=(h % 8 == 7),
                                                skip_group_check=True)
                    ins.then_inc(pe_s.done("out"), 1)
                    pe.wait_ge(vec.sem, vec.at("o", i))
                    for pr in range(PR):
                        ins = pe.transpose(psA_heads[:, pr, :], o[:, 2 * pr:2 * pr + 2, :].rearrange("p h k -> p (h k)"),
                                           core.ident[:, :])
                    ins.then_inc(pe_s.done("oT"), 1)
                    pe.wait_ge(act_s.sem, act_s.at("oT", i))
                    for pr in range(PR):
                        ins = pe.matmul(psB[:, 3, 0:D], oT[:, pr, :], wo[:, pr, :], start=(pr == 0), stop=(pr == PR - 1))
                    ins.then_inc(pe_s.done("proj"), 1)

            @block.scalar
            def _(act):
                with act.Fori(0, TT) as i:
                    act.wait_ge(pe_s.sem, pe_s.at("qkv", i))
                    act.activation(qk[:, :, :, :].rearrange("p a h k -> p (a h k)"),
                                   psA[:, :, :].rearrange("p a n -> p (a n)"), ACT.Copy).then_inc(act_s.done("qk"), 1)
                    act.wait_ge(pe_s.sem, pe_s.at("qkT", i))
                    act.activation(qkT[:, :, :, :].rearrange("p a h k -> p (a h k)"),
                                   psA[:, :, :].rearrange("p a n -> p (a n)"), ACT.Copy).then_inc(act_s.done("qkT"), 1)
                    act.wait_ge(vec.sem, vec.at("shifted", i))
                    act.activation(en[:, :].rearrange("p (h k) -> p h k", k=NN), s[:, :, 0:NN], ACT.Exp)
                    act.activation(e[:, :, :], s[:, :, :], ACT.Exp).then_inc(act_s.done("exp"), 1)
                    act.wait_ge(pe_s.sem, pe_s.at("eT", i))
                    act.activation(nT[:, :], psA[0:2 * H, 2, 0:P], ACT.Copy).then_inc(act_s.done("nT"), 1)
                    act.wait_ge(pe_s.sem, pe_s.at("oT", i))
                    act.activation(oT[:, :, :], psA_heads[:, 0:PR, :], ACT.Copy).then_inc(act_s.done("oT"), 1)

            @block.vector
            def _(dve):
                dve.wait_ge(loaded, N_LOADS)
                dve.tensor_tensor(nks[:, :], nk[:, :], nk[:, :], ALU.mult).then_inc(setup.done("squares"), 1)
                dve.wait_ge(setup.sem, setup.at("squares"))
                dve.tensor_reduce(nss[:, :], nks[:, :], AX.X, ALU.add).then_inc(setup.done("sums"), 1)
                dve.wait_ge(setup.sem, setup.at("sums"))
                dve.tensor_scalar(nss[:, :], nss[:, :], 1e-24, None, ALU.max).then_inc(setup.done("guarded"), 1)
                dve.wait_ge(setup_root, 1)
                dve.tensor_scalar(nk[:, :], nk[:, :], nss[:, 0:1], None, ALU.mult).then_inc(setup.done("scaled"), 1)
                dve.wait_ge(setup.sem, setup.at("scaled"))
                dve.tensor_tensor(nk[:, :], nk[:, :], scale[0:2 * H, 1, :], ALU.mult).then_inc(setup.done("scaled2"), 1)
                dve.wait_ge(setup.sem, setup.at("scaled2"))
                dve.tensor_tensor(nkb[:, :, :], nk[:, None, :].to_broadcast([2 * H, H, DH]),
                                  blockmask[:, :, None].to_broadcast([2 * H, H, DH]), ALU.mult)\
                    .then_inc(setup.done("blocks"), 1)
                dve.wait_ge(setup_T, 1)
                for pr in range(PR):
                    ins = dve.tensor_copy(nkT[:, pr, :], psA[:, 0, pr * 32 + 4 * pr:pr * 32 + 4 * pr + 4])
                ins.then_inc(setup.done("nkT"), 1)

                with dve.Fori(0, TT) as i:
                    dve.tensor_copy(yt[:, :, :], core.yT[:, :, bass.ds(i * P, P)]).then_inc(vec.done("yt"), 1)
                    dve.wait_ge(pe_s.sem, pe_s.at("qkv", i))
                    dve.tensor_copy(v[:, :], psB[:, 0:2, :].rearrange("p a n -> p (a n)")).then_inc(vec.done("v"), 1)
                    dve.wait_ge(act_s.sem, act_s.at("qk", i))
                    dve.tensor_tensor(sq[:, :, :, :], qk[:, :, :, :], qk[:, :, :, :], ALU.mult).then_inc(vec.done("squares"), 1)
                    dve.wait_ge(vec.sem, vec.at("squares", i))
                    dve.tensor_reduce(ss[:, :, :], sq[:, :, :, :], AX.X, ALU.add).then_inc(vec.done("sums"), 1)
                    dve.wait_ge(vec.sem, vec.at("sums", i))
                    dve.tensor_scalar(ss[:, :, :], ss[:, :, :], 1e-24, None, ALU.max).then_inc(vec.done("guarded"), 1)
                    dve.wait_ge(roots.sem, roots.at("norms", i))
                    dve.tensor_tensor(qk[:, :, :, :], qk[:, :, :, :], ss[:, :, :, None].to_broadcast([P, 2, H, DH]),
                                      ALU.mult).then_inc(vec.done("normed"), 1)
                    dve.wait_ge(vec.sem, vec.at("normed", i))
                    dve.tensor_tensor(qk[:, :, :, :], qk[:, :, :, :], scale[:, :, None, :].to_broadcast([P, 2, H, DH]),
                                      ALU.mult).then_inc(vec.done("scaled"), 1)
                    dve.wait_ge(pe_s.sem, pe_s.at("scores", i))
                    dve.scalar_tensor_tensor(s[:, :, NN:J], psB_heads[:, :, 0:N], 8.0, bias[:, :, NN:J], ALU.mult, ALU.add)
                    for odd in range(2):
                        heads = slice(odd * PR, (odd + 1) * PR)
                        ins = dve.scalar_tensor_tensor(
                            s[:, heads, 0:NN], psA[:, 0, 0:2 * H].rearrange("p (a b k) -> p b a k", b=2, k=NN)[:, odd],
                            8.0, bias[:, heads, 0:NN], ALU.mult, ALU.add)
                    ins.then_inc(vec.done("biased"), 1)
                    dve.wait_ge(vec.sem, vec.at("biased", i))
                    dve.tensor_reduce(top[:, :], s[:, :, :], AX.X, ALU.max).then_inc(vec.done("top"), 1)
                    dve.wait_ge(vec.sem, vec.at("top", i))
                    dve.tensor_tensor(s[:, :, :], s[:, :, :], top[:, :, None].to_broadcast([P, H, J]), ALU.subtract)\
                        .then_inc(vec.done("shifted"), 1)
                    dve.wait_ge(act_s.sem, act_s.at("exp", i))
                    dve.tensor_reduce(den[:, :], e[:, :, :], AX.X, ALU.add).then_inc(vec.done("den"), 1)
                    dve.wait_ge(vec.sem, vec.at("den", i))
                    dve.reciprocal(den[:, :], den[:, :]).then_inc(vec.done("rden"), 1)
                    dve.wait_ge(pe_s.sem, pe_s.at("eT", i))
                    dve.tensor_copy(eT[:, :, :], psA[:, 0:2, :].rearrange("p a (h q) -> p (a h) q", q=N))\
                        .then_inc(vec.done("eT"), 1)
                    dve.wait_ge(pe_s.sem, pe_s.at("out", i))
                    den_in_order = den[:, :].rearrange("p (odd a) -> p a odd", odd=2)
                    dve.tensor_tensor(o[:, :, :].rearrange("p (a odd) k -> p a odd k", odd=2),
                                      psB[:, 0:2, :].rearrange("p b (a odd k) -> p (b a) odd k", odd=2, k=DH),
                                      den_in_order[:, :, :, None].to_broadcast([P, PR, 2, DH]), ALU.mult).then_inc(vec.done("o"), 1)
                    dve.wait_ge(pe_s.sem, pe_s.at("proj", i))
                    xi = core.x[:, bass.ds(i, 1), :].rearrange("p a n -> p (a n)")
                    dve.tensor_tensor(xi, xi, psB[:, 3, 0:D], ALU.add).then_inc(vec.done("x"), 1)
                dve.wait_ge(vec.sem, vec.at("x", TT - 1))


def stage_experts(core, tag, router, weights, experts, chunks, gated, keep_top):
    nc, d = core.nc, core.dram
    FIRST = (2 if gated else 1) * DC * P
    WC = FIRST + D
    LATE = 2
    with ExitStack() as ctx:
        sb = lambda name, shape, dt=F32: ctx.enter_context(nc.sbuf_tensor(f"{tag}_{name}", shape, dt))
        sem = lambda name: core.sem(f"{tag}_{name}")
        rw = sb("rw", [P, DC, E])
        iota = sb("iota", [P, E])
        logits = sb("logits", [P, TT, E])
        best, index = sb("best", [P, TT, 8]), sb("index", [P, TT, 8], U32)
        indexf = sb("indexf", [P, TT, 8])
        hot = sb("hot", [P, 2, TT, E])
        share = sb("share", [P, 2, TT])
        wt = sb("wt", [P, TT, E])
        wT = sb("wT", [E, TOK])
        wTd = sb("wTd", [E, E, TOK])
        wb = sb("wb", [P, experts, TOK])
        xh, xl = sb("xh", [P, DC, TOK], F16), sb("xl", [P, DC, TOK], F16)
        w32 = sb("w32", [P, chunks, WC])
        wh, wl = sb("wh", [P, chunks, WC], F16), sb("wl", [P, chunks, WC], F16)
        g = sb("g", [P, 2, TOK])
        sg = sb("sg", [P, 2, TOK])
        hm = sb("hm", [P, 2, TOK])
        hh, hl = sb("hh", [P, 2, TOK], F16), sb("hl", [P, 2, TOK], F16)
        zeros = sb("zeros", [1, 512])

        loaded = sem("loaded")
        second_sem, summed = sem("first_weights"), sem("summed")
        vec = Steps(sem("route_vector"), "x_hi x_lo logits best index indexf hot diff shared_out "
                                         "inverse share weights wT wTd")
        pe_s = Steps(sem("route_tensor"), "logits wT " + " ".join(f"spread{e}" for e in range(E)))
        act_s = Steps(sem("route_scalar"), "exp " + " ".join(f"spread{e}" for e in range(E)))

        w_loaded = [sem(f"w_loaded{k}") for k in range(chunks)]
        w_hi, w_lo = sem("w_hi"), sem("w_lo")
        up_done, gate_w, silu, silu_w = sem("up_done"), sem("gate_w"), sem("silu"), sem("silu_w")
        hidden, hid_hi, hid_lo, down_done = sem("hidden"), sem("hid_hi"), sem("hid_lo"), sem("down_done")

        with ExitStack() as pctx, nc.Block() as block:
            psR = pctx.enter_context(nc.psum_tensor(f"{tag}_psR", [P, TT, E], F32))
            psW = pctx.enter_context(nc.psum_tensor(f"{tag}_psW", [E, TOK], F32))
            psB = pctx.enter_context(nc.psum_tensor(f"{tag}_psB", [P, 2, TOK], F32))

            @block.sync
            def _(sp):
                sp.dma_start(rw[:, :, :], d[router].rearrange("(c p) e -> p c e", p=P)).then_inc(loaded, 16)
                sp.dma_start(iota[:, :], d["c_iota"]).then_inc(loaded, 16)

            @block.tensor
            def _(pe):
                pe.wait_ge(loaded, 32)
                for t in range(TT):
                    for c in range(DC):
                        ins = pe.matmul(psR[:, t, :], core.yT[:, c, t * P:(t + 1) * P], rw[:, c, :],
                                        start=(c == 0), stop=(c == DC - 1))
                ins.then_inc(pe_s.done("logits"), 1)
                pe.wait_ge(vec.sem, vec.at("weights"))
                for t in range(TT):
                    ins = pe.transpose(psW[:, t * P:(t + 1) * P], wt[:, t, :], core.ident[:, :])
                ins.then_inc(pe_s.done("wT"), 1)
                pe.wait_ge(vec.sem, vec.at("wTd"))
                for e in range(E):
                    if e >= 2:
                        pe.wait_ge(act_s.sem, act_s.at(f"spread{e - 2}"))
                    pe.matmul(psB[:, e % 2, :], core.ones[0:E, :], wTd[:, e, :], start=True, stop=True)\
                        .then_inc(pe_s.done(f"spread{e}"), 1)

            @block.scalar
            def _(act):
                act.wait_ge(vec.sem, vec.at("diff"))
                act.activation(share[:, 1, :], share[:, 0, :], ACT.Exp).then_inc(act_s.done("exp"), 1)
                for e in range(E):
                    act.wait_ge(pe_s.sem, pe_s.at(f"spread{e}"))
                    act.activation(wb[:, e, :], psB[:, e % 2, :], ACT.Copy).then_inc(act_s.done(f"spread{e}"), 1)

            @block.vector
            def _(dve):
                dve.tensor_copy(xh[:, :, :], core.yT[:, :, :]).then_inc(vec.done("x_hi"), 1)
                dve.wait_ge(vec.sem, vec.at("x_hi"))
                dve.tensor_tensor(xl[:, :, :], core.yT[:, :, :], xh[:, :, :], ALU.subtract).then_inc(vec.done("x_lo"), 1)
                dve.wait_ge(loaded, 32)
                dve.wait_ge(pe_s.sem, pe_s.at("logits"))
                dve.tensor_copy(logits[:, :, :], psR[:, :, :]).then_inc(vec.done("logits"), 1)
                dve.wait_ge(vec.sem, vec.at("logits"))
                for t in range(TT):
                    ins = dve.max(best[:, t, :], logits[:, t, :])
                ins.then_inc(vec.done("best"), 1)
                dve.wait_ge(vec.sem, vec.at("best"))
                for t in range(TT):
                    ins = dve.max_index(index[:, t, :], best[:, t, :], logits[:, t, :])
                ins.then_inc(vec.done("index"), 1)
                dve.wait_ge(vec.sem, vec.at("index"))
                dve.tensor_copy(indexf[:, :, :], index[:, :, :]).then_inc(vec.done("indexf"), 1)
                dve.wait_ge(vec.sem, vec.at("indexf"))
                for k in range(2):
                    for t in range(TT):
                        ins = dve.tensor_scalar(hot[:, k, t, :], iota[:, :], indexf[:, t, k:k + 1], None, ALU.is_equal)
                ins.then_inc(vec.done("hot"), 1)
                if keep_top == 2:
                    dve.tensor_tensor(share[:, 0, :], best[:, :, 1], best[:, :, 0], ALU.subtract).then_inc(vec.done("diff"), 1)
                else:
                    dve.tensor_scalar(share[:, 0, :], best[:, :, 0], -1.0, 80.0, ALU.mult, ALU.min).then_inc(vec.done("diff"), 1)
                if experts > E:
                    dve.memset(wb[:, E, :], 1.0)
                dve.memset(zeros[:, :], 0.0)
                dve.wait_ge(act_s.sem, act_s.at("exp"))
                dve.tensor_scalar(share[:, 0, :], share[:, 1, :], 1.0, None, ALU.add).then_inc(vec.done("shared_out"), 1)
                dve.wait_ge(vec.sem, vec.at("shared_out"))
                dve.reciprocal(share[:, 0, :], share[:, 0, :]).then_inc(vec.done("inverse"), 1)
                dve.wait_ge(vec.sem, vec.at("inverse"))
                dve.tensor_tensor(share[:, 1, :], share[:, 1, :], share[:, 0, :], ALU.mult).then_inc(vec.done("share"), 1)
                dve.wait_ge(vec.sem, vec.at("share"))
                for t in range(TT):
                    ins = dve.tensor_scalar(wt[:, t, :], hot[:, 0, t, :], share[:, 0, t:t + 1], None, ALU.mult)
                ins.then_inc(second_sem if keep_top == 2 else vec.done("weights"), 1)
                if keep_top == 2:
                    dve.wait_ge(second_sem, 1)
                    for t in range(TT):
                        ins = dve.scalar_tensor_tensor(wt[:, t, :], hot[:, 1, t, :], share[:, 1, t:t + 1], wt[:, t, :],
                                                       ALU.mult, ALU.add)
                    ins.then_inc(vec.done("weights"), 1)
                dve.wait_ge(pe_s.sem, pe_s.at("wT"))
                dve.tensor_copy(wT[:, :], psW[:, :]).then_inc(vec.done("wT"), 1)
                dve.wait_ge(vec.sem, vec.at("wT"))
                dve.tensor_tensor(wTd[:, :, :], wT[:, None, :].to_broadcast([E, E, TOK]),
                                  core.ident[0:E, 0:E, None].to_broadcast([E, E, TOK]), ALU.mult)\
                    .then_inc(vec.done("wTd"), 1)

        with ExitStack() as pctx, nc.Block() as block:
            psY = pctx.enter_context(nc.psum_tensor(f"{tag}_psY", [P, TT, D], F32))
            psG = pctx.enter_context(nc.psum_tensor(f"{tag}_psG", [P, 2, TOK], F32))
            psU = pctx.enter_context(nc.psum_tensor(f"{tag}_psU", [P, 2, TOK], F32))
            START = 1
            n = lambda e, k: e * chunks + k

            @block.sync
            def _(sp):
                def load(e, k):
                    sp.dma_start(w32[:, k, :], d[weights][bass.ds(e, 1), k, :, :].rearrange("a p n -> (a p) n"))\
                        .then_inc(w_loaded[k], 16)

                for k in range(chunks):
                    load(0, k)
                with sp.Fori(0, experts) as e:
                    for k in range(chunks):
                        sp.wait_ge(w_lo, n(e, k) + 1)
                        load(e + 1, k)

            @block.tensor
            def _(pe):
                def first_layers(e, k):
                    s = k % 2
                    pe.wait_ge(w_lo, n(e, k) + 1)
                    pe.wait_ge(hidden, START + n(e, max(k - 1, 0)))
                    for i in range(2 if gated else 1):
                        out = (psG, psU)[i][:, s, :]
                        terms = [(w, x, c) for w, x in ((wh, xh), (wl, xh), (wh, xl)) for c in range(DC)]
                        for j, (w, x, c) in enumerate(terms):
                            col = (i * DC + c) * P
                            ins = pe.matmul(out, w[:, k, col:col + P], x[:, c, :], start=(j == 0),
                                            stop=(j == len(terms) - 1))
                    ins.then_inc(up_done, 1)

                def last_layer(e, k):
                    s = k % 2
                    pe.wait_ge(hid_lo, START + n(e, k) + 1)
                    for t in range(TT):
                        for h, w in ((hh, wh), (hl, wh), (hh, wl)):
                            ins = pe.matmul(psY[:, t, :], h[:, s, t * P:(t + 1) * P], w[:, k, FIRST:WC],
                                            start=False, stop=False, skip_group_check=True)
                    ins.then_inc(down_done, 1)

                for bank in range(2):
                    pe.matmul(psY[:, 2 * bank:2 * bank + 2, :].rearrange("p a n -> p (a n)"), zeros[0:1, 0:P],
                              zeros[0:1, :], start=True, stop=False, skip_group_check=True)
                with pe.Fori(0, experts) as e:
                    for k in range(chunks):
                        first_layers(e, k)
                        if k >= 1:
                            last_layer(e, k - 1)
                    last_layer(e, chunks - 1)

            @block.scalar
            def _(act):
                def split_weights(e, k, first=False):
                    act.wait_ge(w_loaded[k], 16 * e + 16)
                    if not first:
                        act.wait_ge(down_done, START + n(e - 1, k) + 1)
                    act.activation(wh[:, k, :], w32[:, k, :], ACT.Copy).then_inc(w_hi, 1)

                for k in range(chunks):
                    split_weights(0, k, first=True)
                with act.Fori(0, experts) as e:
                    for k in range(chunks):
                        s = k % 2
                        if gated:
                            act.wait_ge(gate_w, n(e, k) + 1)
                            act.activation(sg[:, s, :], g[:, s, :], ACT.Silu).then_inc(silu, 1)
                        act.wait_ge(hidden, START + n(e, k) + 1)
                        act.wait_ge(down_done, START + n(e, max(k - 1, 0)))
                        act.activation(hh[:, s, :], hm[:, s, :], ACT.Copy).then_inc(hid_hi, 1)
                        if k >= LATE:
                            split_weights(e + 1, k - LATE)
                    for k in range(chunks - LATE, chunks):
                        split_weights(e + 1, k)

            if gated:
                @block.gpsimd
                def _(pool):
                    with pool.Fori(0, experts) as e:
                        for k in range(chunks):
                            s = k % 2
                            wait_apart(pool, silu, n(e, k) + 1, core.spare)
                            pool.tensor_tensor(sg[:, s, :], sg[:, s, :],
                                               wb[:, bass.ds(e, 1), :].rearrange("p a n -> p (a n)"), ALU.mult)\
                                .then_inc(silu_w, 1)

            @block.vector
            def _(dve):
                def split_weights(e, k):
                    dve.wait_ge(w_hi, n(e, k) + 1)
                    dve.tensor_tensor(wl[:, k, :], w32[:, k, :], wh[:, k, :], ALU.subtract).then_inc(w_lo, 1)

                for free in (hidden, hid_lo, down_done):
                    dve.sem_inc(free, START)
                for k in range(chunks):
                    split_weights(0, k)
                with dve.Fori(0, experts) as e:
                    w_e = wb[:, bass.ds(e, 1), :].rearrange("p a n -> p (a n)")
                    for k in range(chunks):
                        s = k % 2
                        dve.wait_ge(up_done, n(e, k) + 1)
                        dve.wait_ge(hid_lo, START + n(e, max(k - 1, 0)))
                        if gated:
                            dve.tensor_tensor(g[:, s, :], psG[:, s, :], w_e, ALU.mult).then_inc(gate_w, 1)
                            dve.wait_ge(silu_w, n(e, k) + 1)
                            dve.tensor_tensor(hm[:, s, :], psU[:, s, :], sg[:, s, :], ALU.mult).then_inc(hidden, 1)
                        else:
                            dve.scalar_tensor_tensor(hm[:, s, :], psG[:, s, :], 0.0, w_e, ALU.max, ALU.mult)\
                                .then_inc(hidden, 1)
                        dve.wait_ge(hid_hi, n(e, k) + 1)
                        dve.wait_ge(hidden, START + n(e, k) + 1)
                        dve.wait_ge(down_done, START + n(e, max(k - 1, 0)))
                        dve.tensor_tensor(hl[:, s, :], hm[:, s, :], hh[:, s, :], ALU.subtract).then_inc(hid_lo, 1)
                        if k >= LATE:
                            split_weights(e + 1, k - LATE)
                    for k in range(chunks - LATE, chunks):
                        split_weights(e + 1, k)
                dve.wait_ge(down_done, START + experts * chunks)
                dve.tensor_tensor(core.x[:, :, :], core.x[:, :, :], psY[:, :, :], ALU.add).then_inc(summed, 1)
                dve.wait_ge(summed, 1)


def stage_l1_self(core):
    nc, d = core.nc, core.dram
    DH, NM = 64, 4
    J = NM + N
    DROPPED = J - 64
    PR = H // 2
    W = H * DH
    U = P // 8
    UH = U // 2
    QK_SCALE = 10.0
    halves = [slice(0, N), slice(N, P)]
    with ExitStack() as ctx:
        sb = lambda name, shape, dt=F32: ctx.enter_context(nc.sbuf_tensor(f"l1a_{name}", shape, dt))
        pb = lambda name, shape: ctx.enter_context(nc.psum_tensor(f"l1a_{name}", shape, F32))
        sem = lambda name: core.sem(f"l1a_{name}")
        w = sb("w", [P, DC, 4 * W])
        wo = sb("wo", [P, PR, D])
        bg = sb("bg", [1, W])
        hscale = sb("hscale", [P, H])
        wpre, wpost = sb("wpre", [P, P]), sb("wpost", [P, P])
        mask = sb("mask", [P, 4, U // 4 * J])
        mk, mks, mss = sb("mk", [H * NM, 2 * DH]), sb("mks", [H * NM, DH]), sb("mss", [H * NM, 1])
        mkT = sb("mkT", [P, H * NM])
        mv = sb("mv", [NM, H, DH])
        yt = sb("yt", [P, DC, P])
        qk, sq, ss = sb("qk", [P, 2, H, DH]), sb("sq", [P, 2, H, DH]), sb("ss", [P, 2, H])
        v, gate = sb("v", [P, W]), sb("gate", [P, H, DH])
        qkT = sb("qkT", [P, 2, PR, P])
        sT, sTm = sb("sT", [P, N, H]), sb("sTm", [NM, P, H])
        r = sb("r", [P, U, J])
        s, drop = sb("s", [P, 4, U // 4 * J]), sb("drop", [P, U, J])
        s_rows = s[:, :, :].rearrange("p a (b j) -> p (a b) j", j=J)
        least = sb("least", [P, U, 8])
        low, den = sb("low", [P, U]), sb("den", [P, U])
        e = sb("e", [P, U, J])
        aT, aTm = sb("aT", [P, H, N]), sb("aTm", [NM, H, P])
        o, oT = sb("o", [P, H, DH]), sb("oT", [P, PR, P])
        psA, psB = pb("psA", [P, 4, 512]), pb("psB", [P, 4, 512])
        psA_blocks = psA[:, :, :].rearrange("p a (b q) -> p (a b) q", q=P)

        loaded = sem("loaded")
        setup = Steps(sem("setup"), "squares sums guarded scaled mkT")
        setup_root, setup_T = sem("setup_root"), sem("setup_T")
        vec = Steps(sem("vector"), "yt v gate0 squares sums guarded normed gate1 gate2 gate sT r masked least drop dropped "
                                   "low shifted den rden e aT o x")
        act_s = Steps(sem("scalar"), "qk expgate qkT sTm rm exp aTm oT")
        pe_s = Steps(sem("tensor"), "qk vg qkT sT r mixed aT out oT proj")
        roots = Steps(sem("roots"), "norms")
        N_LOADS = 16 * 12

        with nc.Block() as block:
            @block.sync
            def _(sp):
                for j, name in enumerate(("Wq", "Wk", "Wv", "Wg")):
                    sp.dma_start(w[:, :, j * W:(j + 1) * W], d[f"L1_attn_{name}"].rearrange("(c p) n -> p c n", p=P))\
                        .then_inc(loaded, 16)
                sp.dma_start(wo[:, :, :], d["L1_attn_Wo"].rearrange("(c p) n -> p c n", p=P)).then_inc(loaded, 16)
                sp.dma_start(bg[:, :], d["L1_attn_bg"].partition_broadcast(1)).then_inc(loaded, 16)
                sp.dma_start(hscale[:, :], d["c_head_scale"].partition_broadcast(P)).then_inc(loaded, 16)
                sp.dma_start(wpre[:, :], d["c_pre"]).then_inc(loaded, 16)
                sp.dma_start(wpost[:, :], d["c_post"]).then_inc(loaded, 16)
                sp.dma_start(mask[:, :, :], d["c_rowmask"]).then_inc(loaded, 16)
                sp.dma_start(mk[:, 0:DH], d["L1_attn_mem_k"].rearrange("h m k -> (h m) k")).then_inc(loaded, 16)
                sp.dma_start(mv[:, :, :], d["L1_attn_mem_v"].rearrange("h m k -> m h k")).then_inc(loaded, 16)

            @block.gpsimd
            def _(pool):
                pool.wait_ge(setup.sem, setup.at("guarded"))
                pool.tensor_tensor(mss[:, :], mss[:, :], core.minus_half[0:H * NM, 0:1], ALU.pow).then_inc(setup_root, 1)
                with pool.Fori(0, TT) as i:
                    pool.wait_ge(vec.sem, vec.at("guarded", i))
                    pool.tensor_tensor(ss[:, :, :], ss[:, :, :],
                                       core.minus_half[:, 0:2 * H].rearrange("p (a h) -> p a h", a=2), ALU.pow)\
                        .then_inc(roots.done("norms"), 1)

            @block.tensor
            def _(pe):
                pe.wait_ge(setup.sem, setup.at("scaled"))
                pe.transpose(psA[:, 0, 0:H * NM], mk[:, :], core.ident[0:H * NM, 0:H * NM]).then_inc(setup_T, 1)
                pe.wait_ge(setup.sem, setup.at("mkT"))
                with pe.Fori(0, TT) as i:
                    pe.wait_ge(vec.sem, vec.at("yt", i))
                    for part in range(8):
                        ps = psA[:, part, :] if part < 4 else psB[:, part - 4, :]
                        gates = part >= 6
                        for c in range(DC):
                            ins = pe.matmul(ps, yt[:, c, :], w[:, c, part * 512:(part + 1) * 512],
                                            start=(c == 0), stop=(c == 1 and not gates))
                        if gates:
                            ins = pe.matmul(ps, core.ones[0:1, :], bg[0:1, (part - 6) * 512:(part - 5) * 512],
                                            start=False, stop=True)
                        if part == 3:
                            ins.then_inc(pe_s.done("qk"), 1)
                    ins.then_inc(pe_s.done("vg"), 1)
                    pe.wait_ge(vec.sem, vec.at("normed", i))
                    for a in range(2):
                        for pr in range(PR):
                            ins = pe.transpose(psA_blocks[:, a * PR + pr, :],
                                               qk[:, a, 2 * pr:2 * pr + 2, :].rearrange("p h k -> p (h k)"),
                                               core.ident[:, :])
                    ins.then_inc(pe_s.done("qkT"), 1)
                    pe.wait_ge(act_s.sem, act_s.at("qkT", i))
                    wait_apart(pe, vec.sem, vec.at("gate0", i), core.spare)
                    for pr in range(PR):
                        for odd, rows in enumerate(halves):
                            for half in halves:
                                pe.matmul(psA[half, odd, pr * N:(pr + 1) * N], qkT[rows, 1, pr, half],
                                          qkT[rows, 0, pr, half], start=True, stop=True)
                            h = 2 * pr + odd
                            ins = pe.matmul(psB[0:NM, 2 * odd + pr // 4, pr % 4 * P:(pr % 4 + 1) * P],
                                            mkT[rows, h * NM:(h + 1) * NM], qkT[rows, 0, pr, :], start=True, stop=True)
                    ins.then_inc(pe_s.done("sT"), 1)
                    pe.wait_ge(vec.sem, vec.at("sT", i))
                    pe.wait_ge(act_s.sem, act_s.at("sTm", i))
                    for u in range(U):
                        half, at = halves[u // UH], u % UH
                        pe.matmul(psA[:, u // UH, at * N:(at + 1) * N],
                                  sT[half, at * 8:(at + 1) * 8, :].rearrange("j q h -> j (q h)"),
                                  core.ident[half, half], start=True, stop=True)
                    for u in range(U):
                        ins = pe.matmul(psA[:, 2, u * NM:(u + 1) * NM],
                                        sTm[:, u * 8:(u + 1) * 8, :].rearrange("j q h -> j (q h)"),
                                        core.ident[0:NM, 0:NM], start=True, stop=True)
                    ins.then_inc(pe_s.done("r"), 1)
                    pe.wait_ge(vec.sem, vec.at("r", i))
                    pe.wait_ge(act_s.sem, act_s.at("rm", i))
                    for a in range(4):
                        ins = pe.matmul(psB[:, a, 0:U // 4 * J], wpre[:, :],
                                        r[:, a * 4:(a + 1) * 4, :].rearrange("p u j -> p (u j)"), start=True, stop=True)
                    ins.then_inc(pe_s.done("mixed"), 1)
                    pe.wait_ge(vec.sem, vec.at("e", i))
                    for u in range(U):
                        pe.matmul(psA_blocks[halves[u // UH], u % UH, :], e[:, u, NM:J], wpost[:, :], start=True, stop=True)
                        ins = pe.matmul(psB[0:NM, u // 4, u % 4 * P:(u % 4 + 1) * P], e[:, u, 0:NM], wpost[:, :],
                                        start=True, stop=True)
                    ins.then_inc(pe_s.done("aT"), 1)
                    pe.wait_ge(vec.sem, vec.at("aT", i))
                    pe.wait_ge(act_s.sem, act_s.at("aTm", i))
                    for h in range(H):
                        pe.matmul(psA[:, 2 + h // 8, h % 8 * DH:(h % 8 + 1) * DH], aTm[:, h, :], mv[:, h, :],
                                  start=(h % 8 == 0), stop=False, skip_group_check=True)
                    for h in range(H):
                        for half in halves:
                            ins = pe.matmul(psA[half, 2 + h // 8, h % 8 * DH:(h % 8 + 1) * DH], aT[half, h, :],
                                            v[half, h * DH:(h + 1) * DH], start=False, stop=(h % 8 == 7),
                                            skip_group_check=True)
                    ins.then_inc(pe_s.done("out"), 1)
                    pe.wait_ge(vec.sem, vec.at("o", i))
                    for pr in range(PR):
                        ins = pe.transpose(psA_blocks[:, pr, :], o[:, 2 * pr:2 * pr + 2, :].rearrange("p h k -> p (h k)"),
                                           core.ident[:, :])
                    ins.then_inc(pe_s.done("oT"), 1)
                    pe.wait_ge(act_s.sem, act_s.at("oT", i))
                    for pr in range(PR):
                        ins = pe.matmul(psB[:, 0, 0:D], oT[:, pr, :], wo[:, pr, :], start=(pr == 0), stop=(pr == PR - 1))
                    ins.then_inc(pe_s.done("proj"), 1)

            @block.scalar
            def _(act):
                with act.Fori(0, TT) as i:
                    act.wait_ge(pe_s.sem, pe_s.at("qk", i))
                    act.activation(qk[:, :, :, :].rearrange("p a h k -> p (a h k)"),
                                   psA[:, :, :].rearrange("p a n -> p (a n)"), ACT.Copy).then_inc(act_s.done("qk"), 1)
                    act.wait_ge(vec.sem, vec.at("gate0", i))
                    act.activation(gate[:, :, :], gate[:, :, :], ACT.Exp, scale=-1.0).then_inc(act_s.done("expgate"), 1)
                    act.wait_ge(pe_s.sem, pe_s.at("qkT", i))
                    act.activation(qkT[:, :, :, :].rearrange("p a h k -> p (a h k)"),
                                   psA[:, :, :].rearrange("p a n -> p (a n)"), ACT.Copy).then_inc(act_s.done("qkT"), 1)
                    act.wait_ge(pe_s.sem, pe_s.at("sT", i))
                    act.activation(sTm[:, :, :].rearrange("m q h -> m h q"),
                                   psB[0:NM, :, :].rearrange("m a (b q) -> m (a b) q", q=P), ACT.Copy)\
                        .then_inc(act_s.done("sTm"), 1)
                    act.wait_ge(vec.sem, vec.at("r", i))
                    act.activation(r[:, :, 0:NM], psA[:, 2, 0:U * NM].rearrange("p (u m) -> p u m", m=NM), ACT.Copy,
                                   scale=QK_SCALE).then_inc(act_s.done("rm"), 1)
                    act.wait_ge(vec.sem, vec.at("shifted", i))
                    act.activation(e[:, :, :], s_rows, ACT.Exp, scale=-1.0).then_inc(act_s.done("exp"), 1)
                    act.wait_ge(pe_s.sem, pe_s.at("aT", i))
                    act.activation(aTm[:, :, :].rearrange("m h q -> m q h"),
                                   psB[0:NM, :, :].rearrange("m a (b h) -> m (a b) h", h=H), ACT.Copy)\
                        .then_inc(act_s.done("aTm"), 1)
                    act.wait_ge(pe_s.sem, pe_s.at("oT", i))
                    act.activation(oT[:, :, :], psA_blocks[:, 0:PR, :], ACT.Copy).then_inc(act_s.done("oT"), 1)

            @block.vector
            def _(dve):
                dve.wait_ge(loaded, N_LOADS)
                dve.tensor_tensor(mks[:, :], mk[:, 0:DH], mk[:, 0:DH], ALU.mult).then_inc(setup.done("squares"), 1)
                dve.wait_ge(setup.sem, setup.at("squares"))
                dve.tensor_reduce(mss[:, :], mks[:, :], AX.X, ALU.add).then_inc(setup.done("sums"), 1)
                dve.wait_ge(setup.sem, setup.at("sums"))
                dve.tensor_scalar(mss[:, :], mss[:, :], 1e-24, None, ALU.max).then_inc(setup.done("guarded"), 1)
                dve.wait_ge(setup_root, 1)
                dve.tensor_scalar(mk[:, DH:2 * DH], mk[:, 0:DH], mss[:, 0:1], None, ALU.mult)
                dve.tensor_scalar(mk[:, 0:DH], mk[:, 0:DH], mss[:, 0:1], None, ALU.mult).then_inc(setup.done("scaled"), 1)
                dve.wait_ge(setup_T, 1)
                dve.tensor_copy(mkT[:, :], psA[:, 0, 0:H * NM]).then_inc(setup.done("mkT"), 1)

                with dve.Fori(0, TT) as i:
                    dve.tensor_copy(yt[:, :, :], core.yT[:, :, bass.ds(i * P, P)]).then_inc(vec.done("yt"), 1)
                    dve.wait_ge(pe_s.sem, pe_s.at("vg", i))
                    dve.tensor_copy(v[:, :], psB[:, 0:2, :].rearrange("p a n -> p (a n)")).then_inc(vec.done("v"), 1)
                    dve.tensor_scalar(gate[:, :, :].rearrange("p h k -> p (h k)"),
                                      psB[:, 2:4, :].rearrange("p a n -> p (a n)"), -80.0, None, ALU.max)\
                        .then_inc(vec.done("gate0"), 1)
                    dve.wait_ge(act_s.sem, act_s.at("qk", i))
                    dve.tensor_tensor(sq[:, :, :, :], qk[:, :, :, :], qk[:, :, :, :], ALU.mult).then_inc(vec.done("squares"), 1)
                    dve.wait_ge(vec.sem, vec.at("squares", i))
                    dve.tensor_reduce(ss[:, :, :], sq[:, :, :, :], AX.X, ALU.add).then_inc(vec.done("sums"), 1)
                    dve.wait_ge(vec.sem, vec.at("sums", i))
                    dve.tensor_scalar(ss[:, :, :], ss[:, :, :], 1e-24, None, ALU.max).then_inc(vec.done("guarded"), 1)
                    dve.wait_ge(roots.sem, roots.at("norms", i))
                    dve.tensor_tensor(qk[:, :, :, :], qk[:, :, :, :], ss[:, :, :, None].to_broadcast([P, 2, H, DH]),
                                      ALU.mult).then_inc(vec.done("normed"), 1)
                    dve.wait_ge(act_s.sem, act_s.at("expgate", i))
                    dve.tensor_scalar(gate[:, :, :], gate[:, :, :], 1.0, None, ALU.add).then_inc(vec.done("gate1"), 1)
                    dve.wait_ge(vec.sem, vec.at("gate1", i))
                    dve.reciprocal(gate[:, :, :], gate[:, :, :]).then_inc(vec.done("gate2"), 1)
                    dve.wait_ge(vec.sem, vec.at("gate2", i))
                    dve.tensor_tensor(gate[:, :, :], gate[:, :, :], hscale[:, :, None].to_broadcast([P, H, DH]), ALU.mult)\
                        .then_inc(vec.done("gate"), 1)
                    dve.wait_ge(pe_s.sem, pe_s.at("sT", i))
                    dve.tensor_copy(sT[:, :, :].rearrange("p q h -> p h q"),
                                    psA[:, 0:2, :].rearrange("p a (b q) -> p (a b) q", q=N)).then_inc(vec.done("sT"), 1)
                    dve.wait_ge(pe_s.sem, pe_s.at("r", i))
                    dve.tensor_scalar(r[:, :, NM:J], psA[:, 0:2, :].rearrange("p a (b j) -> p (a b) j", j=N), QK_SCALE, None,
                                      ALU.mult).then_inc(vec.done("r"), 1)
                    dve.wait_ge(pe_s.sem, pe_s.at("mixed", i))
                    dve.scalar_tensor_tensor(s[:, :, :], psB[:, :, 0:U // 4 * J], -1.0, mask[:, :, :], ALU.mult, ALU.add)\
                        .then_inc(vec.done("masked"), 1)
                    wait_apart(dve, vec.sem, vec.at("masked", i), core.spare)
                    for u in range(U):
                        ins = dve.max(least[:, u, :], s_rows[:, u, :])
                    ins.then_inc(vec.done("least"), 1)
                    dve.wait_ge(vec.sem, vec.at("least", i))
                    dve.tensor_tensor(drop[:, :, :], s_rows, least[:, :, DROPPED:DROPPED + 1].to_broadcast([P, U, J]),
                                      ALU.is_gt).then_inc(vec.done("drop"), 1)
                    dve.wait_ge(vec.sem, vec.at("drop", i))
                    dve.scalar_tensor_tensor(s_rows, drop[:, :, :], BIG, s_rows, ALU.mult, ALU.add)\
                        .then_inc(vec.done("dropped"), 1)
                    dve.wait_ge(vec.sem, vec.at("dropped", i))
                    dve.tensor_reduce(low[:, :], s_rows, AX.X, ALU.min).then_inc(vec.done("low"), 1)
                    dve.wait_ge(vec.sem, vec.at("low", i))
                    dve.tensor_tensor(s_rows, s_rows, low[:, :, None].to_broadcast([P, U, J]), ALU.subtract)\
                        .then_inc(vec.done("shifted"), 1)
                    dve.wait_ge(act_s.sem, act_s.at("exp", i))
                    dve.tensor_reduce(den[:, :], e[:, :, :], AX.X, ALU.add).then_inc(vec.done("den"), 1)
                    dve.wait_ge(vec.sem, vec.at("den", i))
                    dve.reciprocal(den[:, :], den[:, :]).then_inc(vec.done("rden"), 1)
                    dve.wait_ge(vec.sem, vec.at("rden", i))
                    dve.tensor_tensor(e[:, :, :], e[:, :, :], den[:, :, None].to_broadcast([P, U, J]), ALU.mult)\
                        .then_inc(vec.done("e"), 1)
                    dve.wait_ge(pe_s.sem, pe_s.at("aT", i))
                    dve.tensor_copy(aT[:, :, :].rearrange("p h q -> p q h"),
                                    psA[:, 0:2, :].rearrange("p a (b h) -> p (a b) h", h=H)).then_inc(vec.done("aT"), 1)
                    dve.wait_ge(pe_s.sem, pe_s.at("out", i))
                    dve.tensor_tensor(o[:, :, :].rearrange("p h k -> p (h k)"), psA[:, 2:4, :].rearrange("p a n -> p (a n)"),
                                      gate[:, :, :].rearrange("p h k -> p (h k)"), ALU.mult).then_inc(vec.done("o"), 1)
                    dve.wait_ge(pe_s.sem, pe_s.at("proj", i))
                    xi = core.x[:, bass.ds(i, 1), :].rearrange("p a n -> p (a n)")
                    dve.tensor_tensor(xi, xi, psB[:, 0, 0:D], ALU.add).then_inc(vec.done("x"), 1)
                dve.wait_ge(vec.sem, vec.at("x", TT - 1))


class Bank:

    def __init__(self, filled, taken, names):
        self.filled, self.taken, self.names = filled, taken, names

    def full(self, name, turn=0):
        return turn * len(self.names) + (self.names.index(name) + 1)

    def free(self, name, turn=0):
        return turn * len(self.names) + (self.names.index(name) + 1)

    def left(self, name, turn=0, ago=0):
        return turn * len(self.names) + (self.names.index(name) + 2 - ago * len(self.names))


class Count:

    def __init__(self, sem, each, primed=0):
        self.sem, self.each, self.primed = sem, each, primed

    def at(self, turn, k):
        return turn * self.each + (k + 1 + self.primed)


def stage_l1_cross(core):
    nc, d = core.nc, core.dram
    DH = 64
    W = H * DH
    PR = H // 2
    HN = H * N
    G = HN // P
    VW = CD + 1
    SCALE = float(DH) ** -0.5
    halves = [slice(0, N), slice(N, P)]

    def tiles(k):
        return [m for m in range(KT) if m * 10 // KT == k]

    POST_T = {2: ["A0"], 4: ["V0"], 6: ["A1"], 8: ["V1"]}
    POST_M = {2: ["B0"], 6: ["B1"]}
    t_jobs = lambda n, main: [f"t{m}" for m in tiles(n - 2)] + (POST_T.get(n, []) if main else [])
    m_jobs = lambda n, main: [f"m{m}.{c}" for m in tiles(n - 3) for c in range(2)] + (POST_M.get(n, []) if main else [])
    t_names = lambda main: [j for n in range(KT) for j in t_jobs(n, main)] + ["sh1"]
    m_names = lambda main: [j for n in range(KT) for j in m_jobs(n, main)] + ["sh0"]

    with ExitStack() as ctx:
        sb = lambda name, shape, dt=F32, to=ctx: to.enter_context(nc.sbuf_tensor(f"l1x_{name}", shape, dt))
        sem = lambda name: core.sem(f"l1x_{name}")
        qAh, qAl = sb("qAh", [P, B + 1, HN], F16), sb("qAl", [P, B, HN], F16)
        qSB = sb("qSB", [P, B + 1, HN], F16)
        q5 = sb("q5", [DH + 1, B + 1, HN], F16)
        wvA, wvB = sb("wvA", [P, W]), sb("wvB", [CB, W])
        gam, bet = sb("gam", [P, CD]), sb("bet", [P, CD])
        loaded, w_loaded = sem("loaded"), sem("w_loaded")

        q_done, q_taken, folded, q_hi, q_lo = sem("q_done"), sem("q_taken"), sem("folded"), sem("q_hi"), sem("q_lo")
        with ExitStack() as inner:
            wq, wkT = sb("wq", [P, DC, W], F32, inner), sb("wkT", [P, PR, 2 * P], F32, inner)
            qT = sb("qT", [P, PR, TOK], F32, inner)
            psQ = inner.enter_context(nc.psum_tensor("l1x_psQ", [P, 4, TOK], F32))
            psF = inner.enter_context(nc.psum_tensor("l1x_psF", [P, 2, 2, TOK], F32))
            with nc.Block() as block:
                @block.sync
                def _(sp):
                    sp.dma_start(wq[:, :, :], d["L1_xattn_Wq"].rearrange("(c p) n -> p c n", p=P)).then_inc(loaded, 16)
                    sp.dma_start(wkT[:, :, :], d["c_wkT"].rearrange("(a p) n -> p a n", p=P)).then_inc(loaded, 16)
                    sp.dma_start(gam[:, :], d["L1_xattn_g_c"].partition_broadcast(P)).then_inc(w_loaded, 16)
                    sp.dma_start(bet[:, :], d["L1_xattn_b_c"].partition_broadcast(P)).then_inc(w_loaded, 16)
                    sp.dma_start(wvA[:, :], d["L1_xattn_Wv"][0:P, :]).then_inc(w_loaded, 16)
                    sp.dma_start(wvB[:, :], d["L1_xattn_Wv"][P:CD, :]).then_inc(w_loaded, 16)
                    sp.wait_ge(w_loaded, 64)

                @block.tensor
                def _(pe):
                    pe.wait_ge(loaded, 32)
                    for pr in range(PR):
                        if pr >= 4:
                            pe.wait_ge(q_taken, pr - 3)
                        for c in range(DC):
                            ins = pe.matmul(psQ[:, pr % 4, :], wq[:, c, pr * P:(pr + 1) * P], core.yT[:, c, :],
                                            start=(c == 0), stop=(c == DC - 1))
                        ins.then_inc(q_done, 1)
                    for h in range(H):
                        pr, r = h // 2, halves[h % 2]
                        pe.wait_ge(q_taken, pr + 1)
                        if h >= 2:
                            pe.wait_ge(q_lo, h - 1)
                        for ab in range(2):
                            ins = pe.matmul(psF[:, h % 2, ab, :], wkT[r, pr, ab * P:(ab + 1) * P], qT[r, pr, :],
                                            start=True, stop=True)
                        ins.then_inc(folded, 1)

                @block.scalar
                def _(act):
                    for pr in range(PR):
                        act.wait_ge(q_done, pr + 1)
                        act.activation(qT[:, pr, :], psQ[:, pr % 4, :], ACT.Copy).then_inc(q_taken, 1)
                    for h in range(H):
                        cols = slice(h * N, (h + 1) * N)
                        act.wait_ge(folded, h + 1)
                        for ab, q in enumerate((qAh, qSB)):
                            ins = act.activation(q[:, 0:B, cols], psF[:, h % 2, ab, :].rearrange("p (b q) -> p b q", q=N),
                                                 ACT.Copy, scale=SCALE)
                        ins.then_inc(q_hi, 1)

                @block.vector
                def _(dve):
                    for q in (qAh, qSB, q5):
                        dve.memset(q[:, B, :], 0.0)
                    for h in range(H):
                        cols = slice(h * N, (h + 1) * N)
                        dve.wait_ge(q_hi, h + 1)
                        for rows, ab, q, hi in ((slice(0, P), 0, qAl, qAh), (slice(0, CB), 1, q5, qSB)):
                            ins = dve.scalar_tensor_tensor(
                                q[rows, 0:B, cols], psF[rows, h % 2, ab, :].rearrange("p (b q) -> p b q", q=N), SCALE,
                                hi[rows, 0:B, cols], ALU.mult, ALU.subtract)
                        ins.then_inc(q_lo, 1)

        raw = sb("raw", [P, KT, CD])
        ch, cl = sb("ch", [P, 2, KT, VW], F16), sb("cl", [P, 2, KT, CD], F16)
        ct = sb("ct", [P, 2, KT, 3 * P], F16)
        c5 = sb("c5", [DH + 1, 2, KT, P], F16)
        stats, aggr, rstd = sb("stats", [P, KT, 6]), sb("aggr", [P, KT, 2]), sb("rstd", [P, KT])
        tops, top = sb("tops", [P, G, KT]), sb("top", [P, G])
        shift = sb("shift", [P, G, DH + 1], F16)
        e32 = sb("e32", [P, 2, 512])
        eh, el = sb("eh", [P, 2, HN], F16), sb("el", [P, 2, HN], F16)
        rden = sb("rden", [P, G])
        a = sb("a", [P, G, CD])
        aT = core.yT
        outT = sb("outT", [P, PR, B + 1, N])

        raw_lo, raw_hi = sem("raw_lo"), sem("raw_hi")
        SPLIT = 7
        statted, aggred = Count(sem("statted"), KT), Count(sem("aggred"), KT)
        eps_added, rooted = Count(sem("eps_added"), KT), Count(sem("rooted"), KT)
        zeroed, scaled = Count(sem("zeroed"), KT), Count(sem("scaled"), KT)
        biased, c_hi, c_lo = Count(sem("biased"), KT), Count(sem("c_hi"), KT), Count(sem("c_lo"), KT)
        topped, shifted = Count(sem("topped"), 1), Count(sem("shifted"), 1)
        scored = Count(sem("scored"), 2 * KT)
        exped, e_split = Count(sem("exped"), 2 * KT, 2), Count(sem("e_split"), 2 * KT, 2)
        weighed = Count(sem("weighed"), KT, 2)
        rdenned, out_taken = Count(sem("rdenned"), 1), Count(sem("out_taken"), 1, 1)
        made = sem("made")

        for main in (False, True):
            name = "loop" if main else "first"
            with ExitStack() as pctx, nc.Block() as block:
                bank = lambda what, n=1: pctx.enter_context(nc.psum_tensor(f"l1x_{what}_{name}", [P, n * 512], F32))
                psT, psM, psS, psO = bank("psT"), bank("psM"), bank("psS", 2), bank("psO", 4)
                bT = Bank(sem(f"T_filled_{name}"), sem(f"T_taken_{name}"), t_names(main))
                bM = Bank(sem(f"M_filled_{name}"), sem(f"M_taken_{name}"), m_names(main))

                def turns(eng, body):
                    if not main:
                        body(None, 0, 0, 0)
                        return
                    with eng.Fori(0, B // 2) as i:
                        for s in range(2):
                            b = i * 2 + s
                            body(b, i * 2 + (s + 1), 1 - s, b)

                @block.sync
                def _(sp):
                    def load(j):
                        src = d["c_ctx"][j, :, :] if isinstance(j, int) else \
                            d["c_ctx"][bass.ds(j, 1), :, :].rearrange("a n k -> (a n) k")
                        src = src.rearrange("(n p) k -> p n k", p=P)
                        return src
                    if not main:
                        for j in range(2):
                            if j:
                                sp.wait_ge(c_lo.sem, c_lo.at(0, SPLIT - 1))
                            sp.dma_start(raw[:, 0:SPLIT, :], load(j)[:, 0:SPLIT, :]).then_inc(raw_lo, 16)
                            if j:
                                sp.wait_ge(c_lo.sem, c_lo.at(0, KT - 1))
                            sp.dma_start(raw[:, SPLIT:KT, :], load(j)[:, SPLIT:KT, :]).then_inc(raw_hi, 16)
                        return
                    with sp.Fori(0, B - 1) as b:
                        sp.wait_ge(c_lo.sem, c_lo.at(b, KT + SPLIT - 1))
                        sp.dma_start(raw[:, 0:SPLIT, :], load(b + 2)[:, 0:SPLIT, :]).then_inc(raw_lo, 16)
                        sp.wait_ge(c_lo.sem, c_lo.at(b, KT + KT - 1))
                        sp.dma_start(raw[:, SPLIT:KT, :], load(b + 2)[:, SPLIT:KT, :]).then_inc(raw_hi, 16)

                @block.gpsimd
                def _(pool):
                    def root(m, j):
                        wait_apart(pool, aggred.sem, aggred.at(j, m), core.spare)
                        pool.tensor_scalar(rstd[:, m:m + 1], aggr[:, m, 1:2], EPS, None, ALU.add).then_inc(eps_added.sem, 1)
                        pool.wait_ge(eps_added.sem, eps_added.at(j, m))
                        pool.tensor_tensor(rstd[:, m:m + 1], rstd[:, m:m + 1], core.minus_half[:, 0:1], ALU.pow)\
                            .then_inc(rooted.sem, 1)

                    def add_beta(m, j):
                        pool.wait_ge(scaled.sem, scaled.at(j, m))
                        pool.tensor_tensor(raw[:, m, :], raw[:, m, :], bet[:, :], ALU.add).then_inc(biased.sem, 1)

                    def body(b, j, slot, turn):
                        for n in range(KT):
                            for m in tiles(n):
                                root(m, j)
                            for m in tiles(n - 1):
                                add_beta(m, j)
                    turns(pool, body)

                @block.tensor
                def _(pe):
                    def side(job, b, j, slot, turn):
                        kind = job[0]
                        if kind == "t":
                            m = int(job[1:])
                            pe.wait_ge(c_lo.sem, c_lo.at(j, m))
                            pe.wait_ge(bT.taken, bT.free(job, turn))
                            pe.matmul(psT[:, 0:P], ch[:, slot, m, 0:P], core.ident16[:, :], start=True, stop=True)
                            pe.matmul(psT[:, P:2 * P], cl[:, slot, m, 0:P], core.ident16[:, :], start=True, stop=True)
                            for rows, c in ((halves[0], ch), (halves[1], cl)):
                                ins = pe.matmul(psT[rows, 2 * P:3 * P], c[:, slot, m, P:CD], core.ident16[:, :],
                                                start=True, stop=True)
                            ins.then_inc(bT.filled, 1)
                        elif kind == "m":
                            m, c = [int(v) for v in job[1:].split(".")]
                            keys = P if m < KT - 1 else TAIL
                            pe.wait_ge(bT.taken, bT.left(f"t{m}", turn))
                            pe.wait_ge(bM.taken, bM.free(job, turn))
                            for g in range(4):
                                cols = slice((4 * c + g) * P, (4 * c + g + 1) * P)
                                for i, (q, x) in enumerate(((qAh, 0), (qSB, 2))):
                                    lhs = q[:, j, cols] if isinstance(j, int) else \
                                        q[:, bass.ds(j, 1), cols].rearrange("p a n -> p (a n)")
                                    ins = pe.matmul(psM[:, g * P:g * P + keys], lhs, ct[:, slot, m, x * P:x * P + keys],
                                                    start=(i == 0), stop=(i == 1))
                            ins.then_inc(bM.filled, 1)
                        elif kind in "AB":
                            half = int(job[1])
                            bank, ps, cols, rows = (bT, psT, slice(0, P), slice(0, P)) if kind == "A" else \
                                (bM, psM, slice(P, CD), slice(0, CB))
                            pe.wait_ge(out_taken.sem, out_taken.at(b, -1))
                            wait_apart(pe, bank.taken, bank.free(job, turn), core.spare)
                            for g in range(4):
                                ins = pe.transpose(ps[rows, g * P:(g + 1) * P], a[:, 4 * half + g, cols], core.ident[:, :])
                            ins.then_inc(bank.filled, 1)
                        elif kind == "V":
                            half = int(job[1])
                            pe.wait_ge(bT.taken, bT.free(job, turn))
                            pe.wait_ge(bM.taken, bM.left(f"B{half}", turn))
                            for k in range(8):
                                h = 8 * half + k
                                out = psT[halves[k % 2], k // 2 * N:(k // 2 + 1) * N]
                                pe.matmul(out, wvA[:, h * DH:(h + 1) * DH], aT[:, 0, k * N:(k + 1) * N], start=True, stop=False)
                                ins = pe.matmul(out, wvB[:, h * DH:(h + 1) * DH], aT[0:CB, 1, k * N:(k + 1) * N],
                                                start=False, stop=True)
                            ins.then_inc(bT.filled, 1)

                    def spread_shift(j, turn):
                        pe.wait_ge(shifted.sem, shifted.at(j, 0))
                        for c, (bank, ps) in enumerate(((bM, psM), (bT, psT))):
                            pe.wait_ge(bank.taken, bank.free(f"sh{c}", turn))
                            for g in range(4):
                                ins = pe.matmul(ps[0:DH + 1, g * P:(g + 1) * P], shift[:, 4 * c + g, :], core.ident16[:, :],
                                                start=True, stop=True)
                            ins.then_inc(bank.filled, 1)

                    def score(n, c, b, s):
                        u, keys = 2 * n + c, (P if n < KT - 1 else TAIL)
                        if n == 0 and c == 0:
                            pe.wait_ge(bM.taken, bM.left("sh0", b, 1))
                            pe.wait_ge(bT.taken, bT.left("sh1", b, 1))
                        pe.wait_ge(exped.sem, exped.at(b, u - 2))
                        passes = ((ct, 0, qAh, P), (ct, P, qAh, P), (ct, 0, qAl, P), (ct, 2 * P, qSB, P), (c5, 0, q5, DH + 1))
                        for i, (x, k, q, rows) in enumerate(passes):
                            ins = pe.matmul(psS[0:keys, c * 512:(c + 1) * 512], x[0:rows, s, n, k:k + keys],
                                            q[0:rows, bass.ds(b, 1), c * 512:(c + 1) * 512].rearrange("p a n -> p (a n)"),
                                            start=(i == 0), stop=(i == len(passes) - 1))
                        ins.then_inc(scored.sem, 1)

                    def weigh(n, c, b, s):
                        keys, e = (P if n < KT - 1 else TAIL), (s + n) % 2
                        pe.wait_ge(e_split.sem, e_split.at(b, 2 * n + c))
                        if n == 0 and c == 0:
                            pe.wait_ge(out_taken.sem, out_taken.at(b, -1))
                        for g in range(4 * c, 4 * c + 4):
                            cols, o = slice(g * P, (g + 1) * P), g // 2 * 512 + g % 2 * VW
                            first = n == 0 and g % 2 == 0
                            pe.matmul(psO[:, o:o + VW], eh[0:keys, e, cols], ch[0:keys, s, n, :],
                                      start=first, stop=False, skip_group_check=True)
                            pe.matmul(psO[:, o:o + CD], eh[0:keys, e, cols], cl[0:keys, s, n, :],
                                      start=False, stop=False, skip_group_check=True)
                            ins = pe.matmul(psO[:, o:o + VW], el[0:keys, e, cols], ch[0:keys, s, n, :],
                                            start=False, stop=(n == KT - 1), skip_group_check=True)
                        if c == 1:
                            ins.then_inc(weighed.sem, 1)

                    def body(b, j, slot, turn):
                        s = 1 - slot
                        for n in range(KT):
                            ms, ts = m_jobs(n, main), t_jobs(n, main)
                            work = []
                            if main:
                                work = [(score, n, 0), (score, n, 1)] + ([(weigh, n - 1, 0), (weigh, n - 1, 1)] if n else [])
                            for k in range(max(len(work), len(ms), len(ts))):
                                if k < len(ms):
                                    side(ms[k], b, j, slot, turn)
                                if k < len(work):
                                    what, tile, c = work[k]
                                    what(tile, c, b, s)
                                if k < len(ts):
                                    side(ts[k], b, j, slot, turn)
                        if main:
                            weigh(KT - 1, 0, b, s)
                        spread_shift(j, turn)
                        if main:
                            weigh(KT - 1, 1, b, s)

                    if not main:
                        pe.wait_ge(made, 1)
                    turns(pe, body)

                @block.scalar
                def _(act):
                    def exp(n, c, b, s):
                        u, keys, e = 2 * n + c, (P if n < KT - 1 else TAIL), (s + n) % 2
                        act.wait_ge(weighed.sem, weighed.at(b, n - 2))
                        act.wait_ge(e_split.sem, e_split.at(b, u - 2))
                        act.wait_ge(scored.sem, scored.at(b, u))
                        ps = psS[0:keys, c * 512:(c + 1) * 512]
                        act.activation(e32[0:keys, c, :], ps, ACT.Exp)
                        act.activation(eh[0:keys, e, c * 512:(c + 1) * 512], ps, ACT.Exp).then_inc(exped.sem, 1)

                    def take(job, b, j, slot, turn):
                        act.wait_ge(bT.filled, bT.full(job, turn))
                        if job[0] == "t":
                            m = int(job[1:])
                            act.activation(ct[:, slot, m, :], psT[:, 0:3 * P], ACT.Copy)
                            act.activation(c5[0:CB, slot, m, :], psT[0:CB, 2 * P:3 * P], ACT.Copy).then_inc(bT.taken, 1)
                        elif job[0] == "A":
                            act.activation(aT[:, 0, :], psT[:, :], ACT.Copy).then_inc(bT.taken, 1)

                    def body(b, j, slot, turn):
                        s = 1 - slot
                        if main:
                            act.wait_ge(weighed.sem, weighed.at(b, -1))
                        for n in range(KT):
                            ts = t_jobs(n, main)
                            for k in range(max(2, len(ts))):
                                if main and k < 2:
                                    exp(n, k, b, s)
                                if k < len(ts) and ts[k][0] != "V":
                                    take(ts[k], b, j, slot, turn)
                            for m in tiles(n - 1):
                                act.wait_ge(biased.sem, biased.at(j, m))
                                act.activation(ch[:, slot, m, 0:CD], raw[:, m, :], ACT.Copy).then_inc(c_hi.sem, 1)
                        for c, (bank, ps) in enumerate(((bM, psM), (bT, psT))):
                            wait_apart(act, bank.filled, bank.full(f"sh{c}", turn), core.spare)
                            out = q5[DH:DH + 1, j, :] if isinstance(j, int) else \
                                q5[DH:DH + 1, bass.ds(j, 1), :].rearrange("p a n -> p (a n)")
                            act.activation(out[:, c * 512:(c + 1) * 512], ps[DH:DH + 1, :], ACT.Copy)\
                                .then_inc(bank.taken, 1)
                    turns(act, body)

                @block.vector
                def _(dve):
                    def stage0(m, j):
                        half_loaded = raw_lo if m < SPLIT else raw_hi
                        dve.wait_ge(half_loaded, j * 16 + 16)
                        dve.bn_stats(stats[:, m, :], raw[:, m, :]).then_inc(statted.sem, 1)
                        wait_apart(dve, statted.sem, statted.at(j, m), core.spare)
                        dve.bn_aggr(aggr[:, m, :], stats[:, m, :]).then_inc(aggred.sem, 1)

                    def stage1(m, j):
                        dve.wait_ge(rooted.sem, rooted.at(j, m))
                        dve.tensor_scalar(raw[:, m, :], raw[:, m, :], aggr[:, m, 0:1], rstd[:, m:m + 1],
                                          ALU.subtract, ALU.mult).then_inc(zeroed.sem, 1)
                        dve.wait_ge(zeroed.sem, zeroed.at(j, m))
                        dve.tensor_tensor(raw[:, m, :], raw[:, m, :], gam[:, :], ALU.mult).then_inc(scaled.sem, 1)

                    def stage2(m, j, slot):
                        dve.wait_ge(c_hi.sem, c_hi.at(j, m))
                        dve.tensor_tensor(cl[:, slot, m, :], raw[:, m, :], ch[:, slot, m, 0:CD], ALU.subtract)\
                            .then_inc(c_lo.sem, 1)

                    def take(job, turn):
                        bank = bT if job[0] == "V" else bM
                        if job[0] == "B":
                            if job == "B1":
                                dve.wait_ge(bT.filled, bT.full("V0", turn))
                            dve.wait_ge(bM.filled, bM.full(job, turn))
                            dve.tensor_copy(aT[0:CB, 1, :], psM[0:CB, :]).then_inc(bM.taken, 1)
                        elif job[0] == "V":
                            half = int(job[1])
                            dve.wait_ge(bT.filled, bT.full(job, turn))
                            dve.tensor_scalar(
                                outT[:, 4 * half:4 * half + 4, bass.ds(turn, 1), :].rearrange("p k a q -> p k (a q)"),
                                psT[:, 0:4 * N].rearrange("p (k q) -> p k q", q=N), 1.0, None, ALU.mult)\
                                .then_inc(bT.taken, 1)
                        else:
                            m, c = [int(v) for v in job[1:].split(".")]
                            keys = P if m < KT - 1 else TAIL
                            dve.wait_ge(bM.filled, bM.full(job, turn))
                            dve.tensor_reduce(tops[:, 4 * c:4 * c + 4, m],
                                              psM[:, :].rearrange("p (g k) -> p g k", k=P)[:, :, 0:keys],
                                              AX.X, ALU.max).then_inc(bM.taken, 1)

                    def lo_half(n, c, b, s):
                        u, keys, e = 2 * n + c, (P if n < KT - 1 else TAIL), (s + n) % 2
                        dve.wait_ge(exped.sem, exped.at(b, u))
                        dve.tensor_tensor(el[0:keys, e, c * 512:(c + 1) * 512], e32[0:keys, c, :],
                                          eh[0:keys, e, c * 512:(c + 1) * 512], ALU.subtract).then_inc(e_split.sem, 1)

                    def body(b, j, slot, turn):
                        s = 1 - slot
                        for n in range(KT):
                            ms, ts = m_jobs(n, main), t_jobs(n, main)
                            for job in ms[0:2]:
                                take(job, turn)
                            for m in tiles(n):
                                stage0(m, j)
                            if main:
                                lo_half(n, 0, b, s)
                            for m in tiles(n - 1):
                                stage1(m, j)
                            for job in ms[2:]:
                                take(job, turn)
                            if main:
                                lo_half(n, 1, b, s)
                            for job in ts:
                                if job[0] == "V":
                                    take(job, turn)
                            for m in tiles(n - 1):
                                stage2(m, j, slot)
                        dve.wait_ge(bM.taken, bM.free("sh0", turn))
                        dve.tensor_reduce(top[:, :], tops[:, :, :], AX.X, ALU.max).then_inc(topped.sem, 1)
                        dve.wait_ge(topped.sem, topped.at(j, 0))
                        dve.tensor_scalar(shift[:, :, DH], top[:, :], -1.0, None, ALU.mult).then_inc(shifted.sem, 1)
                        if main:
                            dve.wait_ge(weighed.sem, weighed.at(b, KT - 1))
                            dve.wait_ge(bT.filled, bT.full("V1", turn))
                            sums = psO[:, :].rearrange("p (k n) -> p k n", n=512)[:, :, 0:2 * VW]\
                                .rearrange("p k (g w) -> p k g w", w=VW)
                            dve.reciprocal(rden[:, :].rearrange("p (k g) -> p k g", g=2), sums[:, :, :, CD])\
                               .then_inc(rdenned.sem, 1)
                            dve.wait_ge(rdenned.sem, rdenned.at(b, 0))
                            dve.tensor_tensor(
                                a[:, :, :].rearrange("p (k g) w -> p k g w", g=2), sums[:, :, :, 0:CD],
                                rden[:, :].rearrange("p (k g) -> p k g", g=2)[:, :, :, None].to_broadcast([P, 4, 2, CD]),
                                ALU.mult).then_inc(out_taken.sem, 1)

                    if main:
                        dve.sem_inc(exped.sem, exped.primed)
                        dve.sem_inc(e_split.sem, e_split.primed)
                        dve.sem_inc(weighed.sem, weighed.primed)
                        dve.sem_inc(out_taken.sem, out_taken.primed)
                    else:
                        dve.memset(a[:, :, :], 0.0)
                        dve.memset(shift[:, :, :], 0.0)
                        dve.memset(c5[DH:DH + 1, :, :, :], 1.0)
                        dve.memset(ch[:, :, :, CD:VW], 1.0).then_inc(made, 1)
                    dve.sem_inc(bT.taken, 1)
                    dve.sem_inc(bM.taken, 1)
                    turns(dve, body)

        wo = sb("wo", [P, PR, D])
        wo_loaded, filled, taken = sem("wo_loaded"), sem("end_filled"), sem("end_taken")
        with ExitStack() as pctx, nc.Block() as block:
            bank = lambda what, n=1: pctx.enter_context(nc.psum_tensor(f"l1x_{what}_end", [P, n, 512], F32))
            psA, psB, psV, psX = bank("psA"), bank("psB"), bank("psV"), bank("psX", 2)
            proj = psX[:, :, :].rearrange("p a (t n) -> p (a t) n", n=D)

            @block.sync
            def _(sp):
                sp.dma_start(wo[:, :, :], d["L1_xattn_Wo"].rearrange("(c p) n -> p c n", p=P)).then_inc(wo_loaded, 16)

            @block.tensor
            def _(pe):
                for half in range(2):
                    if half:
                        pe.wait_ge(taken, 3 * half)
                    for ps, cols, rows in ((psA, slice(0, P), slice(0, P)), (psB, slice(P, CD), slice(0, CB))):
                        for g in range(4):
                            ins = pe.transpose(ps[rows, 0, g * P:(g + 1) * P], a[:, 4 * half + g, cols], core.ident[:, :])
                        ins.then_inc(filled, 1)
                    pe.wait_ge(taken, 3 * half + 2)
                    for k in range(8):
                        h = 8 * half + k
                        out = psV[halves[k % 2], 0, k // 2 * N:(k // 2 + 1) * N]
                        pe.matmul(out, wvA[:, h * DH:(h + 1) * DH], aT[:, 0, k * N:(k + 1) * N], start=True, stop=False)
                        ins = pe.matmul(out, wvB[:, h * DH:(h + 1) * DH], aT[0:CB, 1, k * N:(k + 1) * N],
                                        start=False, stop=True)
                    ins.then_inc(filled, 1)
                pe.wait_ge(taken, 6)
                pe.wait_ge(wo_loaded, 16)
                for t in range(TT):
                    for pr in range(PR):
                        ins = pe.matmul(proj[:, t, :], outT[:, pr, 1 + 2 * t:3 + 2 * t, :].rearrange("p b q -> p (b q)"),
                                        wo[:, pr, :], start=(pr == 0), stop=(pr == PR - 1))
                ins.then_inc(filled, 1)

            @block.vector
            def _(dve):
                for half in range(2):
                    dve.wait_ge(filled, 3 * half + 1)
                    dve.tensor_copy(aT[:, 0, :], psA[:, 0, :]).then_inc(taken, 1)
                    dve.wait_ge(filled, 3 * half + 2)
                    dve.tensor_copy(aT[0:CB, 1, :], psB[0:CB, 0, :]).then_inc(taken, 1)
                    dve.wait_ge(filled, 3 * half + 3)
                    dve.tensor_copy(outT[:, 4 * half:4 * half + 4, B, :],
                                    psV[:, 0, 0:4 * N].rearrange("p (k q) -> p k q", q=N)).then_inc(taken, 1)
                dve.wait_ge(filled, 7)
                dve.tensor_tensor(core.x[:, :, :], core.x[:, :, :], proj[:, :, :], ALU.add).then_inc(taken, 1)
                dve.wait_ge(taken, 7)


STAGES = [
    lambda core: (stage_norm(core, "n0"), stage_l0_cross(core)),
    lambda core: (stage_norm(core, "n1", ("L0_attn_gamma", None, False)), stage_l0_self(core)),
    lambda core: (stage_norm(core, "n2", ("L0_ffn_ln_w", "L0_ffn_ln_b", True)),
                  stage_experts(core, "l0f", "L0_ffn_router_w", "c_l0_experts", E + 1, 4, True, 1)),
    lambda core: (stage_norm(core, "n3", ("L1_xattn_g_x", "L1_xattn_b_x", False)), stage_l1_cross(core)),
    lambda core: (stage_norm(core, "n4"), stage_l1_self(core)),
    lambda core: (stage_norm(core, "n5"), stage_experts(core, "l1f", "c_l1_router", "c_l1_experts", E, 8, False, 2)),
]


def perceiver_program(nc, dram, stages=STAGES):
    with ExitStack() as ctx:
        core = Core(nc, ctx, dram)
        stage_load(core)
        for stage in stages:
            stage(core)
            core.clear_sems()
        stage_store(core)


def _constants():
    import numpy as np
    c = {}
    c["c_ident"] = np.eye(P, dtype=np.float32)
    c["c_headmask"] = (np.arange(P)[:, None] // 16 == np.arange(8)[None, :]).astype(np.float32)
    c["c_half"] = np.repeat(np.array([[1, 0, 0], [0, 1, -1]], np.float32), P // 2, axis=0)
    slope = 2.0 ** (-2.0 ** (-(np.log2(H) - 3.0)))
    slopes = np.array([slope * slope ** h for h in range(H)], np.float32)
    rows, cols = np.arange(N)[:, None], np.arange(N + 2)[None, :]
    alibi = -np.abs(cols - (rows + 2)).astype(np.float32)[:, None, :] * slopes[None, :, None]
    alibi = np.where((cols > rows + 2)[:, None, :], np.float32(-BIG), alibi).astype(np.float32)
    places = np.concatenate([np.arange(0, H, 2), np.arange(1, H, 2)])
    c["c_alibi"] = np.concatenate([alibi, alibi], axis=0)[:, places, :]
    c["c_blockmask"] = (np.arange(2 * H)[:, None] // 2 == np.arange(H)[None, :]).astype(np.float32)
    c["c_iota"] = np.tile(np.arange(E, dtype=np.float32), (P, 1))
    q = np.arange(P // 8)[None, :, None] % 8 * 8 + (np.arange(P) // H)[:, None, None]
    key = np.arange(N + 4)[None, None, :] - 4
    c["c_rowmask"] = np.where(key > q, np.float32(BIG), np.float32(0)).reshape(P, 4, -1)
    return c


def _layouts(inputs):
    import numpy as np
    a = {k: np.ascontiguousarray(v) for k, v in inputs.items()}
    ctx = a.pop("ctx_768")
    t = np.zeros((B + 1, CD, MP), np.float32)
    t[:B, :, :M] = ctx.transpose(0, 2, 1)
    a["c_ctxT"] = t
    rows = np.zeros((B + 1, MP, CD), np.float32)
    rows[:B, :M] = ctx
    a["c_ctx"] = rows
    wkT = a.pop("L1_xattn_Wk").T
    a["c_wkT"] = np.concatenate([wkT, wkT[:, P:]], axis=1)
    null = a.pop("L0_attn_null_kv").reshape(H, 2, 2, 64)
    a["c_null_k"] = np.ascontiguousarray(null[:, :, 0]).reshape(2 * H, 64)
    nv = np.zeros((H, 2, H, 64), np.float32)
    for h in range(H):
        nv[h % 2 * (H // 2) + h // 2, :, h] = null[h, :, 1]
    a["c_null_v"] = nv.reshape(2 * H, H * 64)
    def first(w):
        e, _, f = w.shape
        return w.reshape(e, DC, P, f // P, P).transpose(0, 3, 2, 1, 4).reshape(e, f // P, P, DC * P)

    def last(w):
        e, f, _ = w.shape
        return w.reshape(e, f // P, P, D)

    with_shared = lambda many, one: np.concatenate([a.pop(many), a.pop(one)[None]])
    a["c_l0_experts"] = np.concatenate([first(with_shared("L0_ffn_gate_w", "L0_ffn_sh_gate")),
                                        first(with_shared("L0_ffn_up_w", "L0_ffn_sh_up")),
                                        last(with_shared("L0_ffn_down_w", "L0_ffn_sh_down"))], axis=-1)
    a["c_l1_experts"] = np.concatenate([first(a.pop("L1_ffn_w1").transpose(0, 2, 1)),
                                        last(a.pop("L1_ffn_w2").transpose(0, 2, 1))], axis=-1)
    for name in ("c_l0_experts", "c_l1_experts"):
        a[name] = np.concatenate([a[name], np.zeros_like(a[name][:1])])
    a["c_l1_router"] = np.ascontiguousarray(a.pop("L1_ffn_gate_w").T)
    def on_diagonal(w, row_of):
        out = np.zeros((8, H, 8, H), np.float32)
        for i in range(8):
            for g in range(H):
                out[i, row_of(g), i, :] = w[:, g]
        return out.reshape(P, P)

    a["c_pre"] = on_diagonal(a.pop("L1_attn_W_pre_th"), lambda g: g % 2 * (H // 2) + g // 2)
    a["c_post"] = on_diagonal(a.pop("L1_attn_W_post_th"), lambda g: g)
    a["c_head_scale"] = a.pop("L1_attn_head_scale_params").reshape(H)
    return a


def kernel(**inputs):
    import numpy as _np
    import concourse.bacc as _bacc
    from concourse.bass_utils import run_bass_kernel_spmd as _run

    nc = _bacc.Bacc("TRN2", target_bir_lowering=False, num_devices=1)
    arrays = {**_layouts(inputs), **_constants()}
    dram = {k: nc.dram_tensor(f"in_{k}", a.shape, mybir.dt.from_np(a.dtype), kind="ExternalInput").ap()
            for k, a in arrays.items()}
    dram["out"] = nc.dram_tensor("out_x", (B, N, D), F32, kind="ExternalOutput").ap()
    perceiver_program(nc, dram)
    r = _run(nc, [{f"in_{k}": a for k, a in arrays.items()}], core_ids=[0])
    return r.results[0]["out_x"]
```

```python
from contextlib import ExitStack

import concourse.bass as bass
from concourse import mybir

F32 = mybir.dt.float32
F16 = mybir.dt.float16
U32 = mybir.dt.uint32
ALU = mybir.AluOpType
ACT = mybir.ActivationFunctionType
AX = mybir.AxisListType

P = 128
B, N, D = 8, 64, 256
TOK = B * N
TT = TOK // P
DC = D // P
M, CD = 1601, 192
KT = -(-M // P)
MP = KT * P
TAIL = M - (KT - 1) * P
CB = CD - P
H = 16
E = 8
EPS = 1e-5
BIG = 1e30


class Steps:

    def __init__(self, sem, names):
        self.sem, self.names, self.said = sem, names.split(), 0

    def done(self, name):
        assert self.names[self.said % len(self.names)] == name, (name, self.names[self.said % len(self.names)])
        self.said += 1
        return self.sem

    def at(self, name, turn=0):
        return turn * len(self.names) + self.names.index(name) + 1


class Count:

    def __init__(self, sem, each, primed=0):
        self.sem, self.each, self.primed = sem, each, primed

    def at(self, turn, k):
        return turn * self.each + (k + 1 + self.primed)


def wait_apart(eng, sem, value, spare):
    eng.wait_ge(sem, value)
    eng.sem_inc(spare, 1)


def norm_steps(tag):
    return f"{tag}_stats {tag}_aggr {tag}"


def layer_norm(dve, steps, roots, tag, dst, src, work):
    stats, aggr, rstd = work
    for t in range(TT):
        ins = dve.bn_stats(stats[:, t, :], src[:, t, :])
    ins.then_inc(steps.done(f"{tag}_stats"), 1)
    dve.wait_ge(steps.sem, steps.at(f"{tag}_stats"))
    for t in range(TT):
        ins = dve.bn_aggr(aggr[:, t, :], stats[:, t, :])
    ins.then_inc(steps.done(f"{tag}_aggr"), 1)
    dve.wait_ge(roots.sem, roots.at(tag))
    for t in range(TT):
        ins = dve.tensor_scalar(dst[:, t, :], src[:, t, :], aggr[:, t, 0:1], rstd[:, t:t + 1],
                                ALU.subtract, ALU.mult)
    ins.then_inc(steps.done(tag), 1)
    dve.wait_ge(steps.sem, steps.at(tag))


def layer_norm_root(pool, steps, roots, tag, work, minus_half):
    stats, aggr, rstd = work
    pool.wait_ge(steps.sem, steps.at(f"{tag}_aggr"))
    pool.tensor_scalar(rstd[:, :], aggr[:, :, 1], EPS, None, ALU.add).then_inc(roots.done(f"{tag}_var"), 1)
    pool.wait_ge(roots.sem, roots.at(f"{tag}_var"))
    pool.tensor_tensor(rstd[:, :], rstd[:, :], minus_half, ALU.pow).then_inc(roots.done(tag), 1)


class Core:

    def __init__(self, nc, ctx, dram):
        self.nc, self.dram = nc, dram
        sb = lambda name, shape, dt=F32: ctx.enter_context(nc.sbuf_tensor(name, shape, dt))
        self.sems = []
        self.spare = nc.alloc_semaphore(name="spare")
        self.x = sb("x", [P, TT, D])
        self.y = sb("y", [P, TT, D])
        self.yT = sb("yT", [P, DC, TOK])
        self.ident = sb("ident", [P, P])
        self.ident16 = sb("ident16", [P, P], F16)
        self.ones = sb("ones", [P, P])
        self.minus_half = sb("minus_half", [P, 64])
        self.norm_work = (sb("ln_stats", [P, TT, 6]), sb("ln_aggr", [P, TT, 2]), sb("ln_rstd", [P, TT]))


    def sem(self, name):
        self.sems.append(self.nc.alloc_semaphore(name=name))
        return self.sems[-1]

    def clear_sems(self):
        self.nc.clear_and_free_semaphores(self.sems)
        self.nc.all_engine_barrier()
        self.sems = []


def stage_load(core):
    nc, d = core.nc, core.dram
    loaded, made = core.sem("load_loaded"), core.sem("load_made")
    with nc.Block() as block:
        @block.sync
        def _(sp):
            sp.dma_start(core.x[:, :, :], d["x"].rearrange("(a b) n d -> (b n) a d", b=2)).then_inc(loaded, 16)
            sp.dma_start(core.ident[:, :], d["c_ident"]).then_inc(loaded, 16)
            sp.wait_ge(loaded, 32)

        @block.vector
        def _(dve):
            dve.memset(core.ones[:, :], 1.0)
            dve.memset(core.minus_half[:, :], -0.5)
            dve.wait_ge(loaded, 32)
            dve.tensor_copy(core.ident16[:, :], core.ident[:, :]).then_inc(made, 1)


def stage_store(core):
    nc, d = core.nc, core.dram
    stored = core.sem("stored")
    with nc.Block() as block:
        @block.sync
        def _(sp):
            sp.dma_start(d["out"].rearrange("(a b) n d -> (b n) a d", b=2), core.x[:, :, :]).then_inc(stored, 16)
            sp.wait_ge(stored, 16)


def stage_norm(core, tag, inner, prefetch):
    nc, d = core.nc, core.dram
    gamma, beta, keep = inner or (None, None, False)
    with ExitStack() as ctx:
        sb = lambda name, shape, dt=F32: ctx.enter_context(nc.sbuf_tensor(f"{tag}_{name}", shape, dt))
        g = sb("gamma", [P, D])
        b = sb("beta", [P, D])
        psT = ctx.enter_context(nc.psum_tensor(f"{tag}_psT", [P, DC, TOK], F32))
        loaded = core.sem(f"{tag}_loaded")
        n_loads = sum(v is not None for v in (gamma, beta))
        names = norm_steps("outer")
        if inner:
            names += " " + ("kept " if keep else "") + norm_steps("inner") + " gamma" + (" beta" if beta else "")
        vec = Steps(core.sem(f"{tag}_vector"), names)
        pe_s = Steps(core.sem(f"{tag}_tensor"), "transposed0 transposed1")
        roots = Steps(core.sem(f"{tag}_roots"), "outer_var outer" + (" inner_var inner" if inner else ""))
        last = vec.names[-1]
        done = core.sem(f"{tag}_evacuated")
        with nc.Block() as block:
            @block.sync
            def _(sp):
                if gamma:
                    sp.dma_start(g[:, :], d[gamma].partition_broadcast(P)).then_inc(loaded, 16)
                if beta:
                    sp.dma_start(b[:, :], d[beta].partition_broadcast(P)).then_inc(loaded, 16)
                prefetch(sp)

            @block.gpsimd
            def _(pool):
                for which in roots.names[1::2]:
                    layer_norm_root(pool, vec, roots, which, core.norm_work, core.minus_half[:, 0:TT])

            @block.vector
            def _(dve):
                layer_norm(dve, vec, roots, "outer", core.y, core.x, core.norm_work)
                if inner:
                    if keep:
                        dve.tensor_tensor(core.x[:, :, :], core.x[:, :, :], core.y[:, :, :], ALU.add)\
                           .then_inc(vec.done("kept"), 1)
                        dve.wait_ge(vec.sem, vec.at("kept"))
                    layer_norm(dve, vec, roots, "inner", core.y, core.y, core.norm_work)
                    dve.wait_ge(loaded, 16 * n_loads)
                    dve.tensor_tensor(core.y[:, :, :], core.y[:, :, :],
                                      g[:, None, :].to_broadcast([P, TT, D]), ALU.mult).then_inc(vec.done("gamma"), 1)
                    if beta:
                        dve.wait_ge(vec.sem, vec.at("gamma"))
                        dve.tensor_tensor(core.y[:, :, :], core.y[:, :, :],
                                          b[:, None, :].to_broadcast([P, TT, D]), ALU.add).then_inc(vec.done("beta"), 1)
                dve.wait_ge(pe_s.sem, pe_s.at("transposed0"))
                dve.tensor_copy(core.yT[:, 0, :], psT[:, 0, :]).then_inc(done, 1)

            @block.scalar
            def _(act):
                act.wait_ge(pe_s.sem, pe_s.at("transposed1"))
                act.activation(core.yT[:, 1, :], psT[:, 1, :], ACT.Copy).then_inc(done, 1)

            @block.tensor
            def _(pe):
                pe.wait_ge(vec.sem, vec.at(last))
                for c in range(DC):
                    for t in range(TT):
                        ins = pe.transpose(psT[:, c, t * P:(t + 1) * P], core.y[:, t, c * P:(c + 1) * P],
                                           core.ident[:, :])
                    ins.then_inc(pe_s.done(f"transposed{c}"), 1)


def stage_l0_cross(core, norm):
    nc, d = core.nc, core.dram
    HD = D // H
    HC = H // DC
    PR = H // 2
    VW = 4 * HD + 1
    with ExitStack() as ctx:
        sb = lambda name, shape, dt=F32: ctx.enter_context(nc.sbuf_tensor(f"l0x_{name}", shape, dt))
        pb = lambda name, shape, dt=F32: ctx.enter_context(nc.psum_tensor(f"l0x_{name}", shape, dt))
        sem = lambda name: core.sem(f"l0x_{name}")

        wq, wo = sb("wq", [P, DC, D]), sb("wo", [P, 2, D])
        wA, wB = sb("wA", [P, 2 * D]), sb("wB", [P, 2 * D])
        bias = sb("bias", [97, 2 * D])
        rows = sb("rows", [1, 2, D])
        wAh, wAl, wBh = sb("wAh", [P, 2 * D], F16), sb("wAl", [P, 2 * D], F16), sb("wBh", [P, 2 * D], F16)
        biash = sb("biash", [97, 2 * D], F16)
        w5 = sb("w5", [P, 2 * D], F16)
        gam, bet = sb("gam", [P, D]), sb("bet", [P, D])
        headmask = sb("headmask", [P, HC])
        headmask16 = sb("headmask16", [P, HC], F16)
        qp = sb("qp", [P, TT, D])
        sq = sb("sq", [P, TT, D])
        qn = sb("qn", [P, TT, D])
        qss = sb("qss", [P, TT])
        qT = sb("qT", [P, DC, TOK])
        qTh, qTl = sb("qTh", [P, DC, TOK], F16), sb("qTl", [P, DC, TOK], F16)
        qbh, qbl = sb("qbh", [P, DC, B, HC, N], F16), sb("qbl", [P, DC, B, HC, N], F16)
        cA, cB = sb("cA", [P, MP]), sb("cB", [P, MP])
        cAh, cAl, cS = sb("cAh", [P, MP], F16), sb("cAl", [P, MP], F16), sb("cS", [P, MP], F16)
        c5 = sb("c5", [P, MP], F16)
        kh, kl = sb("kh", [P, 2, D], F16), sb("kl", [P, 2, D], F16)
        ksq = sb("ksq", [P, 2, D])
        kss, rn = sb("kss", [P, 2]), sb("rn", [P, 2])
        v = sb("v", [P, 2, PR, VW], F16)
        e32 = sb("e32", [P, 2, DC, 512])
        eh, el = sb("eh", [P, 2, DC, 512], F16), sb("el", [P, 2, DC, 512], F16)
        o = sb("o", [P, B, PR, VW])
        rd = sb("rd", [P, B, PR])
        att = sb("att", [P, B, PR, HD])
        attT = sb("attT", [P, 2, TOK])

        loaded, consts = sem("loaded"), sem("consts")
        CHUNKS = [(0, 3), (3, 6), (6, 9), (9, KT)]
        SPLIT_AT = [2, 5, 8, 11]
        NC = len(CHUNKS)

        vec = Steps(sem("setup_vector"), "w_hi w_lo bias_hi w5 mask squares sums guarded qn qT_hi qT_lo queries")
        roots = Steps(sem("setup_roots"), "rnorm")
        pe_s = Steps(sem("setup_tensor"), "qp qT")
        act_s = Steps(sem("setup_scalar"), "qp qT")
        N_LOADS = 16 * (3 + 8 + 3 + 2 * PR)
        ctx_loaded = sem("ctx_loaded")

        def load_context(sp, src):
            sp.dma_start(cA[:, :], src[0:P, :]).then_inc(ctx_loaded, 16)
            sp.dma_start(cB[0:CB, :], src[P:CD, :]).then_inc(ctx_loaded, 16)
            sp.dma_start(cB[CB:P, :], src[P:CD, :]).then_inc(ctx_loaded, 16)

        def prefetch(sp):
            sp.dma_start(wq[:, :, :], d["L0_xattn_Wq"].rearrange("(c p) n -> p c n", p=P)).then_inc(loaded, 16)
            sp.dma_start(rows[0:1, 0, :], d["L0_xattn_bq"].partition_broadcast(1)).then_inc(loaded, 16)
            sp.dma_start(rows[0:1, 1, :], d["L0_xattn_bo"].partition_broadcast(1)).then_inc(loaded, 16)
            for j, (w, b) in enumerate((("L0_xattn_Wk", "L0_xattn_bk"), ("L0_xattn_Wv", "L0_xattn_bv"))):
                cols = slice(j * D, (j + 1) * D)
                sp.dma_start(wA[:, cols], d[w][0:P, :]).then_inc(loaded, 16)
                sp.dma_start(wB[0:CB, cols], d[w][P:CD, :]).then_inc(loaded, 16)
                sp.dma_start(wB[CB:P, cols], d[w][P:CD, :]).then_inc(loaded, 16)
                sp.dma_start(bias[64:97, cols], d[b].partition_broadcast(33)).then_inc(loaded, 16)
            sp.dma_start(gam[:, :], d["L0_xattn_ln_gamma"].partition_broadcast(P)).then_inc(loaded, 16)
            sp.dma_start(bet[:, :], d["L0_xattn_ln_beta"].partition_broadcast(P)).then_inc(loaded, 16)
            sp.dma_start(headmask[:, :], d["c_headmask"]).then_inc(loaded, 16)
            for pr in range(PR):
                for hh in range(2):
                    r = (2 * pr + hh) * HD
                    sp.dma_start(wo[pr * HD:(pr + 1) * HD, hh, :], d["L0_xattn_Wo"][r:r + HD, :]).then_inc(loaded, 16)
            load_context(sp, d["c_ctxT"][0, :, :])

        norm(prefetch)
        with ExitStack() as pctx, nc.Block() as block:
            psQ = pctx.enter_context(nc.psum_tensor("l0x_psQ", [P, TT, D], F32))
            psT = pctx.enter_context(nc.psum_tensor("l0x_psT", [P, DC, TOK], F32))

            @block.gpsimd
            def _(pool):
                pool.wait_ge(vec.sem, vec.at("guarded"))
                pool.tensor_tensor(qss[:, :], qss[:, :], core.minus_half[:, 0:TT], ALU.pow).then_inc(roots.done("rnorm"), 1)

            @block.tensor
            def _(pe):
                pe.wait_ge(loaded, N_LOADS)
                for t in range(TT):
                    for c in range(DC):
                        pe.matmul(psQ[:, t, :], core.yT[:, c, t * P:(t + 1) * P], wq[:, c, :], start=(c == 0), stop=False)
                    ins = pe.matmul(psQ[:, t, :], core.ones[0:1, :], rows[0:1, 0, :], start=False, stop=True)
                ins.then_inc(pe_s.done("qp"), 1)
                pe.wait_ge(vec.sem, vec.at("qn"))
                for c in range(DC):
                    for t in range(TT):
                        ins = pe.transpose(psT[:, c, t * P:(t + 1) * P], qn[:, t, c * P:(c + 1) * P], core.ident[:, :])
                ins.then_inc(pe_s.done("qT"), 1)

            @block.scalar
            def _(act):
                act.wait_ge(pe_s.sem, pe_s.at("qp"))
                act.activation(qp[:, :, :], psQ[:, :, :], ACT.Copy).then_inc(act_s.done("qp"), 1)
                act.wait_ge(pe_s.sem, pe_s.at("qT"))
                act.activation(qT[:, :, :], psT[:, :, :], ACT.Copy).then_inc(act_s.done("qT"), 1)

            @block.vector
            def _(dve):
                dve.memset(w5[CB:P, :], 0.0).then_inc(consts, 1)
                dve.memset(c5[CB:P, :], 1.0)
                for s in range(2):
                    dve.memset(v[:, s, :, VW - 1:VW], 1.0)
                dve.wait_ge(loaded, N_LOADS)
                dve.tensor_copy(wAh[:, :], wA[:, :])
                dve.tensor_copy(wBh[:, :], wB[:, :])
                dve.tensor_copy(biash[64:97, :], bias[64:97, :]).then_inc(vec.done("w_hi"), 1)
                dve.wait_ge(vec.sem, vec.at("w_hi"))
                dve.tensor_tensor(wAl[:, :], wA[:, :], wAh[:, :], ALU.subtract).then_inc(vec.done("w_lo"), 1)
                dve.wait_ge(consts, 1)
                dve.tensor_copy(w5[64:65, :], biash[64:65, :]).then_inc(vec.done("bias_hi"), 1)
                dve.tensor_tensor(w5[0:CB, :], wB[0:CB, :], wBh[0:CB, :], ALU.subtract)
                dve.tensor_tensor(w5[96:97, :], bias[96:97, :], biash[96:97, :], ALU.subtract).then_inc(vec.done("w5"), 1)
                dve.tensor_copy(headmask16[:, :], headmask[:, :]).then_inc(vec.done("mask"), 1)
                dve.wait_ge(act_s.sem, act_s.at("qp"))
                dve.tensor_tensor(sq[:, :, :], qp[:, :, :], qp[:, :, :], ALU.mult).then_inc(vec.done("squares"), 1)
                dve.wait_ge(vec.sem, vec.at("squares"))
                dve.tensor_reduce(qss[:, :], sq[:, :, :], AX.X, ALU.add).then_inc(vec.done("sums"), 1)
                dve.wait_ge(vec.sem, vec.at("sums"))
                dve.tensor_scalar(qss[:, :], qss[:, :], 1e-24, None, ALU.max).then_inc(vec.done("guarded"), 1)
                dve.wait_ge(roots.sem, roots.at("rnorm"))
                for t in range(TT):
                    ins = dve.tensor_scalar(qn[:, t, :], qp[:, t, :], qss[:, t:t + 1], float(HD) ** -0.5, ALU.mult, ALU.mult)
                ins.then_inc(vec.done("qn"), 1)
                dve.wait_ge(act_s.sem, act_s.at("qT"))
                dve.tensor_copy(qTh[:, :, :], qT[:, :, :]).then_inc(vec.done("qT_hi"), 1)
                dve.wait_ge(vec.sem, vec.at("qT_hi"))
                dve.tensor_tensor(qTl[:, :, :], qT[:, :, :], qTh[:, :, :], ALU.subtract).then_inc(vec.done("qT_lo"), 1)
                dve.wait_ge(vec.sem, vec.at("qT_lo"))
                for q, blocks in ((qTh, qbh), (qTl, qbl)):
                    for c in range(DC):
                        for b in range(B):
                            ins = dve.tensor_tensor(
                                blocks[:, c, b, :, :], q[:, c, None, b * N:(b + 1) * N].to_broadcast([P, HC, N]),
                                headmask16[:, :, None].to_broadcast([P, HC, N]), ALU.mult)
                ins.then_inc(vec.done("queries"), 1)

        TILES = 2 * KT
        count = lambda name, each=TILES, primed=0: Count(sem(name), each, primed)
        projected, squares, norms = count("projected"), count("squares"), count("norms", primed=2)
        key_sums, rnorms = count("key_sums", primed=2), count("rnorms", primed=2)
        k_hi, k_lo, v_hi, v_lo = count("k_hi"), count("k_lo"), count("v_hi"), count("v_lo", primed=2)
        scored, exped = count("scored", 2 * TILES, 4), count("exped", 2 * TILES, 4)
        e_hi, e_split = count("e_hi", 2 * TILES), count("e_split", 2 * TILES, 4)
        weighed, out_taken = count("weighed", primed=2), count("out_taken", 2, 1)
        ctx_hi = count("ctx_hi", 2 * NC)
        ctx_loA, ctx_loB = count("ctx_loA", 2 * NC), count("ctx_loB", 2 * NC)
        with ExitStack() as pctx, nc.Block() as block:
            psP = pctx.enter_context(nc.psum_tensor("l0x_psP", [P, 2, 2 * D], F32))
            psS = pctx.enter_context(nc.psum_tensor("l0x_psS", [P, 2, 512], F32))
            psO = pctx.enter_context(nc.psum_tensor("l0x_psO", [P, 2, 512], F32))
            psN = pctx.enter_context(nc.psum_tensor("l0x_psN", [P, 512], F32))

            def splits_at(g):
                return [(k, g // KT + 1) for k in range(NC) if SPLIT_AT[k] == g % KT]

            @block.sync
            def _(sp):
                with sp.Fori(0, B) as b:
                    sp.wait_ge(ctx_loA.sem, NC * b + NC)
                    sp.wait_ge(ctx_loB.sem, NC * b + NC)
                    load_context(sp, d["c_ctxT"][bass.ds(b + 1, 1), :, :].rearrange("a k m -> (a k) m"))

            @block.gpsimd
            def _(pool):
                def root(g, i):
                    pool.wait_ge(key_sums.sem, key_sums.at(i, g))
                    pool.wait_ge(exped.sem, exped.at(i, 2 * (g - 2) + 1))
                    pool.tensor_tensor(rn[:, g % 2:g % 2 + 1], kss[:, g % 2:g % 2 + 1], core.minus_half[:, 0:1], ALU.pow)\
                        .then_inc(rnorms.sem, 1)

                def split(k, i, batch):
                    cols = slice(CHUNKS[k][0] * P, CHUNKS[k][1] * P)
                    pool.wait_ge(ctx_hi.sem, ctx_hi.at(i, NC * batch + k))
                    pool.tensor_tensor(cAl[:, cols], cA[:, cols], cAh[:, cols], ALU.subtract).then_inc(ctx_loA.sem, 1)

                for k in range(NC):
                    split(k, 0, 0)
                root(0, 0)
                with pool.Fori(0, B // 2) as i:
                    for g in range(TILES):
                        root(g + 1, i)
                        for k, batch in splits_at(g):
                            split(k, i, batch)

            @block.tensor
            def _(pe):
                def project(g, i):
                    n = g % KT
                    for k, (first, _) in enumerate(CHUNKS):
                        if n == first:
                            pe.wait_ge(ctx_loA.sem, ctx_loA.at(i, NC * (g // KT) + k))
                            pe.wait_ge(ctx_loB.sem, ctx_loB.at(i, NC * (g // KT) + k))
                    pe.wait_ge(v_lo.sem, v_lo.at(i, g - 2))
                    keys, out = slice(n * P, (n + 1) * P), psP[:, g % 2, :]
                    passes = ((wAh, cAh), (wAh, cAl), (wAl, cAh), (wBh, cS), (w5, c5))
                    for c in range(DC):
                        for j, (w, x) in enumerate(passes):
                            pe.matmul(out[:, c * P:(c + 1) * P], w[:, c * P:(c + 1) * P], x[:, keys],
                                      start=(j == 0), stop=(j == 4))
                    for j, (w, x) in enumerate(passes):
                        ins = pe.matmul(out[:, D:2 * D], x[:, keys], w[:, D:2 * D], start=(j == 0), stop=(j == 4))
                    ins.then_inc(projected.sem, 1)

                def key_norms(g, i):
                    pe.wait_ge(squares.sem, squares.at(i, g))
                    pe.wait_ge(key_sums.sem, key_sums.at(i, g - 1))
                    for c in range(DC):
                        ins = pe.matmul(psN[:, g % 2:g % 2 + 1], ksq[:, g % 2, c * P:(c + 1) * P], core.ones[:, 0:1],
                                        start=(c == 0), stop=(c == 1))
                    ins.then_inc(norms.sem, 1)

                def score(g, i):
                    pe.wait_ge(k_lo.sem, k_lo.at(i, g))
                    for c in range(DC):
                        pe.wait_ge(exped.sem, exped.at(i, 2 * (g - 1) + c))
                        cols = slice(c * P, (c + 1) * P)
                        for j, (k, q) in enumerate(((kh, qbh), (kl, qbh), (kh, qbl))):
                            ins = pe.matmul(psS[:, c, :], k[:, g % 2, cols],
                                            q[:, c, bass.ds(i * 2 + g // KT, 1), :, :].rearrange("p a h q -> p (a h q)"),
                                            start=(j == 0), stop=(j == 2))
                        ins.then_inc(scored.sem, 1)

                def weigh(g, i):
                    n, s = g % KT, g % 2
                    rows = P if n < KT - 1 else TAIL
                    pe.wait_ge(v_lo.sem, v_lo.at(i, g))
                    pe.wait_ge(e_split.sem, e_split.at(i, 2 * g + 1))
                    if n == 0:
                        pe.wait_ge(out_taken.sem, out_taken.at(i, g // KT - 1))
                    for pr in range(PR):
                        c, col = pr // (PR // 2), (pr % (PR // 2)) * P
                        out = psO[:, c, (pr % (PR // 2)) * VW:(pr % (PR // 2) + 1) * VW]
                        pe.matmul(out, eh[0:rows, s, c, col:col + P], v[0:rows, s, pr, :],
                                  start=(n == 0 and pr % (PR // 2) == 0), stop=False, skip_group_check=True)
                        ins = pe.matmul(out[:, 2 * HD:VW], el[0:rows, s, c, col:col + P],
                                        v[0:rows, s, pr, 2 * HD:VW], start=False, stop=(n == KT - 1),
                                        skip_group_check=True)
                    ins.then_inc(weighed.sem, 1)

                project(0, 0)
                project(1, 0)
                key_norms(0, 0)
                with pe.Fori(0, B // 2) as i:
                    for g in range(TILES):
                        score(g, i)
                        key_norms(g + 1, i)
                        if g >= 1:
                            weigh(g - 1, i)
                        project(g + 2, i)
                    weigh(TILES - 1, i)

            @block.scalar
            def _(act):
                def square(g, i):
                    act.wait_ge(projected.sem, projected.at(i, g))
                    act.wait_ge(norms.sem, norms.at(i, g - 2))
                    act.activation(ksq[:, g % 2, :], psP[:, g % 2, 0:D], ACT.Square).then_inc(squares.sem, 1)

                def key_hi(g, i):
                    act.wait_ge(scored.sem, scored.at(i, 2 * (g - 2) + 1))
                    act.activation(kh[:, g % 2, :], psP[:, g % 2, 0:D], ACT.Copy).then_inc(k_hi.sem, 1)

                def value_hi(g, i):
                    act.wait_ge(weighed.sem, weighed.at(i, g - 2))
                    act.wait_ge(k_lo.sem, k_lo.at(i, g))
                    act.activation(v[:, g % 2, :, 2 * HD:4 * HD],
                                   psP[:, g % 2, D:2 * D].rearrange("p (a k) -> p a k", k=2 * HD),
                                   ACT.Copy).then_inc(v_hi.sem, 1)

                def exp(g, c, i):
                    act.wait_ge(rnorms.sem, rnorms.at(i, g))
                    act.wait_ge(e_split.sem, e_split.at(i, 2 * (g - 2) + c))
                    act.wait_ge(scored.sem, scored.at(i, 2 * g + c))
                    act.activation(e32[:, g % 2, c, :], psS[:, c, :], ACT.Exp,
                                   scale=rn[:, g % 2:g % 2 + 1]).then_inc(exped.sem, 1)

                def split(k):
                    cols = slice(CHUNKS[k][0] * P, CHUNKS[k][1] * P)
                    act.activation(cAh[:, cols], cA[:, cols], ACT.Copy)
                    act.activation(c5[0:CB, cols], cB[0:CB, cols], ACT.Copy)
                    act.activation(cS[:, cols], cB[:, cols], ACT.Copy).then_inc(ctx_hi.sem, 1)

                act.wait_ge(ctx_loaded, 48)
                for k in range(NC):
                    split(k)
                square(0, 0)
                key_hi(0, 0)
                value_hi(0, 0)
                with act.Fori(0, B // 2) as i:
                    for g in range(TILES):
                        square(g + 1, i)
                        exp(g, 0, i)
                        key_hi(g + 1, i)
                        exp(g, 1, i)
                        value_hi(g + 1, i)
                        for k, batch in splits_at(g):
                            if k == 0:
                                act.wait_ge(ctx_loaded, i * 96 + 48 * (batch + 1))
                            act.wait_ge(projected.sem, projected.at(i, KT * (batch - 1) + CHUNKS[k][1] - 1))
                            split(k)

            @block.vector
            def _(dve):
                def guard(g, i):
                    dve.wait_ge(norms.sem, norms.at(i, g))
                    dve.wait_ge(rnorms.sem, rnorms.at(i, g - 2))
                    dve.tensor_scalar(kss[:, g % 2:g % 2 + 1], psN[:, g % 2:g % 2 + 1], 1e-24, None, ALU.max)\
                        .then_inc(key_sums.sem, 1)

                def key_lo(g, i):
                    dve.wait_ge(k_hi.sem, k_hi.at(i, g))
                    dve.tensor_tensor(kl[:, g % 2, :], psP[:, g % 2, 0:D], kh[:, g % 2, :], ALU.subtract)\
                        .then_inc(k_lo.sem, 1)

                def value_lo(g, i):
                    dve.wait_ge(v_hi.sem, v_hi.at(i, g))
                    dve.tensor_tensor(v[:, g % 2, :, 0:2 * HD],
                                      psP[:, g % 2, D:2 * D].rearrange("p (a k) -> p a k", k=2 * HD),
                                      v[:, g % 2, :, 2 * HD:4 * HD], ALU.subtract).then_inc(v_lo.sem, 1)

                def split_exp(g, c, i):
                    dve.wait_ge(weighed.sem, weighed.at(i, g - 2))
                    dve.wait_ge(exped.sem, exped.at(i, 2 * g + c))
                    dve.tensor_copy(eh[:, g % 2, c, :], e32[:, g % 2, c, :]).then_inc(e_hi.sem, 1)
                    dve.wait_ge(e_hi.sem, e_hi.at(i, 2 * g + c))
                    dve.tensor_tensor(el[:, g % 2, c, :], e32[:, g % 2, c, :], eh[:, g % 2, c, :], ALU.subtract)\
                        .then_inc(e_split.sem, 1)

                def split(k, i, batch):
                    cols = slice(CHUNKS[k][0] * P, CHUNKS[k][1] * P)
                    dve.wait_ge(ctx_hi.sem, ctx_hi.at(i, NC * batch + k))
                    dve.tensor_tensor(cS[CB:P, cols], cB[CB:P, cols], cS[CB:P, cols], ALU.subtract).then_inc(ctx_loB.sem, 1)

                def take_out(g, i):
                    dve.wait_ge(weighed.sem, weighed.at(i, g))
                    dve.tensor_copy(o[:, bass.ds(i * 2 + g // KT, 1), :, :].rearrange("p a (c r) w -> p (a c) (r w)", c=2),
                                    psO[:, :, 0:PR // 2 * VW]).then_inc(out_taken.sem, 1)

                for c in (norms, key_sums, rnorms, v_lo, scored, exped, e_split, weighed, out_taken):
                    dve.sem_inc(c.sem, c.primed)
                for k in range(NC):
                    split(k, 0, 0)
                key_lo(0, 0)
                value_lo(0, 0)
                guard(0, 0)
                with dve.Fori(0, B // 2) as i:
                    for g in range(TILES):
                        guard(g + 1, i)
                        split_exp(g, 0, i)
                        key_lo(g + 1, i)
                        split_exp(g, 1, i)
                        value_lo(g + 1, i)
                        for k, batch in splits_at(g):
                            split(k, i, batch)
                        if g == KT:
                            take_out(KT - 1, i)
                    take_out(TILES - 1, i)

        vec = Steps(sem("out_vector"), "rden sums att x " + norm_steps("ln") + " gamma beta residual")
        pe_s = Steps(sem("out_tensor"), "attT out")
        roots = Steps(sem("out_roots"), "ln_var ln")
        evac = sem("attT_taken")
        with ExitStack() as pctx, nc.Block() as block:
            psT = pctx.enter_context(nc.psum_tensor("l0x_psA", [P, B, P], F32))
            psX = pctx.enter_context(nc.psum_tensor("l0x_psX", [P, TT, D], F32))

            @block.gpsimd
            def _(pool):
                layer_norm_root(pool, vec, roots, "ln", core.norm_work, core.minus_half[:, 0:TT])

            @block.vector
            def _(dve):
                dve.reciprocal(rd[:, :, :], o[:, :, :, VW - 1]).then_inc(vec.done("rden"), 1)
                for hh in range(2):
                    rows, k = slice(hh * N, (hh + 1) * N), hh * HD
                    ins = dve.tensor_tensor(att[rows, :, :, :], o[rows, :, :, k:k + HD],
                                            o[rows, :, :, 2 * HD + k:2 * HD + k + HD], ALU.add)
                ins.then_inc(vec.done("sums"), 1)
                dve.wait_ge(vec.sem, vec.at("sums"))
                dve.tensor_tensor(att[:, :, :, :], att[:, :, :, :], rd[:, :, :, None].to_broadcast([P, B, PR, HD]),
                                  ALU.mult).then_inc(vec.done("att"), 1)
                dve.wait_ge(pe_s.sem, pe_s.at("out"))
                dve.tensor_tensor(qn[:, :, :], psX[:, :, :], qp[:, :, :], ALU.add).then_inc(vec.done("x"), 1)
                dve.wait_ge(vec.sem, vec.at("x"))
                layer_norm(dve, vec, roots, "ln", qn, qn, core.norm_work)
                dve.tensor_tensor(qn[:, :, :], qn[:, :, :], gam[:, None, :].to_broadcast([P, TT, D]), ALU.mult)\
                    .then_inc(vec.done("gamma"), 1)
                dve.wait_ge(vec.sem, vec.at("gamma"))
                dve.tensor_tensor(qn[:, :, :], qn[:, :, :], bet[:, None, :].to_broadcast([P, TT, D]), ALU.add)\
                    .then_inc(vec.done("beta"), 1)
                dve.wait_ge(vec.sem, vec.at("beta"))
                dve.tensor_tensor(core.x[:, :, :], core.x[:, :, :], qn[:, :, :], ALU.add).then_inc(vec.done("residual"), 1)

            @block.tensor
            def _(pe):
                pe.wait_ge(vec.sem, vec.at("att"))
                for b in range(B):
                    ins = pe.transpose(psT[:, b, :], att[:, b, :, :].rearrange("p a k -> p (a k)"), core.ident[:, :])
                ins.then_inc(pe_s.done("attT"), 1)
                pe.wait_ge(evac, 1)
                for t in range(TT):
                    for hh in range(2):
                        pe.matmul(psX[:, t, :], attT[:, hh, t * P:(t + 1) * P], wo[:, hh, :], start=(hh == 0), stop=False)
                    ins = pe.matmul(psX[:, t, :], core.ones[0:1, :], rows[0:1, 1, :], start=False, stop=True)
                ins.then_inc(pe_s.done("out"), 1)

            @block.scalar
            def _(act):
                act.wait_ge(pe_s.sem, pe_s.at("attT"))
                act.activation(attT[:, :, :].rearrange("p h (b q) -> p b h q", b=B),
                               psT[:, :, :].rearrange("p b (h q) -> p b h q", h=2), ACT.Copy).then_inc(evac, 1)


def stage_l0_self(core, norm):
    nc, d = core.nc, core.dram
    DH = 64
    NN = 2
    J = NN + N
    PR = H // 2
    W = H * DH
    halves = [slice(0, N), slice(N, P)]
    place = lambda h: h % 2 * PR + h // 2
    with ExitStack() as ctx:
        sb = lambda name, shape, dt=F32: ctx.enter_context(nc.sbuf_tensor(f"l0a_{name}", shape, dt))
        pb = lambda name, shape: ctx.enter_context(nc.psum_tensor(f"l0a_{name}", shape, F32))
        sem = lambda name: core.sem(f"l0a_{name}")
        w = sb("w", [P, DC, 3 * W])
        wo = sb("wo", [P, PR, D])
        scale = sb("scale", [P, 2, DH])
        bias = sb("bias", [P, H, J])
        nk, nks = sb("nk", [2 * H, DH]), sb("nks", [2 * H, DH])
        nss = sb("nss", [2 * H, 1])
        nkb = sb("nkb", [2 * H, H, DH])
        blockmask = sb("blockmask", [2 * H, H])
        nkT = sb("nkT", [P, PR, 4])
        nv = sb("nv", [2 * H, W])
        yt = sb("yt", [P, DC, P])
        qk = sb("qk", [P, 2, H, DH])
        sq = sb("sq", [P, 2, H, DH])
        ss = sb("ss", [P, 2, H])
        v = sb("v", [P, W])
        qkT = sb("qkT", [P, 2, PR, P])
        s, e = sb("s", [P, H, J]), sb("e", [P, H, J])
        en = sb("en", [P, H * NN])
        top, den = sb("top", [P, H]), sb("den", [P, H])
        eT, nT = sb("eT", [P, H, N]), sb("nT", [2 * H, P])
        o, oT = sb("o", [P, H, DH]), sb("oT", [P, PR, P])

        loaded = sem("loaded")
        setup = Steps(sem("setup"), "squares sums guarded scaled scaled2 blocks nkT")
        setup_root = sem("setup_root")
        setup_T = sem("setup_T")
        vecA = Steps(sem("vector_a"), "yt squares sums guarded normed scaled v")
        vecB = Steps(sem("vector_b"), "biased top shifted den rden eT o x")
        actA, actB = Steps(sem("scalar_a"), "qk qkT"), Steps(sem("scalar_b"), "exp nT oT")
        peA, peB = Steps(sem("tensor_a"), "qk v qkT"), Steps(sem("tensor_b"), "scores eT out oT proj")
        roots = Steps(sem("roots"), "norms")
        N_LOADS = 16 * 9

        def turns(eng, first, both, last):
            first(0)
            with eng.Fori(0, TT - 1) as i:
                both(i)
            last(TT - 1)

        def prefetch(sp):
            sp.dma_start(w[:, :, 0:W], d["L0_attn_w_q"].rearrange("(c p) n -> p c n", p=P)).then_inc(loaded, 16)
            sp.dma_start(w[:, :, W:3 * W], d["L0_attn_w_kv"].rearrange("(c p) n -> p c n", p=P)).then_inc(loaded, 16)
            sp.dma_start(wo[:, :, :], d["L0_attn_w_out"].rearrange("(c p) n -> p c n", p=P)).then_inc(loaded, 16)
            sp.dma_start(scale[:, 0, :], d["L0_attn_q_scale"].partition_broadcast(P)).then_inc(loaded, 16)
            sp.dma_start(scale[:, 1, :], d["L0_attn_k_scale"].partition_broadcast(P)).then_inc(loaded, 16)
            sp.dma_start(bias[:, :, :], d["c_alibi"]).then_inc(loaded, 16)
            sp.dma_start(nk[:, :], d["c_null_k"]).then_inc(loaded, 16)
            sp.dma_start(nv[:, :], d["c_null_v"]).then_inc(loaded, 16)
            sp.dma_start(blockmask[:, :], d["c_blockmask"]).then_inc(loaded, 16)

        norm(prefetch)
        psA = pb("psA", [P, 4, 512])
        psS, psN, psX = pb("psS", [P, 2, 512]), pb("psN", [P, 512]), pb("psX", [P, 512])
        psA_heads = psA[:, :, :].rearrange("p a (b q) -> p (a b) q", q=P)
        psS_heads = psS[:, :, :].rearrange("p a (b q) -> p (a b) q", q=N)
        psS_pairs = psS[:, :, :].rearrange("p a (b q) -> p (a b) q", q=P)
        with nc.Block() as block:
            @block.gpsimd
            def _(pool):
                pool.wait_ge(setup.sem, setup.at("guarded"))
                pool.tensor_tensor(nss[:, :], nss[:, :], core.minus_half[0:2 * H, 0:1], ALU.pow).then_inc(setup_root, 1)
                def root(j):
                    pool.wait_ge(vecA.sem, vecA.at("guarded", j))
                    pool.tensor_tensor(ss[:, :, :], ss[:, :, :],
                                       core.minus_half[:, 0:2 * H].rearrange("p (a h) -> p a h", a=2), ALU.pow)\
                        .then_inc(roots.done("norms"), 1)

                turns(pool, root, lambda i: root(i + 1), lambda i: None)

            @block.tensor
            def _(pe):
                pe.wait_ge(setup.sem, setup.at("blocks"))
                for pr in range(PR):
                    ins = pe.transpose(psA[:, 0, pr * 32:(pr + 1) * 32],
                                       nkb[:, 2 * pr:2 * pr + 2, :].rearrange("k a d -> k (a d)"),
                                       core.ident[0:2 * H, 0:2 * H])
                ins.then_inc(setup_T, 1)
                pe.wait_ge(setup.sem, setup.at("nkT"))

                def project(j, parts, name):
                    for at, part in enumerate(parts):
                        for c in range(DC):
                            ins = pe.matmul(psA[:, at, :], yt[:, c, :], w[:, c, part * 512:(part + 1) * 512],
                                            start=(c == 0), stop=(c == 1))
                    ins.then_inc(peA.done(name), 1)

                def project_qk(j):
                    pe.wait_ge(vecA.sem, vecA.at("yt", j))
                    project(j, range(4), "qk")

                def project_v(j):
                    pe.wait_ge(actA.sem, actA.at("qk", j))
                    project(j, range(4, 6), "v")

                def transpose_qk(j):
                    pe.wait_ge(vecA.sem, vecA.at("v", j))
                    for a in range(2):
                        for pr in range(PR):
                            ins = pe.transpose(psA_heads[:, a * PR + pr, :],
                                               qk[:, a, 2 * pr:2 * pr + 2, :].rearrange("p h k -> p (h k)"),
                                               core.ident[:, :])
                    ins.then_inc(peA.done("qkT"), 1)

                def score(i):
                    wait_apart(pe, actA.sem, actA.at("qkT", i), core.spare)
                    for pr in range(PR):
                        for odd, r in enumerate(halves):
                            for half in halves:
                                pe.matmul(psS_heads[half, odd * PR + pr, :], qkT[r, 0, pr, half], qkT[r, 1, pr, half],
                                          start=True, stop=True)
                    for pr in range(PR):
                        ins = pe.matmul(psN[:, pr * 2 * NN:(pr + 1) * 2 * NN], qkT[:, 0, pr, :], nkT[:, pr, :],
                                        start=True, stop=True)
                    ins.then_inc(peB.done("scores"), 1)

                def transpose_e(i):
                    wait_apart(pe, actB.sem, actB.at("exp", i), core.spare)
                    for h in range(H):
                        for half in halves:
                            pe.matmul(psS_heads[half, h, :], e[half, h, NN:J], core.ident[half, half], start=True, stop=True)
                    ins = pe.matmul(psN[0:2 * H, 0:P], en[:, :], core.ident[:, :], start=True, stop=True)
                    ins.then_inc(peB.done("eT"), 1)

                def weigh(i):
                    pe.wait_ge(vecB.sem, vecB.at("eT", i))
                    pe.wait_ge(actB.sem, actB.at("nT", i))
                    for bank in range(2):
                        pe.matmul(psS[:, bank, :], nT[:, :], nv[:, bank * 512:(bank + 1) * 512], start=True, stop=False,
                                  skip_group_check=True)
                        for h in range(8 * bank, 8 * bank + 8):
                            for half in halves:
                                ins = pe.matmul(psS[half, bank, (h % 8) * DH:(h % 8 + 1) * DH], eT[half, place(h), :],
                                                v[half, h * DH:(h + 1) * DH], start=False, stop=(h % 8 == 7),
                                                skip_group_check=True)
                    ins.then_inc(peB.done("out"), 1)

                def transpose_o(i):
                    pe.wait_ge(vecB.sem, vecB.at("o", i))
                    for pr in range(PR):
                        ins = pe.transpose(psS_pairs[:, pr, :], o[:, 2 * pr:2 * pr + 2, :].rearrange("p h k -> p (h k)"),
                                           core.ident[:, :])
                    ins.then_inc(peB.done("oT"), 1)

                def project_out(i):
                    pe.wait_ge(actB.sem, actB.at("oT", i))
                    for pr in range(PR):
                        ins = pe.matmul(psX[:, 0:D], oT[:, pr, :], wo[:, pr, :], start=(pr == 0), stop=(pr == PR - 1))
                    ins.then_inc(peB.done("proj"), 1)

                def first(j):
                    project_qk(j)
                    project_v(j)
                    transpose_qk(j)

                def both(i):
                    score(i)
                    project_qk(i + 1)
                    transpose_e(i)
                    project_v(i + 1)
                    weigh(i)
                    transpose_qk(i + 1)
                    transpose_o(i)
                    project_out(i)

                def last(i):
                    for step in (score, transpose_e, weigh, transpose_o, project_out):
                        step(i)

                turns(pe, first, both, last)

            @block.scalar
            def _(act):
                def take_qk(j):
                    act.wait_ge(peA.sem, peA.at("qk", j))
                    act.activation(qk[:, :, :, :].rearrange("p a h k -> p (a h k)"),
                                   psA[:, :, :].rearrange("p a n -> p (a n)"), ACT.Copy).then_inc(actA.done("qk"), 1)

                def take_qkT(j):
                    act.wait_ge(peA.sem, peA.at("qkT", j))
                    act.activation(qkT[:, :, :, :].rearrange("p a h k -> p (a h k)"),
                                   psA[:, :, :].rearrange("p a n -> p (a n)"), ACT.Copy).then_inc(actA.done("qkT"), 1)

                def exp(i):
                    act.wait_ge(vecB.sem, vecB.at("shifted", i))
                    act.activation(en[:, :].rearrange("p (h k) -> p h k", k=NN), s[:, :, 0:NN], ACT.Exp)
                    act.activation(e[:, :, :], s[:, :, :], ACT.Exp).then_inc(actB.done("exp"), 1)

                def take_nT(i):
                    act.wait_ge(peB.sem, peB.at("eT", i))
                    act.activation(nT[:, :], psN[0:2 * H, 0:P], ACT.Copy).then_inc(actB.done("nT"), 1)

                def take_oT(i):
                    act.wait_ge(peB.sem, peB.at("oT", i))
                    act.activation(oT[:, :, :], psS_pairs[:, :, :], ACT.Copy).then_inc(actB.done("oT"), 1)

                def first(j):
                    take_qk(j)
                    take_qkT(j)

                def both(i):
                    exp(i)
                    take_qk(i + 1)
                    take_nT(i)
                    take_qkT(i + 1)
                    take_oT(i)

                def last(i):
                    for step in (exp, take_nT, take_oT):
                        step(i)

                turns(act, first, both, last)

            @block.vector
            def _(dve):
                dve.wait_ge(loaded, N_LOADS)
                dve.tensor_tensor(nks[:, :], nk[:, :], nk[:, :], ALU.mult).then_inc(setup.done("squares"), 1)
                dve.wait_ge(setup.sem, setup.at("squares"))
                dve.tensor_reduce(nss[:, :], nks[:, :], AX.X, ALU.add).then_inc(setup.done("sums"), 1)
                dve.wait_ge(setup.sem, setup.at("sums"))
                dve.tensor_scalar(nss[:, :], nss[:, :], 1e-24, None, ALU.max).then_inc(setup.done("guarded"), 1)
                dve.wait_ge(setup_root, 1)
                dve.tensor_scalar(nk[:, :], nk[:, :], nss[:, 0:1], None, ALU.mult).then_inc(setup.done("scaled"), 1)
                dve.wait_ge(setup.sem, setup.at("scaled"))
                dve.tensor_tensor(nk[:, :], nk[:, :], scale[0:2 * H, 1, :], ALU.mult).then_inc(setup.done("scaled2"), 1)
                dve.wait_ge(setup.sem, setup.at("scaled2"))
                dve.tensor_tensor(nkb[:, :, :], nk[:, None, :].to_broadcast([2 * H, H, DH]),
                                  blockmask[:, :, None].to_broadcast([2 * H, H, DH]), ALU.mult)\
                    .then_inc(setup.done("blocks"), 1)
                dve.wait_ge(setup_T, 1)
                for pr in range(PR):
                    ins = dve.tensor_copy(nkT[:, pr, :], psA[:, 0, pr * 32 + 4 * pr:pr * 32 + 4 * pr + 4])
                ins.then_inc(setup.done("nkT"), 1)

                def take_y(j):
                    dve.tensor_copy(yt[:, :, :], core.yT[:, :, bass.ds(j * P, P)]).then_inc(vecA.done("yt"), 1)

                def norms(j):
                    dve.wait_ge(actA.sem, actA.at("qk", j))
                    dve.tensor_tensor(sq[:, :, :, :], qk[:, :, :, :], qk[:, :, :, :], ALU.mult).then_inc(vecA.done("squares"), 1)
                    dve.wait_ge(vecA.sem, vecA.at("squares", j))
                    dve.tensor_reduce(ss[:, :, :], sq[:, :, :, :], AX.X, ALU.add).then_inc(vecA.done("sums"), 1)
                    dve.wait_ge(vecA.sem, vecA.at("sums", j))
                    dve.tensor_scalar(ss[:, :, :], ss[:, :, :], 1e-24, None, ALU.max).then_inc(vecA.done("guarded"), 1)

                def scale_qk(j):
                    dve.wait_ge(roots.sem, roots.at("norms", j))
                    dve.tensor_tensor(qk[:, :, :, :], qk[:, :, :, :], ss[:, :, :, None].to_broadcast([P, 2, H, DH]),
                                      ALU.mult).then_inc(vecA.done("normed"), 1)
                    dve.wait_ge(vecA.sem, vecA.at("normed", j))
                    dve.tensor_tensor(qk[:, :, :, :], qk[:, :, :, :], scale[:, :, None, :].to_broadcast([P, 2, H, DH]),
                                      ALU.mult).then_inc(vecA.done("scaled"), 1)

                def take_v(j):
                    dve.wait_ge(peA.sem, peA.at("v", j))
                    dve.tensor_copy(v[:, :], psA[:, 0:2, :].rearrange("p a n -> p (a n)")).then_inc(vecA.done("v"), 1)

                def softmax(i):
                    dve.wait_ge(peB.sem, peB.at("scores", i))
                    dve.scalar_tensor_tensor(s[:, :, NN:J], psS_heads[:, :, :], 8.0, bias[:, :, NN:J], ALU.mult, ALU.add)
                    for odd in range(2):
                        heads = slice(odd * PR, (odd + 1) * PR)
                        ins = dve.scalar_tensor_tensor(
                            s[:, heads, 0:NN], psN[:, 0:2 * H].rearrange("p (a b k) -> p b a k", b=2, k=NN)[:, odd],
                            8.0, bias[:, heads, 0:NN], ALU.mult, ALU.add)
                    ins.then_inc(vecB.done("biased"), 1)
                    dve.wait_ge(vecB.sem, vecB.at("biased", i))
                    dve.tensor_reduce(top[:, :], s[:, :, :], AX.X, ALU.max).then_inc(vecB.done("top"), 1)
                    dve.wait_ge(vecB.sem, vecB.at("top", i))
                    dve.tensor_tensor(s[:, :, :], s[:, :, :], top[:, :, None].to_broadcast([P, H, J]), ALU.subtract)\
                        .then_inc(vecB.done("shifted"), 1)

                def denominators(i):
                    dve.wait_ge(actB.sem, actB.at("exp", i))
                    dve.tensor_reduce(den[:, :], e[:, :, :], AX.X, ALU.add).then_inc(vecB.done("den"), 1)
                    dve.wait_ge(vecB.sem, vecB.at("den", i))
                    dve.reciprocal(den[:, :], den[:, :]).then_inc(vecB.done("rden"), 1)

                def take_eT(i):
                    dve.wait_ge(peB.sem, peB.at("eT", i))
                    dve.tensor_copy(eT[:, :, :], psS_heads[:, :, :]).then_inc(vecB.done("eT"), 1)

                def take_o(i):
                    dve.wait_ge(peB.sem, peB.at("out", i))
                    den_in_order = den[:, :].rearrange("p (odd a) -> p a odd", odd=2)
                    dve.tensor_tensor(o[:, :, :].rearrange("p (a odd) k -> p a odd k", odd=2),
                                      psS[:, :, :].rearrange("p b (a odd k) -> p (b a) odd k", odd=2, k=DH),
                                      den_in_order[:, :, :, None].to_broadcast([P, PR, 2, DH]), ALU.mult)\
                        .then_inc(vecB.done("o"), 1)

                def residual(i):
                    dve.wait_ge(peB.sem, peB.at("proj", i))
                    xi = core.x[:, bass.ds(i, 1), :].rearrange("p a n -> p (a n)")
                    dve.tensor_tensor(xi, xi, psX[:, 0:D], ALU.add).then_inc(vecB.done("x"), 1)

                def first(j):
                    for step in (take_y, norms, scale_qk, take_v):
                        step(j)

                def both(i):
                    take_y(i + 1)
                    softmax(i)
                    norms(i + 1)
                    denominators(i)
                    take_eT(i)
                    scale_qk(i + 1)
                    dve.wait_ge(peB.sem, peB.at("out", i))
                    take_v(i + 1)
                    take_o(i)
                    residual(i)

                def last(i):
                    for step in (softmax, denominators, take_eT, take_o, residual):
                        step(i)

                turns(dve, first, both, last)
                dve.wait_ge(vecB.sem, vecB.at("x", TT - 1))


def stage_experts(core, norm, tag, router, weights, experts, chunks, gated, keep_top):
    nc, d = core.nc, core.dram
    FIRST = (2 if gated else 1) * DC * P
    WC = FIRST + D
    LATE = 2
    with ExitStack() as ctx:
        sb = lambda name, shape, dt=F32: ctx.enter_context(nc.sbuf_tensor(f"{tag}_{name}", shape, dt))
        sem = lambda name: core.sem(f"{tag}_{name}")
        rw = sb("rw", [P, DC, E])
        iota = sb("iota", [P, E])
        logits = sb("logits", [P, TT, E])
        best, index = sb("best", [P, TT, 8]), sb("index", [P, TT, 8], U32)
        indexf = sb("indexf", [P, TT, 8])
        hot = sb("hot", [P, 2, TT, E])
        share = sb("share", [P, 2, TT])
        wt = sb("wt", [P, TT, E])
        wT = sb("wT", [E, TOK])
        wTd = sb("wTd", [E, E, TOK])
        wb = sb("wb", [P, experts, TOK])
        xh, xl = sb("xh", [P, DC, TOK], F16), sb("xl", [P, DC, TOK], F16)
        w32 = sb("w32", [P, chunks, WC])
        wh, wl = sb("wh", [P, chunks, WC], F16), sb("wl", [P, chunks, WC], F16)
        g = sb("g", [P, 2, TOK])
        sg = sb("sg", [P, 2, TOK])
        hm = sb("hm", [P, 2, TOK])
        hh, hl = sb("hh", [P, 2, TOK], F16), sb("hl", [P, 2, TOK], F16)
        zeros = sb("zeros", [1, 512])

        loaded = sem("loaded")
        second_sem, summed = sem("first_weights"), sem("summed")
        vec = Steps(sem("route_vector"), "x_hi x_lo logits best index indexf hot diff shared_out "
                                         "inverse share weights wT wTd")
        pe_s = Steps(sem("route_tensor"), "logits wT " + " ".join(f"spread{e}" for e in range(E)))
        act_s = Steps(sem("route_scalar"), "exp " + " ".join(f"spread{e}" for e in range(E)))

        w_loaded = [sem(f"w_loaded{k}") for k in range(chunks)]
        w_hi, w_lo = sem("w_hi"), sem("w_lo")
        up_done, gate_w, silu, silu_w = sem("up_done"), sem("gate_w"), sem("silu"), sem("silu_w")
        hidden, hid_hi, hid_lo, down_done = sem("hidden"), sem("hid_hi"), sem("hid_lo"), sem("down_done")

        def load_chunk(sp, e, k):
            sp.dma_start(w32[:, k, :], d[weights][bass.ds(e, 1), k, :, :].rearrange("a p n -> (a p) n"))\
                .then_inc(w_loaded[k], 16)

        def prefetch(sp):
            sp.dma_start(rw[:, :, :], d[router].rearrange("(c p) e -> p c e", p=P)).then_inc(loaded, 16)
            sp.dma_start(iota[:, :], d["c_iota"]).then_inc(loaded, 16)
            for k in range(chunks):
                load_chunk(sp, 0, k)

        norm(prefetch)

        with ExitStack() as pctx, nc.Block() as block:
            psR = pctx.enter_context(nc.psum_tensor(f"{tag}_psR", [P, TT, E], F32))
            psW = pctx.enter_context(nc.psum_tensor(f"{tag}_psW", [E, TOK], F32))
            psB = pctx.enter_context(nc.psum_tensor(f"{tag}_psB", [P, 2, TOK], F32))

            @block.tensor
            def _(pe):
                pe.wait_ge(loaded, 32)
                for t in range(TT):
                    for c in range(DC):
                        ins = pe.matmul(psR[:, t, :], core.yT[:, c, t * P:(t + 1) * P], rw[:, c, :],
                                        start=(c == 0), stop=(c == DC - 1))
                ins.then_inc(pe_s.done("logits"), 1)
                pe.wait_ge(vec.sem, vec.at("weights"))
                for t in range(TT):
                    ins = pe.transpose(psW[:, t * P:(t + 1) * P], wt[:, t, :], core.ident[:, :])
                ins.then_inc(pe_s.done("wT"), 1)
                pe.wait_ge(vec.sem, vec.at("wTd"))
                for e in range(E):
                    if e >= 2:
                        pe.wait_ge(act_s.sem, act_s.at(f"spread{e - 2}"))
                    pe.matmul(psB[:, e % 2, :], core.ones[0:E, :], wTd[:, e, :], start=True, stop=True)\
                        .then_inc(pe_s.done(f"spread{e}"), 1)

            @block.scalar
            def _(act):
                act.wait_ge(vec.sem, vec.at("diff"))
                act.activation(share[:, 1, :], share[:, 0, :], ACT.Exp).then_inc(act_s.done("exp"), 1)
                for e in range(E):
                    act.wait_ge(pe_s.sem, pe_s.at(f"spread{e}"))
                    act.activation(wb[:, e, :], psB[:, e % 2, :], ACT.Copy).then_inc(act_s.done(f"spread{e}"), 1)

            @block.vector
            def _(dve):
                dve.tensor_copy(xh[:, :, :], core.yT[:, :, :]).then_inc(vec.done("x_hi"), 1)
                dve.wait_ge(vec.sem, vec.at("x_hi"))
                dve.tensor_tensor(xl[:, :, :], core.yT[:, :, :], xh[:, :, :], ALU.subtract).then_inc(vec.done("x_lo"), 1)
                dve.wait_ge(loaded, 32)
                dve.wait_ge(pe_s.sem, pe_s.at("logits"))
                dve.tensor_copy(logits[:, :, :], psR[:, :, :]).then_inc(vec.done("logits"), 1)
                dve.wait_ge(vec.sem, vec.at("logits"))
                for t in range(TT):
                    ins = dve.max(best[:, t, :], logits[:, t, :])
                ins.then_inc(vec.done("best"), 1)
                dve.wait_ge(vec.sem, vec.at("best"))
                for t in range(TT):
                    ins = dve.max_index(index[:, t, :], best[:, t, :], logits[:, t, :])
                ins.then_inc(vec.done("index"), 1)
                dve.wait_ge(vec.sem, vec.at("index"))
                dve.tensor_copy(indexf[:, :, :], index[:, :, :]).then_inc(vec.done("indexf"), 1)
                dve.wait_ge(vec.sem, vec.at("indexf"))
                for k in range(2):
                    for t in range(TT):
                        ins = dve.tensor_scalar(hot[:, k, t, :], iota[:, :], indexf[:, t, k:k + 1], None, ALU.is_equal)
                ins.then_inc(vec.done("hot"), 1)
                if keep_top == 2:
                    dve.tensor_tensor(share[:, 0, :], best[:, :, 1], best[:, :, 0], ALU.subtract).then_inc(vec.done("diff"), 1)
                else:
                    dve.tensor_scalar(share[:, 0, :], best[:, :, 0], -1.0, 80.0, ALU.mult, ALU.min).then_inc(vec.done("diff"), 1)
                if experts > E:
                    dve.memset(wb[:, E, :], 1.0)
                dve.memset(zeros[:, :], 0.0)
                dve.wait_ge(act_s.sem, act_s.at("exp"))
                dve.tensor_scalar(share[:, 0, :], share[:, 1, :], 1.0, None, ALU.add).then_inc(vec.done("shared_out"), 1)
                dve.wait_ge(vec.sem, vec.at("shared_out"))
                dve.reciprocal(share[:, 0, :], share[:, 0, :]).then_inc(vec.done("inverse"), 1)
                dve.wait_ge(vec.sem, vec.at("inverse"))
                dve.tensor_tensor(share[:, 1, :], share[:, 1, :], share[:, 0, :], ALU.mult).then_inc(vec.done("share"), 1)
                dve.wait_ge(vec.sem, vec.at("share"))
                for t in range(TT):
                    ins = dve.tensor_scalar(wt[:, t, :], hot[:, 0, t, :], share[:, 0, t:t + 1], None, ALU.mult)
                ins.then_inc(second_sem if keep_top == 2 else vec.done("weights"), 1)
                if keep_top == 2:
                    dve.wait_ge(second_sem, 1)
                    for t in range(TT):
                        ins = dve.scalar_tensor_tensor(wt[:, t, :], hot[:, 1, t, :], share[:, 1, t:t + 1], wt[:, t, :],
                                                       ALU.mult, ALU.add)
                    ins.then_inc(vec.done("weights"), 1)
                dve.wait_ge(pe_s.sem, pe_s.at("wT"))
                dve.tensor_copy(wT[:, :], psW[:, :]).then_inc(vec.done("wT"), 1)
                dve.wait_ge(vec.sem, vec.at("wT"))
                dve.tensor_tensor(wTd[:, :, :], wT[:, None, :].to_broadcast([E, E, TOK]),
                                  core.ident[0:E, 0:E, None].to_broadcast([E, E, TOK]), ALU.mult)\
                    .then_inc(vec.done("wTd"), 1)

        with ExitStack() as pctx, nc.Block() as block:
            psY = pctx.enter_context(nc.psum_tensor(f"{tag}_psY", [P, TT, D], F32))
            psG = pctx.enter_context(nc.psum_tensor(f"{tag}_psG", [P, 2, TOK], F32))
            psU = pctx.enter_context(nc.psum_tensor(f"{tag}_psU", [P, 2, TOK], F32))
            START = 1
            n = lambda e, k: e * chunks + k

            @block.sync
            def _(sp):
                with sp.Fori(0, experts) as e:
                    for k in range(chunks):
                        sp.wait_ge(w_lo, n(e, k) + 1)
                        load_chunk(sp, e + 1, k)

            @block.tensor
            def _(pe):
                def first_layers(e, k):
                    s = k % 2
                    pe.wait_ge(w_lo, n(e, k) + 1)
                    pe.wait_ge(hidden, START + n(e, max(k - 1, 0)))
                    for i in range(2 if gated else 1):
                        out = (psG, psU)[i][:, s, :]
                        terms = [(w, x, c) for w, x in ((wh, xh), (wl, xh), (wh, xl)) for c in range(DC)]
                        for j, (w, x, c) in enumerate(terms):
                            col = (i * DC + c) * P
                            ins = pe.matmul(out, w[:, k, col:col + P], x[:, c, :], start=(j == 0),
                                            stop=(j == len(terms) - 1))
                    ins.then_inc(up_done, 1)

                def last_layer(e, k):
                    s = k % 2
                    pe.wait_ge(hid_lo, START + n(e, k) + 1)
                    for t in range(TT):
                        for h, w in ((hh, wh), (hl, wh), (hh, wl)):
                            ins = pe.matmul(psY[:, t, :], h[:, s, t * P:(t + 1) * P], w[:, k, FIRST:WC],
                                            start=False, stop=False, skip_group_check=True)
                    ins.then_inc(down_done, 1)

                for bank in range(2):
                    pe.matmul(psY[:, 2 * bank:2 * bank + 2, :].rearrange("p a n -> p (a n)"), zeros[0:1, 0:P],
                              zeros[0:1, :], start=True, stop=False, skip_group_check=True)
                with pe.Fori(0, experts) as e:
                    for k in range(chunks):
                        first_layers(e, k)
                        if k >= 1:
                            last_layer(e, k - 1)
                    last_layer(e, chunks - 1)

            @block.scalar
            def _(act):
                def split_weights(e, k, first=False):
                    act.wait_ge(w_loaded[k], 16 * e + 16)
                    if not first:
                        act.wait_ge(down_done, START + n(e - 1, k) + 1)
                    act.activation(wh[:, k, :], w32[:, k, :], ACT.Copy).then_inc(w_hi, 1)

                for k in range(chunks):
                    split_weights(0, k, first=True)
                with act.Fori(0, experts) as e:
                    for k in range(chunks):
                        s = k % 2
                        if gated:
                            act.wait_ge(gate_w, n(e, k) + 1)
                            act.activation(sg[:, s, :], g[:, s, :], ACT.Silu).then_inc(silu, 1)
                        act.wait_ge(hidden, START + n(e, k) + 1)
                        act.wait_ge(down_done, START + n(e, max(k - 1, 0)))
                        act.activation(hh[:, s, :], hm[:, s, :], ACT.Copy).then_inc(hid_hi, 1)
                        if k >= LATE:
                            split_weights(e + 1, k - LATE)
                    for k in range(chunks - LATE, chunks):
                        split_weights(e + 1, k)

            if gated:
                @block.gpsimd
                def _(pool):
                    with pool.Fori(0, experts) as e:
                        for k in range(chunks):
                            s = k % 2
                            wait_apart(pool, silu, n(e, k) + 1, core.spare)
                            pool.tensor_tensor(sg[:, s, :], sg[:, s, :],
                                               wb[:, bass.ds(e, 1), :].rearrange("p a n -> p (a n)"), ALU.mult)\
                                .then_inc(silu_w, 1)

            @block.vector
            def _(dve):
                def split_weights(e, k):
                    dve.wait_ge(w_hi, n(e, k) + 1)
                    dve.tensor_tensor(wl[:, k, :], w32[:, k, :], wh[:, k, :], ALU.subtract).then_inc(w_lo, 1)

                for free in (hidden, hid_lo, down_done):
                    dve.sem_inc(free, START)
                for k in range(chunks):
                    split_weights(0, k)
                with dve.Fori(0, experts) as e:
                    w_e = wb[:, bass.ds(e, 1), :].rearrange("p a n -> p (a n)")
                    for k in range(chunks):
                        s = k % 2
                        dve.wait_ge(up_done, n(e, k) + 1)
                        dve.wait_ge(hid_lo, START + n(e, max(k - 1, 0)))
                        if gated:
                            dve.tensor_tensor(g[:, s, :], psG[:, s, :], w_e, ALU.mult).then_inc(gate_w, 1)
                            dve.wait_ge(silu_w, n(e, k) + 1)
                            dve.tensor_tensor(hm[:, s, :], psU[:, s, :], sg[:, s, :], ALU.mult).then_inc(hidden, 1)
                        else:
                            dve.scalar_tensor_tensor(hm[:, s, :], psG[:, s, :], 0.0, w_e, ALU.max, ALU.mult)\
                                .then_inc(hidden, 1)
                        dve.wait_ge(hid_hi, n(e, k) + 1)
                        dve.wait_ge(hidden, START + n(e, k) + 1)
                        dve.wait_ge(down_done, START + n(e, max(k - 1, 0)))
                        dve.tensor_tensor(hl[:, s, :], hm[:, s, :], hh[:, s, :], ALU.subtract).then_inc(hid_lo, 1)
                        if k >= LATE:
                            split_weights(e + 1, k - LATE)
                    for k in range(chunks - LATE, chunks):
                        split_weights(e + 1, k)
                dve.wait_ge(down_done, START + experts * chunks)
                dve.tensor_tensor(core.x[:, :, :], core.x[:, :, :], psY[:, :, :], ALU.add).then_inc(summed, 1)
                dve.wait_ge(summed, 1)


def stage_l1_self(core, norm):
    nc, d = core.nc, core.dram
    DH, NM = 64, 4
    J = NM + N
    DROPPED = J - 64
    PR = H // 2
    W = H * DH
    U = P // 8
    UH = U // 2
    QK_SCALE = 10.0
    halves = [slice(0, N), slice(N, P)]
    with ExitStack() as ctx:
        sb = lambda name, shape, dt=F32: ctx.enter_context(nc.sbuf_tensor(f"l1a_{name}", shape, dt))
        pb = lambda name, shape: ctx.enter_context(nc.psum_tensor(f"l1a_{name}", shape, F32))
        sem = lambda name: core.sem(f"l1a_{name}")
        w = sb("w", [P, DC, 4 * W])
        wo = sb("wo", [P, PR, D])
        bg = sb("bg", [1, W])
        hscale = sb("hscale", [P, H])
        wpre, wpost = sb("wpre", [P, P]), sb("wpost", [P, P])
        mask = sb("mask", [P, 4, U // 4 * J])
        mk, mks, mss = sb("mk", [H * NM, 2 * DH]), sb("mks", [H * NM, DH]), sb("mss", [H * NM, 1])
        mkT = sb("mkT", [P, H * NM])
        mv = sb("mv", [P, H, DH])
        memrows = sb("memrows", [P, NM])
        yt = sb("yt", [P, DC, P])
        qk, sq, ss = sb("qk", [P, 2, H, DH]), sb("sq", [P, 2, H, DH]), sb("ss", [P, 2, H])
        v, gate = sb("v", [P, W]), sb("gate", [P, H, DH])
        v_next, g_next = sb("v_next", [P, W]), sb("g_next", [P, H, DH])
        qkT = sb("qkT", [P, 2, PR, P])
        sT, sTm = sb("sT", [P, N, H]), sb("sTm", [P, P, H])
        r = sb("r", [P, U, J])
        s, drop = sb("s", [P, 4, U // 4 * J]), sb("drop", [P, U, J])
        s_rows = s[:, :, :].rearrange("p a (b j) -> p (a b) j", j=J)
        least = sb("least", [P, U, 8])
        low, den = sb("low", [P, U]), sb("den", [P, U])
        e = sb("e", [P, U, J])
        aT, aTm = sb("aT", [P, H, N]), sb("aTm", [P, H, P])
        o, oT = sb("o", [P, H, DH]), sb("oT", [P, PR, P])

        loaded = sem("loaded")
        setup = Steps(sem("setup"), "squares sums guarded scaled mkT")
        setup_root, setup_T = sem("setup_root"), sem("setup_T")
        vecA = Steps(sem("vector_a"), "yt squares sums guarded normed g0 g1 g2 v gate")
        vecB = Steps(sem("vector_b"), "sT r masked least drop dropped low shifted den rden e aT o x")
        actA, actB = Steps(sem("scalar_a"), "qk qkT v expgate"), Steps(sem("scalar_b"), "sTm rm exp aTm oT")
        peA, peB = Steps(sem("tensor_a"), "qk qkT vg"), Steps(sem("tensor_b"), "sT r mixed aT out oT proj")
        roots = Steps(sem("roots"), "norms")
        N_LOADS = 16 * 13

        def turns(eng, first, both, last):
            first(0)
            with eng.Fori(0, TT - 1) as i:
                both(i)
            last(TT - 1)

        def prefetch(sp):
            for j, name in enumerate(("Wq", "Wk", "Wv", "Wg")):
                sp.dma_start(w[:, :, j * W:(j + 1) * W], d[f"L1_attn_{name}"].rearrange("(c p) n -> p c n", p=P))\
                    .then_inc(loaded, 16)
            sp.dma_start(wo[:, :, :], d["L1_attn_Wo"].rearrange("(c p) n -> p c n", p=P)).then_inc(loaded, 16)
            sp.dma_start(bg[:, :], d["L1_attn_bg"].partition_broadcast(1)).then_inc(loaded, 16)
            sp.dma_start(hscale[:, :], d["c_head_scale"].partition_broadcast(P)).then_inc(loaded, 16)
            sp.dma_start(wpre[:, :], d["c_pre"]).then_inc(loaded, 16)
            sp.dma_start(wpost[:, :], d["c_post"]).then_inc(loaded, 16)
            sp.dma_start(mask[:, :, :], d["c_rowmask"]).then_inc(loaded, 16)
            sp.dma_start(mk[:, 0:DH], d["L1_attn_mem_k"].rearrange("h m k -> (h m) k")).then_inc(loaded, 16)
            sp.dma_start(mv[:, :, :], d["c_mem_v"]).then_inc(loaded, 16)
            sp.dma_start(memrows[:, :], d["c_memrows"]).then_inc(loaded, 16)

        norm(prefetch)
        psA, psB = pb("psA", [P, 4, 512]), pb("psB", [P, 4, 512])
        psA_blocks = psA[:, :, :].rearrange("p a (b q) -> p (a b) q", q=P)
        psB_blocks = psB[:, :, :].rearrange("p a (b q) -> p (a b) q", q=P)
        quarter = lambda k: slice(32 * k, 32 * k + NM)
        with nc.Block() as block:
            @block.gpsimd
            def _(pool):
                pool.wait_ge(setup.sem, setup.at("guarded"))
                pool.tensor_tensor(mss[:, :], mss[:, :], core.minus_half[0:H * NM, 0:1], ALU.pow).then_inc(setup_root, 1)
                def root(j):
                    pool.wait_ge(vecA.sem, vecA.at("guarded", j))
                    pool.tensor_tensor(ss[:, :, :], ss[:, :, :],
                                       core.minus_half[:, 0:2 * H].rearrange("p (a h) -> p a h", a=2), ALU.pow)\
                        .then_inc(roots.done("norms"), 1)

                turns(pool, root, lambda i: root(i + 1), lambda i: None)

            @block.tensor
            def _(pe):
                pe.wait_ge(setup.sem, setup.at("scaled"))
                pe.transpose(psA[:, 0, 0:H * NM], mk[:, :], core.ident[0:H * NM, 0:H * NM]).then_inc(setup_T, 1)
                pe.wait_ge(setup.sem, setup.at("mkT"))

                def project(parts):
                    for part in parts:
                        ps = psA[:, part % 4, :]
                        gates = part >= 6
                        for c in range(DC):
                            ins = pe.matmul(ps, yt[:, c, :], w[:, c, part * 512:(part + 1) * 512],
                                            start=(c == 0), stop=(c == 1 and not gates))
                        if gates:
                            ins = pe.matmul(ps, core.ones[0:1, :], bg[0:1, (part - 6) * 512:(part - 5) * 512],
                                            start=False, stop=True)
                    return ins

                def project_qk(j):
                    pe.wait_ge(vecA.sem, vecA.at("yt", j))
                    project(range(4)).then_inc(peA.done("qk"), 1)

                def transpose_qk(j):
                    pe.wait_ge(vecA.sem, vecA.at("normed", j))
                    for a in range(2):
                        for pr in range(PR):
                            ins = pe.transpose(psA_blocks[:, a * PR + pr, :],
                                               qk[:, a, 2 * pr:2 * pr + 2, :].rearrange("p h k -> p (h k)"),
                                               core.ident[:, :])
                    ins.then_inc(peA.done("qkT"), 1)

                def project_vg(j):
                    pe.wait_ge(actA.sem, actA.at("qkT", j))
                    project(range(4, 8)).then_inc(peA.done("vg"), 1)

                def score(i):
                    wait_apart(pe, actA.sem, actA.at("qkT", i), core.spare)
                    for pr in range(PR):
                        for odd, rows in enumerate(halves):
                            h = 2 * pr + odd
                            for half in halves:
                                pe.matmul(psB[half, odd, pr * N:(pr + 1) * N], qkT[rows, 1, pr, half],
                                          qkT[rows, 0, pr, half], start=True, stop=True)
                            ins = pe.matmul(psB[quarter(h // 4), 2 + odd, pr % 2 * P:(pr % 2 + 1) * P],
                                            mkT[rows, h * NM:(h + 1) * NM], qkT[rows, 0, pr, :], start=True, stop=True)
                    ins.then_inc(peB.done("sT"), 1)

                def to_rows(i):
                    pe.wait_ge(vecB.sem, vecB.at("sT", i))
                    pe.wait_ge(actB.sem, actB.at("sTm", i))
                    for u in range(U):
                        half, at = halves[u // UH], u % UH
                        pe.matmul(psB[:, u // UH, at * N:(at + 1) * N],
                                  sT[half, at * 8:(at + 1) * 8, :].rearrange("j q h -> j (q h)"),
                                  core.ident[half, half], start=True, stop=True)
                    for u in range(U):
                        ins = pe.matmul(psB[:, 2, u * NM:(u + 1) * NM],
                                        sTm[:, u * 8:(u + 1) * 8, :].rearrange("j q h -> j (q h)"),
                                        memrows[:, :], start=True, stop=True)
                    ins.then_inc(peB.done("r"), 1)

                def mix(i):
                    pe.wait_ge(vecB.sem, vecB.at("r", i))
                    pe.wait_ge(actB.sem, actB.at("rm", i))
                    for a in range(4):
                        ins = pe.matmul(psB[:, a, 0:U // 4 * J], wpre[:, :],
                                        r[:, a * 4:(a + 1) * 4, :].rearrange("p u j -> p (u j)"), start=True, stop=True)
                    ins.then_inc(peB.done("mixed"), 1)

                def mix_back(i):
                    pe.wait_ge(vecB.sem, vecB.at("e", i))
                    for u in range(U):
                        pe.matmul(psB_blocks[halves[u // UH], u % UH, :], e[:, u, NM:J], wpost[:, :], start=True, stop=True)
                        ins = pe.matmul(psB[quarter(u // 4), 2, u % 4 * P:(u % 4 + 1) * P], e[:, u, 0:NM], wpost[:, :],
                                        start=True, stop=True)
                    ins.then_inc(peB.done("aT"), 1)

                def weigh(i):
                    pe.wait_ge(vecB.sem, vecB.at("aT", i))
                    pe.wait_ge(vecA.sem, vecA.at("v", i))
                    pe.wait_ge(actB.sem, actB.at("aTm", i))
                    for h in range(H):
                        pe.matmul(psB[:, 2 + h // 8, h % 8 * DH:(h % 8 + 1) * DH], aTm[:, h, :], mv[:, h, :],
                                  start=(h % 8 == 0), stop=False, skip_group_check=True)
                    for h in range(H):
                        for half in halves:
                            ins = pe.matmul(psB[half, 2 + h // 8, h % 8 * DH:(h % 8 + 1) * DH], aT[half, h, :],
                                            v[half, h * DH:(h + 1) * DH], start=False, stop=(h % 8 == 7),
                                            skip_group_check=True)
                    ins.then_inc(peB.done("out"), 1)

                def transpose_o(i):
                    pe.wait_ge(vecB.sem, vecB.at("o", i))
                    for pr in range(PR):
                        ins = pe.transpose(psB_blocks[:, pr, :], o[:, 2 * pr:2 * pr + 2, :].rearrange("p h k -> p (h k)"),
                                           core.ident[:, :])
                    ins.then_inc(peB.done("oT"), 1)

                def project_out(i):
                    pe.wait_ge(actB.sem, actB.at("oT", i))
                    for pr in range(PR):
                        ins = pe.matmul(psB[:, 2, 0:D], oT[:, pr, :], wo[:, pr, :], start=(pr == 0), stop=(pr == PR - 1))
                    ins.then_inc(peB.done("proj"), 1)

                def first(j):
                    for step in (project_qk, transpose_qk, project_vg):
                        step(j)

                def both(i):
                    score(i)
                    project_qk(i + 1)
                    to_rows(i)
                    mix(i)
                    transpose_qk(i + 1)
                    project_vg(i + 1)
                    for step in (mix_back, weigh, transpose_o, project_out):
                        step(i)
                    pe.wait_ge(vecB.sem, vecB.at("x", i))

                def last(i):
                    for step in (score, to_rows, mix, mix_back, weigh, transpose_o, project_out):
                        step(i)

                turns(pe, first, both, last)

            @block.scalar
            def _(act):
                def take_qk(j):
                    act.wait_ge(peA.sem, peA.at("qk", j))
                    act.activation(qk[:, :, :, :].rearrange("p a h k -> p (a h k)"),
                                   psA[:, :, :].rearrange("p a n -> p (a n)"), ACT.Copy).then_inc(actA.done("qk"), 1)

                def take_qkT(j):
                    act.wait_ge(peA.sem, peA.at("qkT", j))
                    act.activation(qkT[:, :, :, :].rearrange("p a h k -> p (a h k)"),
                                   psA[:, :, :].rearrange("p a n -> p (a n)"), ACT.Copy).then_inc(actA.done("qkT"), 1)

                def take_v(j):
                    act.wait_ge(peA.sem, peA.at("vg", j))
                    act.activation(v_next[:, :], psA[:, 0:2, :].rearrange("p a n -> p (a n)"), ACT.Copy)\
                        .then_inc(actA.done("v"), 1)

                def exp_gate(j):
                    act.wait_ge(vecA.sem, vecA.at("g0", j))
                    act.activation(g_next[:, :, :], g_next[:, :, :], ACT.Exp, scale=-1.0).then_inc(actA.done("expgate"), 1)

                def take_sTm(i):
                    act.wait_ge(peB.sem, peB.at("sT", i))
                    for k in range(4):
                        for odd in range(2):
                            ins = act.activation(
                                sTm[quarter(k), :, odd * PR + 2 * k:odd * PR + 2 * k + 2].rearrange("m q h -> m h q"),
                                psB[quarter(k), 2 + odd, 0:2 * P].rearrange("m (h q) -> m h q", q=P), ACT.Copy)
                    ins.then_inc(actB.done("sTm"), 1)

                def take_rm(i):
                    act.wait_ge(peB.sem, peB.at("r", i))
                    act.activation(r[:, :, 0:NM], psB[:, 2, 0:U * NM].rearrange("p (u m) -> p u m", m=NM), ACT.Copy,
                                   scale=QK_SCALE).then_inc(actB.done("rm"), 1)

                def exp(i):
                    act.wait_ge(vecB.sem, vecB.at("shifted", i))
                    act.activation(e[:, :, :], s_rows, ACT.Exp, scale=-1.0).then_inc(actB.done("exp"), 1)

                def take_aTm(i):
                    act.wait_ge(peB.sem, peB.at("aT", i))
                    for k in range(4):
                        ins = act.activation(aTm[quarter(k), :, 32 * k:32 * (k + 1)].rearrange("m h q -> m q h"),
                                             psB[quarter(k), 2, :].rearrange("m (q h) -> m q h", h=H), ACT.Copy)
                    ins.then_inc(actB.done("aTm"), 1)

                def take_oT(i):
                    act.wait_ge(peB.sem, peB.at("oT", i))
                    act.activation(oT[:, :, :], psB_blocks[:, 0:PR, :], ACT.Copy).then_inc(actB.done("oT"), 1)

                def first(j):
                    for step in (take_qk, take_qkT, take_v, exp_gate):
                        step(j)

                def both(i):
                    take_sTm(i)
                    take_qk(i + 1)
                    take_rm(i)
                    take_qkT(i + 1)
                    exp(i)
                    take_v(i + 1)
                    exp_gate(i + 1)
                    take_aTm(i)
                    take_oT(i)

                def last(i):
                    for step in (take_sTm, take_rm, exp, take_aTm, take_oT):
                        step(i)

                act.wait_ge(setup.sem, setup.at("mkT"))
                turns(act, first, both, last)

            @block.vector
            def _(dve):
                dve.memset(sTm[:, :, :], 0.0)
                dve.memset(aTm[:, :, :], 0.0)
                dve.wait_ge(loaded, N_LOADS)
                dve.tensor_tensor(mks[:, :], mk[:, 0:DH], mk[:, 0:DH], ALU.mult).then_inc(setup.done("squares"), 1)
                dve.wait_ge(setup.sem, setup.at("squares"))
                dve.tensor_reduce(mss[:, :], mks[:, :], AX.X, ALU.add).then_inc(setup.done("sums"), 1)
                dve.wait_ge(setup.sem, setup.at("sums"))
                dve.tensor_scalar(mss[:, :], mss[:, :], 1e-24, None, ALU.max).then_inc(setup.done("guarded"), 1)
                dve.wait_ge(setup_root, 1)
                dve.tensor_scalar(mk[:, DH:2 * DH], mk[:, 0:DH], mss[:, 0:1], None, ALU.mult)
                dve.tensor_scalar(mk[:, 0:DH], mk[:, 0:DH], mss[:, 0:1], None, ALU.mult).then_inc(setup.done("scaled"), 1)
                dve.wait_ge(setup_T, 1)
                dve.tensor_copy(mkT[:, :], psA[:, 0, 0:H * NM]).then_inc(setup.done("mkT"), 1)

                def take_y(j):
                    dve.tensor_copy(yt[:, :, :], core.yT[:, :, bass.ds(j * P, P)]).then_inc(vecA.done("yt"), 1)

                def norms(j):
                    dve.wait_ge(actA.sem, actA.at("qk", j))
                    dve.tensor_tensor(sq[:, :, :, :], qk[:, :, :, :], qk[:, :, :, :], ALU.mult).then_inc(vecA.done("squares"), 1)
                    dve.wait_ge(vecA.sem, vecA.at("squares", j))
                    dve.tensor_reduce(ss[:, :, :], sq[:, :, :, :], AX.X, ALU.add).then_inc(vecA.done("sums"), 1)
                    dve.wait_ge(vecA.sem, vecA.at("sums", j))
                    dve.tensor_scalar(ss[:, :, :], ss[:, :, :], 1e-24, None, ALU.max).then_inc(vecA.done("guarded"), 1)

                def normalise_qk(j):
                    dve.wait_ge(roots.sem, roots.at("norms", j))
                    dve.tensor_tensor(qk[:, :, :, :], qk[:, :, :, :], ss[:, :, :, None].to_broadcast([P, 2, H, DH]),
                                      ALU.mult).then_inc(vecA.done("normed"), 1)

                def clamp_gate(j):
                    dve.wait_ge(peA.sem, peA.at("vg", j))
                    dve.tensor_scalar(g_next[:, :, :].rearrange("p h k -> p (h k)"),
                                      psA[:, 2:4, :].rearrange("p a n -> p (a n)"), -80.0, None, ALU.max)\
                        .then_inc(vecA.done("g0"), 1)

                def invert_gate(j):
                    dve.wait_ge(actA.sem, actA.at("expgate", j))
                    dve.tensor_scalar(g_next[:, :, :], g_next[:, :, :], 1.0, None, ALU.add).then_inc(vecA.done("g1"), 1)
                    dve.wait_ge(vecA.sem, vecA.at("g1", j))
                    dve.reciprocal(g_next[:, :, :], g_next[:, :, :]).then_inc(vecA.done("g2"), 1)

                def keep_v(j):
                    dve.wait_ge(actA.sem, actA.at("v", j))
                    dve.tensor_copy(v[:, :], v_next[:, :]).then_inc(vecA.done("v"), 1)

                def scale_gate(j):
                    dve.wait_ge(vecA.sem, vecA.at("g2", j))
                    dve.tensor_tensor(gate[:, :, :], g_next[:, :, :], hscale[:, :, None].to_broadcast([P, H, DH]), ALU.mult)\
                        .then_inc(vecA.done("gate"), 1)

                def take_sT(i):
                    dve.wait_ge(peB.sem, peB.at("sT", i))
                    for odd in range(2):
                        ins = dve.tensor_copy(sT[:, :, odd * PR:(odd + 1) * PR].rearrange("p q h -> p h q"),
                                              psB[:, odd, :].rearrange("p (b q) -> p b q", q=N))
                    ins.then_inc(vecB.done("sT"), 1)

                def take_r(i):
                    dve.wait_ge(peB.sem, peB.at("r", i))
                    dve.tensor_scalar(r[:, :, NM:J], psB[:, 0:2, :].rearrange("p a (b j) -> p (a b) j", j=N), QK_SCALE, None,
                                      ALU.mult).then_inc(vecB.done("r"), 1)

                def softmax(i):
                    dve.wait_ge(peB.sem, peB.at("mixed", i))
                    dve.scalar_tensor_tensor(s[:, :, :], psB[:, :, 0:U // 4 * J], -1.0, mask[:, :, :], ALU.mult, ALU.add)\
                        .then_inc(vecB.done("masked"), 1)
                    wait_apart(dve, vecB.sem, vecB.at("masked", i), core.spare)
                    for u in range(U):
                        ins = dve.max(least[:, u, :], s_rows[:, u, :])
                    ins.then_inc(vecB.done("least"), 1)
                    dve.wait_ge(vecB.sem, vecB.at("least", i))
                    dve.tensor_tensor(drop[:, :, :], s_rows, least[:, :, DROPPED:DROPPED + 1].to_broadcast([P, U, J]),
                                      ALU.is_gt).then_inc(vecB.done("drop"), 1)
                    dve.wait_ge(vecB.sem, vecB.at("drop", i))
                    dve.scalar_tensor_tensor(s_rows, drop[:, :, :], BIG, s_rows, ALU.mult, ALU.add)\
                        .then_inc(vecB.done("dropped"), 1)
                    dve.wait_ge(vecB.sem, vecB.at("dropped", i))
                    dve.tensor_reduce(low[:, :], s_rows, AX.X, ALU.min).then_inc(vecB.done("low"), 1)
                    dve.wait_ge(vecB.sem, vecB.at("low", i))
                    dve.tensor_tensor(s_rows, s_rows, low[:, :, None].to_broadcast([P, U, J]), ALU.subtract)\
                        .then_inc(vecB.done("shifted"), 1)

                def normalise(i):
                    dve.wait_ge(actB.sem, actB.at("exp", i))
                    dve.tensor_reduce(den[:, :], e[:, :, :], AX.X, ALU.add).then_inc(vecB.done("den"), 1)
                    dve.wait_ge(vecB.sem, vecB.at("den", i))
                    dve.reciprocal(den[:, :], den[:, :]).then_inc(vecB.done("rden"), 1)
                    dve.wait_ge(vecB.sem, vecB.at("rden", i))
                    dve.tensor_tensor(e[:, :, :], e[:, :, :], den[:, :, None].to_broadcast([P, U, J]), ALU.mult)\
                        .then_inc(vecB.done("e"), 1)

                def take_aT(i):
                    dve.wait_ge(peB.sem, peB.at("aT", i))
                    dve.tensor_copy(aT[:, :, :].rearrange("p h q -> p q h"),
                                    psB[:, 0:2, :].rearrange("p a (b h) -> p (a b) h", h=H)).then_inc(vecB.done("aT"), 1)

                def take_o(i):
                    dve.wait_ge(peB.sem, peB.at("out", i))
                    dve.wait_ge(vecA.sem, vecA.at("gate", i))
                    dve.tensor_tensor(o[:, :, :].rearrange("p h k -> p (h k)"), psB[:, 2:4, :].rearrange("p a n -> p (a n)"),
                                      gate[:, :, :].rearrange("p h k -> p (h k)"), ALU.mult).then_inc(vecB.done("o"), 1)

                def residual(i):
                    dve.wait_ge(peB.sem, peB.at("proj", i))
                    xi = core.x[:, bass.ds(i, 1), :].rearrange("p a n -> p (a n)")
                    dve.tensor_tensor(xi, xi, psB[:, 2, 0:D], ALU.add).then_inc(vecB.done("x"), 1)

                def first(j):
                    for step in (take_y, norms, normalise_qk, clamp_gate, invert_gate, keep_v, scale_gate):
                        step(j)

                def both(i):
                    take_y(i + 1)
                    take_sT(i)
                    norms(i + 1)
                    take_r(i)
                    normalise_qk(i + 1)
                    softmax(i)
                    clamp_gate(i + 1)
                    normalise(i)
                    invert_gate(i + 1)
                    take_aT(i)
                    take_o(i)
                    keep_v(i + 1)
                    dve.wait_ge(vecB.sem, vecB.at("o", i))
                    scale_gate(i + 1)
                    residual(i)

                def last(i):
                    for step in (take_sT, take_r, softmax, normalise, take_aT, take_o, residual):
                        step(i)

                turns(dve, first, both, last)
                dve.wait_ge(vecB.sem, vecB.at("x", TT - 1))


class Bank:

    def __init__(self, filled, taken, names):
        self.filled, self.taken, self.names = filled, taken, names

    def full(self, name, turn=0):
        return turn * len(self.names) + (self.names.index(name) + 1)

    def free(self, name, turn=0):
        return turn * len(self.names) + (self.names.index(name) + 1)

    def left(self, name, turn=0, ago=0):
        return turn * len(self.names) + (self.names.index(name) + 2 - ago * len(self.names))


def stage_l1_cross(core, norm):
    nc, d = core.nc, core.dram
    DH = 64
    W = H * DH
    PR = H // 2
    HN = H * N
    G = HN // P
    VW = CD + 1
    SCALE = float(DH) ** -0.5
    halves = [slice(0, N), slice(N, P)]

    def tiles(k):
        return [m for m in range(KT) if m * 10 // KT == k]

    POST_T = {2: ["A0"], 4: ["V0"], 6: ["A1"], 8: ["V1"]}
    POST_M = {2: ["B0"], 6: ["B1"]}
    t_jobs = lambda n, main: [f"t{m}" for m in tiles(n - 2)] + (POST_T.get(n, []) if main else [])
    m_jobs = lambda n, main: [f"m{m}.{c}" for m in tiles(n - 3) for c in range(2)] + (POST_M.get(n, []) if main else [])
    t_names = lambda main: [j for n in range(KT) for j in t_jobs(n, main)] + ["sh1"]
    m_names = lambda main: [j for n in range(KT) for j in m_jobs(n, main)] + ["sh0"]

    with ExitStack() as ctx:
        sb = lambda name, shape, dt=F32, to=ctx: to.enter_context(nc.sbuf_tensor(f"l1x_{name}", shape, dt))
        sem = lambda name: core.sem(f"l1x_{name}")
        qAh, qAl = sb("qAh", [P, B + 1, HN], F16), sb("qAl", [P, B, HN], F16)
        qSB = sb("qSB", [P, B + 1, HN], F16)
        q5 = sb("q5", [DH + 1, B + 1, HN], F16)
        wvA, wvB = sb("wvA", [P, W]), sb("wvB", [CB, W])
        gam, bet = sb("gam", [P, CD]), sb("bet", [P, CD])
        loaded, w_loaded = sem("loaded"), sem("w_loaded")

        raw = sb("raw", [P, KT, CD])
        SPLIT = 7
        raw_loaded = [sem("raw_loaded0"), sem("raw_loaded1")]

        def load_context(sp, j, part):
            tiles = slice(0, SPLIT) if part == 0 else slice(SPLIT, KT)
            src = d["c_ctx"][j, :, :] if isinstance(j, int) else d["c_ctx"][bass.ds(j, 1), :, :].rearrange("a n k -> (a n) k")
            sp.dma_start(raw[:, tiles, :], src.rearrange("(n p) k -> p n k", p=P)[:, tiles, :]).then_inc(raw_loaded[part], 16)

        q_done, q_taken, folded, q_hi, q_lo = sem("q_done"), sem("q_taken"), sem("folded"), sem("q_hi"), sem("q_lo")
        with ExitStack() as inner:
            wq, wkT = sb("wq", [P, DC, W], F32, inner), sb("wkT", [P, PR, 2 * P], F32, inner)
            qT = sb("qT", [P, PR, TOK], F32, inner)
            def prefetch(sp):
                sp.dma_start(wq[:, :, :], d["L1_xattn_Wq"].rearrange("(c p) n -> p c n", p=P)).then_inc(loaded, 16)
                sp.dma_start(wkT[:, :, :], d["c_wkT"].rearrange("(a p) n -> p a n", p=P)).then_inc(loaded, 16)
                sp.dma_start(gam[:, :], d["L1_xattn_g_c"].partition_broadcast(P)).then_inc(w_loaded, 16)
                sp.dma_start(bet[:, :], d["L1_xattn_b_c"].partition_broadcast(P)).then_inc(w_loaded, 16)
                sp.dma_start(wvA[:, :], d["L1_xattn_Wv"][0:P, :]).then_inc(w_loaded, 16)
                sp.dma_start(wvB[:, :], d["L1_xattn_Wv"][P:CD, :]).then_inc(w_loaded, 16)
                load_context(sp, 0, 0)
                load_context(sp, 0, 1)

            norm(prefetch)
            psQ = inner.enter_context(nc.psum_tensor("l1x_psQ", [P, 4, TOK], F32))
            psF = inner.enter_context(nc.psum_tensor("l1x_psF", [P, 2, 2, TOK], F32))
            with nc.Block() as block:
                @block.tensor
                def _(pe):
                    pe.wait_ge(loaded, 32)
                    for pr in range(PR):
                        if pr >= 4:
                            pe.wait_ge(q_taken, pr - 3)
                        for c in range(DC):
                            ins = pe.matmul(psQ[:, pr % 4, :], wq[:, c, pr * P:(pr + 1) * P], core.yT[:, c, :],
                                            start=(c == 0), stop=(c == DC - 1))
                        ins.then_inc(q_done, 1)
                    for h in range(H):
                        pr, r = h // 2, halves[h % 2]
                        pe.wait_ge(q_taken, pr + 1)
                        if h >= 2:
                            pe.wait_ge(q_lo, h - 1)
                        for ab in range(2):
                            ins = pe.matmul(psF[:, h % 2, ab, :], wkT[r, pr, ab * P:(ab + 1) * P], qT[r, pr, :],
                                            start=True, stop=True)
                        ins.then_inc(folded, 1)

                @block.scalar
                def _(act):
                    for pr in range(PR):
                        act.wait_ge(q_done, pr + 1)
                        act.activation(qT[:, pr, :], psQ[:, pr % 4, :], ACT.Copy).then_inc(q_taken, 1)
                    for h in range(H):
                        cols = slice(h * N, (h + 1) * N)
                        act.wait_ge(folded, h + 1)
                        for ab, q in enumerate((qAh, qSB)):
                            ins = act.activation(q[:, 0:B, cols], psF[:, h % 2, ab, :].rearrange("p (b q) -> p b q", q=N),
                                                 ACT.Copy, scale=SCALE)
                        ins.then_inc(q_hi, 1)

                @block.vector
                def _(dve):
                    for q in (qAh, qSB, q5):
                        dve.memset(q[:, B, :], 0.0)
                    for h in range(H):
                        cols = slice(h * N, (h + 1) * N)
                        dve.wait_ge(q_hi, h + 1)
                        for rows, ab, q, hi in ((slice(0, P), 0, qAl, qAh), (slice(0, CB), 1, q5, qSB)):
                            ins = dve.scalar_tensor_tensor(
                                q[rows, 0:B, cols], psF[rows, h % 2, ab, :].rearrange("p (b q) -> p b q", q=N), SCALE,
                                hi[rows, 0:B, cols], ALU.mult, ALU.subtract)
                        ins.then_inc(q_lo, 1)

        ch, cl = sb("ch", [P, 2, KT, VW], F16), sb("cl", [P, 2, KT, CD], F16)
        ct = sb("ct", [P, 2, KT, 3 * P], F16)
        c5 = sb("c5", [DH + 1, 2, KT, P], F16)
        stats, aggr, rstd = sb("stats", [P, KT, 6]), sb("aggr", [P, KT, 2]), sb("rstd", [P, KT])
        tops, top = sb("tops", [P, G, KT]), sb("top", [P, G])
        shift = sb("shift", [P, G, DH + 1], F16)
        e32 = sb("e32", [P, 2, 512])
        eh, el = sb("eh", [P, 2, HN], F16), sb("el", [P, 2, HN], F16)
        rden = sb("rden", [P, G])
        a = sb("a", [P, G, CD])
        aT = core.yT
        outT = sb("outT", [P, PR, B + 1, N])

        statted, aggred = Count(sem("statted"), KT), Count(sem("aggred"), KT)
        eps_added, rooted = Count(sem("eps_added"), KT), Count(sem("rooted"), KT)
        zeroed, scaled = Count(sem("zeroed"), KT), Count(sem("scaled"), KT)
        biased, c_hi, c_lo = Count(sem("biased"), KT), Count(sem("c_hi"), KT), Count(sem("c_lo"), KT)
        topped, shifted = Count(sem("topped"), 1), Count(sem("shifted"), 1)
        scored = Count(sem("scored"), 2 * KT)
        exped, e_split = Count(sem("exped"), 2 * KT, 2), Count(sem("e_split"), 2 * KT, 2)
        weighed = Count(sem("weighed"), KT, 2)
        rdenned, out_taken = Count(sem("rdenned"), 1), Count(sem("out_taken"), 1, 1)
        made = sem("made")

        for main in (False, True):
            name = "loop" if main else "first"
            with ExitStack() as pctx, nc.Block() as block:
                bank = lambda what, n=1: pctx.enter_context(nc.psum_tensor(f"l1x_{what}_{name}", [P, n * 512], F32))
                psT, psM, psS, psO = bank("psT"), bank("psM"), bank("psS", 2), bank("psO", 4)
                bT = Bank(sem(f"T_filled_{name}"), sem(f"T_taken_{name}"), t_names(main))
                bM = Bank(sem(f"M_filled_{name}"), sem(f"M_taken_{name}"), m_names(main))

                def turns(eng, body):
                    if not main:
                        body(None, 0, 0, 0)
                        return
                    with eng.Fori(0, B // 2) as i:
                        for s in range(2):
                            b = i * 2 + s
                            body(b, i * 2 + (s + 1), 1 - s, b)

                @block.sync
                def _(sp):
                    if not main:
                        sp.wait_ge(c_lo.sem, c_lo.at(0, SPLIT - 1))
                        load_context(sp, 1, 0)
                        sp.wait_ge(c_lo.sem, c_lo.at(0, KT - 1))
                        load_context(sp, 1, 1)
                        return
                    with sp.Fori(0, B - 1) as b:
                        sp.wait_ge(c_lo.sem, c_lo.at(b, KT + SPLIT - 1))
                        load_context(sp, b + 2, 0)
                        sp.wait_ge(c_lo.sem, c_lo.at(b, KT + KT - 1))
                        load_context(sp, b + 2, 1)

                @block.gpsimd
                def _(pool):
                    def root(m, j):
                        wait_apart(pool, aggred.sem, aggred.at(j, m), core.spare)
                        pool.tensor_scalar(rstd[:, m:m + 1], aggr[:, m, 1:2], EPS, None, ALU.add).then_inc(eps_added.sem, 1)
                        pool.wait_ge(eps_added.sem, eps_added.at(j, m))
                        pool.tensor_tensor(rstd[:, m:m + 1], rstd[:, m:m + 1], core.minus_half[:, 0:1], ALU.pow)\
                            .then_inc(rooted.sem, 1)

                    def add_beta(m, j):
                        pool.wait_ge(scaled.sem, scaled.at(j, m))
                        pool.tensor_tensor(raw[:, m, :], raw[:, m, :], bet[:, :], ALU.add).then_inc(biased.sem, 1)

                    def body(b, j, slot, turn):
                        for n in range(KT):
                            for m in tiles(n):
                                root(m, j)
                            for m in tiles(n - 1):
                                add_beta(m, j)
                    turns(pool, body)

                @block.tensor
                def _(pe):
                    def side(job, b, j, slot, turn):
                        kind = job[0]
                        if kind == "t":
                            m = int(job[1:])
                            pe.wait_ge(c_lo.sem, c_lo.at(j, m))
                            pe.wait_ge(bT.taken, bT.free(job, turn))
                            pe.matmul(psT[:, 0:P], ch[:, slot, m, 0:P], core.ident16[:, :], start=True, stop=True)
                            pe.matmul(psT[:, P:2 * P], cl[:, slot, m, 0:P], core.ident16[:, :], start=True, stop=True)
                            for rows, c in ((halves[0], ch), (halves[1], cl)):
                                ins = pe.matmul(psT[rows, 2 * P:3 * P], c[:, slot, m, P:CD], core.ident16[:, :],
                                                start=True, stop=True)
                            ins.then_inc(bT.filled, 1)
                        elif kind == "m":
                            m, c = [int(v) for v in job[1:].split(".")]
                            keys = P if m < KT - 1 else TAIL
                            pe.wait_ge(bT.taken, bT.left(f"t{m}", turn))
                            pe.wait_ge(bM.taken, bM.free(job, turn))
                            for g in range(4):
                                cols = slice((4 * c + g) * P, (4 * c + g + 1) * P)
                                for i, (q, x) in enumerate(((qAh, 0), (qSB, 2))):
                                    lhs = q[:, j, cols] if isinstance(j, int) else \
                                        q[:, bass.ds(j, 1), cols].rearrange("p a n -> p (a n)")
                                    ins = pe.matmul(psM[:, g * P:g * P + keys], lhs, ct[:, slot, m, x * P:x * P + keys],
                                                    start=(i == 0), stop=(i == 1))
                            ins.then_inc(bM.filled, 1)
                        elif kind in "AB":
                            half = int(job[1])
                            bank, ps, cols, rows = (bT, psT, slice(0, P), slice(0, P)) if kind == "A" else \
                                (bM, psM, slice(P, CD), slice(0, CB))
                            pe.wait_ge(out_taken.sem, out_taken.at(b, -1))
                            wait_apart(pe, bank.taken, bank.free(job, turn), core.spare)
                            for g in range(4):
                                ins = pe.transpose(ps[rows, g * P:(g + 1) * P], a[:, 4 * half + g, cols], core.ident[:, :])
                            ins.then_inc(bank.filled, 1)
                        elif kind == "V":
                            half = int(job[1])
                            pe.wait_ge(bT.taken, bT.free(job, turn))
                            pe.wait_ge(bM.taken, bM.left(f"B{half}", turn))
                            for k in range(8):
                                h = 8 * half + k
                                out = psT[halves[k % 2], k // 2 * N:(k // 2 + 1) * N]
                                pe.matmul(out, wvA[:, h * DH:(h + 1) * DH], aT[:, 0, k * N:(k + 1) * N], start=True, stop=False)
                                ins = pe.matmul(out, wvB[:, h * DH:(h + 1) * DH], aT[0:CB, 1, k * N:(k + 1) * N],
                                                start=False, stop=True)
                            ins.then_inc(bT.filled, 1)

                    def spread_shift(j, turn):
                        pe.wait_ge(shifted.sem, shifted.at(j, 0))
                        for c, (bank, ps) in enumerate(((bM, psM), (bT, psT))):
                            pe.wait_ge(bank.taken, bank.free(f"sh{c}", turn))
                            for g in range(4):
                                ins = pe.matmul(ps[0:DH + 1, g * P:(g + 1) * P], shift[:, 4 * c + g, :], core.ident16[:, :],
                                                start=True, stop=True)
                            ins.then_inc(bank.filled, 1)

                    def score(n, c, b, s):
                        u, keys = 2 * n + c, (P if n < KT - 1 else TAIL)
                        if n == 0 and c == 0:
                            pe.wait_ge(bM.taken, bM.left("sh0", b, 1))
                            pe.wait_ge(bT.taken, bT.left("sh1", b, 1))
                        pe.wait_ge(exped.sem, exped.at(b, u - 2))
                        passes = ((ct, 0, qAh, P), (ct, P, qAh, P), (ct, 0, qAl, P), (ct, 2 * P, qSB, P), (c5, 0, q5, DH + 1))
                        for i, (x, k, q, rows) in enumerate(passes):
                            ins = pe.matmul(psS[0:keys, c * 512:(c + 1) * 512], x[0:rows, s, n, k:k + keys],
                                            q[0:rows, bass.ds(b, 1), c * 512:(c + 1) * 512].rearrange("p a n -> p (a n)"),
                                            start=(i == 0), stop=(i == len(passes) - 1))
                        ins.then_inc(scored.sem, 1)

                    def weigh(n, c, b, s):
                        keys, e = (P if n < KT - 1 else TAIL), (s + n) % 2
                        pe.wait_ge(e_split.sem, e_split.at(b, 2 * n + c))
                        if n == 0 and c == 0:
                            pe.wait_ge(out_taken.sem, out_taken.at(b, -1))
                        for g in range(4 * c, 4 * c + 4):
                            cols, o = slice(g * P, (g + 1) * P), g // 2 * 512 + g % 2 * VW
                            first = n == 0 and g % 2 == 0
                            pe.matmul(psO[:, o:o + VW], eh[0:keys, e, cols], ch[0:keys, s, n, :],
                                      start=first, stop=False, skip_group_check=True)
                            pe.matmul(psO[:, o:o + CD], eh[0:keys, e, cols], cl[0:keys, s, n, :],
                                      start=False, stop=False, skip_group_check=True)
                            ins = pe.matmul(psO[:, o:o + VW], el[0:keys, e, cols], ch[0:keys, s, n, :],
                                            start=False, stop=(n == KT - 1), skip_group_check=True)
                        if c == 1:
                            ins.then_inc(weighed.sem, 1)

                    def body(b, j, slot, turn):
                        s = 1 - slot
                        for n in range(KT):
                            ms, ts = m_jobs(n, main), t_jobs(n, main)
                            work = []
                            if main:
                                work = [(score, n, 0), (score, n, 1)] + ([(weigh, n - 1, 0), (weigh, n - 1, 1)] if n else [])
                            for k in range(max(len(work), len(ms), len(ts))):
                                if k < len(ms):
                                    side(ms[k], b, j, slot, turn)
                                if k < len(work):
                                    what, tile, c = work[k]
                                    what(tile, c, b, s)
                                if k < len(ts):
                                    side(ts[k], b, j, slot, turn)
                        if main:
                            weigh(KT - 1, 0, b, s)
                        spread_shift(j, turn)
                        if main:
                            weigh(KT - 1, 1, b, s)

                    if not main:
                        pe.wait_ge(made, 1)
                    turns(pe, body)

                @block.scalar
                def _(act):
                    def exp(n, c, b, s):
                        u, keys, e = 2 * n + c, (P if n < KT - 1 else TAIL), (s + n) % 2
                        act.wait_ge(weighed.sem, weighed.at(b, n - 2))
                        act.wait_ge(e_split.sem, e_split.at(b, u - 2))
                        act.wait_ge(scored.sem, scored.at(b, u))
                        ps = psS[0:keys, c * 512:(c + 1) * 512]
                        act.activation(e32[0:keys, c, :], ps, ACT.Exp)
                        act.activation(eh[0:keys, e, c * 512:(c + 1) * 512], ps, ACT.Exp).then_inc(exped.sem, 1)

                    def take(job, b, j, slot, turn):
                        act.wait_ge(bT.filled, bT.full(job, turn))
                        if job[0] == "t":
                            m = int(job[1:])
                            act.activation(ct[:, slot, m, :], psT[:, 0:3 * P], ACT.Copy)
                            act.activation(c5[0:CB, slot, m, :], psT[0:CB, 2 * P:3 * P], ACT.Copy).then_inc(bT.taken, 1)
                        elif job[0] == "A":
                            act.activation(aT[:, 0, :], psT[:, :], ACT.Copy).then_inc(bT.taken, 1)

                    def body(b, j, slot, turn):
                        s = 1 - slot
                        if main:
                            act.wait_ge(weighed.sem, weighed.at(b, -1))
                        for n in range(KT):
                            ts = t_jobs(n, main)
                            for k in range(max(2, len(ts))):
                                if main and k < 2:
                                    exp(n, k, b, s)
                                if k < len(ts) and ts[k][0] != "V":
                                    take(ts[k], b, j, slot, turn)
                            for m in tiles(n - 1):
                                act.wait_ge(biased.sem, biased.at(j, m))
                                act.activation(ch[:, slot, m, 0:CD], raw[:, m, :], ACT.Copy).then_inc(c_hi.sem, 1)
                        for c, (bank, ps) in enumerate(((bM, psM), (bT, psT))):
                            wait_apart(act, bank.filled, bank.full(f"sh{c}", turn), core.spare)
                            out = q5[DH:DH + 1, j, :] if isinstance(j, int) else \
                                q5[DH:DH + 1, bass.ds(j, 1), :].rearrange("p a n -> p (a n)")
                            act.activation(out[:, c * 512:(c + 1) * 512], ps[DH:DH + 1, :], ACT.Copy)\
                                .then_inc(bank.taken, 1)
                    turns(act, body)

                @block.vector
                def _(dve):
                    def stage0(m, j):
                        dve.wait_ge(raw_loaded[m >= SPLIT], j * 16 + 16)
                        dve.bn_stats(stats[:, m, :], raw[:, m, :]).then_inc(statted.sem, 1)
                        wait_apart(dve, statted.sem, statted.at(j, m), core.spare)
                        dve.bn_aggr(aggr[:, m, :], stats[:, m, :]).then_inc(aggred.sem, 1)

                    def stage1(m, j):
                        dve.wait_ge(rooted.sem, rooted.at(j, m))
                        dve.tensor_scalar(raw[:, m, :], raw[:, m, :], aggr[:, m, 0:1], rstd[:, m:m + 1],
                                          ALU.subtract, ALU.mult).then_inc(zeroed.sem, 1)
                        dve.wait_ge(zeroed.sem, zeroed.at(j, m))
                        dve.tensor_tensor(raw[:, m, :], raw[:, m, :], gam[:, :], ALU.mult).then_inc(scaled.sem, 1)

                    def stage2(m, j, slot):
                        dve.wait_ge(c_hi.sem, c_hi.at(j, m))
                        dve.tensor_tensor(cl[:, slot, m, :], raw[:, m, :], ch[:, slot, m, 0:CD], ALU.subtract)\
                            .then_inc(c_lo.sem, 1)

                    def take(job, turn):
                        bank = bT if job[0] == "V" else bM
                        if job[0] == "B":
                            if job == "B1":
                                dve.wait_ge(bT.filled, bT.full("V0", turn))
                            dve.wait_ge(bM.filled, bM.full(job, turn))
                            dve.tensor_copy(aT[0:CB, 1, :], psM[0:CB, :]).then_inc(bM.taken, 1)
                        elif job[0] == "V":
                            half = int(job[1])
                            dve.wait_ge(bT.filled, bT.full(job, turn))
                            dve.tensor_scalar(
                                outT[:, 4 * half:4 * half + 4, bass.ds(turn, 1), :].rearrange("p k a q -> p k (a q)"),
                                psT[:, 0:4 * N].rearrange("p (k q) -> p k q", q=N), 1.0, None, ALU.mult)\
                                .then_inc(bT.taken, 1)
                        else:
                            m, c = [int(v) for v in job[1:].split(".")]
                            keys = P if m < KT - 1 else TAIL
                            dve.wait_ge(bM.filled, bM.full(job, turn))
                            dve.tensor_reduce(tops[:, 4 * c:4 * c + 4, m],
                                              psM[:, :].rearrange("p (g k) -> p g k", k=P)[:, :, 0:keys],
                                              AX.X, ALU.max).then_inc(bM.taken, 1)

                    def lo_half(n, c, b, s):
                        u, keys, e = 2 * n + c, (P if n < KT - 1 else TAIL), (s + n) % 2
                        dve.wait_ge(exped.sem, exped.at(b, u))
                        dve.tensor_tensor(el[0:keys, e, c * 512:(c + 1) * 512], e32[0:keys, c, :],
                                          eh[0:keys, e, c * 512:(c + 1) * 512], ALU.subtract).then_inc(e_split.sem, 1)

                    def body(b, j, slot, turn):
                        s = 1 - slot
                        for n in range(KT):
                            ms, ts = m_jobs(n, main), t_jobs(n, main)
                            for job in ms[0:2]:
                                take(job, turn)
                            for m in tiles(n):
                                stage0(m, j)
                            if main:
                                lo_half(n, 0, b, s)
                            for m in tiles(n - 1):
                                stage1(m, j)
                            for job in ms[2:]:
                                take(job, turn)
                            if main:
                                lo_half(n, 1, b, s)
                            for job in ts:
                                if job[0] == "V":
                                    take(job, turn)
                            for m in tiles(n - 1):
                                stage2(m, j, slot)
                        dve.wait_ge(bM.taken, bM.free("sh0", turn))
                        dve.tensor_reduce(top[:, :], tops[:, :, :], AX.X, ALU.max).then_inc(topped.sem, 1)
                        dve.wait_ge(topped.sem, topped.at(j, 0))
                        dve.tensor_scalar(shift[:, :, DH], top[:, :], -1.0, None, ALU.mult).then_inc(shifted.sem, 1)
                        if main:
                            dve.wait_ge(weighed.sem, weighed.at(b, KT - 1))
                            dve.wait_ge(bT.filled, bT.full("V1", turn))
                            sums = psO[:, :].rearrange("p (k n) -> p k n", n=512)[:, :, 0:2 * VW]\
                                .rearrange("p k (g w) -> p k g w", w=VW)
                            dve.reciprocal(rden[:, :].rearrange("p (k g) -> p k g", g=2), sums[:, :, :, CD])\
                               .then_inc(rdenned.sem, 1)
                            dve.wait_ge(rdenned.sem, rdenned.at(b, 0))
                            dve.tensor_tensor(
                                a[:, :, :].rearrange("p (k g) w -> p k g w", g=2), sums[:, :, :, 0:CD],
                                rden[:, :].rearrange("p (k g) -> p k g", g=2)[:, :, :, None].to_broadcast([P, 4, 2, CD]),
                                ALU.mult).then_inc(out_taken.sem, 1)

                    if main:
                        dve.sem_inc(exped.sem, exped.primed)
                        dve.sem_inc(e_split.sem, e_split.primed)
                        dve.sem_inc(weighed.sem, weighed.primed)
                        dve.sem_inc(out_taken.sem, out_taken.primed)
                    else:
                        dve.wait_ge(w_loaded, 64)
                        dve.memset(a[:, :, :], 0.0)
                        dve.memset(shift[:, :, :], 0.0)
                        dve.memset(c5[DH:DH + 1, :, :, :], 1.0)
                        dve.memset(ch[:, :, :, CD:VW], 1.0).then_inc(made, 1)
                    dve.sem_inc(bT.taken, 1)
                    dve.sem_inc(bM.taken, 1)
                    turns(dve, body)

        wo = sb("wo", [P, PR, D])
        wo_loaded, filled, taken = sem("wo_loaded"), sem("end_filled"), sem("end_taken")
        with ExitStack() as pctx, nc.Block() as block:
            bank = lambda what, n=1: pctx.enter_context(nc.psum_tensor(f"l1x_{what}_end", [P, n, 512], F32))
            psA, psB, psV, psX = bank("psA"), bank("psB"), bank("psV"), bank("psX", 2)
            proj = psX[:, :, :].rearrange("p a (t n) -> p (a t) n", n=D)

            @block.sync
            def _(sp):
                sp.dma_start(wo[:, :, :], d["L1_xattn_Wo"].rearrange("(c p) n -> p c n", p=P)).then_inc(wo_loaded, 16)

            @block.tensor
            def _(pe):
                for half in range(2):
                    if half:
                        pe.wait_ge(taken, 3 * half)
                    for ps, cols, rows in ((psA, slice(0, P), slice(0, P)), (psB, slice(P, CD), slice(0, CB))):
                        for g in range(4):
                            ins = pe.transpose(ps[rows, 0, g * P:(g + 1) * P], a[:, 4 * half + g, cols], core.ident[:, :])
                        ins.then_inc(filled, 1)
                    pe.wait_ge(taken, 3 * half + 2)
                    for k in range(8):
                        h = 8 * half + k
                        out = psV[halves[k % 2], 0, k // 2 * N:(k // 2 + 1) * N]
                        pe.matmul(out, wvA[:, h * DH:(h + 1) * DH], aT[:, 0, k * N:(k + 1) * N], start=True, stop=False)
                        ins = pe.matmul(out, wvB[:, h * DH:(h + 1) * DH], aT[0:CB, 1, k * N:(k + 1) * N],
                                        start=False, stop=True)
                    ins.then_inc(filled, 1)
                pe.wait_ge(taken, 6)
                pe.wait_ge(wo_loaded, 16)
                for t in range(TT):
                    for pr in range(PR):
                        ins = pe.matmul(proj[:, t, :], outT[:, pr, 1 + 2 * t:3 + 2 * t, :].rearrange("p b q -> p (b q)"),
                                        wo[:, pr, :], start=(pr == 0), stop=(pr == PR - 1))
                ins.then_inc(filled, 1)

            @block.vector
            def _(dve):
                for half in range(2):
                    dve.wait_ge(filled, 3 * half + 1)
                    dve.tensor_copy(aT[:, 0, :], psA[:, 0, :]).then_inc(taken, 1)
                    dve.wait_ge(filled, 3 * half + 2)
                    dve.tensor_copy(aT[0:CB, 1, :], psB[0:CB, 0, :]).then_inc(taken, 1)
                    dve.wait_ge(filled, 3 * half + 3)
                    dve.tensor_copy(outT[:, 4 * half:4 * half + 4, B, :],
                                    psV[:, 0, 0:4 * N].rearrange("p (k q) -> p k q", q=N)).then_inc(taken, 1)
                dve.wait_ge(filled, 7)
                dve.tensor_tensor(core.x[:, :, :], core.x[:, :, :], proj[:, :, :], ALU.add).then_inc(taken, 1)
                dve.wait_ge(taken, 7)


def norm(core, tag, inner=None):
    return lambda prefetch: stage_norm(core, tag, inner, prefetch)


STAGES = [
    lambda core: stage_l0_cross(core, norm(core, "n0")),
    lambda core: stage_l0_self(core, norm(core, "n1", ("L0_attn_gamma", None, False))),
    lambda core: stage_experts(core, norm(core, "n2", ("L0_ffn_ln_w", "L0_ffn_ln_b", True)),
                               "l0f", "L0_ffn_router_w", "c_l0_experts", E + 1, 4, True, 1),
    lambda core: stage_l1_cross(core, norm(core, "n3", ("L1_xattn_g_x", "L1_xattn_b_x", False))),
    lambda core: stage_l1_self(core, norm(core, "n4")),
    lambda core: stage_experts(core, norm(core, "n5"), "l1f", "c_l1_router", "c_l1_experts", E, 8, False, 2),
]


def perceiver_program(nc, dram, stages=STAGES):
    with ExitStack() as ctx:
        core = Core(nc, ctx, dram)
        stage_load(core)
        for stage in stages:
            stage(core)
            core.clear_sems()
        stage_store(core)


def _constants():
    import numpy as np
    c = {}
    c["c_ident"] = np.eye(P, dtype=np.float32)
    c["c_headmask"] = (np.arange(P)[:, None] // 16 == np.arange(8)[None, :]).astype(np.float32)
    slope = 2.0 ** (-2.0 ** (-(np.log2(H) - 3.0)))
    slopes = np.array([slope * slope ** h for h in range(H)], np.float32)
    rows, cols = np.arange(N)[:, None], np.arange(N + 2)[None, :]
    alibi = -np.abs(cols - (rows + 2)).astype(np.float32)[:, None, :] * slopes[None, :, None]
    alibi = np.where((cols > rows + 2)[:, None, :], np.float32(-BIG), alibi).astype(np.float32)
    places = np.concatenate([np.arange(0, H, 2), np.arange(1, H, 2)])
    c["c_alibi"] = np.concatenate([alibi, alibi], axis=0)[:, places, :]
    c["c_blockmask"] = (np.arange(2 * H)[:, None] // 2 == np.arange(H)[None, :]).astype(np.float32)
    c["c_memrows"] = (np.arange(P)[:, None] % 32 == np.arange(4)[None, :]).astype(np.float32)
    c["c_iota"] = np.tile(np.arange(E, dtype=np.float32), (P, 1))
    q = np.arange(P // 8)[None, :, None] % 8 * 8 + (np.arange(P) // H)[:, None, None]
    key = np.arange(N + 4)[None, None, :] - 4
    c["c_rowmask"] = np.where(key > q, np.float32(BIG), np.float32(0)).reshape(P, 4, -1)
    return c


def _layouts(inputs):
    import numpy as np
    a = {k: np.ascontiguousarray(v) for k, v in inputs.items()}
    ctx = a.pop("ctx_768")
    t = np.zeros((B + 1, CD, MP), np.float32)
    t[:B, :, :M] = ctx.transpose(0, 2, 1)
    a["c_ctxT"] = t
    rows = np.zeros((B + 1, MP, CD), np.float32)
    rows[:B, :M] = ctx
    a["c_ctx"] = rows
    wkT = a.pop("L1_xattn_Wk").T
    a["c_wkT"] = np.concatenate([wkT, wkT[:, P:]], axis=1)
    null = a.pop("L0_attn_null_kv").reshape(H, 2, 2, 64)
    a["c_null_k"] = np.ascontiguousarray(null[:, :, 0]).reshape(2 * H, 64)
    nv = np.zeros((H, 2, H, 64), np.float32)
    for h in range(H):
        nv[h % 2 * (H // 2) + h // 2, :, h] = null[h, :, 1]
    a["c_null_v"] = nv.reshape(2 * H, H * 64)
    def first(w):
        e, _, f = w.shape
        return w.reshape(e, DC, P, f // P, P).transpose(0, 3, 2, 1, 4).reshape(e, f // P, P, DC * P)

    def last(w):
        e, f, _ = w.shape
        return w.reshape(e, f // P, P, D)

    with_shared = lambda many, one: np.concatenate([a.pop(many), a.pop(one)[None]])
    a["c_l0_experts"] = np.concatenate([first(with_shared("L0_ffn_gate_w", "L0_ffn_sh_gate")),
                                        first(with_shared("L0_ffn_up_w", "L0_ffn_sh_up")),
                                        last(with_shared("L0_ffn_down_w", "L0_ffn_sh_down"))], axis=-1)
    a["c_l1_experts"] = np.concatenate([first(a.pop("L1_ffn_w1").transpose(0, 2, 1)),
                                        last(a.pop("L1_ffn_w2").transpose(0, 2, 1))], axis=-1)
    for name in ("c_l0_experts", "c_l1_experts"):
        a[name] = np.concatenate([a[name], np.zeros_like(a[name][:1])])
    a["c_l1_router"] = np.ascontiguousarray(a.pop("L1_ffn_gate_w").T)
    def on_diagonal(w, row_of):
        out = np.zeros((8, H, 8, H), np.float32)
        for i in range(8):
            for g in range(H):
                out[i, row_of(g), i, :] = w[:, g]
        return out.reshape(P, P)

    a["c_pre"] = on_diagonal(a.pop("L1_attn_W_pre_th"), lambda g: g % 2 * (H // 2) + g // 2)
    a["c_post"] = on_diagonal(a.pop("L1_attn_W_post_th"), lambda g: g)
    mem_v = np.zeros((4, 32, H, 64), np.float32)
    mem_v[:, :4] = a.pop("L1_attn_mem_v").transpose(1, 0, 2)
    a["c_mem_v"] = mem_v.reshape(P, H, 64)
    a["c_head_scale"] = a.pop("L1_attn_head_scale_params").reshape(H)
    return a


def kernel(**inputs):
    import numpy as _np
    import concourse.bacc as _bacc
    from concourse.bass_utils import run_bass_kernel_spmd as _run

    nc = _bacc.Bacc("TRN2", target_bir_lowering=False, num_devices=1)
    arrays = {**_layouts(inputs), **_constants()}
    dram = {k: nc.dram_tensor(f"in_{k}", a.shape, mybir.dt.from_np(a.dtype), kind="ExternalInput").ap()
            for k, a in arrays.items()}
    dram["out"] = nc.dram_tensor("out_x", (B, N, D), F32, kind="ExternalOutput").ap()
    perceiver_program(nc, dram)
    r = _run(nc, [{f"in_{k}": a for k, a in arrays.items()}], core_ids=[0])
    return r.results[0]["out_x"]
```

```python
from contextlib import ExitStack

import concourse.bass as bass
from concourse import mybir

F32 = mybir.dt.float32
F16 = mybir.dt.float16
U32 = mybir.dt.uint32
ALU = mybir.AluOpType
ACT = mybir.ActivationFunctionType
AX = mybir.AxisListType

P = 128
B, N, D = 8, 64, 256
TOK = B * N
TT = TOK // P
DC = D // P
M, CD = 1601, 192
KT = -(-M // P)
MP = KT * P
TAIL = M - (KT - 1) * P
CB = CD - P
H = 16
E = 8
EPS = 1e-5
BIG = 1e30


class Steps:

    def __init__(self, sem, names):
        self.sem, self.names, self.said = sem, names.split(), 0

    def done(self, name):
        assert self.names[self.said % len(self.names)] == name, (name, self.names[self.said % len(self.names)])
        self.said += 1
        return self.sem

    def at(self, name, turn=0):
        return turn * len(self.names) + self.names.index(name) + 1


class Count:

    def __init__(self, sem, each, primed=0):
        self.sem, self.each, self.primed = sem, each, primed

    def at(self, turn, k):
        return turn * self.each + (k + 1 + self.primed)


def wait_apart(eng, sem, value, spare):
    eng.wait_ge(sem, value)
    eng.sem_inc(spare, 1)


def norm_steps(tag):
    return f"{tag}_stats {tag}_aggr {tag}"


def layer_norm(dve, steps, roots, tag, dst, src, work):
    stats, aggr, rstd = work
    for t in range(TT):
        ins = dve.bn_stats(stats[:, t, :], src[:, t, :])
    ins.then_inc(steps.done(f"{tag}_stats"), 1)
    dve.wait_ge(steps.sem, steps.at(f"{tag}_stats"))
    for t in range(TT):
        ins = dve.bn_aggr(aggr[:, t, :], stats[:, t, :])
    ins.then_inc(steps.done(f"{tag}_aggr"), 1)
    dve.wait_ge(roots.sem, roots.at(tag))
    for t in range(TT):
        ins = dve.tensor_scalar(dst[:, t, :], src[:, t, :], aggr[:, t, 0:1], rstd[:, t:t + 1],
                                ALU.subtract, ALU.mult)
    ins.then_inc(steps.done(tag), 1)
    dve.wait_ge(steps.sem, steps.at(tag))


def layer_norm_root(pool, steps, roots, tag, work, minus_half):
    stats, aggr, rstd = work
    pool.wait_ge(steps.sem, steps.at(f"{tag}_aggr"))
    pool.tensor_scalar(rstd[:, :], aggr[:, :, 1], EPS, None, ALU.add).then_inc(roots.done(f"{tag}_var"), 1)
    pool.wait_ge(roots.sem, roots.at(f"{tag}_var"))
    pool.tensor_tensor(rstd[:, :], rstd[:, :], minus_half, ALU.pow).then_inc(roots.done(tag), 1)


class Core:

    def __init__(self, nc, ctx, dram):
        self.nc, self.dram = nc, dram
        sb = lambda name, shape, dt=F32: ctx.enter_context(nc.sbuf_tensor(name, shape, dt))
        self.sems = []
        self.spare = nc.alloc_semaphore(name="spare")
        self.x = sb("x", [P, TT, D])
        self.y = sb("y", [P, TT, D])
        self.yT = sb("yT", [P, DC, TOK])
        self.ident = sb("ident", [P, P])
        self.ident16 = sb("ident16", [P, P], F16)
        self.ones = sb("ones", [P, P])
        self.minus_half = sb("minus_half", [P, 64])
        self.norm_work = (sb("ln_stats", [P, TT, 6]), sb("ln_aggr", [P, TT, 2]), sb("ln_rstd", [P, TT]))


    def sem(self, name):
        self.sems.append(self.nc.alloc_semaphore(name=name))
        return self.sems[-1]

    def clear_sems(self):
        self.nc.clear_and_free_semaphores(self.sems)
        self.nc.all_engine_barrier()
        self.sems = []


def stage_load(core):
    nc, d = core.nc, core.dram
    loaded, made = core.sem("load_loaded"), core.sem("load_made")
    with nc.Block() as block:
        @block.sync
        def _(sp):
            sp.dma_start(core.x[:, :, :], d["x"].rearrange("(a b) n d -> (b n) a d", b=2)).then_inc(loaded, 16)
            sp.dma_start(core.ident[:, :], d["c_ident"]).then_inc(loaded, 16)
            sp.wait_ge(loaded, 32)

        @block.vector
        def _(dve):
            dve.memset(core.ones[:, :], 1.0)
            dve.memset(core.minus_half[:, :], -0.5)
            dve.wait_ge(loaded, 32)
            dve.tensor_copy(core.ident16[:, :], core.ident[:, :]).then_inc(made, 1)


def stage_store(core):
    nc, d = core.nc, core.dram
    stored = core.sem("stored")
    with nc.Block() as block:
        @block.sync
        def _(sp):
            sp.dma_start(d["out"].rearrange("(a b) n d -> (b n) a d", b=2), core.x[:, :, :]).then_inc(stored, 16)
            sp.wait_ge(stored, 16)


def stage_norm(core, tag, inner, prefetch):
    nc, d = core.nc, core.dram
    gamma, beta, keep = inner or (None, None, False)
    with ExitStack() as ctx:
        sb = lambda name, shape, dt=F32: ctx.enter_context(nc.sbuf_tensor(f"{tag}_{name}", shape, dt))
        g, b = sb("gamma", [P, DC]), sb("beta", [P, DC])
        psT = ctx.enter_context(nc.psum_tensor(f"{tag}_psT", [P, DC, TOK], F32))
        loaded = core.sem(f"{tag}_loaded")
        n_loads = DC * sum(v is not None for v in (gamma, beta))
        names = norm_steps("outer")
        if inner:
            names += " " + ("kept " if keep else "") + norm_steps("inner")
        vec = Steps(core.sem(f"{tag}_vector"), names)
        pe_s = Steps(core.sem(f"{tag}_tensor"), "transposed0 transposed1")
        roots = Steps(core.sem(f"{tag}_roots"), "outer_var outer" + (" inner_var inner" if inner else ""))
        last = vec.names[-1]
        done = core.sem(f"{tag}_evacuated")
        with nc.Block() as block:
            @block.sync
            def _(sp):
                for name, columns in ((gamma, g), (beta, b)):
                    for c in range(DC if name else 0):
                        sp.dma_start(columns[:, c:c + 1], d[name].rearrange("(c p o) -> c p o", p=P, o=1)[c])\
                            .then_inc(loaded, 16)
                prefetch(sp)

            @block.gpsimd
            def _(pool):
                for which in roots.names[1::2]:
                    layer_norm_root(pool, vec, roots, which, core.norm_work, core.minus_half[:, 0:TT])

            @block.vector
            def _(dve):
                layer_norm(dve, vec, roots, "outer", core.y, core.x, core.norm_work)
                if inner:
                    if keep:
                        dve.tensor_tensor(core.x[:, :, :], core.x[:, :, :], core.y[:, :, :], ALU.add)\
                           .then_inc(vec.done("kept"), 1)
                        dve.wait_ge(vec.sem, vec.at("kept"))
                    layer_norm(dve, vec, roots, "inner", core.y, core.y, core.norm_work)
                    dve.wait_ge(loaded, 16 * n_loads)
                    for c in range(DC):
                        dve.wait_ge(pe_s.sem, pe_s.at(f"transposed{c}"))
                        more = (b[:, c:c + 1], ALU.mult, ALU.add) if beta else (None, ALU.mult)
                        dve.tensor_scalar(core.yT[:, c, :], psT[:, c, :], g[:, c:c + 1], *more).then_inc(done, 1)
                else:
                    dve.wait_ge(pe_s.sem, pe_s.at("transposed0"))
                    dve.tensor_copy(core.yT[:, 0, :], psT[:, 0, :]).then_inc(done, 1)

            @block.scalar
            def _(act):
                if not inner:
                    act.wait_ge(pe_s.sem, pe_s.at("transposed1"))
                    act.activation(core.yT[:, 1, :], psT[:, 1, :], ACT.Copy).then_inc(done, 1)

            @block.tensor
            def _(pe):
                pe.wait_ge(vec.sem, vec.at(last))
                for c in range(DC):
                    for t in range(TT):
                        ins = pe.transpose(psT[:, c, t * P:(t + 1) * P], core.y[:, t, c * P:(c + 1) * P],
                                           core.ident[:, :])
                    ins.then_inc(pe_s.done(f"transposed{c}"), 1)


def stage_l0_cross(core, norm):
    nc, d = core.nc, core.dram
    HD = D // H
    HC = H // DC
    PR = H // 2
    VW = 4 * HD + 1
    with ExitStack() as ctx:
        sb = lambda name, shape, dt=F32: ctx.enter_context(nc.sbuf_tensor(f"l0x_{name}", shape, dt))
        pb = lambda name, shape, dt=F32: ctx.enter_context(nc.psum_tensor(f"l0x_{name}", shape, dt))
        sem = lambda name: core.sem(f"l0x_{name}")

        wq, wo = sb("wq", [P, DC, D]), sb("wo", [P, 2, D])
        wA, wB = sb("wA", [P, 2 * D]), sb("wB", [P, 2 * D])
        bias = sb("bias", [97, 2 * D])
        rows = sb("rows", [1, 2, D])
        wAh, wAl, wBh = sb("wAh", [P, 2 * D], F16), sb("wAl", [P, 2 * D], F16), sb("wBh", [P, 2 * D], F16)
        biash = sb("biash", [97, 2 * D], F16)
        w5 = sb("w5", [P, 2 * D], F16)
        gam, bet = sb("gam", [P, D]), sb("bet", [P, D])
        headmask = sb("headmask", [P, HC])
        qp = sb("qp", [P, TT, D])
        sq = sb("sq", [P, TT, D])
        qn = sb("qn", [P, TT, D])
        qss = sb("qss", [P, TT])
        qT = sb("qT", [P, DC, TOK])
        qTh, qTl = sb("qTh", [P, DC, TOK], F16), sb("qTl", [P, DC, TOK], F16)
        qbh, qbl = sb("qbh", [P, DC, B, HC, N], F16), sb("qbl", [P, DC, B, HC, N], F16)
        cA, cB = sb("cA", [P, MP]), sb("cB", [P, MP])
        cAh, cAl, cS = sb("cAh", [P, MP], F16), sb("cAl", [P, MP], F16), sb("cS", [P, MP], F16)
        c5 = sb("c5", [P, MP], F16)
        kh, kl = sb("kh", [P, 2, D], F16), sb("kl", [P, 2, D], F16)
        ksq = sb("ksq", [P, 2, D])
        kss, rn = sb("kss", [P, 2]), sb("rn", [P, 2])
        v = sb("v", [P, 2, PR, VW], F16)
        e32 = sb("e32", [P, 2, DC, 512])
        eh, el = sb("eh", [P, 2, DC, 512], F16), sb("el", [P, 2, DC, 512], F16)
        o = sb("o", [P, B, PR, VW])
        rd = sb("rd", [P, B, PR])
        att = sb("att", [P, B, PR, HD])
        attT = sb("attT", [P, 2, TOK])

        loaded, consts = sem("loaded"), sem("consts")
        CHUNKS = [(0, 3), (3, 6), (6, 9), (9, KT)]
        SPLIT_AT = [2, 5, 8, 11]
        NC = len(CHUNKS)

        vec = Steps(sem("setup_vector"), "w_hi w_lo bias_hi w5 squares sums guarded qn qT_hi qT_lo queries")
        roots = Steps(sem("setup_roots"), "rnorm")
        pe_s = Steps(sem("setup_tensor"), "qp qT")
        act_s = Steps(sem("setup_scalar"), "qp qT")
        N_LOADS = 16 * (3 + 8 + 3 + 1)
        ctx_loaded = sem("ctx_loaded")

        def load_context(sp, src):
            sp.dma_start(cA[:, :], src[0:P, :]).then_inc(ctx_loaded, 16)
            sp.dma_start(cB[0:CB, :], src[P:CD, :]).then_inc(ctx_loaded, 16)
            sp.dma_start(cB[CB:P, :], src[P:CD, :]).then_inc(ctx_loaded, 16)

        def prefetch(sp):
            sp.dma_start(wq[:, :, :], d["L0_xattn_Wq"].rearrange("(c p) n -> p c n", p=P)).then_inc(loaded, 16)
            sp.dma_start(rows[0:1, 0, :], d["L0_xattn_bq"].partition_broadcast(1)).then_inc(loaded, 16)
            sp.dma_start(rows[0:1, 1, :], d["L0_xattn_bo"].partition_broadcast(1)).then_inc(loaded, 16)
            for j, (w, b) in enumerate((("L0_xattn_Wk", "L0_xattn_bk"), ("L0_xattn_Wv", "L0_xattn_bv"))):
                cols = slice(j * D, (j + 1) * D)
                sp.dma_start(wA[:, cols], d[w][0:P, :]).then_inc(loaded, 16)
                sp.dma_start(wB[0:CB, cols], d[w][P:CD, :]).then_inc(loaded, 16)
                sp.dma_start(wB[CB:P, cols], d[w][P:CD, :]).then_inc(loaded, 16)
                sp.dma_start(bias[64:97, cols], d[b].partition_broadcast(33)).then_inc(loaded, 16)
            sp.dma_start(gam[:, :], d["L0_xattn_ln_gamma"].partition_broadcast(P)).then_inc(loaded, 16)
            sp.dma_start(bet[:, :], d["L0_xattn_ln_beta"].partition_broadcast(P)).then_inc(loaded, 16)
            sp.dma_start(headmask[:, :], d["c_headmask"]).then_inc(loaded, 16)
            sp.dma_start(wo[:, :, :], d["c_l0x_wo"]).then_inc(loaded, 16)
            load_context(sp, d["c_ctxT"][0, :, :])

        norm(prefetch)

        ctx_hi = Count(sem("ctx_hi"), 2 * NC)
        ctx_loA, ctx_loB = Count(sem("ctx_loA"), 2 * NC), Count(sem("ctx_loB"), 2 * NC)

        def split_hiA(act, k):
            cols = slice(CHUNKS[k][0] * P, CHUNKS[k][1] * P)
            act.activation(cAh[:, cols], cA[:, cols], ACT.Copy)

        def split_hiB(act, k):
            cols = slice(CHUNKS[k][0] * P, CHUNKS[k][1] * P)
            act.activation(c5[0:CB, cols], cB[0:CB, cols], ACT.Copy)
            act.activation(cS[:, cols], cB[:, cols], ACT.Copy).then_inc(ctx_hi.sem, 1)

        def split_loA(pool, k, i, batch):
            cols = slice(CHUNKS[k][0] * P, CHUNKS[k][1] * P)
            pool.wait_ge(ctx_hi.sem, ctx_hi.at(i, NC * batch + k))
            pool.tensor_tensor(cAl[:, cols], cA[:, cols], cAh[:, cols], ALU.subtract).then_inc(ctx_loA.sem, 1)

        def split_loB(dve, k, i, batch):
            cols = slice(CHUNKS[k][0] * P, CHUNKS[k][1] * P)
            dve.wait_ge(ctx_hi.sem, ctx_hi.at(i, NC * batch + k))
            dve.tensor_tensor(cS[CB:P, cols], cB[CB:P, cols], cS[CB:P, cols], ALU.subtract).then_inc(ctx_loB.sem, 1)
        with ExitStack() as pctx, nc.Block() as block:
            psQ = pctx.enter_context(nc.psum_tensor("l0x_psQ", [P, TT, D], F32))
            psT = pctx.enter_context(nc.psum_tensor("l0x_psT", [P, DC, TOK], F32))

            @block.gpsimd
            def _(pool):
                for k in range(NC):
                    split_loA(pool, k, 0, 0)
                pool.wait_ge(vec.sem, vec.at("guarded"))
                pool.tensor_tensor(qss[:, :], qss[:, :], core.minus_half[:, 0:TT], ALU.pow).then_inc(roots.done("rnorm"), 1)

            @block.tensor
            def _(pe):
                pe.wait_ge(loaded, N_LOADS)
                for t in range(TT):
                    for c in range(DC):
                        pe.matmul(psQ[:, t, :], core.yT[:, c, t * P:(t + 1) * P], wq[:, c, :], start=(c == 0), stop=False)
                    ins = pe.matmul(psQ[:, t, :], core.ones[0:1, :], rows[0:1, 0, :], start=False, stop=True)
                ins.then_inc(pe_s.done("qp"), 1)
                pe.wait_ge(vec.sem, vec.at("qn"))
                for c in range(DC):
                    for t in range(TT):
                        ins = pe.transpose(psT[:, c, t * P:(t + 1) * P], qn[:, t, c * P:(c + 1) * P], core.ident[:, :])
                ins.then_inc(pe_s.done("qT"), 1)

            @block.scalar
            def _(act):
                act.wait_ge(ctx_loaded, 48)
                for k in range(NC):
                    split_hiA(act, k)
                    split_hiB(act, k)
                act.wait_ge(pe_s.sem, pe_s.at("qp"))
                act.activation(qp[:, :, :], psQ[:, :, :], ACT.Copy).then_inc(act_s.done("qp"), 1)
                act.wait_ge(pe_s.sem, pe_s.at("qT"))
                act.activation(qT[:, :, :], psT[:, :, :], ACT.Copy).then_inc(act_s.done("qT"), 1)

            @block.vector
            def _(dve):
                dve.memset(w5[CB:P, :], 0.0).then_inc(consts, 1)
                dve.memset(c5[CB:P, :], 1.0)
                for s in range(2):
                    dve.memset(v[:, s, :, VW - 1:VW], 1.0)
                dve.wait_ge(loaded, N_LOADS)
                dve.tensor_copy(wAh[:, :], wA[:, :])
                dve.tensor_copy(wBh[:, :], wB[:, :])
                dve.tensor_copy(biash[64:97, :], bias[64:97, :]).then_inc(vec.done("w_hi"), 1)
                dve.wait_ge(vec.sem, vec.at("w_hi"))
                dve.tensor_tensor(wAl[:, :], wA[:, :], wAh[:, :], ALU.subtract).then_inc(vec.done("w_lo"), 1)
                dve.wait_ge(consts, 1)
                dve.tensor_copy(w5[64:65, :], biash[64:65, :]).then_inc(vec.done("bias_hi"), 1)
                dve.tensor_tensor(w5[0:CB, :], wB[0:CB, :], wBh[0:CB, :], ALU.subtract)
                dve.tensor_tensor(w5[96:97, :], bias[96:97, :], biash[96:97, :], ALU.subtract).then_inc(vec.done("w5"), 1)
                for k in range(NC):
                    split_loB(dve, k, 0, 0)
                dve.wait_ge(act_s.sem, act_s.at("qp"))
                dve.tensor_tensor(sq[:, :, :], qp[:, :, :], qp[:, :, :], ALU.mult).then_inc(vec.done("squares"), 1)
                dve.wait_ge(vec.sem, vec.at("squares"))
                dve.tensor_reduce(qss[:, :], sq[:, :, :], AX.X, ALU.add).then_inc(vec.done("sums"), 1)
                dve.wait_ge(vec.sem, vec.at("sums"))
                dve.tensor_scalar(qss[:, :], qss[:, :], 1e-24, None, ALU.max).then_inc(vec.done("guarded"), 1)
                dve.wait_ge(roots.sem, roots.at("rnorm"))
                for t in range(TT):
                    ins = dve.tensor_scalar(qn[:, t, :], qp[:, t, :], qss[:, t:t + 1], float(HD) ** -0.5, ALU.mult, ALU.mult)
                ins.then_inc(vec.done("qn"), 1)
                dve.wait_ge(act_s.sem, act_s.at("qT"))
                dve.tensor_copy(qTh[:, :, :], qT[:, :, :]).then_inc(vec.done("qT_hi"), 1)
                dve.wait_ge(vec.sem, vec.at("qT_hi"))
                dve.tensor_tensor(qTl[:, :, :], qT[:, :, :], qTh[:, :, :], ALU.subtract).then_inc(vec.done("qT_lo"), 1)
                dve.wait_ge(vec.sem, vec.at("qT_lo"))
                for q, blocks in ((qTh, qbh), (qTl, qbl)):
                    for c in range(DC):
                        for h in range(HC):
                            ins = dve.tensor_scalar(blocks[:, c, :, h, :], q[:, c, :].rearrange("p (b n) -> p b n", n=N),
                                                    headmask[:, h:h + 1], None, ALU.mult)
                ins.then_inc(vec.done("queries"), 1)

        TILES = 2 * KT
        count = lambda name, each=TILES, primed=0: Count(sem(name), each, primed)
        projected, squares, norms = count("projected"), count("squares"), count("norms", primed=2)
        key_sums, rnorms = count("key_sums", primed=2), count("rnorms", primed=2)
        k_hi, k_lo, v_hi, v_lo = count("k_hi"), count("k_lo"), count("v_hi"), count("v_lo", primed=2)
        scored, exped = count("scored", 2 * TILES, 4), count("exped", 2 * TILES, 4)
        e_hi, e_split = count("e_hi", 2 * TILES), count("e_split", 2 * TILES, 4)
        weighed, out_taken = count("weighed", primed=2), count("out_taken", 2, 1)
        with ExitStack() as pctx, nc.Block() as block:
            psP = pctx.enter_context(nc.psum_tensor("l0x_psP", [P, 2, 2 * D], F32))
            psS = pctx.enter_context(nc.psum_tensor("l0x_psS", [P, 2, 512], F32))
            psO = pctx.enter_context(nc.psum_tensor("l0x_psO", [P, 2, 512], F32))
            psN = pctx.enter_context(nc.psum_tensor("l0x_psN", [P, 512], F32))

            def splits_at(g):
                return [(k, g // KT + 1) for k in range(NC) if SPLIT_AT[k] == g % KT]

            @block.sync
            def _(sp):
                with sp.Fori(0, B) as b:
                    sp.wait_ge(ctx_loA.sem, NC * b + NC)
                    sp.wait_ge(ctx_loB.sem, NC * b + NC)
                    load_context(sp, d["c_ctxT"][bass.ds(b + 1, 1), :, :].rearrange("a k m -> (a k) m"))

            @block.gpsimd
            def _(pool):
                def root(g, i):
                    pool.wait_ge(key_sums.sem, key_sums.at(i, g))
                    pool.wait_ge(exped.sem, exped.at(i, 2 * (g - 2) + 1))
                    pool.tensor_tensor(rn[:, g % 2:g % 2 + 1], kss[:, g % 2:g % 2 + 1], core.minus_half[:, 0:1], ALU.pow)\
                        .then_inc(rnorms.sem, 1)

                root(0, 0)
                with pool.Fori(0, B // 2) as i:
                    for g in range(TILES):
                        root(g + 1, i)
                        for k, batch in splits_at(g - 1):
                            split_loA(pool, k, i, batch)

            @block.tensor
            def _(pe):
                def project(g, i):
                    n = g % KT
                    for k, (first, _) in enumerate(CHUNKS):
                        if n == first:
                            pe.wait_ge(ctx_loA.sem, ctx_loA.at(i, NC * (g // KT) + k))
                            pe.wait_ge(ctx_loB.sem, ctx_loB.at(i, NC * (g // KT) + k))
                    pe.wait_ge(v_lo.sem, v_lo.at(i, g - 2))
                    keys, out = slice(n * P, (n + 1) * P), psP[:, g % 2, :]
                    passes = ((wAh, cAh), (wAh, cAl), (wAl, cAh), (wBh, cS), (w5, c5))
                    for c in range(DC):
                        for j, (w, x) in enumerate(passes):
                            pe.matmul(out[:, c * P:(c + 1) * P], w[:, c * P:(c + 1) * P], x[:, keys],
                                      start=(j == 0), stop=(j == 4))
                    for j, (w, x) in enumerate(passes):
                        ins = pe.matmul(out[:, D:2 * D], x[:, keys], w[:, D:2 * D], start=(j == 0), stop=(j == 4))
                    ins.then_inc(projected.sem, 1)

                def key_norms(g, i):
                    pe.wait_ge(squares.sem, squares.at(i, g))
                    pe.wait_ge(key_sums.sem, key_sums.at(i, g - 1))
                    for c in range(DC):
                        ins = pe.matmul(psN[:, g % 2:g % 2 + 1], ksq[:, g % 2, c * P:(c + 1) * P], core.ones[:, 0:1],
                                        start=(c == 0), stop=(c == 1))
                    ins.then_inc(norms.sem, 1)

                def score(g, i):
                    pe.wait_ge(k_lo.sem, k_lo.at(i, g))
                    for c in range(DC):
                        pe.wait_ge(exped.sem, exped.at(i, 2 * (g - 1) + c))
                        cols = slice(c * P, (c + 1) * P)
                        for j, (k, q) in enumerate(((kh, qbh), (kl, qbh), (kh, qbl))):
                            ins = pe.matmul(psS[:, c, :], k[:, g % 2, cols],
                                            q[:, c, bass.ds(i * 2 + g // KT, 1), :, :].rearrange("p a h q -> p (a h q)"),
                                            start=(j == 0), stop=(j == 2))
                        ins.then_inc(scored.sem, 1)

                def weigh(g, i):
                    n, s = g % KT, g % 2
                    rows = P if n < KT - 1 else TAIL
                    pe.wait_ge(v_lo.sem, v_lo.at(i, g))
                    pe.wait_ge(e_split.sem, e_split.at(i, 2 * g + 1))
                    if n == 0:
                        pe.wait_ge(out_taken.sem, out_taken.at(i, g // KT - 1))
                    for pr in range(PR):
                        c, col = pr // (PR // 2), (pr % (PR // 2)) * P
                        out = psO[:, c, (pr % (PR // 2)) * VW:(pr % (PR // 2) + 1) * VW]
                        pe.matmul(out, eh[0:rows, s, c, col:col + P], v[0:rows, s, pr, :],
                                  start=(n == 0 and pr % (PR // 2) == 0), stop=False, skip_group_check=True)
                        ins = pe.matmul(out[:, 2 * HD:VW], el[0:rows, s, c, col:col + P],
                                        v[0:rows, s, pr, 2 * HD:VW], start=False, stop=(n == KT - 1),
                                        skip_group_check=True)
                    ins.then_inc(weighed.sem, 1)

                project(0, 0)
                project(1, 0)
                key_norms(0, 0)
                with pe.Fori(0, B // 2) as i:
                    for g in range(TILES):
                        score(g, i)
                        key_norms(g + 1, i)
                        if g >= 1:
                            weigh(g - 1, i)
                        project(g + 2, i)
                    weigh(TILES - 1, i)

            @block.scalar
            def _(act):
                def square(g, i):
                    act.wait_ge(projected.sem, projected.at(i, g))
                    act.wait_ge(norms.sem, norms.at(i, g - 2))
                    act.activation(ksq[:, g % 2, :], psP[:, g % 2, 0:D], ACT.Square).then_inc(squares.sem, 1)

                def key_hi(g, i):
                    act.wait_ge(scored.sem, scored.at(i, 2 * (g - 2) + 1))
                    act.activation(kh[:, g % 2, :], psP[:, g % 2, 0:D], ACT.Copy).then_inc(k_hi.sem, 1)

                def value_hi(g, i):
                    act.wait_ge(weighed.sem, weighed.at(i, g - 2))
                    act.wait_ge(k_lo.sem, k_lo.at(i, g))
                    act.activation(v[:, g % 2, :, 2 * HD:4 * HD],
                                   psP[:, g % 2, D:2 * D].rearrange("p (a k) -> p a k", k=2 * HD),
                                   ACT.Copy).then_inc(v_hi.sem, 1)

                def exp(g, c, i):
                    act.wait_ge(rnorms.sem, rnorms.at(i, g))
                    act.wait_ge(e_split.sem, e_split.at(i, 2 * (g - 2) + c))
                    act.wait_ge(scored.sem, scored.at(i, 2 * g + c))
                    act.activation(e32[:, g % 2, c, :], psS[:, c, :], ACT.Exp,
                                   scale=rn[:, g % 2:g % 2 + 1]).then_inc(exped.sem, 1)

                square(0, 0)
                key_hi(0, 0)
                value_hi(0, 0)
                with act.Fori(0, B // 2) as i:
                    for g in range(TILES):
                        square(g + 1, i)
                        key_hi(g + 1, i)
                        exp(g, 0, i)
                        exp(g, 1, i)
                        value_hi(g + 1, i)
                        for k, batch in splits_at(g):
                            if k == 0:
                                act.wait_ge(ctx_loaded, i * 96 + 48 * (batch + 1))
                            act.wait_ge(projected.sem, projected.at(i, KT * (batch - 1) + CHUNKS[k][1] - 1))
                            split_hiA(act, k)
                        for k, batch in splits_at(g - 1):
                            split_hiB(act, k)

            @block.vector
            def _(dve):
                def guard(g, i):
                    dve.wait_ge(norms.sem, norms.at(i, g))
                    dve.wait_ge(rnorms.sem, rnorms.at(i, g - 2))
                    dve.tensor_scalar(kss[:, g % 2:g % 2 + 1], psN[:, g % 2:g % 2 + 1], 1e-24, None, ALU.max)\
                        .then_inc(key_sums.sem, 1)

                def key_lo(g, i):
                    dve.wait_ge(k_hi.sem, k_hi.at(i, g))
                    dve.tensor_tensor(kl[:, g % 2, :], psP[:, g % 2, 0:D], kh[:, g % 2, :], ALU.subtract)\
                        .then_inc(k_lo.sem, 1)

                def value_lo(g, i):
                    dve.wait_ge(v_hi.sem, v_hi.at(i, g))
                    dve.tensor_tensor(v[:, g % 2, :, 0:2 * HD],
                                      psP[:, g % 2, D:2 * D].rearrange("p (a k) -> p a k", k=2 * HD),
                                      v[:, g % 2, :, 2 * HD:4 * HD], ALU.subtract).then_inc(v_lo.sem, 1)

                def split_exp(g, c, i):
                    dve.wait_ge(weighed.sem, weighed.at(i, g - 2))
                    dve.wait_ge(exped.sem, exped.at(i, 2 * g + c))
                    dve.tensor_copy(eh[:, g % 2, c, :], e32[:, g % 2, c, :]).then_inc(e_hi.sem, 1)
                    dve.wait_ge(e_hi.sem, e_hi.at(i, 2 * g + c))
                    dve.tensor_tensor(el[:, g % 2, c, :], e32[:, g % 2, c, :], eh[:, g % 2, c, :], ALU.subtract)\
                        .then_inc(e_split.sem, 1)

                def take_out(g, i):
                    dve.wait_ge(weighed.sem, weighed.at(i, g))
                    dve.tensor_copy(o[:, bass.ds(i * 2 + g // KT, 1), :, :].rearrange("p a (c r) w -> p (a c) (r w)", c=2),
                                    psO[:, :, 0:PR // 2 * VW]).then_inc(out_taken.sem, 1)

                for c in (norms, key_sums, rnorms, v_lo, scored, exped, e_split, weighed, out_taken):
                    dve.sem_inc(c.sem, c.primed)
                key_lo(0, 0)
                value_lo(0, 0)
                guard(0, 0)
                with dve.Fori(0, B // 2) as i:
                    for g in range(TILES):
                        key_lo(g + 1, i)
                        split_exp(g, 0, i)
                        guard(g + 1, i)
                        split_exp(g, 1, i)
                        value_lo(g + 1, i)
                        for k, batch in splits_at(g - 1):
                            split_loB(dve, k, i, batch)
                        if g == KT:
                            take_out(KT - 1, i)
                    take_out(TILES - 1, i)

        vec = Steps(sem("out_vector"), "rden sums att x " + norm_steps("ln") + " gamma beta residual")
        pe_s = Steps(sem("out_tensor"), "attT out")
        roots = Steps(sem("out_roots"), "ln_var ln")
        evac = sem("attT_taken")
        with ExitStack() as pctx, nc.Block() as block:
            psT = pctx.enter_context(nc.psum_tensor("l0x_psA", [P, B, P], F32))
            psX = pctx.enter_context(nc.psum_tensor("l0x_psX", [P, TT, D], F32))

            @block.gpsimd
            def _(pool):
                layer_norm_root(pool, vec, roots, "ln", core.norm_work, core.minus_half[:, 0:TT])

            @block.vector
            def _(dve):
                dve.reciprocal(rd[:, :, :], o[:, :, :, VW - 1]).then_inc(vec.done("rden"), 1)
                for hh in range(2):
                    rows, k = slice(hh * N, (hh + 1) * N), hh * HD
                    ins = dve.tensor_tensor(att[rows, :, :, :], o[rows, :, :, k:k + HD],
                                            o[rows, :, :, 2 * HD + k:2 * HD + k + HD], ALU.add)
                ins.then_inc(vec.done("sums"), 1)
                dve.wait_ge(vec.sem, vec.at("sums"))
                dve.tensor_tensor(att[:, :, :, :], att[:, :, :, :], rd[:, :, :, None].to_broadcast([P, B, PR, HD]),
                                  ALU.mult).then_inc(vec.done("att"), 1)
                dve.wait_ge(pe_s.sem, pe_s.at("out"))
                dve.tensor_tensor(qn[:, :, :], psX[:, :, :], qp[:, :, :], ALU.add).then_inc(vec.done("x"), 1)
                dve.wait_ge(vec.sem, vec.at("x"))
                layer_norm(dve, vec, roots, "ln", qn, qn, core.norm_work)
                dve.tensor_tensor(qn[:, :, :], qn[:, :, :], gam[:, None, :].to_broadcast([P, TT, D]), ALU.mult)\
                    .then_inc(vec.done("gamma"), 1)
                dve.wait_ge(vec.sem, vec.at("gamma"))
                dve.tensor_tensor(qn[:, :, :], qn[:, :, :], bet[:, None, :].to_broadcast([P, TT, D]), ALU.add)\
                    .then_inc(vec.done("beta"), 1)
                dve.wait_ge(vec.sem, vec.at("beta"))
                dve.tensor_tensor(core.x[:, :, :], core.x[:, :, :], qn[:, :, :], ALU.add).then_inc(vec.done("residual"), 1)

            @block.tensor
            def _(pe):
                pe.wait_ge(vec.sem, vec.at("att"))
                for b in range(B):
                    ins = pe.transpose(psT[:, b, :], att[:, b, :, :].rearrange("p a k -> p (a k)"), core.ident[:, :])
                ins.then_inc(pe_s.done("attT"), 1)
                pe.wait_ge(evac, 1)
                for t in range(TT):
                    for hh in range(2):
                        pe.matmul(psX[:, t, :], attT[:, hh, t * P:(t + 1) * P], wo[:, hh, :], start=(hh == 0), stop=False)
                    ins = pe.matmul(psX[:, t, :], core.ones[0:1, :], rows[0:1, 1, :], start=False, stop=True)
                ins.then_inc(pe_s.done("out"), 1)

            @block.scalar
            def _(act):
                act.wait_ge(pe_s.sem, pe_s.at("attT"))
                act.activation(attT[:, :, :].rearrange("p h (b q) -> p b h q", b=B),
                               psT[:, :, :].rearrange("p b (h q) -> p b h q", h=2), ACT.Copy).then_inc(evac, 1)


def stage_l0_self(core, norm):
    nc, d = core.nc, core.dram
    DH = 64
    NN = 2
    J = NN + N
    PR = H // 2
    W = H * DH
    halves = [slice(0, N), slice(N, P)]
    place = lambda h: h % 2 * PR + h // 2
    with ExitStack() as ctx:
        sb = lambda name, shape, dt=F32: ctx.enter_context(nc.sbuf_tensor(f"l0a_{name}", shape, dt))
        pb = lambda name, shape: ctx.enter_context(nc.psum_tensor(f"l0a_{name}", shape, F32))
        sem = lambda name: core.sem(f"l0a_{name}")
        w = sb("w", [P, DC, 3 * W])
        wo = sb("wo", [P, PR, D])
        scale = sb("scale", [P, 2])
        bias = sb("bias", [P, H, J])
        nk, nks = sb("nk", [2 * H, DH]), sb("nks", [2 * H, DH])
        nss = sb("nss", [2 * H, 1])
        nkb = sb("nkb", [2 * H, H, DH])
        blockmask = sb("blockmask", [2 * H, H])
        nkT = sb("nkT", [P, PR, 4])
        nv = sb("nv", [2 * H, W])
        yt = sb("yt", [P, DC, P])
        qk = sb("qk", [P, 2, H, DH])
        sq = sb("sq", [P, 2, H, DH])
        ss = sb("ss", [P, 2, H])
        v = sb("v", [P, W])
        qkT = sb("qkT", [P, 2, PR, P])
        s, e = sb("s", [P, H, J]), sb("e", [P, H, J])
        en = sb("en", [P, H * NN])
        top, den = sb("top", [P, H]), sb("den", [P, H])
        eT, nT = sb("eT", [P, H, N]), sb("nT", [2 * H, P])
        o, oT = sb("o", [P, H, DH]), sb("oT", [P, PR, P])

        loaded, rest_loaded = sem("loaded"), sem("rest_loaded")
        setup = Steps(sem("setup"), "scale squares sums guarded normed blocks nkT")
        setup_root = sem("setup_root")
        setup_T = sem("setup_T")
        vecA = Steps(sem("vector_a"), "yt sums guarded normed qT")
        vecB = Steps(sem("vector_b"), "biased top shifted den rden o")
        actA, actB = Steps(sem("scalar_a"), "qk v kT"), Steps(sem("scalar_b"), "exp eT oT")
        peA, peB = Steps(sem("tensor_a"), "qk v kT qT"), Steps(sem("tensor_b"), "scores eT out oT")
        roots = Steps(sem("roots"), "norms")
        pe_out, vec_out = Steps(sem("tensor_out"), "proj"), Steps(sem("vector_out"), "x")
        N_LOADS, N_REST = 16 * 8, 16 * 4

        def turns(eng, first, both, last):
            first(0)
            both(0)
            with eng.Fori(1, TT - 1) as i:
                both(i, True)
            last(TT - 1)

        def prefetch(sp):
            w_kv = d["L0_attn_w_kv"].rearrange("(c p) n -> p c n", p=P)
            sp.dma_start(nk[:, :], d["c_null_k"]).then_inc(loaded, 16)
            for half in halves:
                sp.dma_start(scale[half, 0:1], d["L0_attn_q_scale"].rearrange("(k o) -> k o", o=1)).then_inc(loaded, 16)
                sp.dma_start(scale[half, 1:2], d["L0_attn_k_scale"].rearrange("(k o) -> k o", o=1)).then_inc(loaded, 16)
            sp.dma_start(blockmask[:, :], d["c_blockmask"]).then_inc(loaded, 16)
            sp.dma_start(w[:, :, 0:W], d["L0_attn_w_q"].rearrange("(c p) n -> p c n", p=P)).then_inc(loaded, 16)
            sp.dma_start(w[:, :, W:2 * W], w_kv[:, :, 0:W]).then_inc(loaded, 16)
            sp.dma_start(w[:, :, 2 * W:3 * W], w_kv[:, :, W:2 * W]).then_inc(rest_loaded, 16)
            sp.dma_start(bias[:, :, :], d["c_alibi"]).then_inc(rest_loaded, 16)
            sp.dma_start(nv[:, :], d["c_null_v"]).then_inc(rest_loaded, 16)
            sp.dma_start(wo[:, :, :], d["L0_attn_w_out"].rearrange("(c p) n -> p c n", p=P)).then_inc(rest_loaded, 16)

        norm(prefetch)
        psA = pb("psA", [P, 4, 512])
        psS, psN, psX = pb("psS", [P, 2, 512]), pb("psN", [P, 512]), pb("psX", [P, 512])
        psA_heads = psA[:, :, :].rearrange("p a (b q) -> p (a b) q", q=P)
        psS_heads = psS[:, :, :].rearrange("p a (b q) -> p (a b) q", q=N)
        psS_pairs = psS[:, :, :].rearrange("p a (b q) -> p (a b) q", q=P)
        with nc.Block() as block:
            @block.gpsimd
            def _(pool):
                pool.wait_ge(setup.sem, setup.at("guarded"))
                pool.tensor_tensor(nss[:, :], nss[:, :], core.minus_half[0:2 * H, 0:1], ALU.pow).then_inc(setup_root, 1)
                def root(j):
                    pool.wait_ge(vecA.sem, vecA.at("guarded", j))
                    pool.tensor_tensor(ss[:, :, :], ss[:, :, :],
                                       core.minus_half[:, 0:2 * H].rearrange("p (a h) -> p a h", a=2), ALU.pow)\
                        .then_inc(roots.done("norms"), 1)

                turns(pool, root, lambda i, more=False: root(i + 1), lambda i: None)

            @block.tensor
            def _(pe):
                def transpose_null():
                    pe.wait_ge(setup.sem, setup.at("blocks"))
                    for pr in range(PR):
                        ins = pe.transpose(psX[:, pr * 32:(pr + 1) * 32],
                                           nkb[:, 2 * pr:2 * pr + 2, :].rearrange("k a d -> k (a d)"),
                                           core.ident[0:2 * H, 0:2 * H])
                    ins.then_inc(setup_T, 1)

                def project(j, parts, name):
                    for at, part in enumerate(parts):
                        for c in range(DC):
                            ins = pe.matmul(psA[:, at, :], yt[:, c, :], w[:, c, part * 512:(part + 1) * 512],
                                            start=(c == 0), stop=(c == 1))
                    ins.then_inc(peA.done(name), 1)

                def project_qk(j):
                    pe.wait_ge(vecA.sem, vecA.at("yt", j))
                    project(j, range(4), "qk")

                def project_v(j):
                    pe.wait_ge(actA.sem, actA.at("qk", j))
                    project(j, range(4, 6), "v")

                def transpose_qk(j):
                    pe.wait_ge(vecA.sem, vecA.at("normed", j))
                    pe.wait_ge(actA.sem, actA.at("v", j))
                    for a, name in ((1, "kT"), (0, "qT")):
                        for pr in range(PR):
                            ins = pe.transpose(psA_heads[:, a * PR + pr, :],
                                               qk[:, a, 2 * pr:2 * pr + 2, :].rearrange("p h k -> p (h k)"),
                                               core.ident[:, :])
                        ins.then_inc(peA.done(name), 1)

                def score(i):
                    pe.wait_ge(setup.sem, setup.at("nkT"))
                    wait_apart(pe, actA.sem, actA.at("kT", i), core.spare)
                    wait_apart(pe, vecA.sem, vecA.at("qT", i), core.spare)
                    for pr in range(PR):
                        for odd, r in enumerate(halves):
                            for half in halves:
                                pe.matmul(psS_heads[half, odd * PR + pr, :], qkT[r, 0, pr, half], qkT[r, 1, pr, half],
                                          start=True, stop=True)
                    for pr in range(PR):
                        ins = pe.matmul(psN[:, pr * 2 * NN:(pr + 1) * 2 * NN], qkT[:, 0, pr, :], nkT[:, pr, :],
                                        start=True, stop=True)
                    ins.then_inc(peB.done("scores"), 1)

                def transpose_e(i):
                    wait_apart(pe, actB.sem, actB.at("exp", i), core.spare)
                    for h in range(H):
                        for half in halves:
                            pe.matmul(psS_heads[half, h, :], e[half, h, NN:J], core.ident[half, half], start=True, stop=True)
                    ins = pe.matmul(psN[0:2 * H, 0:P], en[:, :], core.ident[:, :], start=True, stop=True)
                    ins.then_inc(peB.done("eT"), 1)

                def weigh(i):
                    pe.wait_ge(actB.sem, actB.at("eT", i))
                    pe.wait_ge(actA.sem, actA.at("v", i))
                    for bank in range(2):
                        pe.matmul(psS[:, bank, :], nT[:, :], nv[:, bank * 512:(bank + 1) * 512], start=True, stop=False,
                                  skip_group_check=True)
                        for h in range(8 * bank, 8 * bank + 8):
                            for half in halves:
                                ins = pe.matmul(psS[half, bank, (h % 8) * DH:(h % 8 + 1) * DH], eT[half, place(h), :],
                                                v[half, h * DH:(h + 1) * DH], start=False, stop=(h % 8 == 7),
                                                skip_group_check=True)
                    ins.then_inc(peB.done("out"), 1)

                def transpose_o(i):
                    pe.wait_ge(vecB.sem, vecB.at("o", i))
                    for pr in range(PR):
                        ins = pe.transpose(psS_pairs[:, pr, :], o[:, 2 * pr:2 * pr + 2, :].rearrange("p h k -> p (h k)"),
                                           core.ident[:, :])
                    ins.then_inc(peB.done("oT"), 1)

                def project_out(i):
                    pe.wait_ge(actB.sem, actB.at("oT", i))
                    for pr in range(PR):
                        ins = pe.matmul(psX[:, 0:D], oT[:, pr, :], wo[:, pr, :], start=(pr == 0), stop=(pr == PR - 1))
                    ins.then_inc(pe_out.done("proj"), 1)

                def first(j):
                    pe.wait_ge(loaded, N_LOADS)
                    project_qk(j)
                    transpose_null()
                    pe.wait_ge(rest_loaded, N_REST)
                    project_v(j)
                    transpose_qk(j)

                def both(i, more=False):
                    score(i)
                    project_qk(i + 1)
                    transpose_e(i)
                    project_v(i + 1)
                    weigh(i)
                    if more:
                        project_out(i - 1)
                    transpose_o(i)
                    transpose_qk(i + 1)
                    wait_apart(pe, actB.sem, actB.at("oT", i), core.spare)

                def last(i):
                    for step in (score, transpose_e, weigh):
                        step(i)
                    project_out(i - 1)
                    transpose_o(i)
                    pe.wait_ge(vec_out.sem, vec_out.at("x", i - 1))
                    project_out(i)

                turns(pe, first, both, last)

            @block.scalar
            def _(act):
                def take_qk(j):
                    act.wait_ge(peA.sem, peA.at("qk", j))
                    for out, what in ((sq, ACT.Square), (qk, ACT.Copy)):
                        ins = act.activation(out[:, :, :, :].rearrange("p a h k -> p (a h k)"),
                                             psA[:, :, :].rearrange("p a n -> p (a n)"), what)
                    ins.then_inc(actA.done("qk"), 1)

                def take_v(j):
                    act.wait_ge(peA.sem, peA.at("v", j))
                    act.activation(v[:, :], psA[:, 0:2, :].rearrange("p a n -> p (a n)"), ACT.Copy)\
                        .then_inc(actA.done("v"), 1)

                def take_kT(j):
                    act.wait_ge(peA.sem, peA.at("kT", j))
                    act.activation(qkT[:, 1, :, :].rearrange("p h k -> p (h k)"),
                                   psA[:, 2:4, :].rearrange("p a n -> p (a n)"), ACT.Copy).then_inc(actA.done("kT"), 1)

                def exp(i):
                    act.wait_ge(vecB.sem, vecB.at("shifted", i))
                    act.activation(en[:, :].rearrange("p (h k) -> p h k", k=NN), s[:, :, 0:NN], ACT.Exp)
                    act.activation(e[:, :, :], s[:, :, :], ACT.Exp).then_inc(actB.done("exp"), 1)

                def take_eT(i):
                    act.wait_ge(peB.sem, peB.at("eT", i))
                    act.activation(eT[:, :, :], psS_heads[:, :, :], ACT.Copy)
                    act.activation(nT[:, :], psN[0:2 * H, 0:P], ACT.Copy).then_inc(actB.done("eT"), 1)

                def take_oT(i):
                    act.wait_ge(peB.sem, peB.at("oT", i))
                    act.activation(oT[:, :, :], psS_pairs[:, :, :], ACT.Copy).then_inc(actB.done("oT"), 1)

                def first(j):
                    for step in (take_qk, take_v, take_kT):
                        step(j)

                def both(i, more=False):
                    exp(i)
                    take_qk(i + 1)
                    take_eT(i)
                    act.wait_ge(peB.sem, peB.at("out", i))
                    take_v(i + 1)
                    take_oT(i)
                    take_kT(i + 1)

                def last(i):
                    for step in (exp, take_eT, take_oT):
                        step(i)

                turns(act, first, both, last)

            @block.vector
            def _(dve):
                def null_keys():
                    dve.wait_ge(loaded, N_LOADS)
                    dve.tensor_tensor(scale[:, 0:1], scale[:, 0:1], scale[:, 1:2], ALU.mult)\
                        .then_inc(setup.done("scale"), 1)
                    dve.tensor_tensor(nks[:, :], nk[:, :], nk[:, :], ALU.mult).then_inc(setup.done("squares"), 1)
                    dve.wait_ge(setup.sem, setup.at("squares"))
                    dve.tensor_reduce(nss[:, :], nks[:, :], AX.X, ALU.add).then_inc(setup.done("sums"), 1)
                    dve.wait_ge(setup.sem, setup.at("sums"))
                    dve.tensor_scalar(nss[:, :], nss[:, :], 1e-24, None, ALU.max).then_inc(setup.done("guarded"), 1)
                    dve.wait_ge(setup_root, 1)
                    dve.tensor_scalar(nk[:, :], nk[:, :], nss[:, 0:1], None, ALU.mult).then_inc(setup.done("normed"), 1)
                    dve.wait_ge(setup.sem, setup.at("normed"))
                    dve.tensor_tensor(nkb[:, :, :], nk[:, None, :].to_broadcast([2 * H, H, DH]),
                                      blockmask[:, :, None].to_broadcast([2 * H, H, DH]), ALU.mult)\
                        .then_inc(setup.done("blocks"), 1)
                    dve.wait_ge(setup_T, 1)
                    for pr in range(PR):
                        ins = dve.tensor_copy(nkT[:, pr, :], psX[:, pr * 32 + 4 * pr:pr * 32 + 4 * pr + 4])
                    ins.then_inc(setup.done("nkT"), 1)

                def take_y(j):
                    dve.tensor_copy(yt[:, :, :], core.yT[:, :, bass.ds(j * P, P)]).then_inc(vecA.done("yt"), 1)

                def norms(j):
                    dve.wait_ge(actA.sem, actA.at("qk", j))
                    dve.tensor_reduce(ss[:, :, :], sq[:, :, :, :], AX.X, ALU.add).then_inc(vecA.done("sums"), 1)
                    dve.wait_ge(vecA.sem, vecA.at("sums", j))
                    dve.tensor_scalar(ss[:, :, :], ss[:, :, :], 1e-24, None, ALU.max).then_inc(vecA.done("guarded"), 1)

                def norm_qk(j):
                    dve.wait_ge(roots.sem, roots.at("norms", j))
                    dve.tensor_tensor(qk[:, :, :, :], qk[:, :, :, :], ss[:, :, :, None].to_broadcast([P, 2, H, DH]),
                                      ALU.mult).then_inc(vecA.done("normed"), 1)

                def take_qT(j):
                    dve.wait_ge(peA.sem, peA.at("qT", j))
                    dve.tensor_scalar(qkT[:, 0, :, :].rearrange("p h k -> p (h k)"),
                                      psA[:, 0:2, :].rearrange("p a n -> p (a n)"), scale[:, 0:1], None, ALU.mult)\
                        .then_inc(vecA.done("qT"), 1)

                def softmax(i):
                    dve.wait_ge(peB.sem, peB.at("scores", i))
                    dve.scalar_tensor_tensor(s[:, :, NN:J], psS_heads[:, :, :], 8.0, bias[:, :, NN:J], ALU.mult, ALU.add)
                    for odd in range(2):
                        heads = slice(odd * PR, (odd + 1) * PR)
                        ins = dve.scalar_tensor_tensor(
                            s[:, heads, 0:NN], psN[:, 0:2 * H].rearrange("p (a b k) -> p b a k", b=2, k=NN)[:, odd],
                            8.0, bias[:, heads, 0:NN], ALU.mult, ALU.add)
                    ins.then_inc(vecB.done("biased"), 1)
                    dve.wait_ge(vecB.sem, vecB.at("biased", i))
                    dve.tensor_reduce(top[:, :], s[:, :, :], AX.X, ALU.max).then_inc(vecB.done("top"), 1)
                    dve.wait_ge(vecB.sem, vecB.at("top", i))
                    dve.tensor_tensor(s[:, :, :], s[:, :, :], top[:, :, None].to_broadcast([P, H, J]), ALU.subtract)\
                        .then_inc(vecB.done("shifted"), 1)

                def denominators(i):
                    dve.wait_ge(actB.sem, actB.at("exp", i))
                    dve.tensor_reduce(den[:, :], e[:, :, :], AX.X, ALU.add).then_inc(vecB.done("den"), 1)
                    dve.wait_ge(vecB.sem, vecB.at("den", i))
                    dve.reciprocal(den[:, :], den[:, :]).then_inc(vecB.done("rden"), 1)

                def take_o(i):
                    dve.wait_ge(peB.sem, peB.at("out", i))
                    dve.wait_ge(vecB.sem, vecB.at("rden", i))
                    den_in_order = den[:, :].rearrange("p (odd a) -> p a odd", odd=2)
                    dve.tensor_tensor(o[:, :, :].rearrange("p (a odd) k -> p a odd k", odd=2),
                                      psS[:, :, :].rearrange("p b (a odd k) -> p (b a) odd k", odd=2, k=DH),
                                      den_in_order[:, :, :, None].to_broadcast([P, PR, 2, DH]), ALU.mult)\
                        .then_inc(vecB.done("o"), 1)

                def residual(i):
                    dve.wait_ge(pe_out.sem, pe_out.at("proj", i))
                    xi = core.x[:, bass.ds(i, 1), :].rearrange("p a n -> p (a n)")
                    dve.tensor_tensor(xi, xi, psX[:, 0:D], ALU.add).then_inc(vec_out.done("x"), 1)

                def first(j):
                    take_y(j)
                    null_keys()
                    for step in (norms, norm_qk, take_qT):
                        step(j)
                    dve.wait_ge(rest_loaded, N_REST)

                def both(i, more=False):
                    take_y(i + 1)
                    softmax(i)
                    norms(i + 1)
                    denominators(i)
                    take_o(i)
                    norm_qk(i + 1)
                    if more:
                        residual(i - 1)
                    take_qT(i + 1)

                def last(i):
                    for step in (softmax, denominators, take_o):
                        step(i)
                    residual(i - 1)
                    residual(i)

                turns(dve, first, both, last)
                dve.wait_ge(vec_out.sem, vec_out.at("x", TT - 1))


def stage_experts(core, norm, tag, router, weights, experts, chunks, gated, keep_top):
    nc, d = core.nc, core.dram
    FIRST = (2 if gated else 1) * DC * P
    WC = FIRST + D
    with ExitStack() as ctx:
        sb = lambda name, shape, dt=F32: ctx.enter_context(nc.sbuf_tensor(f"{tag}_{name}", shape, dt))
        sem = lambda name: core.sem(f"{tag}_{name}")
        rw = sb("rw", [P, DC, E])
        iota = sb("iota", [P, E])
        logits = sb("logits", [P, TT, E])
        best, index = sb("best", [P, TT, 8]), sb("index", [P, TT, 8], U32)
        indexf = sb("indexf", [P, TT, 8])
        hot = sb("hot", [P, 2, TT, E])
        share = sb("share", [P, 2, TT])
        wt = sb("wt", [P, TT, E])
        wT = sb("wT", [E, TOK])
        wb = sb("wb", [P, experts, TOK])
        xh, xl = sb("xh", [P, DC, TOK], F16), sb("xl", [P, DC, TOK], F16)
        w32 = sb("w32", [P, chunks, WC])
        wh, wl = sb("wh", [P, chunks, WC], F16), sb("wl", [P, chunks, WC], F16)
        g = sb("g", [P, 2, TOK])
        sg = sb("sg", [P, 2, TOK])
        hm = sb("hm", [P, 2, TOK])
        hh, hl = sb("hh", [P, 2, TOK], F16), sb("hl", [P, 2, TOK], F16)
        zeros = sb("zeros", [1, 512], F16)

        loaded = sem("loaded")
        second_sem, summed = sem("first_weights"), sem("summed")
        vec = Steps(sem("route_vector"), "x_hi x_lo logits best index indexf hot diff shared_out "
                                         "inverse share weights wT")
        pe_s = Steps(sem("route_tensor"), "logits wT " + " ".join(f"spread{e}" for e in range(E)))
        act_s = Steps(sem("route_scalar"), "exp " + " ".join(f"spread{e}" for e in range(E)))

        w_loaded = [sem(f"w_loaded{k}") for k in range(chunks)]
        w_hi, w_lo = sem("w_hi"), sem("w_lo")
        up_done, gate_w, silu, silu_w = sem("up_done"), sem("gate_w"), sem("silu"), sem("silu_w")
        hidden, hid_hi, hid_lo, down_done = sem("hidden"), sem("hid_hi"), sem("hid_lo"), sem("down_done")

        def load_chunk(sp, e, k):
            sp.dma_start(w32[:, k, :], d[weights][bass.ds(e, 1), k, :, :].rearrange("a p n -> (a p) n"))\
                .then_inc(w_loaded[k], 16)

        def prefetch(sp):
            sp.dma_start(rw[:, :, :], d[router].rearrange("(c p) e -> p c e", p=P)).then_inc(loaded, 16)
            sp.dma_start(iota[:, :], d["c_iota"]).then_inc(loaded, 16)
            for k in range(chunks):
                load_chunk(sp, 0, k)

        norm(prefetch)

        with ExitStack() as pctx, nc.Block() as block:
            psR = pctx.enter_context(nc.psum_tensor(f"{tag}_psR", [P, TT, E], F32))
            psW = pctx.enter_context(nc.psum_tensor(f"{tag}_psW", [E, TOK], F32))
            psB = pctx.enter_context(nc.psum_tensor(f"{tag}_psB", [P, 2, TOK], F32))

            @block.tensor
            def _(pe):
                pe.wait_ge(loaded, 32)
                for t in range(TT):
                    for c in range(DC):
                        ins = pe.matmul(psR[:, t, :], core.yT[:, c, t * P:(t + 1) * P], rw[:, c, :],
                                        start=(c == 0), stop=(c == DC - 1))
                ins.then_inc(pe_s.done("logits"), 1)
                pe.wait_ge(vec.sem, vec.at("weights"))
                for t in range(TT):
                    ins = pe.transpose(psW[:, t * P:(t + 1) * P], wt[:, t, :], core.ident[:, :])
                ins.then_inc(pe_s.done("wT"), 1)
                pe.wait_ge(vec.sem, vec.at("wT"))
                for e in range(E):
                    if e >= 2:
                        pe.wait_ge(act_s.sem, act_s.at(f"spread{e - 2}"))
                    pe.matmul(psB[:, e % 2, :], core.ident[0:E, e:e + 1].to_broadcast([E, P]), wT[:, :], start=True, stop=True)\
                        .then_inc(pe_s.done(f"spread{e}"), 1)

            @block.scalar
            def _(act):
                act.wait_ge(vec.sem, vec.at("diff"))
                act.activation(share[:, 1, :], share[:, 0, :], ACT.Exp).then_inc(act_s.done("exp"), 1)
                for e in range(E):
                    act.wait_ge(pe_s.sem, pe_s.at(f"spread{e}"))
                    act.activation(wb[:, e, :], psB[:, e % 2, :], ACT.Copy).then_inc(act_s.done(f"spread{e}"), 1)

            @block.vector
            def _(dve):
                if experts > E:
                    dve.memset(wb[:, E, :], 1.0)
                dve.memset(zeros[:, :], 0.0)
                dve.tensor_copy(xh[:, :, :], core.yT[:, :, :]).then_inc(vec.done("x_hi"), 1)
                dve.wait_ge(vec.sem, vec.at("x_hi"))
                dve.tensor_tensor(xl[:, :, :], core.yT[:, :, :], xh[:, :, :], ALU.subtract).then_inc(vec.done("x_lo"), 1)
                dve.wait_ge(loaded, 32)
                dve.wait_ge(pe_s.sem, pe_s.at("logits"))
                dve.tensor_copy(logits[:, :, :], psR[:, :, :]).then_inc(vec.done("logits"), 1)
                dve.wait_ge(vec.sem, vec.at("logits"))
                for t in range(TT):
                    ins = dve.max(best[:, t, :], logits[:, t, :])
                ins.then_inc(vec.done("best"), 1)
                dve.wait_ge(vec.sem, vec.at("best"))
                for t in range(TT):
                    ins = dve.max_index(index[:, t, :], best[:, t, :], logits[:, t, :])
                ins.then_inc(vec.done("index"), 1)
                dve.wait_ge(vec.sem, vec.at("index"))
                dve.tensor_copy(indexf[:, :, :], index[:, :, :]).then_inc(vec.done("indexf"), 1)
                dve.wait_ge(vec.sem, vec.at("indexf"))
                for k in range(2):
                    for t in range(TT):
                        ins = dve.tensor_scalar(hot[:, k, t, :], iota[:, :], indexf[:, t, k:k + 1], None, ALU.is_equal)
                ins.then_inc(vec.done("hot"), 1)
                if keep_top == 2:
                    dve.tensor_tensor(share[:, 0, :], best[:, :, 1], best[:, :, 0], ALU.subtract).then_inc(vec.done("diff"), 1)
                else:
                    dve.tensor_scalar(share[:, 0, :], best[:, :, 0], -1.0, 80.0, ALU.mult, ALU.min).then_inc(vec.done("diff"), 1)
                dve.wait_ge(act_s.sem, act_s.at("exp"))
                dve.tensor_scalar(share[:, 0, :], share[:, 1, :], 1.0, None, ALU.add).then_inc(vec.done("shared_out"), 1)
                dve.wait_ge(vec.sem, vec.at("shared_out"))
                dve.reciprocal(share[:, 0, :], share[:, 0, :]).then_inc(vec.done("inverse"), 1)
                dve.wait_ge(vec.sem, vec.at("inverse"))
                dve.tensor_tensor(share[:, 1, :], share[:, 1, :], share[:, 0, :], ALU.mult).then_inc(vec.done("share"), 1)
                dve.wait_ge(vec.sem, vec.at("share"))
                for t in range(TT):
                    ins = dve.tensor_scalar(wt[:, t, :], hot[:, 0, t, :], share[:, 0, t:t + 1], None, ALU.mult)
                ins.then_inc(second_sem if keep_top == 2 else vec.done("weights"), 1)
                if keep_top == 2:
                    dve.wait_ge(second_sem, 1)
                    for t in range(TT):
                        ins = dve.scalar_tensor_tensor(wt[:, t, :], hot[:, 1, t, :], share[:, 1, t:t + 1], wt[:, t, :],
                                                       ALU.mult, ALU.add)
                    ins.then_inc(vec.done("weights"), 1)
                dve.wait_ge(pe_s.sem, pe_s.at("wT"))
                dve.tensor_copy(wT[:, :], psW[:, :]).then_inc(vec.done("wT"), 1)

        AHEAD = chunks - 3
        START = 1
        STEPS = experts * chunks
        count = lambda sem_, primed=0: Count(sem_, 1, primed)
        hi, lo, up = count(w_hi), count(w_lo), count(up_done)
        gated_in, silued, weighted = count(gate_w), count(silu), count(silu_w)
        hid, hidh, hidl, down = count(hidden, START), count(hid_hi), count(hid_lo, START), count(down_done, START)
        with ExitStack() as pctx, nc.Block() as block:
            psY = pctx.enter_context(nc.psum_tensor(f"{tag}_psY", [P, TT, D], F32))
            psG = pctx.enter_context(nc.psum_tensor(f"{tag}_psG", [P, 2, TOK], F32))
            psU = pctx.enter_context(nc.psum_tensor(f"{tag}_psU", [P, 2, TOK], F32))

            def steps(eng, step, end):
                for k in range(chunks):
                    step(0, k)
                with eng.Fori(0, experts - 1) as e:
                    for k in range(chunks):
                        step(e * chunks + chunks, k)
                end(STEPS)

            catch_up, j = [], 2
            for k in range(chunks):
                until = min(j + 2, k + AHEAD + 1)
                catch_up.append(list(range(j, until)))
                j = max(j, until)

            def split_at(base, k):
                return catch_up[k] if isinstance(base, int) else [k + AHEAD]

            @block.sync
            def _(sp):
                with sp.Fori(0, experts - 1) as e:
                    for k in range(chunks):
                        sp.wait_ge(lo.sem, lo.at(e * chunks, k))
                        load_chunk(sp, e + 1, k)
                for k in range(AHEAD):
                    sp.wait_ge(lo.sem, lo.at(STEPS - chunks, k))
                    load_chunk(sp, experts, k)

            @block.tensor
            def _(pe):
                def first_layers(base, k):
                    s = k % 2
                    pe.wait_ge(lo.sem, lo.at(base, k))
                    pe.wait_ge(hid.sem, max(hid.at(base, k - 2), START) if isinstance(base, int) else hid.at(base, k - 2))
                    for i in range(2 if gated else 1):
                        out = (psG, psU)[i][:, s, :]
                        terms = [(w, x, c) for w, x in ((wh, xh), (wl, xh), (wh, xl)) for c in range(DC)]
                        for j, (w, x, c) in enumerate(terms):
                            col = (i * DC + c) * P
                            ins = pe.matmul(out, w[:, k, col:col + P], x[:, c, :], start=(j == 0),
                                            stop=(j == len(terms) - 1))
                    ins.then_inc(up.sem, 1)

                def last_layer(base, k):
                    s, chunk = k % 2, k % chunks
                    pe.wait_ge(hidl.sem, hidl.at(base, k))
                    for t in range(TT):
                        for h, w in ((hh, wh), (hl, wh), (hh, wl)):
                            ins = pe.matmul(psY[:, t, :], h[:, s, t * P:(t + 1) * P], w[:, chunk, FIRST:WC],
                                            start=False, stop=False, skip_group_check=True)
                    ins.then_inc(down.sem, 1)

                for bank in range(2):
                    pe.matmul(psY[:, 2 * bank:2 * bank + 2, :].rearrange("p a n -> p (a n)"), zeros[0:1, 0:P],
                              zeros[0:1, :], start=True, stop=False, skip_group_check=True)

                def step(base, k):
                    first_layers(base, k)
                    if not isinstance(base, int) or k >= 2:
                        last_layer(base, k - 2)

                def end(base):
                    last_layer(base, -2)
                    last_layer(base, -1)

                steps(pe, step, end)

            @block.scalar
            def _(act):
                def split_weights(base, k):
                    chunk = k % chunks
                    if isinstance(base, int):
                        act.wait_ge(w_loaded[chunk], 16 * ((base + k) // chunks) + 16)
                        if base + k >= chunks:
                            act.wait_ge(down.sem, down.at(base, k - chunks))
                    else:
                        act.wait_ge(w_loaded[chunk], base * (16 // chunks) + (k // chunks) * 16 + 16)
                        act.wait_ge(down.sem, down.at(base, k - chunks))
                    act.activation(wh[:, chunk, :], w32[:, chunk, :], ACT.Copy).then_inc(hi.sem, 1)

                def hidden_hi(base, k):
                    act.wait_ge(hid.sem, hid.at(base, k))
                    act.wait_ge(down.sem, max(down.at(base, k - 2), START) if isinstance(base, int) else down.at(base, k - 2))
                    act.activation(hh[:, k % 2, :], hm[:, k % 2, :], ACT.Copy).then_inc(hidh.sem, 1)

                def step(base, k):
                    for j in split_at(base, k):
                        split_weights(base, j)
                    if gated:
                        act.wait_ge(gated_in.sem, gated_in.at(base, k))
                        act.activation(sg[:, k % 2, :], g[:, k % 2, :], ACT.Silu).then_inc(silued.sem, 1)
                    if not isinstance(base, int) or k >= 1:
                        hidden_hi(base, k - 1)

                for k in range(2):
                    split_weights(0, k)
                steps(act, step, lambda base: hidden_hi(base, -1))

            if gated:
                @block.gpsimd
                def _(pool):
                    def step(base, k):
                        s = k % 2
                        wait_apart(pool, silued.sem, silued.at(base, k), core.spare)
                        e = 0 if isinstance(base, int) else base // chunks
                        pool.tensor_tensor(sg[:, s, :], sg[:, s, :],
                                           wb[:, bass.ds(e, 1), :].rearrange("p a n -> p (a n)"), ALU.mult)\
                            .then_inc(weighted.sem, 1)

                    steps(pool, step, lambda base: None)

            @block.vector
            def _(dve):
                def expert_weight(base, k):
                    if isinstance(base, int):
                        e = (base + k) // chunks
                    else:
                        e = base // chunks + (k // chunks)
                    return wb[:, bass.ds(e, 1), :].rearrange("p a n -> p (a n)")

                def split_weights(base, k):
                    chunk = k % chunks
                    dve.wait_ge(hi.sem, hi.at(base, k))
                    dve.tensor_tensor(wl[:, chunk, :], w32[:, chunk, :], wh[:, chunk, :], ALU.subtract).then_inc(lo.sem, 1)

                def hidden_units(base, k):
                    s = k % 2
                    dve.wait_ge(hidl.sem, max(hidl.at(base, k - 2), START) if isinstance(base, int) else hidl.at(base, k - 2))
                    if gated:
                        dve.wait_ge(weighted.sem, weighted.at(base, k))
                        dve.tensor_tensor(hm[:, s, :], psU[:, s, :], sg[:, s, :], ALU.mult).then_inc(hid.sem, 1)
                    else:
                        dve.wait_ge(up.sem, up.at(base, k))
                        dve.scalar_tensor_tensor(hm[:, s, :], psG[:, s, :], 0.0, expert_weight(base, k), ALU.max, ALU.mult)\
                            .then_inc(hid.sem, 1)

                def hidden_lo(base, k):
                    s = k % 2
                    dve.wait_ge(hid.sem, hid.at(base, k))
                    dve.wait_ge(hidh.sem, hidh.at(base, k))
                    dve.tensor_tensor(hl[:, s, :], hm[:, s, :], hh[:, s, :], ALU.subtract).then_inc(hidl.sem, 1)

                def step(base, k):
                    for j in split_at(base, k):
                        split_weights(base, j)
                    if gated:
                        dve.wait_ge(up.sem, up.at(base, k))
                        dve.tensor_tensor(g[:, k % 2, :], psG[:, k % 2, :], expert_weight(base, k), ALU.mult)\
                            .then_inc(gated_in.sem, 1)
                    if not isinstance(base, int) or k >= 1:
                        hidden_units(base, k - 1)
                        hidden_lo(base, k - 1)

                def end(base):
                    hidden_units(base, -1)
                    hidden_lo(base, -1)

                for free in (hid, hidl, down):
                    dve.sem_inc(free.sem, START)
                for k in range(2):
                    split_weights(0, k)
                steps(dve, step, end)
                dve.wait_ge(down.sem, down.at(0, STEPS - 1))
                dve.tensor_tensor(core.x[:, :, :], core.x[:, :, :], psY[:, :, :], ALU.add).then_inc(summed, 1)
                dve.wait_ge(summed, 1)


def stage_l1_self(core, norm):
    nc, d = core.nc, core.dram
    DH, NM = 64, 4
    J = NM + N
    DROPPED = J - 64
    PR = H // 2
    W = H * DH
    U = P // 8
    UH = U // 2
    QK_SCALE = 10.0
    halves = [slice(0, N), slice(N, P)]
    with ExitStack() as ctx:
        sb = lambda name, shape, dt=F32: ctx.enter_context(nc.sbuf_tensor(f"l1a_{name}", shape, dt))
        pb = lambda name, shape: ctx.enter_context(nc.psum_tensor(f"l1a_{name}", shape, F32))
        sem = lambda name: core.sem(f"l1a_{name}")
        w = sb("w", [P, DC, 4 * W])
        wo = sb("wo", [P, PR, D])
        bg = sb("bg", [1, W])
        hscale = sb("hscale", [P, H])
        wpre, wpost = sb("wpre", [P, P]), sb("wpost", [P, P])
        mask = sb("mask", [P, 4, U // 4 * J])
        mk, mks, mss = sb("mk", [H * NM, 2 * DH]), sb("mks", [H * NM, DH]), sb("mss", [H * NM, 1])
        mkT = sb("mkT", [P, H * NM])
        mv = sb("mv", [P, H, DH])
        memrows = sb("memrows", [P, NM])
        yt = sb("yt", [P, DC, P])
        qk, sq, ss = sb("qk", [P, 2, H, DH]), sb("sq", [P, 2, H, DH]), sb("ss", [P, 2, H])
        v, gate = sb("v", [P, W]), sb("gate", [P, H, DH])
        v_next, g_next = sb("v_next", [P, W]), sb("g_next", [P, H, DH])
        qkT = sb("qkT", [P, 2, PR, P])
        sT, sTm = sb("sT", [P, N, H]), sb("sTm", [P, P, H])
        r = sb("r", [P, U, J])
        s, drop = sb("s", [P, 4, U // 4 * J]), sb("drop", [P, U, J])
        s_rows = s[:, :, :].rearrange("p a (b j) -> p (a b) j", j=J)
        least = sb("least", [P, U, 8])
        low, den = sb("low", [P, U]), sb("den", [P, U])
        e = sb("e", [P, U, J])
        aT, aTm = sb("aT", [P, H, N]), sb("aTm", [P, H, P])
        o, oT = sb("o", [P, H, DH]), sb("oT", [P, PR, P])

        loaded, rest_loaded = sem("loaded"), sem("rest_loaded")
        setup = Steps(sem("setup"), "squares sums guarded scaled mkT")
        setup_root, setup_T = sem("setup_root"), sem("setup_T")
        vecA = Steps(sem("vector_a"), "yt sums guarded g0 normed g1 g2 v gate")
        vecB = Steps(sem("vector_b"), "sT r masked least drop dropped low shifted den rden e aT o")
        actA, actB = Steps(sem("scalar_a"), "qk v expgate qkT"), Steps(sem("scalar_b"), "sTm rm exp aTm oT")
        peA, peB = Steps(sem("tensor_a"), "qk vg qkT"), Steps(sem("tensor_b"), "sT r mixed aT out oT")
        roots = Steps(sem("roots"), "norms")
        pe_out, vec_out = Steps(sem("tensor_out"), "proj"), Steps(sem("vector_out"), "x")
        N_LOADS, N_REST = 16 * 3, 16 * 10

        def turns(eng, first, both, last):
            first(0)
            both(0)
            with eng.Fori(1, TT - 1) as i:
                both(i, True)
            last(TT - 1)

        def prefetch(sp):
            def load_w(k, to):
                sp.dma_start(w[:, :, k * W:(k + 1) * W],
                             d[("L1_attn_Wq", "L1_attn_Wk", "L1_attn_Wv", "L1_attn_Wg")[k]].rearrange("(c p) n -> p c n", p=P))\
                    .then_inc(to, 16)

            sp.dma_start(mk[:, 0:DH], d["L1_attn_mem_k"].rearrange("h m k -> (h m) k")).then_inc(loaded, 16)
            load_w(0, loaded)
            load_w(1, loaded)
            sp.dma_start(bg[:, :], d["L1_attn_bg"].partition_broadcast(1)).then_inc(rest_loaded, 16)
            load_w(2, rest_loaded)
            load_w(3, rest_loaded)
            sp.dma_start(hscale[:, :], d["c_head_scale"].partition_broadcast(P)).then_inc(rest_loaded, 16)
            sp.dma_start(memrows[:, :], d["c_memrows"]).then_inc(rest_loaded, 16)
            sp.dma_start(wpre[:, :], d["c_pre"]).then_inc(rest_loaded, 16)
            sp.dma_start(mask[:, :, :], d["c_rowmask"]).then_inc(rest_loaded, 16)
            sp.dma_start(wpost[:, :], d["c_post"]).then_inc(rest_loaded, 16)
            sp.dma_start(mv[:, :, :], d["c_mem_v"]).then_inc(rest_loaded, 16)
            sp.dma_start(wo[:, :, :], d["L1_attn_Wo"].rearrange("(c p) n -> p c n", p=P)).then_inc(rest_loaded, 16)

        norm(prefetch)
        psA, psB = pb("psA", [P, 4, 512]), pb("psB", [P, 4, 512])
        psA_blocks = psA[:, :, :].rearrange("p a (b q) -> p (a b) q", q=P)
        psB_blocks = psB[:, :, :].rearrange("p a (b q) -> p (a b) q", q=P)
        quarter = lambda k: slice(32 * k, 32 * k + NM)
        with nc.Block() as block:
            @block.gpsimd
            def _(pool):
                pool.wait_ge(setup.sem, setup.at("guarded"))
                pool.tensor_tensor(mss[:, :], mss[:, :], core.minus_half[0:H * NM, 0:1], ALU.pow).then_inc(setup_root, 1)
                def root(j):
                    pool.wait_ge(vecA.sem, vecA.at("guarded", j))
                    pool.tensor_tensor(ss[:, :, :], ss[:, :, :],
                                       core.minus_half[:, 0:2 * H].rearrange("p (a h) -> p a h", a=2), ALU.pow)\
                        .then_inc(roots.done("norms"), 1)

                turns(pool, root, lambda i, more=False: root(i + 1), lambda i: None)

            @block.tensor
            def _(pe):

                def project(parts):
                    for part in parts:
                        ps = psA[:, part % 4, :]
                        gates = part >= 6
                        for c in range(DC):
                            ins = pe.matmul(ps, yt[:, c, :], w[:, c, part * 512:(part + 1) * 512],
                                            start=(c == 0), stop=(c == 1 and not gates))
                        if gates:
                            ins = pe.matmul(ps, core.ones[0:1, :], bg[0:1, (part - 6) * 512:(part - 5) * 512],
                                            start=False, stop=True)
                    return ins

                def project_qk(j):
                    pe.wait_ge(vecA.sem, vecA.at("yt", j))
                    project(range(4)).then_inc(peA.done("qk"), 1)

                def transpose_qk(j):
                    pe.wait_ge(actA.sem, actA.at("v", j))
                    pe.wait_ge(vecA.sem, vecA.at("normed", j))
                    for a in range(2):
                        for pr in range(PR):
                            ins = pe.transpose(psA_blocks[:, a * PR + pr, :],
                                               qk[:, a, 2 * pr:2 * pr + 2, :].rearrange("p h k -> p (h k)"),
                                               core.ident[:, :])
                    ins.then_inc(peA.done("qkT"), 1)

                def project_vg(j):
                    pe.wait_ge(actA.sem, actA.at("qk", j))
                    project(range(4, 8)).then_inc(peA.done("vg"), 1)

                def score(i):
                    pe.wait_ge(setup.sem, setup.at("mkT"))
                    wait_apart(pe, actA.sem, actA.at("qkT", i), core.spare)
                    for pr in range(PR):
                        for odd, rows in enumerate(halves):
                            h = 2 * pr + odd
                            for half in halves:
                                pe.matmul(psB[half, odd, pr * N:(pr + 1) * N], qkT[rows, 1, pr, half],
                                          qkT[rows, 0, pr, half], start=True, stop=True)
                            ins = pe.matmul(psB[quarter(h // 4), 2 + odd, pr % 2 * P:(pr % 2 + 1) * P],
                                            mkT[rows, h * NM:(h + 1) * NM], qkT[rows, 0, pr, :], start=True, stop=True)
                    ins.then_inc(peB.done("sT"), 1)

                def to_rows(i):
                    pe.wait_ge(vecB.sem, vecB.at("sT", i))
                    pe.wait_ge(actB.sem, actB.at("sTm", i))
                    for u in range(U):
                        half, at = halves[u // UH], u % UH
                        pe.matmul(psB[:, u // UH, at * N:(at + 1) * N],
                                  sT[half, at * 8:(at + 1) * 8, :].rearrange("j q h -> j (q h)"),
                                  core.ident[half, half], start=True, stop=True)
                    for u in range(U):
                        ins = pe.matmul(psB[:, 2, u * NM:(u + 1) * NM],
                                        sTm[:, u * 8:(u + 1) * 8, :].rearrange("j q h -> j (q h)"),
                                        memrows[:, :], start=True, stop=True)
                    ins.then_inc(peB.done("r"), 1)

                def mix(i):
                    pe.wait_ge(vecB.sem, vecB.at("r", i))
                    pe.wait_ge(actB.sem, actB.at("rm", i))
                    for a in range(4):
                        ins = pe.matmul(psB[:, a, 0:U // 4 * J], wpre[:, :],
                                        r[:, a * 4:(a + 1) * 4, :].rearrange("p u j -> p (u j)"), start=True, stop=True)
                    ins.then_inc(peB.done("mixed"), 1)

                def mix_back(i):
                    pe.wait_ge(vecB.sem, vecB.at("e", i))
                    for u in range(U):
                        pe.matmul(psB_blocks[halves[u // UH], u % UH, :], e[:, u, NM:J], wpost[:, :], start=True, stop=True)
                        ins = pe.matmul(psB[quarter(u // 4), 2, u % 4 * P:(u % 4 + 1) * P], e[:, u, 0:NM], wpost[:, :],
                                        start=True, stop=True)
                    ins.then_inc(peB.done("aT"), 1)

                def weigh(i):
                    pe.wait_ge(vecB.sem, vecB.at("aT", i))
                    pe.wait_ge(vecA.sem, vecA.at("v", i))
                    pe.wait_ge(actB.sem, actB.at("aTm", i))
                    for h in range(H):
                        pe.matmul(psB[:, 2 + h // 8, h % 8 * DH:(h % 8 + 1) * DH], aTm[:, h, :], mv[:, h, :],
                                  start=(h % 8 == 0), stop=False, skip_group_check=True)
                    for h in range(H):
                        for half in halves:
                            ins = pe.matmul(psB[half, 2 + h // 8, h % 8 * DH:(h % 8 + 1) * DH], aT[half, h, :],
                                            v[half, h * DH:(h + 1) * DH], start=False, stop=(h % 8 == 7),
                                            skip_group_check=True)
                    ins.then_inc(peB.done("out"), 1)

                def transpose_o(i):
                    pe.wait_ge(vecB.sem, vecB.at("o", i))
                    for pr in range(PR):
                        ins = pe.transpose(psB_blocks[:, pr, :], o[:, 2 * pr:2 * pr + 2, :].rearrange("p h k -> p (h k)"),
                                           core.ident[:, :])
                    ins.then_inc(peB.done("oT"), 1)

                def project_out(i):
                    pe.wait_ge(actB.sem, actB.at("oT", i))
                    for pr in range(PR):
                        ins = pe.matmul(psB[:, 3, 0:D], oT[:, pr, :], wo[:, pr, :], start=(pr == 0), stop=(pr == PR - 1))
                    ins.then_inc(pe_out.done("proj"), 1)

                def first(j):
                    pe.wait_ge(loaded, N_LOADS)
                    project_qk(j)
                    pe.wait_ge(setup.sem, setup.at("scaled"))
                    pe.transpose(psB[:, 0, 0:H * NM], mk[:, :], core.ident[0:H * NM, 0:H * NM]).then_inc(setup_T, 1)
                    pe.wait_ge(rest_loaded, N_REST)
                    project_vg(j)
                    transpose_qk(j)

                def both(i, more=False):
                    score(i)
                    project_qk(i + 1)
                    to_rows(i)
                    mix(i)
                    project_vg(i + 1)
                    if more:
                        pe.wait_ge(vecB.sem, vecB.at("masked", i))
                        project_out(i - 1)
                    mix_back(i)
                    transpose_qk(i + 1)
                    weigh(i)
                    transpose_o(i)
                    wait_apart(pe, actB.sem, actB.at("oT", i), core.spare)

                def last(i):
                    for step in (score, to_rows, mix):
                        step(i)
                    pe.wait_ge(vecB.sem, vecB.at("masked", i))
                    project_out(i - 1)
                    for step in (mix_back, weigh, transpose_o, project_out):
                        step(i)

                turns(pe, first, both, last)

            @block.scalar
            def _(act):
                def take_qk(j):
                    act.wait_ge(peA.sem, peA.at("qk", j))
                    for out, what in ((sq, ACT.Square), (qk, ACT.Copy)):
                        ins = act.activation(out[:, :, :, :].rearrange("p a h k -> p (a h k)"),
                                             psA[:, :, :].rearrange("p a n -> p (a n)"), what)
                    ins.then_inc(actA.done("qk"), 1)

                def take_qkT(j):
                    act.wait_ge(peA.sem, peA.at("qkT", j))
                    act.activation(qkT[:, :, :, :].rearrange("p a h k -> p (a h k)"),
                                   psA[:, :, :].rearrange("p a n -> p (a n)"), ACT.Copy).then_inc(actA.done("qkT"), 1)

                def take_v(j):
                    act.wait_ge(peA.sem, peA.at("vg", j))
                    act.activation(v_next[:, :], psA[:, 0:2, :].rearrange("p a n -> p (a n)"), ACT.Copy)\
                        .then_inc(actA.done("v"), 1)

                def exp_gate(j):
                    act.wait_ge(vecA.sem, vecA.at("g0", j))
                    act.activation(g_next[:, :, :], g_next[:, :, :], ACT.Exp, scale=-1.0).then_inc(actA.done("expgate"), 1)

                def take_sTm(i):
                    act.wait_ge(peB.sem, peB.at("sT", i))
                    for k in range(4):
                        for odd in range(2):
                            ins = act.activation(
                                sTm[quarter(k), :, odd * PR + 2 * k:odd * PR + 2 * k + 2].rearrange("m q h -> m h q"),
                                psB[quarter(k), 2 + odd, 0:2 * P].rearrange("m (h q) -> m h q", q=P), ACT.Copy)
                    ins.then_inc(actB.done("sTm"), 1)

                def take_rm(i):
                    act.wait_ge(peB.sem, peB.at("r", i))
                    act.activation(r[:, :, 0:NM], psB[:, 2, 0:U * NM].rearrange("p (u m) -> p u m", m=NM), ACT.Copy,
                                   scale=QK_SCALE).then_inc(actB.done("rm"), 1)

                def exp(i):
                    act.wait_ge(vecB.sem, vecB.at("shifted", i))
                    act.activation(e[:, :, :], s_rows, ACT.Exp, scale=-1.0).then_inc(actB.done("exp"), 1)

                def take_aTm(i):
                    act.wait_ge(peB.sem, peB.at("aT", i))
                    for k in range(4):
                        ins = act.activation(aTm[quarter(k), :, 32 * k:32 * (k + 1)].rearrange("m h q -> m q h"),
                                             psB[quarter(k), 2, :].rearrange("m (q h) -> m q h", h=H), ACT.Copy)
                    ins.then_inc(actB.done("aTm"), 1)

                def take_oT(i):
                    act.wait_ge(peB.sem, peB.at("oT", i))
                    act.activation(oT[:, :, :], psB_blocks[:, 0:PR, :], ACT.Copy).then_inc(actB.done("oT"), 1)

                def first(j):
                    for step in (take_qk, take_v, exp_gate, take_qkT):
                        step(j)
                    act.wait_ge(setup.sem, setup.at("mkT"))

                def both(i, more=False):
                    take_sTm(i)
                    take_qk(i + 1)
                    take_rm(i)
                    exp(i)
                    take_v(i + 1)
                    exp_gate(i + 1)
                    take_aTm(i)
                    take_qkT(i + 1)
                    take_oT(i)

                def last(i):
                    for step in (take_sTm, take_rm, exp, take_aTm, take_oT):
                        step(i)

                turns(act, first, both, last)

            @block.vector
            def _(dve):
                def memory_keys():
                    dve.memset(sTm[:, :, :], 0.0)
                    dve.memset(aTm[:, :, :], 0.0)
                    dve.wait_ge(loaded, N_LOADS)
                    dve.tensor_tensor(mks[:, :], mk[:, 0:DH], mk[:, 0:DH], ALU.mult).then_inc(setup.done("squares"), 1)
                    dve.wait_ge(setup.sem, setup.at("squares"))
                    dve.tensor_reduce(mss[:, :], mks[:, :], AX.X, ALU.add).then_inc(setup.done("sums"), 1)
                    dve.wait_ge(setup.sem, setup.at("sums"))
                    dve.tensor_scalar(mss[:, :], mss[:, :], 1e-24, None, ALU.max).then_inc(setup.done("guarded"), 1)
                    dve.wait_ge(setup_root, 1)
                    dve.tensor_scalar(mk[:, DH:2 * DH], mk[:, 0:DH], mss[:, 0:1], None, ALU.mult)
                    dve.tensor_scalar(mk[:, 0:DH], mk[:, 0:DH], mss[:, 0:1], None, ALU.mult).then_inc(setup.done("scaled"), 1)
                    dve.wait_ge(setup_T, 1)
                    dve.tensor_copy(mkT[:, :], psB[:, 0, 0:H * NM]).then_inc(setup.done("mkT"), 1)

                def take_y(j):
                    dve.tensor_copy(yt[:, :, :], core.yT[:, :, bass.ds(j * P, P)]).then_inc(vecA.done("yt"), 1)

                def norms(j):
                    dve.wait_ge(actA.sem, actA.at("qk", j))
                    dve.tensor_reduce(ss[:, :, :], sq[:, :, :, :], AX.X, ALU.add).then_inc(vecA.done("sums"), 1)
                    dve.wait_ge(vecA.sem, vecA.at("sums", j))
                    dve.tensor_scalar(ss[:, :, :], ss[:, :, :], 1e-24, None, ALU.max).then_inc(vecA.done("guarded"), 1)

                def normalise_qk(j):
                    dve.wait_ge(roots.sem, roots.at("norms", j))
                    dve.tensor_tensor(qk[:, :, :, :], qk[:, :, :, :], ss[:, :, :, None].to_broadcast([P, 2, H, DH]),
                                      ALU.mult).then_inc(vecA.done("normed"), 1)

                def clamp_gate(j):
                    dve.wait_ge(peA.sem, peA.at("vg", j))
                    dve.tensor_scalar(g_next[:, :, :].rearrange("p h k -> p (h k)"),
                                      psA[:, 2:4, :].rearrange("p a n -> p (a n)"), -80.0, None, ALU.max)\
                        .then_inc(vecA.done("g0"), 1)

                def add_one(j):
                    dve.wait_ge(actA.sem, actA.at("expgate", j))
                    dve.tensor_scalar(g_next[:, :, :], g_next[:, :, :], 1.0, None, ALU.add).then_inc(vecA.done("g1"), 1)

                def invert_gate(j):
                    dve.wait_ge(vecA.sem, vecA.at("g1", j))
                    dve.reciprocal(g_next[:, :, :], g_next[:, :, :]).then_inc(vecA.done("g2"), 1)

                def keep_v(j):
                    dve.wait_ge(actA.sem, actA.at("v", j))
                    dve.tensor_copy(v[:, :], v_next[:, :]).then_inc(vecA.done("v"), 1)

                def scale_gate(j):
                    dve.wait_ge(vecA.sem, vecA.at("g2", j))
                    dve.tensor_tensor(gate[:, :, :], g_next[:, :, :], hscale[:, :, None].to_broadcast([P, H, DH]), ALU.mult)\
                        .then_inc(vecA.done("gate"), 1)

                def take_sT(i):
                    dve.wait_ge(peB.sem, peB.at("sT", i))
                    for odd in range(2):
                        ins = dve.tensor_copy(sT[:, :, odd * PR:(odd + 1) * PR].rearrange("p q h -> p h q"),
                                              psB[:, odd, :].rearrange("p (b q) -> p b q", q=N))
                    ins.then_inc(vecB.done("sT"), 1)

                def take_r(i):
                    dve.wait_ge(peB.sem, peB.at("r", i))
                    dve.tensor_scalar(r[:, :, NM:J], psB[:, 0:2, :].rearrange("p a (b j) -> p (a b) j", j=N), QK_SCALE, None,
                                      ALU.mult).then_inc(vecB.done("r"), 1)

                def softmax(i):
                    dve.wait_ge(peB.sem, peB.at("mixed", i))
                    dve.scalar_tensor_tensor(s[:, :, :], psB[:, :, 0:U // 4 * J], -1.0, mask[:, :, :], ALU.mult, ALU.add)\
                        .then_inc(vecB.done("masked"), 1)
                    wait_apart(dve, vecB.sem, vecB.at("masked", i), core.spare)
                    for u in range(U):
                        ins = dve.max(least[:, u, :], s_rows[:, u, :])
                    ins.then_inc(vecB.done("least"), 1)
                    dve.wait_ge(vecB.sem, vecB.at("least", i))
                    dve.tensor_tensor(drop[:, :, :], s_rows, least[:, :, DROPPED:DROPPED + 1].to_broadcast([P, U, J]),
                                      ALU.is_gt).then_inc(vecB.done("drop"), 1)
                    dve.wait_ge(vecB.sem, vecB.at("drop", i))
                    dve.scalar_tensor_tensor(s_rows, drop[:, :, :], BIG, s_rows, ALU.mult, ALU.add)\
                        .then_inc(vecB.done("dropped"), 1)
                    dve.wait_ge(vecB.sem, vecB.at("dropped", i))
                    dve.tensor_reduce(low[:, :], s_rows, AX.X, ALU.min).then_inc(vecB.done("low"), 1)
                    dve.wait_ge(vecB.sem, vecB.at("low", i))
                    dve.tensor_tensor(s_rows, s_rows, low[:, :, None].to_broadcast([P, U, J]), ALU.subtract)\
                        .then_inc(vecB.done("shifted"), 1)

                def normalise(i):
                    dve.wait_ge(actB.sem, actB.at("exp", i))
                    dve.tensor_reduce(den[:, :], e[:, :, :], AX.X, ALU.add).then_inc(vecB.done("den"), 1)
                    dve.wait_ge(vecB.sem, vecB.at("den", i))
                    dve.reciprocal(den[:, :], den[:, :]).then_inc(vecB.done("rden"), 1)
                    dve.wait_ge(vecB.sem, vecB.at("rden", i))
                    dve.tensor_tensor(e[:, :, :], e[:, :, :], den[:, :, None].to_broadcast([P, U, J]), ALU.mult)\
                        .then_inc(vecB.done("e"), 1)

                def take_aT(i):
                    dve.wait_ge(peB.sem, peB.at("aT", i))
                    dve.tensor_copy(aT[:, :, :].rearrange("p h q -> p q h"),
                                    psB[:, 0:2, :].rearrange("p a (b h) -> p (a b) h", h=H)).then_inc(vecB.done("aT"), 1)

                def take_o(i):
                    dve.wait_ge(peB.sem, peB.at("out", i))
                    dve.wait_ge(vecA.sem, vecA.at("gate", i))
                    dve.tensor_tensor(o[:, :, :].rearrange("p h k -> p (h k)"), psB[:, 2:4, :].rearrange("p a n -> p (a n)"),
                                      gate[:, :, :].rearrange("p h k -> p (h k)"), ALU.mult).then_inc(vecB.done("o"), 1)

                def residual(i):
                    dve.wait_ge(pe_out.sem, pe_out.at("proj", i))
                    xi = core.x[:, bass.ds(i, 1), :].rearrange("p a n -> p (a n)")
                    dve.tensor_tensor(xi, xi, psB[:, 3, 0:D], ALU.add).then_inc(vec_out.done("x"), 1)

                def first(j):
                    take_y(j)
                    memory_keys()
                    norms(j)
                    dve.wait_ge(rest_loaded, N_REST)
                    for step in (clamp_gate, normalise_qk, add_one, invert_gate, keep_v, scale_gate):
                        step(j)

                def both(i, more=False):
                    take_y(i + 1)
                    take_sT(i)
                    norms(i + 1)
                    take_r(i)
                    softmax(i)
                    normalise(i)
                    clamp_gate(i + 1)
                    normalise_qk(i + 1)
                    add_one(i + 1)
                    if more:
                        residual(i - 1)
                    take_aT(i)
                    invert_gate(i + 1)
                    take_o(i)
                    keep_v(i + 1)
                    dve.wait_ge(vecB.sem, vecB.at("o", i))
                    scale_gate(i + 1)

                def last(i):
                    for step in (take_sT, take_r, softmax, normalise):
                        step(i)
                    residual(i - 1)
                    for step in (take_aT, take_o, residual):
                        step(i)

                turns(dve, first, both, last)
                dve.wait_ge(vec_out.sem, vec_out.at("x", TT - 1))


class Bank:

    def __init__(self, ps, filled, taken, names, banks=1):
        self.ps, self.filled, self.taken, self.names, self.banks = ps, filled, taken, names, banks

    def bank(self, name):
        return self.ps[:, self.names.index(name) % self.banks, :]

    def full(self, name, turn=0):
        return turn * len(self.names) + (self.names.index(name) + 1)

    def free(self, name, turn=0):
        if self.banks > 1:
            return max(self.names.index(name) + 2 - self.banks, 1)
        return turn * len(self.names) + (self.names.index(name) + 1)

    def left(self, name, turn=0, ago=0):
        return turn * len(self.names) + (self.names.index(name) + 2 - ago * len(self.names))


def stage_l1_cross(core, norm):
    nc, d = core.nc, core.dram
    DH = 64
    W = H * DH
    PR = H // 2
    HN = H * N
    G = HN // P
    VW = CD + 1
    SCALE = float(DH) ** -0.5
    halves = [slice(0, N), slice(N, P)]

    def tiles(k):
        return [m for m in range(KT) if m * 10 // KT == k]

    POST_T = {2: ["A0"], 4: ["V0"], 6: ["A1"], 8: ["V1"]}
    POST_M = {2: ["B0"], 6: ["B1"]}
    t_jobs = lambda n, main: [f"t{m}" for m in tiles(n - 2)] + POST_T.get(n, []) if main else [f"t{n - 1}"] * (1 <= n <= KT)
    m_jobs = lambda n, main: [f"m{m}.{c}" for m in tiles(n - 3) for c in range(2)] + POST_M.get(n, []) if main else \
        [f"m{n - 2}.{c}" for c in range(2)] * (2 <= n < KT + 2)
    t_names = lambda main: [j for n in range(KT + 2) for j in t_jobs(n, main)] + ["sh1"]
    m_names = lambda main: [j for n in range(KT + 2) for j in m_jobs(n, main)] + ["sh0"]

    with ExitStack() as ctx:
        sb = lambda name, shape, dt=F32, to=ctx: to.enter_context(nc.sbuf_tensor(f"l1x_{name}", shape, dt))
        sem = lambda name: core.sem(f"l1x_{name}")
        qAh, qAl = sb("qAh", [P, B + 1, HN], F16), sb("qAl", [P, B, HN], F16)
        qSB = sb("qSB", [P, B + 1, HN], F16)
        q5 = sb("q5", [DH + 1, B + 1, HN], F16)
        wvA, wvB = sb("wvA", [P, W]), sb("wvB", [CB, W])
        gam, bet = sb("gam", [P, CD]), sb("bet", [P, CD])
        loaded, w_loaded = sem("loaded"), sem("w_loaded")

        raw = sb("raw", [P, KT, CD])
        SPLIT = 7
        raw_loaded = [sem("raw_loaded0"), sem("raw_loaded1")]

        def load_context(sp, j, part):
            tiles = slice(0, SPLIT) if part == 0 else slice(SPLIT, KT)
            src = d["c_ctx"][j, :, :] if isinstance(j, int) else d["c_ctx"][bass.ds(j, 1), :, :].rearrange("a n k -> (a n) k")
            sp.dma_start(raw[:, tiles, :], src.rearrange("(n p) k -> p n k", p=P)[:, tiles, :]).then_inc(raw_loaded[part], 16)

        stats, aggr, rstd = sb("stats", [P, KT, 6]), sb("aggr", [P, KT, 2]), sb("rstd", [P, KT])
        statted, aggred = Count(sem("statted"), KT), Count(sem("aggred"), KT)
        eps_added, rooted = Count(sem("eps_added"), KT), Count(sem("rooted"), KT)
        zeroed, scaled = Count(sem("zeroed"), KT), Count(sem("scaled"), KT)
        biased = Count(sem("biased"), KT)

        def stage0(dve, m, j):
            dve.wait_ge(raw_loaded[m >= SPLIT], j * 16 + 16)
            dve.bn_stats(stats[:, m, :], raw[:, m, :]).then_inc(statted.sem, 1)
            wait_apart(dve, statted.sem, statted.at(j, m), core.spare)
            dve.bn_aggr(aggr[:, m, :], stats[:, m, :]).then_inc(aggred.sem, 1)

        def stage1(dve, m, j):
            dve.wait_ge(rooted.sem, rooted.at(j, m))
            dve.tensor_scalar(raw[:, m, :], raw[:, m, :], aggr[:, m, 0:1], rstd[:, m:m + 1],
                              ALU.subtract, ALU.mult).then_inc(zeroed.sem, 1)
            dve.wait_ge(zeroed.sem, zeroed.at(j, m))
            dve.tensor_tensor(raw[:, m, :], raw[:, m, :], gam[:, :], ALU.mult).then_inc(scaled.sem, 1)

        def root(pool, m, j):
            wait_apart(pool, aggred.sem, aggred.at(j, m), core.spare)
            pool.tensor_scalar(rstd[:, m:m + 1], aggr[:, m, 1:2], EPS, None, ALU.add).then_inc(eps_added.sem, 1)
            pool.wait_ge(eps_added.sem, eps_added.at(j, m))
            pool.tensor_tensor(rstd[:, m:m + 1], rstd[:, m:m + 1], core.minus_half[:, 0:1], ALU.pow)\
                .then_inc(rooted.sem, 1)

        def add_beta(pool, m, j):
            pool.wait_ge(scaled.sem, scaled.at(j, m))
            pool.tensor_tensor(raw[:, m, :], raw[:, m, :], bet[:, :], ALU.add).then_inc(biased.sem, 1)

        q_done, q_taken, folded, q_hi, q_lo = sem("q_done"), sem("q_taken"), sem("folded"), sem("q_hi"), sem("q_lo")
        with ExitStack() as inner:
            wq, wkT = sb("wq", [P, DC, W], F32, inner), sb("wkT", [P, PR, 2 * P], F32, inner)
            qT = sb("qT", [P, PR, 2, TOK], F32, inner)
            zeroed_q = sem("zeroed_q")
            def prefetch(sp):
                sp.dma_start(wq[:, :, :], d["L1_xattn_Wq"].rearrange("(c p) n -> p c n", p=P)).then_inc(loaded, 16)
                sp.dma_start(wkT[:, :, :], d["c_wkT"].rearrange("(a p) n -> p a n", p=P)).then_inc(loaded, 16)
                sp.dma_start(gam[:, :], d["L1_xattn_g_c"].partition_broadcast(P)).then_inc(w_loaded, 16)
                sp.dma_start(bet[:, :], d["L1_xattn_b_c"].partition_broadcast(P)).then_inc(w_loaded, 16)
                sp.dma_start(wvA[:, :], d["L1_xattn_Wv"][0:P, :]).then_inc(w_loaded, 16)
                sp.dma_start(wvB[:, :], d["L1_xattn_Wv"][P:CD, :]).then_inc(w_loaded, 16)
                load_context(sp, 0, 0)
                load_context(sp, 0, 1)

            norm(prefetch)
            psQ = inner.enter_context(nc.psum_tensor("l1x_psQ", [P, PR, TOK], F32))
            psF = psQ[:, :, :].rearrange("p (s ab) n -> p s ab n", ab=2)
            with nc.Block() as block:
                @block.gpsimd
                def _(pool):
                    for m in range(KT):
                        root(pool, m, 0)
                    for m in range(KT):
                        add_beta(pool, m, 0)

                @block.tensor
                def _(pe):
                    pe.wait_ge(loaded, 32)
                    for pr in range(PR):
                        for c in range(DC):
                            ins = pe.matmul(psQ[:, pr, :], wq[:, c, pr * P:(pr + 1) * P], core.yT[:, c, :],
                                            start=(c == 0), stop=(c == DC - 1))
                        ins.then_inc(q_done, 1)
                    for h in range(H):
                        pr = h // 2
                        pe.wait_ge(q_taken, max(pr + 1, min(2 * h + 2, PR)))
                        if h == 0:
                            pe.wait_ge(zeroed_q, 1)
                        if h >= 4:
                            pe.wait_ge(q_lo, h - 3)
                        for ab in range(2):
                            ins = pe.matmul(psF[:, h % 4, ab, :], wkT[:, pr, ab * P:(ab + 1) * P], qT[:, pr, h % 2, :],
                                            start=True, stop=True)
                        ins.then_inc(folded, 1)

                @block.scalar
                def _(act):
                    for pr in range(PR):
                        act.wait_ge(q_done, pr + 1)
                        for odd, r in enumerate(halves):
                            ins = act.activation(qT[r, pr, odd, :], psQ[r, pr, :], ACT.Copy)
                        ins.then_inc(q_taken, 1)
                    for h in range(H):
                        cols = slice(h * N, (h + 1) * N)
                        act.wait_ge(folded, h + 1)
                        for ab, q in enumerate((qAh, qSB)):
                            ins = act.activation(q[:, 0:B, cols], psF[:, h % 4, ab, :].rearrange("p (b q) -> p b q", q=N),
                                                 ACT.Copy, scale=SCALE)
                        ins.then_inc(q_hi, 1)

                @block.vector
                def _(dve):
                    for q in (qAh, qSB, q5):
                        dve.memset(q[:, B, :], 0.0)
                    for odd, r in enumerate(halves):
                        ins = dve.memset(qT[r, :, 1 - odd, :], 0.0)
                    ins.then_inc(zeroed_q, 1)
                    for m in range(KT):
                        stage0(dve, m, 0)
                    dve.wait_ge(w_loaded, 64)
                    for m in range(KT):
                        stage1(dve, m, 0)
                    for h in range(H):
                        cols = slice(h * N, (h + 1) * N)
                        dve.wait_ge(q_hi, h + 1)
                        for rows, ab, q, hi in ((slice(0, P), 0, qAl, qAh), (slice(0, CB), 1, q5, qSB)):
                            ins = dve.scalar_tensor_tensor(
                                q[rows, 0:B, cols], psF[rows, h % 4, ab, :].rearrange("p (b q) -> p b q", q=N), SCALE,
                                hi[rows, 0:B, cols], ALU.mult, ALU.subtract)
                        ins.then_inc(q_lo, 1)

        ch, cl = sb("ch", [P, 2, KT, VW], F16), sb("cl", [P, 2, KT, CD], F16)
        ct = sb("ct", [P, 2, KT, 3 * P], F16)
        c5 = sb("c5", [DH + 1, 2, KT, P], F16)
        tops, top = sb("tops", [P, G, KT]), sb("top", [P, G])
        shift = sb("shift", [P, G, DH + 1], F16)
        e32 = sb("e32", [P, 2, 512])
        eh, el = sb("eh", [P, 2, HN], F16), sb("el", [P, 2, HN], F16)
        rden = sb("rden", [P, G])
        a = sb("a", [P, G, CD])
        aT = core.yT
        outT = sb("outT", [P, PR, B + 1, N])

        c_hi, c_lo = Count(sem("c_hi"), KT), Count(sem("c_lo"), KT)
        topped, shifted = Count(sem("topped"), 1), Count(sem("shifted"), 1)
        scored = Count(sem("scored"), 2 * KT)
        exped, e_split = Count(sem("exped"), 2 * KT, 2), Count(sem("e_split"), 2 * KT, 2)
        weighed = Count(sem("weighed"), KT, 2)
        rdenned, out_taken = Count(sem("rdenned"), 1), Count(sem("out_taken"), 1, 1)
        made = sem("made")

        for main in (False, True):
            name = "loop" if main else "first"
            with ExitStack() as pctx, nc.Block() as block:
                bank = lambda what, n=1: pctx.enter_context(nc.psum_tensor(f"l1x_{what}_{name}", [P, n * 512], F32))
                psS, psO = (bank("psS", 2), bank("psO", 4)) if main else (None, None)
                banks = (1, 1) if main else (2, 4)
                split_banks = lambda ps: ps[:, :].rearrange("p (k n) -> p k n", n=512)
                bT = Bank(split_banks(bank("psT", banks[0])), sem(f"T_filled_{name}"), sem(f"T_taken_{name}"),
                          t_names(main), banks[0])
                bM = Bank(split_banks(bank("psM", banks[1])), sem(f"M_filled_{name}"), sem(f"M_taken_{name}"),
                          m_names(main), banks[1])

                def turns(eng, body):
                    if not main:
                        body(None, 0, 0, 0)
                        return
                    with eng.Fori(0, B // 2) as i:
                        for s in range(2):
                            b = i * 2 + s
                            body(b, i * 2 + (s + 1), 1 - s, b)

                @block.sync
                def _(sp):
                    if not main:
                        sp.wait_ge(c_lo.sem, c_lo.at(0, SPLIT - 1))
                        load_context(sp, 1, 0)
                        sp.wait_ge(c_lo.sem, c_lo.at(0, KT - 1))
                        load_context(sp, 1, 1)
                        return
                    with sp.Fori(0, B - 1) as b:
                        sp.wait_ge(c_lo.sem, c_lo.at(b, KT + SPLIT - 1))
                        load_context(sp, b + 2, 0)
                        sp.wait_ge(c_lo.sem, c_lo.at(b, KT + KT - 1))
                        load_context(sp, b + 2, 1)

                @block.gpsimd
                def _(pool):
                    def body(b, j, slot, turn):
                        for n in range(KT):
                            for m in tiles(n):
                                root(pool, m, j)
                            for m in tiles(n - 1):
                                add_beta(pool, m, j)
                    if main:
                        turns(pool, body)

                @block.tensor
                def _(pe):
                    def side(job, b, j, slot, turn):
                        kind = job[0]
                        ps = (bT if kind in "tAV" else bM).bank(job)
                        if kind == "t":
                            m = int(job[1:])
                            pe.wait_ge(c_lo.sem, c_lo.at(j, m))
                            pe.wait_ge(bT.taken, bT.free(job, turn))
                            pe.matmul(ps[:, 0:P], ch[:, slot, m, 0:P], core.ident16[:, :], start=True, stop=True)
                            pe.matmul(ps[:, P:2 * P], cl[:, slot, m, 0:P], core.ident16[:, :], start=True, stop=True)
                            for rows, c in ((halves[0], ch), (halves[1], cl)):
                                ins = pe.matmul(ps[rows, 2 * P:3 * P], c[:, slot, m, P:CD], core.ident16[:, :],
                                                start=True, stop=True)
                            ins.then_inc(bT.filled, 1)
                        elif kind == "m":
                            m, c = [int(v) for v in job[1:].split(".")]
                            keys = P if m < KT - 1 else TAIL
                            pe.wait_ge(bT.taken, bT.left(f"t{m}", turn))
                            pe.wait_ge(bM.taken, bM.free(job, turn))
                            for g in range(4):
                                cols = slice((4 * c + g) * P, (4 * c + g + 1) * P)
                                for i, (q, x) in enumerate(((qAh, 0), (qSB, 2))):
                                    lhs = q[:, j, cols] if isinstance(j, int) else \
                                        q[:, bass.ds(j, 1), cols].rearrange("p a n -> p (a n)")
                                    ins = pe.matmul(ps[:, g * P:g * P + keys], lhs, ct[:, slot, m, x * P:x * P + keys],
                                                    start=(i == 0), stop=(i == 1))
                            ins.then_inc(bM.filled, 1)
                        elif kind in "AB":
                            half = int(job[1])
                            bank, cols, rows = (bT, slice(0, P), slice(0, P)) if kind == "A" else \
                                (bM, slice(P, CD), slice(0, CB))
                            pe.wait_ge(out_taken.sem, out_taken.at(b, -1))
                            wait_apart(pe, bank.taken, bank.free(job, turn), core.spare)
                            for g in range(4):
                                ins = pe.transpose(ps[rows, g * P:(g + 1) * P], a[:, 4 * half + g, cols], core.ident[:, :])
                            ins.then_inc(bank.filled, 1)
                        elif kind == "V":
                            half = int(job[1])
                            pe.wait_ge(bT.taken, bT.free(job, turn))
                            pe.wait_ge(bM.taken, bM.left(f"B{half}", turn))
                            for k in range(8):
                                h = 8 * half + k
                                out = ps[halves[k % 2], k // 2 * N:(k // 2 + 1) * N]
                                pe.matmul(out, wvA[:, h * DH:(h + 1) * DH], aT[:, 0, k * N:(k + 1) * N], start=True, stop=False)
                                ins = pe.matmul(out, wvB[:, h * DH:(h + 1) * DH], aT[0:CB, 1, k * N:(k + 1) * N],
                                                start=False, stop=True)
                            ins.then_inc(bT.filled, 1)

                    def spread_shift(j, turn):
                        pe.wait_ge(shifted.sem, shifted.at(j, 0))
                        for c, bank in enumerate((bM, bT)):
                            ps = bank.bank(f"sh{c}")
                            pe.wait_ge(bank.taken, bank.free(f"sh{c}", turn))
                            for g in range(4):
                                ins = pe.matmul(ps[0:DH + 1, g * P:(g + 1) * P], shift[:, 4 * c + g, :], core.ident16[:, :],
                                                start=True, stop=True)
                            ins.then_inc(bank.filled, 1)

                    def score(n, c, b, s):
                        u, keys = 2 * n + c, (P if n < KT - 1 else TAIL)
                        if n == 0 and c == 0:
                            pe.wait_ge(bM.taken, bM.left("sh0", b, 1))
                            pe.wait_ge(bT.taken, bT.left("sh1", b, 1))
                        pe.wait_ge(exped.sem, exped.at(b, u - 2))
                        passes = ((ct, 0, qAh, P), (ct, P, qAh, P), (ct, 0, qAl, P), (ct, 2 * P, qSB, P), (c5, 0, q5, DH + 1))
                        for i, (x, k, q, rows) in enumerate(passes):
                            ins = pe.matmul(psS[0:keys, c * 512:(c + 1) * 512], x[0:rows, s, n, k:k + keys],
                                            q[0:rows, bass.ds(b, 1), c * 512:(c + 1) * 512].rearrange("p a n -> p (a n)"),
                                            start=(i == 0), stop=(i == len(passes) - 1))
                        ins.then_inc(scored.sem, 1)

                    def weigh(n, c, b, s):
                        keys, e = (P if n < KT - 1 else TAIL), (s + n) % 2
                        pe.wait_ge(e_split.sem, e_split.at(b, 2 * n + c))
                        if n == 0 and c == 0:
                            pe.wait_ge(out_taken.sem, out_taken.at(b, -1))
                        for g in range(4 * c, 4 * c + 4):
                            cols, o = slice(g * P, (g + 1) * P), g // 2 * 512 + g % 2 * VW
                            first = n == 0 and g % 2 == 0
                            pe.matmul(psO[:, o:o + VW], eh[0:keys, e, cols], ch[0:keys, s, n, :],
                                      start=first, stop=False, skip_group_check=True)
                            pe.matmul(psO[:, o:o + CD], eh[0:keys, e, cols], cl[0:keys, s, n, :],
                                      start=False, stop=False, skip_group_check=True)
                            ins = pe.matmul(psO[:, o:o + VW], el[0:keys, e, cols], ch[0:keys, s, n, :],
                                            start=False, stop=(n == KT - 1), skip_group_check=True)
                        if c == 1:
                            ins.then_inc(weighed.sem, 1)

                    def body(b, j, slot, turn):
                        s = 1 - slot
                        for n in range(KT if main else KT + 2):
                            ms, ts = m_jobs(n, main), t_jobs(n, main)
                            work = []
                            if main:
                                work = [(score, n, 0), (score, n, 1)] + ([(weigh, n - 1, 0), (weigh, n - 1, 1)] if n else [])
                            for k in range(max(len(work), len(ms), len(ts))):
                                if k < len(ms):
                                    side(ms[k], b, j, slot, turn)
                                if k < len(work):
                                    what, tile, c = work[k]
                                    what(tile, c, b, s)
                                if k < len(ts):
                                    side(ts[k], b, j, slot, turn)
                        if main:
                            weigh(KT - 1, 0, b, s)
                        spread_shift(j, turn)
                        if main:
                            weigh(KT - 1, 1, b, s)

                    if not main:
                        pe.wait_ge(made, 1)
                    turns(pe, body)

                @block.scalar
                def _(act):
                    def exp(n, c, b, s):
                        u, keys, e = 2 * n + c, (P if n < KT - 1 else TAIL), (s + n) % 2
                        act.wait_ge(weighed.sem, weighed.at(b, n - 2))
                        act.wait_ge(e_split.sem, e_split.at(b, u - 2))
                        act.wait_ge(scored.sem, scored.at(b, u))
                        ps = psS[0:keys, c * 512:(c + 1) * 512]
                        act.activation(e32[0:keys, c, :], ps, ACT.Exp)
                        act.activation(eh[0:keys, e, c * 512:(c + 1) * 512], ps, ACT.Exp).then_inc(exped.sem, 1)

                    def take(job, b, j, slot, turn):
                        act.wait_ge(bT.filled, bT.full(job, turn))
                        ps = bT.bank(job)
                        if job[0] == "t":
                            m = int(job[1:])
                            act.activation(ct[:, slot, m, :], ps[:, 0:3 * P], ACT.Copy)
                            act.activation(c5[0:CB, slot, m, :], ps[0:CB, 2 * P:3 * P], ACT.Copy).then_inc(bT.taken, 1)
                        elif job[0] == "A":
                            act.activation(aT[:, 0, :], ps[:, :], ACT.Copy).then_inc(bT.taken, 1)

                    def body(b, j, slot, turn):
                        s = 1 - slot
                        if main:
                            act.wait_ge(weighed.sem, weighed.at(b, -1))
                        for n in range(KT if main else KT + 2):
                            ts = t_jobs(n, main)
                            for k in range(max(2, len(ts))):
                                if main and k < 2:
                                    exp(n, k, b, s)
                                if k < len(ts) and ts[k][0] != "V":
                                    take(ts[k], b, j, slot, turn)
                            for m in (tiles(n - 1) if main else [n] * (n < KT)):
                                act.wait_ge(biased.sem, biased.at(j, m))
                                act.activation(ch[:, slot, m, 0:CD], raw[:, m, :], ACT.Copy).then_inc(c_hi.sem, 1)
                        for c, bank in enumerate((bM, bT)):
                            ps = bank.bank(f"sh{c}")
                            wait_apart(act, bank.filled, bank.full(f"sh{c}", turn), core.spare)
                            out = q5[DH:DH + 1, j, :] if isinstance(j, int) else \
                                q5[DH:DH + 1, bass.ds(j, 1), :].rearrange("p a n -> p (a n)")
                            act.activation(out[:, c * 512:(c + 1) * 512], ps[DH:DH + 1, :], ACT.Copy)\
                                .then_inc(bank.taken, 1)
                    turns(act, body)

                @block.vector
                def _(dve):
                    def stage2(m, j, slot):
                        dve.wait_ge(c_hi.sem, c_hi.at(j, m))
                        dve.tensor_tensor(cl[:, slot, m, :], raw[:, m, :], ch[:, slot, m, 0:CD], ALU.subtract)\
                            .then_inc(c_lo.sem, 1)

                    def take(job, turn):
                        ps = (bT if job[0] == "V" else bM).bank(job)
                        if job[0] == "B":
                            if job == "B1":
                                dve.wait_ge(bT.filled, bT.full("V0", turn))
                            dve.wait_ge(bM.filled, bM.full(job, turn))
                            dve.tensor_copy(aT[0:CB, 1, :], ps[0:CB, :]).then_inc(bM.taken, 1)
                        elif job[0] == "V":
                            half = int(job[1])
                            dve.wait_ge(bT.filled, bT.full(job, turn))
                            dve.tensor_scalar(
                                outT[:, 4 * half:4 * half + 4, bass.ds(turn, 1), :].rearrange("p k a q -> p k (a q)"),
                                ps[:, 0:4 * N].rearrange("p (k q) -> p k q", q=N), 1.0, None, ALU.mult)\
                                .then_inc(bT.taken, 1)
                        else:
                            m, c = [int(v) for v in job[1:].split(".")]
                            keys = P if m < KT - 1 else TAIL
                            dve.wait_ge(bM.filled, bM.full(job, turn))
                            dve.tensor_reduce(tops[:, 4 * c:4 * c + 4, m],
                                              ps[:, :].rearrange("p (g k) -> p g k", k=P)[:, :, 0:keys],
                                              AX.X, ALU.max).then_inc(bM.taken, 1)

                    def lo_half(n, c, b, s):
                        u, keys, e = 2 * n + c, (P if n < KT - 1 else TAIL), (s + n) % 2
                        dve.wait_ge(exped.sem, exped.at(b, u))
                        dve.tensor_tensor(el[0:keys, e, c * 512:(c + 1) * 512], e32[0:keys, c, :],
                                          eh[0:keys, e, c * 512:(c + 1) * 512], ALU.subtract).then_inc(e_split.sem, 1)

                    def body(b, j, slot, turn):
                        s = 1 - slot
                        for n in range(KT if main else KT + 2):
                            ms, ts = m_jobs(n, main), t_jobs(n, main)
                            for job in ms[0:2]:
                                take(job, turn)
                            if main:
                                for m in tiles(n):
                                    stage0(dve, m, j)
                                lo_half(n, 0, b, s)
                                for m in tiles(n - 1):
                                    stage1(dve, m, j)
                            for job in ms[2:]:
                                take(job, turn)
                            if main:
                                lo_half(n, 1, b, s)
                            for job in ts:
                                if job[0] == "V":
                                    take(job, turn)
                            for m in (tiles(n - 1) if main else [n] * (n < KT)):
                                stage2(m, j, slot)
                        dve.wait_ge(bM.taken, bM.left(bM.names[-2], turn))
                        dve.tensor_reduce(top[:, :], tops[:, :, :], AX.X, ALU.max).then_inc(topped.sem, 1)
                        dve.wait_ge(topped.sem, topped.at(j, 0))
                        dve.tensor_scalar(shift[:, :, DH], top[:, :], -1.0, None, ALU.mult).then_inc(shifted.sem, 1)
                        if main:
                            dve.wait_ge(weighed.sem, weighed.at(b, KT - 1))
                            dve.wait_ge(bT.filled, bT.full("V1", turn))
                            sums = psO[:, :].rearrange("p (k n) -> p k n", n=512)[:, :, 0:2 * VW]\
                                .rearrange("p k (g w) -> p k g w", w=VW)
                            dve.reciprocal(rden[:, :].rearrange("p (k g) -> p k g", g=2), sums[:, :, :, CD])\
                               .then_inc(rdenned.sem, 1)
                            dve.wait_ge(rdenned.sem, rdenned.at(b, 0))
                            dve.tensor_tensor(
                                a[:, :, :].rearrange("p (k g) w -> p k g w", g=2), sums[:, :, :, 0:CD],
                                rden[:, :].rearrange("p (k g) -> p k g", g=2)[:, :, :, None].to_broadcast([P, 4, 2, CD]),
                                ALU.mult).then_inc(out_taken.sem, 1)

                    if main:
                        dve.sem_inc(exped.sem, exped.primed)
                        dve.sem_inc(e_split.sem, e_split.primed)
                        dve.sem_inc(weighed.sem, weighed.primed)
                        dve.sem_inc(out_taken.sem, out_taken.primed)
                    else:
                        dve.memset(a[:, :, :], 0.0)
                        dve.memset(shift[:, :, :], 0.0)
                        dve.memset(c5[DH:DH + 1, :, :, :], 1.0)
                        dve.memset(ch[:, :, :, CD:VW], 1.0).then_inc(made, 1)
                    dve.sem_inc(bT.taken, 1)
                    dve.sem_inc(bM.taken, 1)
                    turns(dve, body)

        wo = sb("wo", [P, PR, D])
        wo_loaded, filled, taken = sem("wo_loaded"), sem("end_filled"), sem("end_taken")
        with ExitStack() as pctx, nc.Block() as block:
            bank = lambda what, n=1: pctx.enter_context(nc.psum_tensor(f"l1x_{what}_end", [P, n, 512], F32))
            psA, psB, psV, psX = bank("psA"), bank("psB"), bank("psV"), bank("psX", 2)
            proj = psX[:, :, :].rearrange("p a (t n) -> p (a t) n", n=D)

            @block.sync
            def _(sp):
                sp.dma_start(wo[:, :, :], d["L1_xattn_Wo"].rearrange("(c p) n -> p c n", p=P)).then_inc(wo_loaded, 16)

            @block.tensor
            def _(pe):
                for half in range(2):
                    if half:
                        pe.wait_ge(taken, 3 * half)
                    for ps, cols, rows in ((psA, slice(0, P), slice(0, P)), (psB, slice(P, CD), slice(0, CB))):
                        for g in range(4):
                            ins = pe.transpose(ps[rows, 0, g * P:(g + 1) * P], a[:, 4 * half + g, cols], core.ident[:, :])
                        ins.then_inc(filled, 1)
                    pe.wait_ge(taken, 3 * half + 2)
                    for k in range(8):
                        h = 8 * half + k
                        out = psV[halves[k % 2], 0, k // 2 * N:(k // 2 + 1) * N]
                        pe.matmul(out, wvA[:, h * DH:(h + 1) * DH], aT[:, 0, k * N:(k + 1) * N], start=True, stop=False)
                        ins = pe.matmul(out, wvB[:, h * DH:(h + 1) * DH], aT[0:CB, 1, k * N:(k + 1) * N],
                                        start=False, stop=True)
                    ins.then_inc(filled, 1)
                pe.wait_ge(taken, 6)
                pe.wait_ge(wo_loaded, 16)
                for t in range(TT):
                    for pr in range(PR):
                        ins = pe.matmul(proj[:, t, :], outT[:, pr, 1 + 2 * t:3 + 2 * t, :].rearrange("p b q -> p (b q)"),
                                        wo[:, pr, :], start=(pr == 0), stop=(pr == PR - 1))
                ins.then_inc(filled, 1)

            @block.vector
            def _(dve):
                for half in range(2):
                    dve.wait_ge(filled, 3 * half + 1)
                    dve.tensor_copy(aT[:, 0, :], psA[:, 0, :]).then_inc(taken, 1)
                    dve.wait_ge(filled, 3 * half + 2)
                    dve.tensor_copy(aT[0:CB, 1, :], psB[0:CB, 0, :]).then_inc(taken, 1)
                    dve.wait_ge(filled, 3 * half + 3)
                    dve.tensor_copy(outT[:, 4 * half:4 * half + 4, B, :],
                                    psV[:, 0, 0:4 * N].rearrange("p (k q) -> p k q", q=N)).then_inc(taken, 1)
                dve.wait_ge(filled, 7)
                dve.tensor_tensor(core.x[:, :, :], core.x[:, :, :], proj[:, :, :], ALU.add).then_inc(taken, 1)
                dve.wait_ge(taken, 7)


def norm(core, tag, inner=None):
    return lambda prefetch: stage_norm(core, tag, inner, prefetch)


STAGES = [
    lambda core: stage_l0_cross(core, norm(core, "n0")),
    lambda core: stage_l0_self(core, norm(core, "n1", ("L0_attn_gamma", None, False))),
    lambda core: stage_experts(core, norm(core, "n2", ("L0_ffn_ln_w", "L0_ffn_ln_b", True)),
                               "l0f", "L0_ffn_router_w", "c_l0_experts", E + 1, 4, True, 1),
    lambda core: stage_l1_cross(core, norm(core, "n3", ("L1_xattn_g_x", "L1_xattn_b_x", False))),
    lambda core: stage_l1_self(core, norm(core, "n4")),
    lambda core: stage_experts(core, norm(core, "n5"), "l1f", "c_l1_router", "c_l1_experts", E, 8, False, 2),
]


def perceiver_program(nc, dram, stages=STAGES):
    with ExitStack() as ctx:
        core = Core(nc, ctx, dram)
        stage_load(core)
        for stage in stages:
            stage(core)
            core.clear_sems()
        stage_store(core)


def _constants():
    import numpy as np
    c = {}
    c["c_ident"] = np.eye(P, dtype=np.float32)
    c["c_headmask"] = (np.arange(P)[:, None] // 16 == np.arange(8)[None, :]).astype(np.float32)
    slope = 2.0 ** (-2.0 ** (-(np.log2(H) - 3.0)))
    slopes = np.array([slope * slope ** h for h in range(H)], np.float32)
    rows, cols = np.arange(N)[:, None], np.arange(N + 2)[None, :]
    alibi = -np.abs(cols - (rows + 2)).astype(np.float32)[:, None, :] * slopes[None, :, None]
    alibi = np.where((cols > rows + 2)[:, None, :], np.float32(-BIG), alibi).astype(np.float32)
    places = np.concatenate([np.arange(0, H, 2), np.arange(1, H, 2)])
    c["c_alibi"] = np.concatenate([alibi, alibi], axis=0)[:, places, :]
    c["c_blockmask"] = (np.arange(2 * H)[:, None] // 2 == np.arange(H)[None, :]).astype(np.float32)
    c["c_memrows"] = (np.arange(P)[:, None] % 32 == np.arange(4)[None, :]).astype(np.float32)
    c["c_iota"] = np.tile(np.arange(E, dtype=np.float32), (P, 1))
    q = np.arange(P // 8)[None, :, None] % 8 * 8 + (np.arange(P) // H)[:, None, None]
    key = np.arange(N + 4)[None, None, :] - 4
    c["c_rowmask"] = np.where(key > q, np.float32(BIG), np.float32(0)).reshape(P, 4, -1)
    return c


def _layouts(inputs):
    import numpy as np
    a = {k: np.ascontiguousarray(v) for k, v in inputs.items()}
    ctx = a.pop("ctx_768")
    t = np.zeros((B + 1, CD, MP), np.float32)
    t[:B, :, :M] = ctx.transpose(0, 2, 1)
    a["c_ctxT"] = t
    rows = np.zeros((B + 1, MP, CD), np.float32)
    rows[:B, :M] = ctx
    a["c_ctx"] = rows
    a["c_l0x_wo"] = a.pop("L0_xattn_Wo").reshape(H // 2, 2, D // H, D).transpose(0, 2, 1, 3).reshape(P, 2, D)
    wkT = a.pop("L1_xattn_Wk").T
    a["c_wkT"] = np.concatenate([wkT, wkT[:, P:]], axis=1)
    null = a.pop("L0_attn_null_kv").reshape(H, 2, 2, 64)
    a["c_null_k"] = np.ascontiguousarray(null[:, :, 0]).reshape(2 * H, 64)
    nv = np.zeros((H, 2, H, 64), np.float32)
    for h in range(H):
        nv[h % 2 * (H // 2) + h // 2, :, h] = null[h, :, 1]
    a["c_null_v"] = nv.reshape(2 * H, H * 64)
    def first(w):
        e, _, f = w.shape
        return w.reshape(e, DC, P, f // P, P).transpose(0, 3, 2, 1, 4).reshape(e, f // P, P, DC * P)

    def last(w):
        e, f, _ = w.shape
        return w.reshape(e, f // P, P, D)

    with_shared = lambda many, one: np.concatenate([a.pop(many), a.pop(one)[None]])
    a["c_l0_experts"] = np.concatenate([first(with_shared("L0_ffn_gate_w", "L0_ffn_sh_gate")),
                                        first(with_shared("L0_ffn_up_w", "L0_ffn_sh_up")),
                                        last(with_shared("L0_ffn_down_w", "L0_ffn_sh_down"))], axis=-1)
    a["c_l1_experts"] = np.concatenate([first(a.pop("L1_ffn_w1").transpose(0, 2, 1)),
                                        last(a.pop("L1_ffn_w2").transpose(0, 2, 1))], axis=-1)
    for name in ("c_l0_experts", "c_l1_experts"):
        a[name] = np.concatenate([a[name], np.zeros_like(a[name][:1])])
    a["c_l1_router"] = np.ascontiguousarray(a.pop("L1_ffn_gate_w").T)
    def on_diagonal(w, row_of):
        out = np.zeros((8, H, 8, H), np.float32)
        for i in range(8):
            for g in range(H):
                out[i, row_of(g), i, :] = w[:, g]
        return out.reshape(P, P)

    a["c_pre"] = on_diagonal(a.pop("L1_attn_W_pre_th"), lambda g: g % 2 * (H // 2) + g // 2)
    a["c_post"] = on_diagonal(a.pop("L1_attn_W_post_th"), lambda g: g)
    mem_v = np.zeros((4, 32, H, 64), np.float32)
    mem_v[:, :4] = a.pop("L1_attn_mem_v").transpose(1, 0, 2)
    a["c_mem_v"] = mem_v.reshape(P, H, 64)
    a["c_head_scale"] = a.pop("L1_attn_head_scale_params").reshape(H)
    return a


def kernel(**inputs):
    import numpy as _np
    import concourse.bacc as _bacc
    from concourse.bass_utils import run_bass_kernel_spmd as _run

    nc = _bacc.Bacc("TRN2", target_bir_lowering=False, num_devices=1)
    arrays = {**_layouts(inputs), **_constants()}
    dram = {k: nc.dram_tensor(f"in_{k}", a.shape, mybir.dt.from_np(a.dtype), kind="ExternalInput").ap()
            for k, a in arrays.items()}
    dram["out"] = nc.dram_tensor("out_x", (B, N, D), F32, kind="ExternalOutput").ap()
    perceiver_program(nc, dram)
    r = _run(nc, [{f"in_{k}": a for k, a in arrays.items()}], core_ids=[0])
    return r.results[0]["out_x"]
```
